# Optimizing a Trainium2 kernel written in Bass

```python
import numpy as np
import jax
import jax.numpy as jnp

def _softmax(x, axis=-1):
    return jax.nn.softmax(x, axis=axis)

def _gelu(x):
    return jax.nn.gelu(x, approximate=True)

def _silu(x):
    return jax.nn.silu(x)

def _sigmoid(x):
    return jax.nn.sigmoid(x)

def _layernorm(x, axis=-1, eps=1e-05):
    m = jnp.mean(x, axis=axis, keepdims=True)
    v = jnp.var(x, axis=axis, keepdims=True)
    return (x - m) / jnp.sqrt(v + eps)

def _scatter_add(tgt, idx, src, axis=0):
    return tgt.at[idx].add(src)

def _segment_sum(src, seg, n):
    return jax.ops.segment_sum(src, seg, n)
kernel_name = 'mk_flamingo_gated_d4_seqx_r4_ca3a4e'

def setup_inputs(seed: int=0):
    np.random.seed(seed)
    _w = jnp.asarray

    def _rec_inputs():
        import jax
        import jax.numpy as jnp
        _rk = jax.random.key(seed)
        x = -0.0002928 + 1 * jax.random.normal(jax.random.fold_in(_rk, 1), (2, 1024, 256), jnp.float32)
        _lenS = 1024 - jax.random.randint(jax.random.fold_in(_rk, 7), (2,), 0, max(1, 1024 // 4) + 1, jnp.int32)
        _lenS2 = 64 - jax.random.randint(jax.random.fold_in(_rk, 8), (2,), 0, max(1, 64 // 4) + 1, jnp.int32)
        _ctx_512P = jax.random.normal(jax.random.fold_in(_rk, 11), (2, 16, 128), jnp.float32)
        _ctx_512c = jax.random.dirichlet(jax.random.fold_in(_rk, 511), 0.3 * jnp.ones((16,), jnp.float32), (2, 64))
        _ctx_512t = jnp.einsum('bsk,bkd->bsd', _ctx_512c, _ctx_512P)
        _ctx_512t = _ctx_512t * jax.lax.rsqrt(jnp.mean(jnp.square(_ctx_512t)) + 1e-12) * 0.953939
        ctx_512 = -1.52775e-05 + 0.999936 * (_ctx_512t + 0.3 * jax.random.normal(jax.random.fold_in(_rk, 611), (2, 64, 128), jnp.float32))
        _g = jax.random.normal(jax.random.fold_in(_rk, 9001), (2, 4), jnp.float32)
        _g = jnp.sign(_g) * jnp.maximum(jnp.abs(_g), 1.0) + (_g == 0) * 1.0
        g_xattn = _g[0]
        g_ffn = _g[1]
        return (x, ctx_512, g_xattn, g_ffn)
    x, ctx_512, g_xattn, g_ffn = _rec_inputs()

    def _L0_xattn_setup():
        import jax, jax.numpy as jnp
        import numpy as np
        NUM_HEADS = 16
        HEAD_DIM = 64
        Q_DIM = 256
        KV_DIM = 128
        INNER = NUM_HEADS * HEAD_DIM
        key = jax.random.key(seed)
        ks = jax.random.split(key, 7)
        B, N, M = (32, 128, 512)
        q = jax.random.normal(ks[0], (B, N, Q_DIM), dtype=jnp.float32)
        kv = jax.random.normal(ks[1], (B, M, KV_DIM), dtype=jnp.float32)
        Wq = jax.random.normal(ks[2], (Q_DIM, INNER), dtype=jnp.float32) / np.sqrt(Q_DIM)
        Wk = jax.random.normal(ks[3], (KV_DIM, INNER), dtype=jnp.float32) / np.sqrt(KV_DIM)
        Wv = jax.random.normal(ks[4], (KV_DIM, INNER), dtype=jnp.float32) / np.sqrt(KV_DIM)
        Wo = jax.random.normal(ks[5], (INNER, Q_DIM), dtype=jnp.float32) / np.sqrt(INNER)
        bo = jax.random.normal(ks[6], (Q_DIM,), dtype=jnp.float32) * 0.01
        return {'q': q, 'kv': kv, 'Wq': Wq, 'Wk': Wk, 'Wv': Wv, 'Wo': Wo, 'bo': bo}
    _L0_xattn_all = _L0_xattn_setup()
    _L0_xattn_in = {k: v for k, v in _L0_xattn_all.items() if k in ('Wq', 'Wk', 'Wv', 'Wo', 'bo')}
    del _L0_xattn_all

    def _L0_ffn_setup():
        import math
        import jax, jax.numpy as jnp
        import numpy as np
        B, S, D, F, E = (8, 512, 256, 1024, 8)
        CAPACITY_FACTOR = 1.0
        key = jax.random.key(seed)
        k1, k2, k3, k4 = jax.random.split(key, 4)
        x = jax.random.normal(k1, (B, S, D), dtype=jnp.float32)
        Wr = jax.random.normal(k2, (D, E), dtype=jnp.float32) * (1.0 / math.sqrt(D))
        W1 = jax.random.normal(k3, (E, D, F), dtype=jnp.float32) * (1.0 / math.sqrt(D))
        W2 = jax.random.normal(k4, (E, F, D), dtype=jnp.float32) * (1.0 / math.sqrt(F))
        return {'x': x, 'Wr': Wr, 'W1': W1, 'W2': W2}
    _L0_ffn_all = _L0_ffn_setup()
    _L0_ffn_in = {k: v for k, v in _L0_ffn_all.items() if k in ('Wr', 'W1', 'W2')}
    del _L0_ffn_all

    def _L1_xattn_setup():
        import jax, jax.numpy as jnp
        import numpy as np
        B, LQ, LK = (8, 512, 512)
        QD, KD, VD = (256, 128, 128)
        key = jax.random.key(seed)
        ks = jax.random.split(key, 9)
        s = 0.02
        return {'query': jax.random.normal(ks[0], (B, LQ, QD), jnp.float32), 'key': jax.random.normal(ks[1], (B, LK, KD), jnp.float32), 'value': jax.random.normal(ks[2], (B, LK, VD), jnp.float32), 'Wq': jax.random.normal(ks[3], (QD, QD), jnp.float32) * s, 'bq': jnp.zeros((QD,), jnp.float32), 'Wk': jax.random.normal(ks[4], (KD, QD), jnp.float32) * s, 'bk': jnp.zeros((QD,), jnp.float32), 'Wv': jax.random.normal(ks[5], (VD, QD), jnp.float32) * s, 'bv': jnp.zeros((QD,), jnp.float32)}
    _L1_xattn_all = _L1_xattn_setup()
    _L1_xattn_in = {k: v for k, v in _L1_xattn_all.items() if k in ('Wq', 'bq', 'Wk', 'bk', 'Wv', 'bv')}
    del _L1_xattn_all

    def _L1_ffn_setup():
        import jax, jax.numpy as jnp
        import numpy as np
        B, T, D, R, E = (32, 256, 256, 64, 8)
        key = jax.random.key(seed)
        ks = jax.random.split(key, 12)
        inp = {}
        inp['x'] = jax.random.normal(ks[0], (B, T, D), dtype=jnp.float32)
        inp['base_W'] = jax.random.normal(ks[1], (D, D), dtype=jnp.float32) * (1.0 / np.sqrt(D))
        inp['base_b'] = jax.random.normal(ks[2], (D,), dtype=jnp.float32) * 0.01
        inp['disc_mu'] = jax.random.normal(ks[3], (E, D), dtype=jnp.float32) * 0.5
        inp['disc_sigma'] = jax.random.uniform(ks[4], (E, D), dtype=jnp.float32, minval=0.5, maxval=1.5)
        inp['down_W'] = jax.random.normal(ks[5], (E, D, R), dtype=jnp.float32) * (1.0 / np.sqrt(D))
        inp['down_b'] = jax.random.normal(ks[6], (E, R), dtype=jnp.float32) * 0.01
        inp['up_W'] = jax.random.normal(ks[7], (E, R, D), dtype=jnp.float32) * (1.0 / np.sqrt(R))
        inp['up_b'] = jax.random.normal(ks[8], (E, D), dtype=jnp.float32) * 0.01
        inp['conv_W'] = jax.random.normal(ks[9], (E, D, D), dtype=jnp.float32) * 0.02
        inp['conv_b'] = jax.random.normal(ks[10], (E, D), dtype=jnp.float32) * 0.01
        return inp
    _L1_ffn_all = _L1_ffn_setup()
    _L1_ffn_in = {k: v for k, v in _L1_ffn_all.items() if k in ('base_W', 'base_b', 'disc_mu', 'disc_sigma', 'down_W', 'down_b', 'up_W', 'up_b', 'conv_W', 'conv_b')}
    del _L1_ffn_all

    def _L2_xattn_setup():
        import jax, jax.numpy as jnp
        import numpy as np
        DIM = 256
        LATENT_DIM = 128
        NUM_HEADS = 16
        HEAD_DIM = DIM // NUM_HEADS
        SCALE = HEAD_DIM ** (-0.5)
        key = jax.random.key(seed)
        k1, k2, k3, k4, k5 = jax.random.split(key, 5)
        B, xN, zN = (2, 512, 512)
        x = jax.random.normal(k1, (B, xN, DIM), dtype=jnp.float32)
        z = jax.random.normal(k2, (B, zN, LATENT_DIM), dtype=jnp.float32)
        Wq = jax.random.normal(k3, (DIM, DIM), dtype=jnp.float32) * DIM ** (-0.5)
        Wkv = jax.random.normal(k4, (2 * DIM, LATENT_DIM), dtype=jnp.float32) * LATENT_DIM ** (-0.5)
        Wo = jax.random.normal(k5, (DIM, DIM), dtype=jnp.float32) * DIM ** (-0.5)
        return {'x': x, 'z': z, 'Wq': Wq, 'Wkv': Wkv, 'Wo': Wo}
    _L2_xattn_all = _L2_xattn_setup()
    _L2_xattn_in = {k: v for k, v in _L2_xattn_all.items() if k in ('Wq', 'Wkv', 'Wo')}
    del _L2_xattn_all

    def _L2_ffn_setup():
        import jax, jax.numpy as jnp
        import numpy as np
        D_MODEL, D_FF, RANK = (256, 1024, 64)
        B, S = (4, 1024)
        key = jax.random.key(seed)
        ks = jax.random.split(key, 7)
        return {'x': jax.random.normal(ks[0], (B, S, D_MODEL), dtype=jnp.float32), 'U1': jax.random.normal(ks[1], (D_MODEL, RANK), dtype=jnp.float32) * 0.02, 'V1': jax.random.normal(ks[2], (RANK, D_FF), dtype=jnp.float32) * 0.02, 'b1': jnp.zeros((D_FF,), dtype=jnp.float32), 'U2': jax.random.normal(ks[3], (D_FF, RANK), dtype=jnp.float32) * 0.02, 'V2': jax.random.normal(ks[4], (RANK, D_MODEL), dtype=jnp.float32) * 0.02, 'b2': jnp.zeros((D_MODEL,), dtype=jnp.float32)}
    _L2_ffn_all = _L2_ffn_setup()
    _L2_ffn_in = {k: v for k, v in _L2_ffn_all.items() if k in ('U1', 'V1', 'b1', 'U2', 'V2', 'b2')}
    del _L2_ffn_all

    def _L3_xattn_setup():
        import jax, jax.numpy as jnp
        import numpy as np
        H, D, C1, C2, S, M, B, W = (16, 32, 256, 128, 512, 128, 2, 4)

        def _ln(x, g, b):
            m = jnp.mean(x, -1, keepdims=True)
            v = jnp.var(x, -1, keepdims=True)
            return (x - m) * jax.lax.rsqrt(v + 1e-05) * g + b

        def _mha(x, y, wq, wk, wv, li1_w, li1_b, lnx_g, lnx_b, lny_g, lny_b, ln3_g, ln3_b, li2_w, li2_b, li3_w, li3_b, causal):
            xn = _ln(x, lnx_g, lnx_b)
            yn = _ln(y, lny_g, lny_b)
            q = jnp.einsum('bsc,hcd->bhsd', xn, wq)
            k = jnp.einsum('btc,hcd->bhtd', yn, wk)
            v = jnp.einsum('btc,hcd->bhtd', yn, wv)
            a = jax.nn.softmax(jnp.einsum('bhsd,bhtd->bhst', q, k) * D ** (-0.5), axis=-1)
            if causal:
                s, t = (a.shape[-2], a.shape[-1])
                mask = (jnp.arange(t)[None, :] > jnp.arange(s)[:, None]).astype(a.dtype)
                a = a * mask
            o = jnp.einsum('bhst,bhtd->bhsd', a, v)
            o = o.transpose(0, 2, 1, 3).reshape(x.shape[0], x.shape[1], H * D)
            x_out = x + o @ li1_w + li1_b
            h = jax.nn.gelu(_ln(x_out, ln3_g, ln3_b) @ li2_w + li2_b, approximate=False)
            return x_out + h @ li3_w + li3_b
        key = jax.random.key(seed)
        ks = iter(jax.random.split(key, 64))

        def w(shape, scale=0.02):
            return jax.random.normal(next(ks), shape, jnp.float32) * scale
        inp = {'xx': jax.random.normal(next(ks), (B, S, C1), jnp.float32), 'ee': jax.random.normal(next(ks), (B, M, C2), jnp.float32), 'ln1_g': jnp.ones(C1, jnp.float32), 'ln1_b': jnp.zeros(C1, jnp.float32), 'ln2_g': jnp.ones(C1, jnp.float32), 'ln2_b': jnp.zeros(C1, jnp.float32)}
        for pfx, cy in (('a1', C1), ('a2', C2)):
            inp[pfx + '_wq'] = w((H, C1, D))
            inp[pfx + '_wk'] = w((H, cy, D))
            inp[pfx + '_wv'] = w((H, cy, D))
            inp[pfx + '_li1_w'] = w((H * D, C1))
            inp[pfx + '_li1_b'] = jnp.zeros(C1, jnp.float32)
            inp[pfx + '_lnx_g'] = jnp.ones(C1, jnp.float32)
            inp[pfx + '_lnx_b'] = jnp.zeros(C1, jnp.float32)
            inp[pfx + '_lny_g'] = jnp.ones(cy, jnp.float32)
            inp[pfx + '_lny_b'] = jnp.zeros(cy, jnp.float32)
            inp[pfx + '_ln3_g'] = jnp.ones(C1, jnp.float32)
            inp[pfx + '_ln3_b'] = jnp.zeros(C1, jnp.float32)
            inp[pfx + '_li2_w'] = w((C1, C1 * W))
            inp[pfx + '_li2_b'] = jnp.zeros(C1 * W, jnp.float32)
            inp[pfx + '_li3_w'] = w((C1 * W, C1))
            inp[pfx + '_li3_b'] = jnp.zeros(C1, jnp.float32)
        inp['training'] = 0
        return inp
    _L3_xattn_all = _L3_xattn_setup()
    _L3_xattn_in = {k: v for k, v in _L3_xattn_all.items() if k in ('ln1_g', 'ln1_b', 'ln2_g', 'ln2_b', 'a1_wq', 'a1_wk', 'a1_wv', 'a1_li1_w', 'a1_li1_b', 'a1_lnx_g', 'a1_lnx_b', 'a1_lny_g', 'a1_lny_b', 'a1_ln3_g', 'a1_ln3_b', 'a1_li2_w', 'a1_li2_b', 'a1_li3_w', 'a1_li3_b', 'a2_wq', 'a2_wk', 'a2_wv', 'a2_li1_w', 'a2_li1_b', 'a2_lnx_g', 'a2_lnx_b', 'a2_lny_g', 'a2_lny_b', 'a2_ln3_g', 'a2_ln3_b', 'a2_li2_w', 'a2_li2_b', 'a2_li3_w', 'a2_li3_b')}
    del _L3_xattn_all

    def _L3_ffn_setup():
        import jax, jax.numpy as jnp
        import numpy as np
        B, S, D, F, E, K = (4, 512, 256, 1024, 8, 2)
        FS = 256
        LN_EPS = 1e-05

        def _swiglu(x, gu_w, dn_w):
            gate, up = jnp.split(x @ gu_w, 2, axis=-1)
            gate = jnp.clip(gate, -10.0, 10.0)
            return jax.nn.silu(gate) * up @ dn_w
        key = jax.random.key(seed)
        ks = jax.random.split(key, 6)
        s = 0.02
        return {'x': jax.random.normal(ks[0], (B, S, D), jnp.float32), 'ln_gamma': jnp.ones((D,), jnp.float32), 'ln_beta': jnp.zeros((D,), jnp.float32), 'router_w': jax.random.normal(ks[1], (D, E), jnp.float32) * s, 'gate_up_w': jax.random.normal(ks[2], (E, D, 2 * F), jnp.float32) * s, 'down_w': jax.random.normal(ks[3], (E, F, D), jnp.float32) * s, 'shared_gate_up_w': jax.random.normal(ks[4], (D, 2 * FS), jnp.float32) * s, 'shared_down_w': jax.random.normal(ks[5], (FS, D), jnp.float32) * s}
    _L3_ffn_all = _L3_ffn_setup()
    _L3_ffn_in = {k: v for k, v in _L3_ffn_all.items() if k in ('ln_gamma', 'ln_beta', 'router_w', 'gate_up_w', 'down_w', 'shared_gate_up_w', 'shared_down_w')}
    del _L3_ffn_all
    return {'x': x, 'ctx_512': ctx_512, 'g_xattn': g_xattn, 'g_ffn': g_ffn, 'L0_xattn_Wq': _L0_xattn_in['Wq'], 'L0_xattn_Wk': _L0_xattn_in['Wk'], 'L0_xattn_Wv': _L0_xattn_in['Wv'], 'L0_xattn_Wo': _L0_xattn_in['Wo'], 'L0_xattn_bo': _L0_xattn_in['bo'], 'L0_ffn_Wr': _L0_ffn_in['Wr'], 'L0_ffn_W1': _L0_ffn_in['W1'], 'L0_ffn_W2': _L0_ffn_in['W2'], 'L1_xattn_Wq': _L1_xattn_in['Wq'], 'L1_xattn_bq': _L1_xattn_in['bq'], 'L1_xattn_Wk': _L1_xattn_in['Wk'], 'L1_xattn_bk': _L1_xattn_in['bk'], 'L1_xattn_Wv': _L1_xattn_in['Wv'], 'L1_xattn_bv': _L1_xattn_in['bv'], 'L1_ffn_base_W': _L1_ffn_in['base_W'], 'L1_ffn_base_b': _L1_ffn_in['base_b'], 'L1_ffn_disc_mu': _L1_ffn_in['disc_mu'], 'L1_ffn_disc_sigma': _L1_ffn_in['disc_sigma'], 'L1_ffn_down_W': _L1_ffn_in['down_W'], 'L1_ffn_down_b': _L1_ffn_in['down_b'], 'L1_ffn_up_W': _L1_ffn_in['up_W'], 'L1_ffn_up_b': _L1_ffn_in['up_b'], 'L1_ffn_conv_W': _L1_ffn_in['conv_W'], 'L1_ffn_conv_b': _L1_ffn_in['conv_b'], 'L2_xattn_Wq': _L2_xattn_in['Wq'], 'L2_xattn_Wkv': _L2_xattn_in['Wkv'], 'L2_xattn_Wo': _L2_xattn_in['Wo'], 'L2_ffn_U1': _L2_ffn_in['U1'], 'L2_ffn_V1': _L2_ffn_in['V1'], 'L2_ffn_b1': _L2_ffn_in['b1'], 'L2_ffn_U2': _L2_ffn_in['U2'], 'L2_ffn_V2': _L2_ffn_in['V2'], 'L2_ffn_b2': _L2_ffn_in['b2'], 'L3_xattn_ln1_g': _L3_xattn_in['ln1_g'], 'L3_xattn_ln1_b': _L3_xattn_in['ln1_b'], 'L3_xattn_ln2_g': _L3_xattn_in['ln2_g'], 'L3_xattn_ln2_b': _L3_xattn_in['ln2_b'], 'L3_xattn_a1_wq': _L3_xattn_in['a1_wq'], 'L3_xattn_a1_wk': _L3_xattn_in['a1_wk'], 'L3_xattn_a1_wv': _L3_xattn_in['a1_wv'], 'L3_xattn_a1_li1_w': _L3_xattn_in['a1_li1_w'], 'L3_xattn_a1_li1_b': _L3_xattn_in['a1_li1_b'], 'L3_xattn_a1_lnx_g': _L3_xattn_in['a1_lnx_g'], 'L3_xattn_a1_lnx_b': _L3_xattn_in['a1_lnx_b'], 'L3_xattn_a1_lny_g': _L3_xattn_in['a1_lny_g'], 'L3_xattn_a1_lny_b': _L3_xattn_in['a1_lny_b'], 'L3_xattn_a1_ln3_g': _L3_xattn_in['a1_ln3_g'], 'L3_xattn_a1_ln3_b': _L3_xattn_in['a1_ln3_b'], 'L3_xattn_a1_li2_w': _L3_xattn_in['a1_li2_w'], 'L3_xattn_a1_li2_b': _L3_xattn_in['a1_li2_b'], 'L3_xattn_a1_li3_w': _L3_xattn_in['a1_li3_w'], 'L3_xattn_a1_li3_b': _L3_xattn_in['a1_li3_b'], 'L3_xattn_a2_wq': _L3_xattn_in['a2_wq'], 'L3_xattn_a2_wk': _L3_xattn_in['a2_wk'], 'L3_xattn_a2_wv': _L3_xattn_in['a2_wv'], 'L3_xattn_a2_li1_w': _L3_xattn_in['a2_li1_w'], 'L3_xattn_a2_li1_b': _L3_xattn_in['a2_li1_b'], 'L3_xattn_a2_lnx_g': _L3_xattn_in['a2_lnx_g'], 'L3_xattn_a2_lnx_b': _L3_xattn_in['a2_lnx_b'], 'L3_xattn_a2_lny_g': _L3_xattn_in['a2_lny_g'], 'L3_xattn_a2_lny_b': _L3_xattn_in['a2_lny_b'], 'L3_xattn_a2_ln3_g': _L3_xattn_in['a2_ln3_g'], 'L3_xattn_a2_ln3_b': _L3_xattn_in['a2_ln3_b'], 'L3_xattn_a2_li2_w': _L3_xattn_in['a2_li2_w'], 'L3_xattn_a2_li2_b': _L3_xattn_in['a2_li2_b'], 'L3_xattn_a2_li3_w': _L3_xattn_in['a2_li3_w'], 'L3_xattn_a2_li3_b': _L3_xattn_in['a2_li3_b'], 'L3_ffn_ln_gamma': _L3_ffn_in['ln_gamma'], 'L3_ffn_ln_beta': _L3_ffn_in['ln_beta'], 'L3_ffn_router_w': _L3_ffn_in['router_w'], 'L3_ffn_gate_up_w': _L3_ffn_in['gate_up_w'], 'L3_ffn_down_w': _L3_ffn_in['down_w'], 'L3_ffn_shared_gate_up_w': _L3_ffn_in['shared_gate_up_w'], 'L3_ffn_shared_down_w': _L3_ffn_in['shared_down_w']}

def reference(x, ctx_512, g_xattn, g_ffn, L0_xattn_Wq, L0_xattn_Wk, L0_xattn_Wv, L0_xattn_Wo, L0_xattn_bo, L0_ffn_Wr, L0_ffn_W1, L0_ffn_W2, L1_xattn_Wq, L1_xattn_bq, L1_xattn_Wk, L1_xattn_bk, L1_xattn_Wv, L1_xattn_bv, L1_ffn_base_W, L1_ffn_base_b, L1_ffn_disc_mu, L1_ffn_disc_sigma, L1_ffn_down_W, L1_ffn_down_b, L1_ffn_up_W, L1_ffn_up_b, L1_ffn_conv_W, L1_ffn_conv_b, L2_xattn_Wq, L2_xattn_Wkv, L2_xattn_Wo, L2_ffn_U1, L2_ffn_V1, L2_ffn_b1, L2_ffn_U2, L2_ffn_V2, L2_ffn_b2, L3_xattn_ln1_g, L3_xattn_ln1_b, L3_xattn_ln2_g, L3_xattn_ln2_b, L3_xattn_a1_wq, L3_xattn_a1_wk, L3_xattn_a1_wv, L3_xattn_a1_li1_w, L3_xattn_a1_li1_b, L3_xattn_a1_lnx_g, L3_xattn_a1_lnx_b, L3_xattn_a1_lny_g, L3_xattn_a1_lny_b, L3_xattn_a1_ln3_g, L3_xattn_a1_ln3_b, L3_xattn_a1_li2_w, L3_xattn_a1_li2_b, L3_xattn_a1_li3_w, L3_xattn_a1_li3_b, L3_xattn_a2_wq, L3_xattn_a2_wk, L3_xattn_a2_wv, L3_xattn_a2_li1_w, L3_xattn_a2_li1_b, L3_xattn_a2_lnx_g, L3_xattn_a2_lnx_b, L3_xattn_a2_lny_g, L3_xattn_a2_lny_b, L3_xattn_a2_ln3_g, L3_xattn_a2_ln3_b, L3_xattn_a2_li2_w, L3_xattn_a2_li2_b, L3_xattn_a2_li3_w, L3_xattn_a2_li3_b, L3_ffn_ln_gamma, L3_ffn_ln_beta, L3_ffn_router_w, L3_ffn_gate_up_w, L3_ffn_down_w, L3_ffn_shared_gate_up_w, L3_ffn_shared_down_w):
    import jax
    import jax.numpy as jnp

    def _L0_xattn_ref(q, kv, Wq, Wk, Wv, Wo, bo):
        import jax, jax.numpy as jnp
        import numpy as np
        NUM_HEADS = 16
        HEAD_DIM = 64
        Q_DIM = 256
        KV_DIM = 128
        INNER = NUM_HEADS * HEAD_DIM
        B, N, _ = q.shape
        M = kv.shape[1]
        scale = HEAD_DIM ** (-0.5)
        qh = (q @ Wq).reshape(B, N, NUM_HEADS, HEAD_DIM).transpose(0, 2, 1, 3)
        kh = (kv @ Wk).reshape(B, M, NUM_HEADS, HEAD_DIM).transpose(0, 2, 1, 3)
        vh = (kv @ Wv).reshape(B, M, NUM_HEADS, HEAD_DIM).transpose(0, 2, 1, 3)
        scores = jnp.einsum('bhnd,bhmd->bhnm', qh, kh) * scale
        attn = jax.nn.softmax(scores, axis=-1)
        out = jnp.einsum('bhnm,bhmd->bhnd', attn, vh)
        out = out.transpose(0, 2, 1, 3).reshape(B, N, INNER)
        return out @ Wo + bo

    def _L0_ffn_ref(x, Wr, W1, W2):
        import math
        import jax, jax.numpy as jnp
        import numpy as np
        B, S, D, F, E = (8, 512, 256, 1024, 8)
        CAPACITY_FACTOR = 1.0
        b, s, d = x.shape
        t = b * s
        cap = max(math.ceil(t * CAPACITY_FACTOR / E), 1)
        xf = x.reshape(t, d)
        probs = jax.nn.softmax(xf.astype(jnp.float32) @ Wr, axis=-1)
        eidx = jnp.argmax(probs, axis=-1)
        p_tok = jnp.take_along_axis(probs, eidx[:, None], axis=1)[:, 0]
        onehot = jax.nn.one_hot(eidx, E, dtype=jnp.int32)
        rank_all = jnp.cumsum(onehot, axis=0) - onehot
        rank = jnp.take_along_axis(rank_all, eidx[:, None], axis=1)[:, 0]
        keep = rank < cap
        slot = jnp.where(keep, rank, cap)
        dispatch = jnp.zeros((E, cap + 1), dtype=jnp.int32).at[eidx, slot].set(jnp.arange(t, dtype=jnp.int32))
        valid = jnp.zeros((E, cap + 1), dtype=bool).at[eidx, slot].set(keep)
        dispatch = dispatch[:, :cap]
        valid = valid[:, :cap]
        xe = xf[dispatch]
        h = jnp.maximum(jnp.einsum('ecd,edf->ecf', xe, W1), 0.0)
        ye = jnp.einsum('ecf,efd->ecd', h, W2)
        pe = p_tok[dispatch]
        ye = ye * (pe * valid.astype(ye.dtype))[:, :, None]
        y = jnp.zeros((t, d), dtype=x.dtype).at[dispatch.reshape(-1)].add(ye.reshape(E * cap, d).astype(x.dtype))
        return y.reshape(b, s, d)

    def _L1_xattn_ref(query, key, value, Wq, bq, Wk, bk, Wv, bv):
        import jax, jax.numpy as jnp
        import numpy as np
        B, LQ, LK = (8, 512, 512)
        QD, KD, VD = (256, 128, 128)
        q = jnp.einsum('bld,de->ble', query, Wq) + bq
        k = jnp.einsum('bld,de->ble', key, Wk) + bk
        v = jnp.einsum('bld,de->ble', value, Wv) + bv
        scores = jnp.einsum('bqe,bke->bqk', q, k)
        attn = jax.nn.softmax(scores, axis=-1)
        out = jnp.einsum('bqk,bke->bqe', attn, v)
        return out

    def _L1_ffn_ref(x, base_W, base_b, disc_mu, disc_sigma, down_W, down_b, up_W, up_b, conv_W, conv_b):
        import jax, jax.numpy as jnp
        import numpy as np
        B, T, D, R, E = (32, 256, 256, 64, 8)
        base = jnp.einsum('btd,od->bto', x, base_W) + base_b
        m1 = x.mean(axis=1)
        m2 = (x * x).mean(axis=1)
        inv_var = 1.0 / (disc_sigma * disc_sigma)
        losses = (jnp.einsum('bd,ed->eb', m2, inv_var) - 2.0 * jnp.einsum('bd,ed->eb', m1, disc_mu * inv_var) + jnp.sum(disc_mu * disc_mu * inv_var, axis=1)[:, None]) / D
        idx = jnp.argmin(losses, axis=0)
        Wd, bd = (down_W[idx], down_b[idx])
        Wu, bu = (up_W[idx], up_b[idx])
        Wc, bc = (conv_W[idx], conv_b[idx])
        h = jax.nn.relu(jnp.einsum('btd,bdr->btr', x, Wd) + bd[:, None, :])
        a = jnp.einsum('btr,brd->btd', h, Wu) + bu[:, None, :]
        y = jnp.einsum('btd,bod->bto', a, Wc) + bc[:, None, :]
        return base + y

    def _L2_xattn_ref(x, z, Wq, Wkv, Wo):
        import jax, jax.numpy as jnp
        import numpy as np
        DIM = 256
        LATENT_DIM = 128
        NUM_HEADS = 16
        HEAD_DIM = DIM // NUM_HEADS
        SCALE = HEAD_DIM ** (-0.5)
        B, xN, _ = x.shape
        _, zN, _ = z.shape
        Q = (x @ Wq.T).reshape(B, xN, NUM_HEADS, HEAD_DIM)
        KV = (z @ Wkv.T).reshape(B, zN, 2, NUM_HEADS, HEAD_DIM)
        K = KV[:, :, 0]
        V = KV[:, :, 1]
        attn = jnp.einsum('bqhd,bkhd->bhqk', Q, K) * SCALE
        attn = jax.nn.softmax(attn, axis=-1)
        O = jnp.einsum('bhqk,bkhd->bqhd', attn, V).reshape(B, xN, DIM)
        return O @ Wo.T

    def _L2_ffn_ref(x, U1, V1, b1, U2, V2, b2):
        import jax, jax.numpy as jnp
        import numpy as np
        D_MODEL, D_FF, RANK = (256, 1024, 64)
        B, S = (4, 1024)
        P = jnp.einsum('bsd,dr->bsr', x, U1)
        H = jax.nn.gelu(jnp.einsum('bsr,rf->bsf', P, V1) + b1)
        Q = jnp.einsum('bsf,fr->bsr', H, U2)
        return jnp.einsum('bsr,rd->bsd', Q, V2) + b2

    def _L3_xattn_ref(xx, ee, ln1_g, ln1_b, ln2_g, ln2_b, a1_wq, a1_wk, a1_wv, a1_li1_w, a1_li1_b, a1_lnx_g, a1_lnx_b, a1_lny_g, a1_lny_b, a1_ln3_g, a1_ln3_b, a1_li2_w, a1_li2_b, a1_li3_w, a1_li3_b, a2_wq, a2_wk, a2_wv, a2_li1_w, a2_li1_b, a2_lnx_g, a2_lnx_b, a2_lny_g, a2_lny_b, a2_ln3_g, a2_ln3_b, a2_li2_w, a2_li2_b, a2_li3_w, a2_li3_b, training):
        import jax, jax.numpy as jnp
        import numpy as np
        H, D, C1, C2, S, M, B, W = (16, 32, 256, 128, 512, 128, 2, 4)

        def _ln(x, g, b):
            m = jnp.mean(x, -1, keepdims=True)
            v = jnp.var(x, -1, keepdims=True)
            return (x - m) * jax.lax.rsqrt(v + 1e-05) * g + b

        def _mha(x, y, wq, wk, wv, li1_w, li1_b, lnx_g, lnx_b, lny_g, lny_b, ln3_g, ln3_b, li2_w, li2_b, li3_w, li3_b, causal):
            xn = _ln(x, lnx_g, lnx_b)
            yn = _ln(y, lny_g, lny_b)
            q = jnp.einsum('bsc,hcd->bhsd', xn, wq)
            k = jnp.einsum('btc,hcd->bhtd', yn, wk)
            v = jnp.einsum('btc,hcd->bhtd', yn, wv)
            a = jax.nn.softmax(jnp.einsum('bhsd,bhtd->bhst', q, k) * D ** (-0.5), axis=-1)
            if causal:
                s, t = (a.shape[-2], a.shape[-1])
                mask = (jnp.arange(t)[None, :] > jnp.arange(s)[:, None]).astype(a.dtype)
                a = a * mask
            o = jnp.einsum('bhst,bhtd->bhsd', a, v)
            o = o.transpose(0, 2, 1, 3).reshape(x.shape[0], x.shape[1], H * D)
            x_out = x + o @ li1_w + li1_b
            h = jax.nn.gelu(_ln(x_out, ln3_g, ln3_b) @ li2_w + li2_b, approximate=False)
            return x_out + h @ li3_w + li3_b
        x = _ln(xx, ln1_g, ln1_b)
        x = x + _mha(x, x, a1_wq, a1_wk, a1_wv, a1_li1_w, a1_li1_b, a1_lnx_g, a1_lnx_b, a1_lny_g, a1_lny_b, a1_ln3_g, a1_ln3_b, a1_li2_w, a1_li2_b, a1_li3_w, a1_li3_b, causal=True)
        x = _ln(x, ln2_g, ln2_b)
        return x + _mha(x, ee, a2_wq, a2_wk, a2_wv, a2_li1_w, a2_li1_b, a2_lnx_g, a2_lnx_b, a2_lny_g, a2_lny_b, a2_ln3_g, a2_ln3_b, a2_li2_w, a2_li2_b, a2_li3_w, a2_li3_b, causal=False)

    def _L3_ffn_ref(x, ln_gamma, ln_beta, router_w, gate_up_w, down_w, shared_gate_up_w, shared_down_w):
        import jax, jax.numpy as jnp
        import numpy as np
        B, S, D, F, E, K = (4, 512, 256, 1024, 8, 2)
        FS = 256
        LN_EPS = 1e-05

        def _swiglu(x, gu_w, dn_w):
            gate, up = jnp.split(x @ gu_w, 2, axis=-1)
            gate = jnp.clip(gate, -10.0, 10.0)
            return jax.nn.silu(gate) * up @ dn_w
        b, s, d = x.shape
        xf = x.reshape(-1, d)
        mu = jnp.mean(xf, axis=-1, keepdims=True)
        var = jnp.var(xf, axis=-1, keepdims=True)
        xn = (xf - mu) * jax.lax.rsqrt(var + LN_EPS) * ln_gamma + ln_beta
        logits = xn @ router_w
        probs = jax.nn.softmax(logits, axis=-1)
        topv, topi = jax.lax.top_k(probs, K)
        topv = topv / jnp.sum(topv, axis=-1, keepdims=True)
        comb = jnp.sum(jax.nn.one_hot(topi, E, dtype=xn.dtype) * topv[..., None], axis=1)
        out = jnp.zeros_like(xf)
        for e in range(E):
            out = out + comb[:, e:e + 1] * _swiglu(xn, gate_up_w[e], down_w[e])
        out = out + _swiglu(xn, shared_gate_up_w, shared_down_w)
        return out.reshape(b, s, d)
    x = x + jnp.tanh(g_xattn[0]) * _L0_xattn_ref(_layernorm(x, axis=-1), ctx_512, L0_xattn_Wq, L0_xattn_Wk, L0_xattn_Wv, L0_xattn_Wo, L0_xattn_bo)
    x = x + jnp.tanh(g_ffn[0]) * _L0_ffn_ref(_layernorm(x, axis=-1), L0_ffn_Wr, L0_ffn_W1, L0_ffn_W2)
    x = x + jnp.tanh(g_xattn[1]) * _L1_xattn_ref(_layernorm(x, axis=-1), ctx_512, ctx_512, L1_xattn_Wq, L1_xattn_bq, L1_xattn_Wk, L1_xattn_bk, L1_xattn_Wv, L1_xattn_bv)
    x = x + jnp.tanh(g_ffn[1]) * _L1_ffn_ref(_layernorm(x, axis=-1), L1_ffn_base_W, L1_ffn_base_b, L1_ffn_disc_mu, L1_ffn_disc_sigma, L1_ffn_down_W, L1_ffn_down_b, L1_ffn_up_W, L1_ffn_up_b, L1_ffn_conv_W, L1_ffn_conv_b)
    x = x + jnp.tanh(g_xattn[2]) * _L2_xattn_ref(_layernorm(x, axis=-1), ctx_512, L2_xattn_Wq, L2_xattn_Wkv, L2_xattn_Wo)
    x = x + jnp.tanh(g_ffn[2]) * _L2_ffn_ref(_layernorm(x, axis=-1), L2_ffn_U1, L2_ffn_V1, L2_ffn_b1, L2_ffn_U2, L2_ffn_V2, L2_ffn_b2)
    x = x + jnp.tanh(g_xattn[3]) * _L3_xattn_ref(_layernorm(x, axis=-1), ctx_512, L3_xattn_ln1_g, L3_xattn_ln1_b, L3_xattn_ln2_g, L3_xattn_ln2_b, L3_xattn_a1_wq, L3_xattn_a1_wk, L3_xattn_a1_wv, L3_xattn_a1_li1_w, L3_xattn_a1_li1_b, L3_xattn_a1_lnx_g, L3_xattn_a1_lnx_b, L3_xattn_a1_lny_g, L3_xattn_a1_lny_b, L3_xattn_a1_ln3_g, L3_xattn_a1_ln3_b, L3_xattn_a1_li2_w, L3_xattn_a1_li2_b, L3_xattn_a1_li3_w, L3_xattn_a1_li3_b, L3_xattn_a2_wq, L3_xattn_a2_wk, L3_xattn_a2_wv, L3_xattn_a2_li1_w, L3_xattn_a2_li1_b, L3_xattn_a2_lnx_g, L3_xattn_a2_lnx_b, L3_xattn_a2_lny_g, L3_xattn_a2_lny_b, L3_xattn_a2_ln3_g, L3_xattn_a2_ln3_b, L3_xattn_a2_li2_w, L3_xattn_a2_li2_b, L3_xattn_a2_li3_w, L3_xattn_a2_li3_b, 0)
    x = x + jnp.tanh(g_ffn[3]) * _L3_ffn_ref(_layernorm(x, axis=-1), L3_ffn_ln_gamma, L3_ffn_ln_beta, L3_ffn_router_w, L3_ffn_gate_up_w, L3_ffn_down_w, L3_ffn_shared_gate_up_w, L3_ffn_shared_down_w)
    return x

_drawn_inputs = setup_inputs


def setup_inputs(seed=0):
    import zlib

    import numpy as np

    out = dict(_drawn_inputs(seed))
    spreads = {'L1_xattn_bq': (0.0, 0.594),
     'L1_xattn_bk': (0.0, 2.0),
     'L1_xattn_bv': (0.0, 0.1),
     'L2_ffn_b1': (0.0, 0.8),
     'L2_ffn_b2': (0.0, 0.8),
     'L3_xattn_ln1_g': (1.0, 0.571),
     'L3_xattn_ln1_b': (0.0, 0.551),
     'L3_xattn_ln2_g': (1.0, 0.54),
     'L3_xattn_ln2_b': (0.0, 0.542),
     'L3_xattn_a1_li1_b': (0.0, 0.8),
     'L3_xattn_a1_lnx_g': (1.0, 0.6),
     'L3_xattn_a1_lnx_b': (0.0, 2.0),
     'L3_xattn_a1_lny_g': (1.0, 0.6),
     'L3_xattn_a1_lny_b': (0.0, 2.0),
     'L3_xattn_a1_ln3_g': (1.0, 0.6),
     'L3_xattn_a1_ln3_b': (0.0, 2.0),
     'L3_xattn_a1_li2_b': (0.0, 0.8),
     'L3_xattn_a1_li3_b': (0.0, 0.8),
     'L3_xattn_a2_li1_b': (0.0, 0.8),
     'L3_xattn_a2_lnx_g': (1.0, 0.6),
     'L3_xattn_a2_lnx_b': (0.0, 2.0),
     'L3_xattn_a2_lny_g': (1.0, 0.6),
     'L3_xattn_a2_lny_b': (0.0, 2.0),
     'L3_xattn_a2_ln3_g': (1.0, 0.6),
     'L3_xattn_a2_ln3_b': (0.0, 2.0),
     'L3_xattn_a2_li2_b': (0.0, 0.8),
     'L3_xattn_a2_li3_b': (0.0, 2.0),
     'L3_ffn_ln_gamma': (1.0, 0.6),
     'L3_ffn_ln_beta': (0.0, 2.0)}
    factors = {'L0_xattn_bo': 3.68,
     'L1_ffn_base_b': 8.0,
     'L1_ffn_down_b': 47.92,
     'L1_ffn_up_b': 34.077,
     'L1_ffn_conv_b': 8.0,
     'L2_ffn_U1': 8.0,
     'L2_ffn_V1': 8.0,
     'L2_ffn_U2': 8.0,
     'L2_ffn_V2': 8.0,
     'L3_xattn_a1_wq': 48.0,
     'L3_xattn_a1_wk': 47.686,
     'L3_xattn_a2_wq': 52.473,
     'L3_xattn_a2_wk': 52.692,
     'g_ffn': 21.556,
     'L3_xattn_a1_wv': 5.066,
     'L3_xattn_a1_li1_w': 5.256,
     'L3_xattn_a1_li2_w': 6.343,
     'L3_xattn_a1_li3_w': 6.011,
     'L3_xattn_a2_wv': 5.398,
     'L3_xattn_a2_li1_w': 5.313,
     'L3_xattn_a2_li2_w': 6.733,
     'L3_xattn_a2_li3_w': 5.98,
     'L3_ffn_router_w': 8.0,
     'L3_ffn_gate_up_w': 8.0,
     'L3_ffn_down_w': 8.0,
     'L3_ffn_shared_gate_up_w': 8.0,
     'L3_ffn_shared_down_w': 8.0}
    for name, (base, spread) in spreads.items():
        noise = np.random.default_rng([zlib.crc32(name.encode()), seed]).standard_normal(out[name].shape)
        drawn = base * np.exp(spread * noise) if base else spread * noise
        out[name] = jnp.asarray(drawn.astype(out[name].dtype))
    for name, factor in factors.items():
        out[name] = (out[name] * factor).astype(out[name].dtype)
    return out
```

```python
from contextlib import ExitStack

import concourse.bass as bass
from concourse import mybir

F32 = mybir.dt.float32
I32 = mybir.dt.int32
BF16 = mybir.dt.bfloat16
ALU = mybir.AluOpType
ACT = mybir.ActivationFunctionType
AX_X = mybir.AxisListType.X

P = 128
D = 256
DC = D // P
B = 2
T = 2048
TILES = T // P
PAIRS = TILES // 2
TOK = T // B
KEYS = 64
KD = 128
FF = 1024
FC = FF // P
E = 8
PAIR = 2 * P
TOP2_TILES = 2 * T // PAIR + E - 1
EPS = 1e-5
NEWTON_SEED = float(0x5F3759DF)


def named_semaphores(nc, stage):
    taken = []

    def sem(name):
        taken.append(nc.alloc_semaphore(f"{stage}_{name}"))
        return taken[-1]

    def clear_semaphores():
        nc.clear_and_free_semaphores(taken)
        nc.all_engine_barrier()

    return sem, clear_semaphores


def make_core(nc, ctx):
    def sb(name, shape, dtype=F32):
        return ctx.enter_context(nc.sbuf_tensor(name, shape, dtype))

    return {
        "nc": nc,
        "x": sb("x_tokens", [P, TILES, D]),
        "xt": sb("x_features", [P, DC, T]),
        "xn": sb("xn_tokens", [P, TILES, D]),
        "ident": sb("ident", [P, P]),
        "gate_attn": sb("gate_attn", [P, 4]),
        "gate_ffn": sb("gate_ffn", [P, 4]),
        "ctx_t": sb("ctx_t", [P, B * KEYS]),
        "ctx_norm_t": sb("ctx_norm_t", [P, B * KEYS]),
        "ps": ctx.enter_context(nc.psum_tensor("banks", [P, 8, 512], F32)),
    }


def tiles_of(tensor):
    return lambda i: tensor[:, i, :]


def pair_of(tensor, j):
    return tensor[:, 2 * j:2 * j + 2, :].rearrange("p u d -> p (u d)")


def rows(ap, n=P):
    return ap.rearrange("(a n) -> a n", a=1).partition_broadcast(n)


def columns(ap):
    return ap.rearrange("(c p) -> p c", p=P)


def newton_root(eng, drain, var, v, t, y):
    eng.tensor_scalar(v, var, EPS, None, ALU.add)
    drain()
    eng.tensor_scalar(y.bitcast(I32), v.bitcast(I32), -0.5, NEWTON_SEED, ALU.mult, ALU.add)
    drain()
    for step in range(3):
        eng.tensor_tensor(t, y, y, ALU.mult)
        drain()
        eng.tensor_tensor(t, t, v, ALU.mult)
        drain()
        eng.tensor_scalar(t, t, -0.5, 1.5, ALU.mult, ALU.add)
        drain()
        last = eng.tensor_tensor(y, t, y, ALU.mult)
        if step < 2:
            drain()
    return last


def vector_root(nc, dve, var, h, t, y):
    nc.vector.tensor_scalar(t, var, EPS, None, ALU.add)
    nc.vector.tensor_scalar(h, var, EPS, -0.5, ALU.add, ALU.mult)
    dve.drain()
    nc.vector.tensor_scalar(y.bitcast(I32), t.bitcast(I32), -0.5, NEWTON_SEED, ALU.mult, ALU.add)
    dve.drain()
    for step in range(3):
        nc.vector.tensor_tensor(t, y, y, ALU.mult)
        dve.drain()
        nc.vector.tensor_tensor(t, t, h, ALU.mult)
        dve.drain()
        nc.vector.scalar_tensor_tensor(y, t, 1.5, y, ALU.add, ALU.mult)
        dve.drain()


def layer_norm(core, ctx, sem, name, on_vector=False):
    nc, ps = core["nc"], core["ps"]

    def sb(part, shape):
        return ctx.enter_context(nc.sbuf_tensor(f"{name}_{part}", shape, F32))

    stats = sb("stats", [P, 2, 2, 6])
    mv = sb("mv", [P, 2, 2, 2])
    rs = sb("rs", [P, 2, 2])
    v = sb("v", [P, 2])
    t = sb("t", [P, 2])
    measured, rooted, normalised = sem(name + "_measured"), sem(name + "_rooted"), sem(name + "_normalised")
    turned, stored = sem(name + "_turned"), sem(name + "_stored")

    def measure(dve, j, src):
        p = j % 2
        for u in range(2):
            nc.vector.bn_stats(stats[:, p, u, :], src(2 * j + u))
        dve.drain()
        nc.vector.bn_aggr(mv[:, p, 0, :], stats[:, p, 0, :])
        last = nc.vector.bn_aggr(mv[:, p, 1, :], stats[:, p, 1, :])
        if on_vector:
            dve.drain()
            vector_root(nc, dve, mv[:, p, :, 1], v[:, :], t[:, :], rs[:, p, :])
        else:
            last.then_inc(measured, 1)

    def root(pool, j):
        assert not on_vector
        pool.wait_ge(measured, j + 1)
        if j >= 2:
            pool.wait_ge(normalised, j - 1)
        newton_root(nc.gpsimd, pool.drain, mv[:, j % 2, :, 1], v[:, :], t[:, :], rs[:, j % 2, :]).then_inc(rooted, 1)

    def normalise(dve, j, src, dst):
        if not on_vector:
            dve.wait_ge(rooted, j + 1)
        p = j % 2
        for u in range(2):
            last = nc.vector.tensor_scalar(dst(2 * j + u), src(2 * j + u), mv[:, p, u, 0:1],
                                           rs[:, p, u:u + 1], ALU.subtract, ALU.mult)
        last.then_inc(normalised, 1)

    def turn(pe, j, src, bank=7):
        pe.wait_ge(normalised, j + 1)
        if j >= 1:
            pe.wait_ge(stored, j)
        for c in range(DC):
            for u in range(2):
                last = nc.tensor.transpose(ps[:, bank, c * PAIR + u * P:c * PAIR + (u + 1) * P],
                                           src(2 * j + u)[:, c * P:(c + 1) * P], core["ident"][:, :])
        last.then_inc(turned, 1)

    def store(act, j, dsts, bank=7):
        act.wait_ge(turned, j + 1)
        for dst, gamma, beta in dsts:
            if gamma is None:
                last = nc.scalar.activation(dst[:, :, PAIR * j:PAIR * (j + 1)],
                                            ps[:, bank, :].rearrange("p (c n) -> p c n", c=DC), ACT.Copy)
            else:
                for c in range(DC):
                    last = nc.scalar.activation(
                        dst[:, c, PAIR * j:PAIR * (j + 1)], ps[:, bank, c * PAIR:(c + 1) * PAIR],
                        ACT.Identity, bias=beta[:, c:c + 1], scale=gamma[:, c:c + 1])
        last.then_inc(stored, 1)

    return measure, root, normalise, turn, store, stored


def stage_start(core, a):
    nc, ps = core["nc"], core["ps"]
    with ExitStack() as ctx:
        def sb(name, shape):
            return ctx.enter_context(nc.sbuf_tensor(name, shape, F32))

        sem, clear_semaphores = named_semaphores(nc, "start")
        x_in, small_in = [sem(f"x_in{j}") for j in range(PAIRS)], sem("small_in")
        ident_zero, ident_made = sem("ident_zero"), sem("ident_made")
        ctx_measured, ctx_rooted, ctx_normalised = sem("ctx_measured"), sem("ctx_rooted"), sem("ctx_normalised")
        ctx_turned = sem("ctx_turned")
        norm_measure, norm_root, norm_normalise, norm_turn, norm_store, norm_stored = layer_norm(core, ctx, sem, "norm")
        c_in = sb("c_in", [P, KD])
        c_norm = sb("c_norm", [P, KD])
        c_stats, c_mv, c_small = sb("c_stats", [P, 6]), sb("c_mv", [P, 2]), sb("c_small", [P, 3])
        c_gb = sb("c_gb", [P, 2])
        g_in = sb("g_in", [P, 8])

        with nc.Block() as block:
            @block.sync
            def _(sp):
                for j in range(PAIRS):
                    sp.dma_start(core["x"][:, 2 * j:2 * j + 2, :],
                                 a["x"].rearrange("b (t p) d -> p (b t) d", p=P)[:, 2 * j:2 * j + 2, :]).then_inc(x_in[j], 16)

            @block.scalar
            def _(act):
                act.dma_start(c_in[:, :], a["ctx_512"].rearrange("b k d -> (b k) d")).then_inc(small_in, 16)
                act.dma_start(g_in[:, 0:4], rows(a["g_xattn"])).then_inc(small_in, 16)
                act.dma_start(g_in[:, 4:8], rows(a["g_ffn"])).then_inc(small_in, 16)
                act.dma_start(c_gb[:, 0:1], columns(a["L3_xattn_a2_lny_g"])).then_inc(small_in, 16)
                act.dma_start(c_gb[:, 1:2], columns(a["L3_xattn_a2_lny_b"])).then_inc(small_in, 16)
                act.wait_ge(small_in, 80)
                nc.scalar.activation(core["gate_attn"][:, :], g_in[:, 0:4], ACT.Tanh)
                nc.scalar.activation(core["gate_ffn"][:, :], g_in[:, 4:8], ACT.Tanh)
                act.wait_ge(ctx_turned, 2)
                nc.scalar.activation(core["ctx_t"][:, :], ps[:, 0, 0:P], ACT.Copy)
                nc.scalar.activation(core["ctx_norm_t"][:, :], ps[:, 1, 0:P], ACT.Identity,
                                     bias=c_gb[:, 1:2], scale=c_gb[:, 0:1])
                for j in range(PAIRS):
                    norm_store(act, j, [(core["xt"], None, None)])

            @block.gpsimd
            def _(pool):
                nc.gpsimd.memset(core["ident"][:, :], 0.0).then_inc(ident_zero, 1)
                pool.wait_ge(ident_zero, 1)
                nc.gpsimd.affine_select(out=core["ident"][:, :], in_=core["ident"][:, :], compare_op=ALU.not_equal,
                                        fill=1.0, base=0, pattern=[[-1, P]],
                                        channel_multiplier=1).then_inc(ident_made, 1)
                pool.wait_ge(ctx_measured, 1)
                newton_root(nc.gpsimd, pool.drain, c_mv[:, 1:2], c_small[:, 0:1], c_small[:, 1:2],
                            c_small[:, 2:3]).then_inc(ctx_rooted, 1)
                for j in range(PAIRS):
                    norm_root(pool, j)

            @block.vector
            def _(dve):
                dve.wait_ge(small_in, 80)
                nc.vector.bn_stats(c_stats[:, :], c_in[:, :])
                dve.drain()
                nc.vector.bn_aggr(c_mv[:, :], c_stats[:, :]).then_inc(ctx_measured, 1)
                dve.wait_ge(ctx_rooted, 1)
                nc.vector.tensor_scalar(c_norm[:, :], c_in[:, :], c_mv[:, 0:1], c_small[:, 2:3],
                                        ALU.subtract, ALU.mult).then_inc(ctx_normalised, 1)
                for j in range(PAIRS + 1):
                    if j < PAIRS:
                        dve.wait_ge(x_in[j], 16)
                        norm_measure(dve, j, tiles_of(core["x"]))
                    if j >= 1:
                        norm_normalise(dve, j - 1, tiles_of(core["x"]), tiles_of(core["xn"]))

            @block.tensor
            def _(pe):
                pe.wait_ge(ident_made, 1)
                pe.wait_ge(small_in, 80)
                nc.tensor.transpose(ps[:, 0, 0:P], c_in[:, :], core["ident"][:, :]).then_inc(ctx_turned, 1)
                pe.wait_ge(ctx_normalised, 1)
                nc.tensor.transpose(ps[:, 1, 0:P], c_norm[:, :], core["ident"][:, :]).then_inc(ctx_turned, 1)
                for j in range(PAIRS):
                    norm_turn(pe, j, tiles_of(core["xn"]))
        clear_semaphores()


def stage_attention(core, a, name, width, scale, layout, source, out_tile, gate, bias, norm_out, context):
    nc, ps = core["nc"], core["ps"]
    HEADS = 16
    HK = HEADS * KEYS
    chunks = HEADS * width // P
    per = P // width
    with ExitStack() as ctx:
        def sb(part, shape):
            return ctx.enter_context(nc.sbuf_tensor(f"{name}_{part}", shape, F32))

        sem, clear_semaphores = named_semaphores(nc, name)
        w_in, w_turned, w_stored = sem("w_in"), sem("w_turned"), sem("w_stored")
        mask_set, mask_made = sem("mask_set"), sem("mask_made")
        kv_ready, kv_stored, blocks_made = sem("kv_ready"), sem("kv_stored"), sem("blocks_made")
        fold_ready, fold_stored = sem("fold_ready"), sem("fold_stored")
        bias_made, bias_added = sem("bias_made"), sem("bias_added")
        scores_ready, centred, exped = sem("scores_ready"), sem("centred"), sem("exped")
        probs_ready, probs_turned, probs_stored = sem("probs_ready"), sem("probs_turned"), sem("probs_stored")
        out_ready, out_added = sem("out_ready"), sem("out_added")
        norm_measure, norm_root, norm_normalise, norm_turn, norm_store, norm_stored = layer_norm(core, ctx, sem, name + "_norm")

        wq_t = sb("wq_t", [P, chunks, D])
        wo = sb("wo", [P, chunks, D])
        mask = sb("mask", [P, per])
        kv = sb("kv", [P, chunks, 2, B, KEYS])
        blk = sb("blk", [P, 2, 2, B, per, KEYS])
        fold_q = sb("fold_q", [P, B, DC, HK])
        fold_v = sb("fold_v", [P, B, HK // P, D])
        bias_row = sb("bias_row", [P, D])
        ex = sb("ex", [P, 2, HEADS, KEYS])
        mx = sb("mx", [P, 2, HEADS])
        sm = sb("sm", [P, 2, HEADS])
        pt = sb("pt", [P, 2, HK])
        gb = sb("gb", [P, 2, DC])
        loads, turns, wk, wv = layout(sb, wq_t, wo)
        if bias:
            loads = loads + [(bias_row[:, :], rows(a[bias]))]
        if norm_out:
            loads += [(gb[:, k, :], columns(a[n])) for k, n in enumerate(norm_out)]
        gamma, beta = (gb[:, 0, :], gb[:, 1, :]) if norm_out else (None, None)

        folds = []
        for c in range(chunks):
            for b in range(B):
                for dc in range(DC):
                    folds.append((c, wq_t[:, c, dc * P:(dc + 1) * P],
                                  blk[:, c % 2, 0, b].rearrange("p h k -> p (h k)"), per * KEYS,
                                  fold_q[:, b, dc, c * per * KEYS:(c + 1) * per * KEYS]))
                for m in range(per // 2):
                    folds.append((c, blk[:, c % 2, 1, b, 2 * m:2 * m + 2].rearrange("p h k -> p (h k)"),
                                  wo[:, c, :], D, fold_v[:, b, c * per // 2 + m, :]))
        per_chunk = len(folds) // chunks

        with nc.Block() as block:
            @block.sync
            def _(sp):
                for dst, src in loads:
                    sp.dma_start(dst, src).then_inc(w_in, 16)

            @block.gpsimd
            def _(pool):
                nc.gpsimd.memset(mask[:, :], 1.0).then_inc(mask_set, 1)
                pool.wait_ge(mask_set, 1)
                nc.gpsimd.affine_select(out=mask[:, :], in_=mask[:, :], compare_op=ALU.is_ge, fill=0.0, base=0,
                                        pattern=[[-width, per]], channel_multiplier=1).then_inc(mask_set, 1)
                pool.wait_ge(mask_set, 2)
                nc.gpsimd.affine_select(out=mask[:, :], in_=mask[:, :], compare_op=ALU.is_ge, fill=0.0,
                                        base=width - 1, pattern=[[width, per]],
                                        channel_multiplier=-1).then_inc(mask_made, 1)
                if bias:
                    pool.wait_ge(bias_made, 1)
                for j in range(PAIRS):
                    if bias:
                        for u in range(2):
                            i = 2 * j + u
                            last = nc.gpsimd.tensor_tensor(out_tile(i), source(i), bias_row[:, :], ALU.add)
                        last.then_inc(bias_added, 1)
                    if j >= 1:
                        norm_root(pool, j - 1)
                norm_root(pool, PAIRS - 1)

            @block.tensor
            def _(pe):
                pe.wait_ge(w_in, 16 * len(loads))
                for n, (srcs, _) in enumerate(turns):
                    if n >= 2:
                        pe.wait_ge(w_stored, n - 1)
                    for q, src in enumerate(srcs):
                        last = nc.tensor.transpose(ps[:, n % 2, q * P:(q + 1) * P], src, core["ident"][:, :])
                    last.then_inc(w_turned, 1)
                pe.wait_ge(w_stored, len(turns))

                def keys_values(c):
                    if c >= 2:
                        pe.wait_ge(kv_stored, c - 1)
                    nc.tensor.matmul(ps[:, c % 2, 0:P], wk[:, c * P:(c + 1) * P], context[:, :],
                                     start=True, stop=True)
                    nc.tensor.matmul(ps[:, c % 2, P:2 * P], wv[:, c * P:(c + 1) * P], context[:, :],
                                     start=True, stop=True).then_inc(kv_ready, 1)

                keys_values(0)
                for n, (c, lhs, rhs, cols, _) in enumerate(folds):
                    if n % per_chunk == 0:
                        if c + 1 < chunks:
                            keys_values(c + 1)
                        pe.wait_ge(blocks_made, c + 1)
                    if n >= 4:
                        pe.wait_ge(fold_stored, n - 3)
                    nc.tensor.matmul(ps[:, 2 + n % 4, 0:cols], lhs, rhs, start=True,
                                     stop=True).then_inc(fold_ready, 1)
                pe.wait_ge(fold_stored, len(folds))

                for i in range(TILES + 5):
                    if i < TILES:
                        b = i // (TILES // B)
                        if i >= 2:
                            pe.wait_ge(centred, i - 1)
                        for h in range(2):
                            for dc in range(DC):
                                last = nc.tensor.matmul(ps[:, 2 * (i % 2) + h, :], core["xt"][:, dc, i * P:(i + 1) * P],
                                                        fold_q[:, b, dc, h * 512:(h + 1) * 512],
                                                        start=(dc == 0), stop=(dc == DC - 1))
                        last.then_inc(scores_ready, 1)
                    if 1 <= i <= TILES:
                        k = i - 1
                        pe.wait_ge(probs_ready, k + 1)
                        if k >= 1:
                            pe.wait_ge(probs_stored, k)
                        for c in range(HK // P):
                            last = nc.tensor.transpose(ps[:, 4 + c // 4, (c % 4) * P:(c % 4 + 1) * P],
                                                       ex[:, k % 2, 2 * c:2 * c + 2, :].rearrange("p h k -> p (h k)"),
                                                       core["ident"][:, :])
                        last.then_inc(probs_turned, 1)
                    if i >= 5 and i % 2 == 1:
                        norm_turn(pe, (i - 5) // 2, tiles_of(core["xn"]))
                    if 2 <= i <= TILES + 1:
                        k = i - 2
                        pe.wait_ge(probs_stored, k + 1)
                        if k >= 1:
                            pe.wait_ge(out_added, k)
                        for c in range(HK // P):
                            last = nc.tensor.matmul(ps[:, 6, 0:D],
                                                    pt[:, k % 2, c * P:(c + 1) * P],
                                                    fold_v[:, k // (TILES // B), c, :],
                                                    start=(c == 0), stop=(c == HK // P - 1))
                        last.then_inc(out_ready, 1)

            @block.scalar
            def _(act):
                for n, (srcs, dst) in enumerate(turns):
                    act.wait_ge(w_turned, n + 1)
                    nc.scalar.activation(dst, ps[:, n % 2, 0:P * len(srcs)], ACT.Copy).then_inc(w_stored, 1)

                def store_kv(c):
                    act.wait_ge(kv_ready, c + 1)
                    nc.scalar.activation(kv[:, c].rearrange("p a b k -> p (a b k)"), ps[:, c % 2, 0:2 * P],
                                         ACT.Copy).then_inc(kv_stored, 1)

                store_kv(0)
                for n, (c, _, _, cols, dst) in enumerate(folds):
                    if n % per_chunk == 0 and c + 1 < chunks:
                        store_kv(c + 1)
                    act.wait_ge(fold_ready, n + 1)
                    nc.scalar.activation(dst, ps[:, 2 + n % 4, 0:cols], ACT.Copy).then_inc(fold_stored, 1)

                for i in range(TILES + 5):
                    if i < TILES:
                        act.wait_ge(centred, i + 1)
                        nc.scalar.activation(ex[:, i % 2], ex[:, i % 2], ACT.Exp, scale=scale).then_inc(exped, 1)
                    if 1 <= i <= TILES:
                        k = i - 1
                        act.wait_ge(probs_turned, k + 1)
                        if k >= 2:
                            act.wait_ge(out_ready, k - 1)
                        nc.scalar.activation(pt[:, k % 2, :], ps[:, 4:6, :].rearrange("p a n -> p (a n)"),
                                             ACT.Copy).then_inc(probs_stored, 1)
                    if i >= 5 and i % 2 == 1:
                        norm_store(act, (i - 5) // 2, [(core["xt"], gamma, beta)])

            @block.vector
            def _(dve):
                dve.wait_ge(w_in, 16 * len(loads))
                if not bias:
                    pass
                elif gate is None:
                    nc.vector.tensor_copy(bias_row[:, 0:1], bias_row[:, 0:1]).then_inc(bias_made, 1)
                else:
                    nc.vector.tensor_scalar(bias_row[:, :], bias_row[:, :], gate, None, ALU.mult).then_inc(bias_made, 1)
                dve.wait_ge(mask_made, 1)
                for c in range(chunks):
                    dve.wait_ge(kv_stored, c + 1)
                    if c >= 2:
                        dve.wait_ge(fold_ready, per_chunk * (c - 1))
                    for kind in range(2):
                        for b in range(B):
                            last = nc.vector.tensor_tensor(
                                blk[:, c % 2, kind, b],
                                kv[:, c, kind, b, :].unsqueeze(1).to_broadcast([P, per, KEYS]),
                                mask[:, :].unsqueeze(2).to_broadcast([P, per, KEYS]), ALU.mult)
                    last.then_inc(blocks_made, 1)

                for i in range(TILES + 3):
                    if 1 <= i <= TILES:
                        k = i - 1
                        dve.wait_ge(exped, k + 1)
                        nc.vector.tensor_reduce(sm[:, k % 2, :], ex[:, k % 2], AX_X, ALU.add)
                        dve.drain()
                        nc.vector.reciprocal(sm[:, k % 2, :], sm[:, k % 2, :])
                        dve.drain()
                        nc.vector.tensor_tensor(ex[:, k % 2], ex[:, k % 2],
                                                sm[:, k % 2, :].unsqueeze(2).to_broadcast([P, HEADS, KEYS]),
                                                ALU.mult).then_inc(probs_ready, 1)
                    if i < TILES:
                        dve.wait_ge(scores_ready, i + 1)
                        scores = ps[:, 2 * (i % 2):2 * (i % 2) + 2, :].rearrange("p a (h k) -> p (a h) k", k=KEYS)
                        nc.vector.tensor_reduce(mx[:, i % 2, :], scores, AX_X, ALU.max)
                        dve.drain()
                        if i >= 2:
                            dve.wait_ge(probs_turned, i - 1)
                        nc.vector.tensor_tensor(ex[:, i % 2], scores,
                                                mx[:, i % 2, :].unsqueeze(2).to_broadcast([P, HEADS, KEYS]),
                                                ALU.subtract).then_inc(centred, 1)
                    if i >= 4 and i % 2 == 0:
                        norm_normalise(dve, (i - 4) // 2, out_tile, tiles_of(core["xn"]))
                    if 2 <= i <= TILES + 1:
                        k = i - 2
                        dve.wait_ge(out_ready, k + 1)
                        if bias:
                            dve.wait_ge(bias_added, k // 2 + 1)
                        out = ps[:, 6, 0:D]
                        if gate is None:
                            nc.vector.tensor_tensor(out_tile(k), out, out_tile(k), ALU.add).then_inc(out_added, 1)
                        else:
                            nc.vector.scalar_tensor_tensor(out_tile(k), out, gate, out_tile(k), ALU.mult,
                                                           ALU.add).then_inc(out_added, 1)
                        if k % 2 == 1:
                            dve.drain()
                            norm_measure(dve, k // 2, out_tile)
        clear_semaphores()


def layout_l0(core, a):
    def layout(sb, wq_t, wo):
        wq = sb("wq", [P, DC, 1024])
        wk, wv = sb("wk", [P, 1024]), sb("wv", [P, 1024])
        loads = [(wq[:, :, :], a["L0_xattn_Wq"].rearrange("(c p) n -> p c n", p=P)),
                 (wk[:, :], a["L0_xattn_Wk"]), (wv[:, :], a["L0_xattn_Wv"]),
                 (wo[:, :, :], a["L0_xattn_Wo"].rearrange("(c p) n -> p c n", p=P))]
        turns = [([wq[:, dc, c * P:(c + 1) * P] for c in (2 * q, 2 * q + 1) for dc in range(DC)],
                  wq_t[:, 2 * q:2 * q + 2, :].rearrange("p c d -> p (c d)")) for q in range(4)]
        return loads, turns, wk, wv
    return layout


def first(t):
    return isinstance(t, int) and t == 0


def later(t):
    return not (isinstance(t, int) and t < 2)


def copy_bank(nc, dst, bank_ap):
    return nc.scalar.activation(dst, bank_ap, ACT.Copy)


def stage_experts(core, a, name, *, top, rows_tiles, capacity, router, w1, w2, swiglu, gate, affine=None,
                  shared=None, norm_behind=True):
    nc, ps = core["nc"], core["ps"]
    ROWS = rows_tiles * PAIR
    WIDE = 2 * FF if swiglu else FF
    HALF = 2 if swiglu else 1
    xs = nc.dram_tensor(f"{name}_rows", [ROWS, D], F32, kind="Internal").ap()
    ys = nc.dram_tensor(f"{name}_results", [ROWS + P, D], F32, kind="Internal").ap()
    with ExitStack() as ctx:
        def sb(part, shape, dtype=F32):
            return ctx.enter_context(nc.sbuf_tensor(f"{name}_{part}", shape, dtype))

        sem, clear_semaphores = named_semaphores(nc, name)
        small_in, made, zeroed = sem("small_in"), sem("made"), sem("zeroed")
        logits_ready, shifted, exped = sem("logits_ready"), sem("shifted"), sem("exped")
        chosen, counted, slots_made = sem("chosen"), sem("counted"), sem("slots_made")
        scattered = sem("scattered")
        if not capacity:
            owners_made = sem("owners_made")
        w1_in, w2_in = [sem("w1_in0"), sem("w1_in1")], [sem("w2_in0"), sem("w2_in1")]
        rows_in, y_sent = [sem("rows_in0"), sem("rows_in1")], [sem("y_sent0"), sem("y_sent1")]
        rows_turned, rows_stored = sem("rows_turned"), sem("rows_stored")
        hid_ready, hid_stored = sem("hid_ready"), sem("hid_stored")
        clipped, silued = sem("clipped"), sem("silued")
        out_ready, y_stored = sem("out_ready"), sem("y_stored")
        gathered, added = [sem(f"gathered{q}") for q in range(4)], sem("added")
        if norm_behind:
            norm_measure, norm_root, norm_normalise, norm_turn, norm_store, norm_stored = layer_norm(core, ctx, sem, name + "_norm", on_vector=True)
        else:
            x_sent = sem("x_sent")

        wr = sb("wr", [P, DC, E])
        tri = sb("tri", [P, P])
        ones = sb("ones", [P, P])
        iota_e = sb("iota_e", [P, E])
        iota_t = sb("iota_t", [P, rows_tiles])
        pr = sb("pr", [P, TILES, E])
        eq = sb("eq", [P, TILES, E])
        hot = [sb(f"hot{k}", [P, TILES, E]) for k in range(top)]
        hots = sb("hots", [P, TILES, E])
        best = sb("best", [P, top, TILES])
        col = sb("col", [P, 2, TILES])
        total = sb("total", [P, TILES, E])
        scan = [sb("scan0", [P, TILES, E]), sb("scan1", [P, TILES, E])]
        ends = [sb("ends0", [P, E]), sb("ends1", [P, E])]
        need = sb("need", [P, E])
        need_i = sb("need_i", [P, E], I32)
        owner = sb("owner", [P, rows_tiles, E])
        owner_f = sb("owner_f", [P, rows_tiles])
        owner_i = sb("owner_i", [P, rows_tiles], I32)
        slot_f = sb("slot_f", [P, TILES])
        slot = sb("slot", [P, top, TILES], I32)
        weight = sb("weight", [P, top, TILES])
        zero = sb("zero", [P, 2 * D])
        w1_sb = sb("w1", [P, 2, DC, WIDE])
        w2_sb = sb("w2", [P, 2, FC, D])
        xr = sb("xr", [P, 2, 2, D])
        xrt = sb("xrt", [P, 2, DC, PAIR])
        sg = sb("sg", [P, 4, PAIR])
        ht = sb("ht", [P, 2, FC, PAIR])
        yt = sb("yt", [P, 2, 2, D])
        yg = sb("yg", [P, 4, D])
        loads = [(wr[:, :, :], a[router].rearrange("(c p) e -> p c e", p=P))]
        if affine:
            gb = sb("gb", [P, 2, DC])
            loads += [(gb[:, k, :], columns(a[n])) for k, n in enumerate(affine)]
        if shared:
            FS = 256
            SC = FS // P
            s1 = sb("s1", [P, DC, 2 * FS])
            s2 = sb("s2", [P, SC, D])
            loads += [(s1[:, :, :], a[shared[0]].rearrange("(c p) n -> p c n", p=P)),
                      (s2[:, :, :], a[shared[1]].rearrange("(c p) n -> p c n", p=P))]
            s_hid_ready, s_clipped, s_silued = sem("s_hid_ready"), sem("s_clipped"), sem("s_silued")
            s_hid_stored, s_out_ready, s_added = sem("s_hid_stored"), sem("s_out_ready"), sem("s_added")

        w1_rows = a[w1].rearrange("e (c p) n -> e p c n", p=P)
        w2_rows = a[w2].rearrange("e (c p) n -> e p c n", p=P)
        xs_rows = xs.rearrange("(t u p) d -> t p u d", u=2, p=P)
        ys_rows = ys[0:ROWS, :].rearrange("(t u p) d -> t p u d", u=2, p=P)
        zero_loads = rows_tiles

        LOOPS = (rows_tiles - 4) // 2
        FIRST_LEFT = 3 + 2 * LOOPS

        with nc.Block() as block:
            @block.sync
            def _(sp):
                for dst, src in loads:
                    sp.dma_start(dst, src).then_inc(small_in, 16)
                sp.wait_ge(made, 6)
                for n in range(zero_loads):
                    sp.dma_start(xs.rearrange("(n p r) d -> n p (r d)", p=P, r=2)[n], zero[:, :]).then_inc(zeroed, 16)
                sp.dma_start(ys[ROWS:ROWS + P, :], zero[:, 0:D]).then_inc(zeroed, 16)

                def expert_of(t):
                    return t if capacity else sp.value_load(owner_i[0:1, bass.ds(t, 1)], min_val=0, max_val=E - 1)

                def load_w1(e, p):
                    sp.dma_start(w1_sb[:, p], w1_rows[bass.ds(e, 1)].rearrange("a p c n -> p (a c) n")).then_inc(w1_in[p], 16)

                def load_w2(e, p):
                    sp.dma_start(w2_sb[:, p], w2_rows[bass.ds(e, 1)].rearrange("a p c n -> p (a c) n")).then_inc(w2_in[p], 16)

                def load_rows(t, p):
                    sp.dma_start(xr[:, p], xs_rows[bass.ds(t, 1)].rearrange("a p u d -> p (a u) d")).then_inc(rows_in[p], 16)

                def load(jj, p):
                    t = 2 * jj + p
                    e = expert_of(t)
                    sp.wait_ge(hid_ready, FC * (t - 1))
                    load_w1(e, p)
                    sp.wait_ge(rows_turned, t - 1)
                    load_rows(t, p)
                    sp.wait_ge(out_ready, t - 1)
                    load_w2(e, p)

                if not capacity:
                    sp.wait_ge(owners_made, 1)
                for t in range(2):
                    e = expert_of(t)
                    load_w1(e, t)
                    load_w2(e, t)
                sp.wait_ge(slots_made, 1)
                sp.wait_ge(scattered, 16 * TILES * top)
                for t in range(2):
                    load_rows(t, t)
                load(1, 0)
                with sp.Fori(1, 1 + LOOPS) as jj:
                    load(jj, 1)
                    load(jj + 1, 0)
                for t in range(FIRST_LEFT, rows_tiles):
                    load(t // 2, t % 2)
                if not norm_behind:
                    for i in range(TILES):
                        sp.wait_ge(added, top * (i + 1))
                        sp.dma_start(a["out"].rearrange("b (t p) d -> p (b t) d", p=P)[:, i, :],
                                     core["x"][:, i, :]).then_inc(x_sent, 16)
                    sp.wait_ge(x_sent, 16 * TILES)

            @block.gpsimd
            def _(pool):
                nc.gpsimd.memset(tri[:, :], 1.0).then_inc(made, 1)
                nc.gpsimd.memset(ones[:, :], 1.0).then_inc(made, 1)
                nc.gpsimd.memset(zero[:, :], 0.0).then_inc(made, 1)
                nc.gpsimd.iota(iota_e[:, :], [[1, E]], base=0, channel_multiplier=0,
                               allow_small_or_imprecise_dtypes=True).then_inc(made, 1)
                nc.gpsimd.iota(iota_t[:, :], [[1, rows_tiles]], base=0, channel_multiplier=0,
                               allow_small_or_imprecise_dtypes=True).then_inc(made, 1)
                pool.wait_ge(made, 5)
                nc.gpsimd.affine_select(out=tri[:, :], in_=tri[:, :], compare_op=ALU.is_gt, fill=0.0, base=0,
                                        pattern=[[1, P]], channel_multiplier=-1).then_inc(made, 1)
                pool.wait_ge(zeroed, 16 * (zero_loads + 1))
                pool.wait_ge(slots_made, 1)
                for k in range(top):
                    for i in range(TILES):
                        pool.indirect_dma_start(xs, bass.IndirectOffsetOnAxis(ap=slot[:, k, i:i + 1], axis=0),
                                                core["xn"][:, i, :], None, bounds_check=ROWS - 1,
                                                oob_is_err=False).then_inc(scattered, 16)

                def send(jj, p):
                    t = 2 * jj + p
                    pool.wait_ge(y_stored, t + 1)
                    pool.dma_start(ys_rows[bass.ds(t, 1)].rearrange("a p u d -> p (a u) d"), yt[:, p]).then_inc(y_sent[p], 16)

                for t in range(3):
                    send(t // 2, t % 2)
                with pool.Fori(1, 1 + LOOPS) as jj:
                    send(jj, 1)
                    send(jj + 1, 0)
                for t in range(FIRST_LEFT, rows_tiles):
                    send(t // 2, t % 2)
                for p in range(2):
                    pool.wait_ge(y_sent[p], 16 * ((rows_tiles + 1 - p) // 2))
                for n in range(TILES * top):
                    i, k = n // top, n % top
                    if n >= 4:
                        pool.wait_ge(added, n - 3)
                    pool.indirect_dma_start(yg[:, n % 4, :], None, ys,
                                            bass.IndirectOffsetOnAxis(ap=slot[:, k, i:i + 1], axis=0),
                                            bounds_check=ROWS + P - 1, oob_is_err=False).then_inc(gathered[n % 4], 16)

            @block.tensor
            def _(pe):
                pe.wait_ge(small_in, 16 * len(loads))
                for i in range(TILES):
                    for dc in range(DC):
                        last = nc.tensor.matmul(ps[:, 0, i * E:(i + 1) * E], core["xt"][:, dc, i * P:(i + 1) * P],
                                                wr[:, dc, :], start=(dc == 0), stop=(dc == DC - 1))
                last.then_inc(logits_ready, 1)
                pe.wait_ge(made, 6)
                pe.wait_ge(chosen, 1)
                nc.tensor.matmul(ps[:, 5, 0:P], tri[:, :], hots[:, :, :].rearrange("p t e -> p (t e)"),
                                 start=True, stop=True)
                nc.tensor.matmul(ps[:, 6, 0:P], ones[:, :], hots[:, :, :].rearrange("p t e -> p (t e)"),
                                 start=True, stop=True).then_inc(counted, 1)

                if shared:
                    for j in range(PAIRS + 1):
                        if j < PAIRS:
                            for f in range(SC):
                                n = SC * j + f
                                if n >= 2:
                                    pe.wait_ge(s_hid_stored, n - 1)
                                for h in range(2):
                                    for dc in range(DC):
                                        last = nc.tensor.matmul(
                                            ps[:, 1 + n % 2, h * PAIR:(h + 1) * PAIR],
                                            s1[:, dc, h * FS + f * P:h * FS + (f + 1) * P],
                                            core["xt"][:, dc, PAIR * j:PAIR * (j + 1)],
                                            start=(dc == 0), stop=(dc == DC - 1))
                                last.then_inc(s_hid_ready, 1)
                        if j >= 1:
                            q = j - 1
                            pe.wait_ge(s_hid_stored, SC * j)
                            if q >= 2:
                                pe.wait_ge(s_added, q - 1)
                            for u in range(2):
                                for f in range(SC):
                                    last = nc.tensor.matmul(ps[:, 3 + q % 2, u * D:(u + 1) * D],
                                                            ht[:, q % 2, f, u * P:(u + 1) * P], s2[:, f, :],
                                                            start=(f == 0), stop=(f == SC - 1))
                            last.then_inc(s_out_ready, 1)
                    pe.wait_ge(s_added, PAIRS)

                def turn(jj, p):
                    t = 2 * jj + p
                    pe.wait_ge(rows_in[p], 16 * jj + 16)
                    if not first(t):
                        pe.wait_ge(rows_stored, t)
                    for c in range(DC):
                        for u in range(2):
                            last = nc.tensor.transpose(ps[:, 7, c * PAIR + u * P:c * PAIR + (u + 1) * P],
                                                       xr[:, p, u, c * P:(c + 1) * P], core["ident"][:, :])
                    last.then_inc(rows_turned, 1)

                def hidden(jj, p):
                    t = 2 * jj + p
                    pe.wait_ge(w1_in[p], 16 * jj + 16)
                    pe.wait_ge(rows_stored, t + 1)
                    for f in range(FC):
                        if not (first(t) and f < 4):
                            pe.wait_ge(hid_stored, FC * t + (f - 3))
                        for h in range(HALF):
                            for dc in range(DC):
                                last = nc.tensor.matmul(ps[:, f % 4, h * PAIR:(h + 1) * PAIR],
                                                        w1_sb[:, p, dc, h * FF + f * P:h * FF + (f + 1) * P],
                                                        xrt[:, p, dc, :], start=(dc == 0), stop=(dc == DC - 1))
                        last.then_inc(hid_ready, 1)

                def output(jj, p):
                    t = 2 * jj + p
                    pe.wait_ge(w2_in[p], 16 * jj + 16)
                    pe.wait_ge(hid_stored, FC * t + FC)
                    if later(t):
                        pe.wait_ge(y_stored, t - 1)
                    for u in range(2):
                        for f in range(FC):
                            last = nc.tensor.matmul(ps[:, 4 + p, u * D:(u + 1) * D],
                                                    ht[:, p, f, u * P:(u + 1) * P], w2_sb[:, p, f, :],
                                                    start=(f == 0), stop=(f == FC - 1))
                    last.then_inc(out_ready, 1)

                pe.wait_ge(slots_made, 1)
                turn(0, 0)
                for t in range(3):
                    hidden(t // 2, t % 2)
                    turn((t + 1) // 2, (t + 1) % 2)
                    if t >= 1:
                        output((t - 1) // 2, (t - 1) % 2)
                with pe.Fori(1, 1 + LOOPS) as jj:
                    hidden(jj, 1)
                    turn(jj + 1, 0)
                    output(jj, 0)
                    hidden(jj + 1, 0)
                    turn(jj + 1, 1)
                    output(jj, 1)
                for t in range(FIRST_LEFT, rows_tiles):
                    hidden(t // 2, t % 2)
                    if t + 1 < rows_tiles:
                        turn((t + 1) // 2, (t + 1) % 2)
                    output((t - 1) // 2, (t - 1) % 2)
                output((rows_tiles - 1) // 2, (rows_tiles - 1) % 2)
                if norm_behind:
                    for j in range(PAIRS):
                        norm_turn(pe, j, tiles_of(core["xn"]))

            @block.scalar
            def _(act):
                act.wait_ge(small_in, 16 * len(loads))
                act.wait_ge(shifted, 1)
                nc.scalar.activation(pr[:, :, :], pr[:, :, :], ACT.Exp).then_inc(exped, 1)
                if shared:
                    for n in range(SC * PAIRS):
                        act.wait_ge(s_clipped, n + 1)
                        nc.scalar.activation(sg[:, n % 4, :], sg[:, n % 4, :], ACT.Silu).then_inc(s_silued, 1)

                def store_rows(jj, p):
                    t = 2 * jj + p
                    act.wait_ge(rows_turned, t + 1)
                    if later(t):
                        act.wait_ge(hid_ready, FC * (t - 1))
                    if affine:
                        for c in range(DC):
                            last = nc.scalar.activation(xrt[:, p, c, :], ps[:, 7, c * PAIR:(c + 1) * PAIR], ACT.Identity,
                                                        bias=gb[:, 1, c:c + 1], scale=gb[:, 0, c:c + 1])
                    else:
                        last = copy_bank(nc, xrt[:, p].rearrange("p c n -> p (c n)"), ps[:, 7, :])
                    last.then_inc(rows_stored, 1)

                def activate(jj, p):
                    t = 2 * jj + p
                    for f in range(FC):
                        if swiglu:
                            act.wait_ge(clipped, FC * t + (f + 1))
                            nc.scalar.activation(sg[:, f % 4, :], sg[:, f % 4, :], ACT.Silu).then_inc(silued, 1)
                        else:
                            act.wait_ge(hid_ready, FC * t + (f + 1))
                            if f == 0 and later(t):
                                act.wait_ge(out_ready, t - 1)
                            nc.scalar.activation(ht[:, p, f, :], ps[:, f % 4, 0:PAIR], ACT.Relu).then_inc(hid_stored, 1)

                def store_y(jj, p):
                    t = 2 * jj + p
                    act.wait_ge(out_ready, t + 1)
                    if later(t):
                        act.wait_ge(y_sent[p], 16 * jj)
                    copy_bank(nc, yt[:, p].rearrange("p u d -> p (u d)"), ps[:, 4 + p, :]).then_inc(y_stored, 1)

                store_rows(0, 0)
                for t in range(3):
                    activate(t // 2, t % 2)
                    store_rows((t + 1) // 2, (t + 1) % 2)
                    if t >= 1:
                        store_y((t - 1) // 2, (t - 1) % 2)
                with act.Fori(1, 1 + LOOPS) as jj:
                    activate(jj, 1)
                    store_rows(jj + 1, 0)
                    store_y(jj, 0)
                    activate(jj + 1, 0)
                    store_rows(jj + 1, 1)
                    store_y(jj, 1)
                for t in range(FIRST_LEFT, rows_tiles):
                    activate(t // 2, t % 2)
                    if t + 1 < rows_tiles:
                        store_rows((t + 1) // 2, (t + 1) % 2)
                    store_y((t - 1) // 2, (t - 1) % 2)
                store_y((rows_tiles - 1) // 2, (rows_tiles - 1) % 2)
                if norm_behind:
                    for j in range(PAIRS):
                        norm_store(act, j, [(core["xt"], None, None)])

            @block.vector
            def _(dve):
                def over_experts(x):
                    return x.unsqueeze(2).to_broadcast([P, TILES, E])

                def over_tiles(x):
                    return x.unsqueeze(1).to_broadcast([P, TILES, E])

                tt, stt, ts = nc.vector.tensor_tensor, nc.vector.scalar_tensor_tensor, nc.vector.tensor_scalar
                reduce = nc.vector.tensor_reduce
                dve.wait_ge(logits_ready, 1)
                logits = ps[:, 0, 0:TILES * E].rearrange("p (t e) -> p t e", e=E)
                reduce(col[:, 0, :], logits, AX_X, ALU.max)
                dve.drain()
                tt(pr[:, :, :], logits, over_experts(col[:, 0, :]), ALU.subtract).then_inc(shifted, 1)
                dve.wait_ge(exped, 1)
                reduce(col[:, 0, :], pr[:, :, :], AX_X, ALU.add)
                dve.drain()
                nc.vector.reciprocal(col[:, 0, :], col[:, 0, :])
                dve.drain()
                tt(pr[:, :, :], pr[:, :, :], over_experts(col[:, 0, :]), ALU.mult)
                dve.wait_ge(made, 6)
                for k in range(top):
                    dve.drain()
                    reduce(best[:, k, :], pr[:, :, :], AX_X, ALU.max)
                    dve.drain()
                    tt(eq[:, :, :], pr[:, :, :], over_experts(best[:, k, :]), ALU.is_equal)
                    dve.drain()
                    stt(eq[:, :, :], eq[:, :, :], -float(E), over_tiles(iota_e[:, :]), ALU.mult, ALU.add)
                    dve.drain()
                    reduce(col[:, 1, :], eq[:, :, :], AX_X, ALU.min)
                    dve.drain()
                    tt(hot[k][:, :, :], eq[:, :, :], over_experts(col[:, 1, :]), ALU.is_equal)
                    dve.drain()
                    if k + 1 < top:
                        stt(pr[:, :, :], hot[k][:, :, :], -2.0, pr[:, :, :], ALU.mult, ALU.add)
                if top == 1:
                    nc.vector.tensor_copy(hots[:, :, :], hot[0][:, :, :]).then_inc(chosen, 1)
                    ts(weight[:, 0, :], best[:, 0, :], gate, None, ALU.mult)
                else:
                    tt(hots[:, :, :], hot[0][:, :, :], hot[1][:, :, :], ALU.add).then_inc(chosen, 1)
                    tt(col[:, 0, :], best[:, 0, :], best[:, 1, :], ALU.add)
                    dve.drain()
                    nc.vector.reciprocal(col[:, 0, :], col[:, 0, :])
                    dve.drain()
                    for k in range(2):
                        stt(weight[:, k, :], best[:, k, :], gate, col[:, 0, :], ALU.mult, ALU.mult)
                dve.wait_ge(counted, 1)
                counts = ps[:, 6, 0:TILES * E].rearrange("p (t e) -> p t e", e=E)
                nc.vector.tensor_copy(total[:, :, :], counts)
                nc.vector.tensor_copy(scan[0][:, :, :], counts)
                dve.drain()
                for n, step in enumerate((1, 2, 4, 8)):
                    x, y = scan[n % 2], scan[1 - n % 2]
                    nc.vector.tensor_copy(y[:, 0:step, :], x[:, 0:step, :])
                    tt(y[:, step:, :], x[:, step:, :], x[:, 0:TILES - step, :], ALU.add)
                    dve.drain()
                if capacity:
                    ts(ends[0][:, :], iota_e[:, :], float(capacity), None, ALU.mult)
                else:
                    ts(need_i[:, :], scan[0][:, TILES - 1, :], float(PAIR - 1), None, ALU.add)
                    dve.drain()
                    ts(need_i[:, :], need_i[:, :], 8, None, ALU.arith_shift_right)
                    dve.drain()
                    nc.vector.tensor_copy(need[:, :], need_i[:, :])
                    nc.vector.tensor_copy(ends[0][:, :], need_i[:, :])
                    dve.drain()
                    for n, step in enumerate((1, 2, 4)):
                        x, y = ends[n % 2], ends[1 - n % 2]
                        nc.vector.tensor_copy(y[:, 0:step], x[:, 0:step])
                        tt(y[:, step:], x[:, step:], x[:, 0:E - step], ALU.add)
                        dve.drain()
                    tt(owner[:, :, :], iota_t[:, :].unsqueeze(2).to_broadcast([P, rows_tiles, E]),
                       ends[1][:, :].unsqueeze(1).to_broadcast([P, rows_tiles, E]), ALU.is_ge)
                    dve.drain()
                    reduce(owner_f[:, :], owner[:, :, :], AX_X, ALU.add)
                    dve.drain()
                    ts(owner_i[:, :], owner_f[:, :], float(E - 1), None, ALU.min).then_inc(owners_made, 1)
                    tt(ends[0][:, :], ends[1][:, :], need[:, :], ALU.subtract)
                    dve.drain()
                    ts(ends[0][:, :], ends[0][:, :], float(PAIR), None, ALU.mult)
                tt(scan[0][:, :, :], scan[0][:, :, :], total[:, :, :], ALU.subtract)
                dve.drain()
                tt(scan[0][:, :, :], scan[0][:, :, :], ps[:, 5, 0:TILES * E].rearrange("p (t e) -> p t e", e=E), ALU.add)
                dve.drain()
                tt(scan[1][:, :, :], scan[0][:, :, :], over_tiles(ends[0][:, :]), ALU.add)
                dve.drain()
                for k in range(top):
                    tt(eq[:, :, :], hot[k][:, :, :], scan[1][:, :, :], ALU.mult)
                    dve.drain()
                    reduce(slot_f[:, :], eq[:, :, :], AX_X, ALU.add)
                    dve.drain()
                    if capacity:
                        tt(eq[:, :, :], hot[k][:, :, :], scan[0][:, :, :], ALU.mult)
                        dve.drain()
                        reduce(col[:, 0, :], eq[:, :, :], AX_X, ALU.add)
                        dve.drain()
                        ts(col[:, 0, :], col[:, 0, :], float(capacity), None, ALU.is_lt)
                        dve.drain()
                        stt(slot_f[:, :], slot_f[:, :], float(-ROWS), col[:, 0, :], ALU.add, ALU.mult)
                        dve.drain()
                        ts(slot_f[:, :], slot_f[:, :], float(ROWS), None, ALU.add)
                        dve.drain()
                    last = nc.vector.tensor_copy(slot[:, k, :], slot_f[:, :])
                    dve.drain()
                nc.vector.tensor_copy(slot_f[:, :], slot_f[:, :]).then_inc(slots_made, 1)

                if shared:
                    def s_clip(n):
                        dve.wait_ge(s_hid_ready, n + 1)
                        ts(sg[:, n % 4, :], ps[:, 1 + n % 2, 0:PAIR], 10.0, -10.0, ALU.min,
                           ALU.max).then_inc(s_clipped, 1)

                    def s_multiply(n):
                        q = n // SC
                        dve.wait_ge(s_silued, n + 1)
                        if q >= 2:
                            dve.wait_ge(s_out_ready, q - 1)
                        tt(ht[:, q % 2, n % SC, :], sg[:, n % 4, :], ps[:, 1 + n % 2, PAIR:2 * PAIR],
                           ALU.mult).then_inc(s_hid_stored, 1)

                    for j in range(PAIRS + 1):
                        if j < PAIRS:
                            s_clip(2 * j)
                            s_clip(2 * j + 1)
                            s_multiply(2 * j)
                            s_multiply(2 * j + 1)
                        if j >= 1:
                            q = j - 1
                            dve.wait_ge(s_out_ready, j)
                            x2 = core["x"][:, 2 * q:2 * q + 2, :].rearrange("p u d -> p (u d)")
                            stt(x2, ps[:, 3 + q % 2, :], gate, x2, ALU.mult, ALU.add).then_inc(s_added, 1)

                if swiglu:
                    def clip(t, f):
                        dve.wait_ge(hid_ready, FC * t + (f + 1))
                        ts(sg[:, f % 4, :], ps[:, f % 4, 0:PAIR], 10.0, -10.0, ALU.min, ALU.max).then_inc(clipped, 1)

                    def multiply(t, p, f):
                        dve.wait_ge(silued, FC * t + (f + 1))
                        if f == 0 and later(t):
                            dve.wait_ge(out_ready, t - 1)
                        tt(ht[:, p, f, :], sg[:, f % 4, :], ps[:, f % 4, PAIR:2 * PAIR], ALU.mult).then_inc(hid_stored, 1)

                    def gates(jj, p):
                        t = 2 * jj + p
                        clip(t, 0)
                        for f in range(1, FC):
                            clip(t, f)
                            multiply(t, p, f - 1)
                        multiply(t, p, FC - 1)

                    for t in range(3):
                        gates(t // 2, t % 2)
                    with dve.Fori(1, 1 + LOOPS) as jj:
                        gates(jj, 1)
                        gates(jj + 1, 0)
                    for t in range(FIRST_LEFT, rows_tiles):
                        gates(t // 2, t % 2)
                for n in range(TILES * top):
                    i, k = n // top, n % top
                    dve.wait_ge(gathered[n % 4], 16 * (n // 4 + 1))
                    stt(core["x"][:, i, :], yg[:, n % 4, :], weight[:, k, i:i + 1], core["x"][:, i, :], ALU.mult,
                        ALU.add).then_inc(added, 1)
                    dve.drain()
                    if norm_behind and n % (2 * top) == 2 * top - 1:
                        j = n // (2 * top)
                        norm_measure(dve, j, tiles_of(core["x"]))
                        norm_normalise(dve, j, tiles_of(core["x"]), tiles_of(core["xn"]))
        clear_semaphores()


def stage_one_head(core, a):
    nc, ps = core["nc"], core["ps"]
    gate = core["gate_attn"][:, 1:2]
    BK = B * KEYS
    with ExitStack() as ctx:
        def sb(part, shape):
            return ctx.enter_context(nc.sbuf_tensor(f"l1a_{part}", shape, F32))

        sem, clear_semaphores = named_semaphores(nc, "l1a")
        w_in, zeroed, w_ready, w_stored = sem("w_in"), sem("zeroed"), sem("w_ready"), sem("w_stored")
        kv_ready, kv_stored, fold_ready, fold_stored = sem("kv_ready"), sem("kv_stored"), sem("fold_ready"), sem("fold_stored")
        values_made = sem("values_made")
        scores_ready, centred, exped = sem("scores_ready"), sem("centred"), sem("exped")
        probs_ready, probs_turned, probs_stored = sem("probs_ready"), sem("probs_turned"), sem("probs_stored")
        out_ready, out_added = sem("out_ready"), sem("out_added")
        norm_measure, norm_root, norm_normalise, norm_turn, norm_store, norm_stored = layer_norm(core, ctx, sem, "l1a_norm", on_vector=True)
        wq, wq_t = sb("wq", [P, DC, D]), sb("wq_t", [P, DC, D])
        wk, wv = sb("wk", [P, D]), sb("wv", [P, D])
        bq, bk, bv = sb("bq", [P, DC]), sb("bk", [P, DC]), sb("bv", [P, D])
        bq_wide = sb("bq_wide", [P, DC, P])
        keys_t, values = sb("keys_t", [P, DC, BK]), sb("values", [P, D])
        fold_q, score_bias = sb("fold_q", [P, DC, BK]), sb("score_bias", [P, BK])
        ex = sb("ex", [P, B, 2, 2, BK])
        mx, sm = sb("mx", [P, 2, 2]), sb("sm", [P, 2, 2])
        pt = sb("pt", [P, 2, PAIR])
        loads = [(wq[:, :, :], a["L1_xattn_Wq"].rearrange("(c p) n -> p c n", p=P)), (wk[:, :], a["L1_xattn_Wk"]),
                 (wv[:, :], a["L1_xattn_Wv"]), (bq[:, :], columns(a["L1_xattn_bq"])),
                 (bk[:, :], columns(a["L1_xattn_bk"])), (bv[:, :], rows(a["L1_xattn_bv"]))]

        def own(j):
            b = j // (PAIRS // B)
            return ex[:, b, j % 2, :, b * KEYS:(b + 1) * KEYS]

        with nc.Block() as block:
            @block.sync
            def _(sp):
                for dst, src in loads:
                    sp.dma_start(dst, src).then_inc(w_in, 16)

            @block.gpsimd
            def _(pool):
                nc.gpsimd.memset(ex[:, :, :, :, :], 0.0).then_inc(zeroed, 1)

            @block.tensor
            def _(pe):
                pe.wait_ge(w_in, 16 * len(loads))
                for ec in range(DC):
                    for dc in range(DC):
                        last = nc.tensor.transpose(ps[:, 0, ec * D + dc * P:ec * D + (dc + 1) * P],
                                                   wq[:, dc, ec * P:(ec + 1) * P], core["ident"][:, :])
                last.then_inc(w_ready, 1)
                for ec in range(DC):
                    nc.tensor.matmul(ps[:, 1, ec * BK:(ec + 1) * BK], wk[:, ec * P:(ec + 1) * P], core["ctx_t"][:, :],
                                     start=True, stop=True)
                nc.tensor.matmul(ps[:, 2, 0:D], core["ctx_t"][:, :], wv[:, :], start=True, stop=True).then_inc(kv_ready, 1)
                pe.wait_ge(w_stored, 1)
                pe.wait_ge(kv_stored, 1)
                pe.wait_ge(values_made, 1)
                for dc in range(DC):
                    for ec in range(DC):
                        nc.tensor.matmul(ps[:, 3, dc * BK:(dc + 1) * BK], wq_t[:, ec, dc * P:(dc + 1) * P],
                                         keys_t[:, ec, :], start=(ec == 0), stop=(ec == DC - 1))
                for ec in range(DC):
                    last = nc.tensor.matmul(ps[:, 4, 0:BK], bq_wide[:, ec, :], keys_t[:, ec, :],
                                            start=(ec == 0), stop=(ec == DC - 1))
                last.then_inc(fold_ready, 1)
                pe.wait_ge(fold_stored, 2)
                for j in range(PAIRS + 3):
                    if j < PAIRS:
                        b = j // (PAIRS // B)
                        if j >= 2:
                            pe.wait_ge(centred, j - 1)
                        for u in range(2):
                            i = 2 * j + u
                            for dc in range(DC):
                                last = nc.tensor.matmul(ps[:, j % 2, u * KEYS:(u + 1) * KEYS],
                                                        core["xt"][:, dc, i * P:(i + 1) * P],
                                                        fold_q[:, dc, b * KEYS:(b + 1) * KEYS],
                                                        start=(dc == 0), stop=(dc == DC - 1))
                        last.then_inc(scores_ready, 1)
                    if 1 <= j <= PAIRS:
                        k = j - 1
                        pe.wait_ge(probs_ready, k + 1)
                        if k >= 1:
                            pe.wait_ge(probs_stored, k)
                        for u in range(2):
                            last = nc.tensor.transpose(ps[:, 4, u * P:(u + 1) * P],
                                                       ex[:, k // (PAIRS // B), k % 2, u, :], core["ident"][:, :])
                        last.then_inc(probs_turned, 1)
                    if j >= 3:
                        norm_turn(pe, j - 3, tiles_of(core["xn"]))
                    if 2 <= j <= PAIRS + 1:
                        k = j - 2
                        pe.wait_ge(probs_stored, k + 1)
                        if k >= 2:
                            pe.wait_ge(out_added, k - 1)
                        for u in range(2):
                            last = nc.tensor.matmul(ps[:, 5 + k % 2, u * D:(u + 1) * D], pt[:, k % 2, u * P:(u + 1) * P],
                                                    values[:, :], start=True, stop=True)
                        last.then_inc(out_ready, 1)

            @block.scalar
            def _(act):
                act.wait_ge(w_ready, 1)
                copy_bank(nc, wq_t[:, :, :].rearrange("p c d -> p (c d)"), ps[:, 0, :]).then_inc(w_stored, 1)
                act.wait_ge(kv_ready, 1)
                for ec in range(DC):
                    last = nc.scalar.activation(keys_t[:, ec, :], ps[:, 1, ec * BK:(ec + 1) * BK], ACT.Identity,
                                                bias=bk[:, ec:ec + 1])
                last.then_inc(kv_stored, 1)
                act.wait_ge(fold_ready, 1)
                copy_bank(nc, fold_q[:, :, :].rearrange("p c k -> p (c k)"), ps[:, 3, 0:DC * BK]).then_inc(fold_stored, 1)
                copy_bank(nc, score_bias[:, :], ps[:, 4, 0:BK]).then_inc(fold_stored, 1)
                for j in range(PAIRS + 3):
                    if j < PAIRS:
                        act.wait_ge(centred, j + 1)
                        nc.scalar.activation(own(j), own(j), ACT.Exp).then_inc(exped, 1)
                    if 1 <= j <= PAIRS:
                        k = j - 1
                        act.wait_ge(probs_turned, k + 1)
                        if k >= 2:
                            act.wait_ge(out_ready, k - 1)
                        copy_bank(nc, pt[:, k % 2, :], ps[:, 4, 0:PAIR]).then_inc(probs_stored, 1)
                    if j >= 3:
                        norm_store(act, j - 3, [(core["xt"], None, None)])

            @block.vector
            def _(dve):
                dve.wait_ge(w_in, 16 * len(loads))
                nc.vector.tensor_copy(bq_wide[:, :, :], bq[:, :].unsqueeze(2).to_broadcast([P, DC, P]))
                dve.wait_ge(kv_ready, 1)
                nc.vector.tensor_tensor(values[:, :], ps[:, 2, 0:D], bv[:, :], ALU.add).then_inc(values_made, 1)
                dve.wait_ge(fold_stored, 2)
                dve.wait_ge(zeroed, 1)
                for j in range(PAIRS + 3):
                    if 1 <= j <= PAIRS:
                        k = j - 1
                        dve.wait_ge(exped, k + 1)
                        nc.vector.tensor_reduce(sm[:, k % 2, :], own(k), AX_X, ALU.add)
                        dve.drain()
                        nc.vector.reciprocal(sm[:, k % 2, :], sm[:, k % 2, :])
                        dve.drain()
                        nc.vector.tensor_tensor(own(k), own(k), sm[:, k % 2, :].unsqueeze(2).to_broadcast([P, 2, KEYS]),
                                                ALU.mult).then_inc(probs_ready, 1)
                    if j < PAIRS:
                        b = j // (PAIRS // B)
                        dve.wait_ge(scores_ready, j + 1)
                        if j >= 2:
                            dve.wait_ge(probs_turned, j - 1)
                        nc.vector.tensor_tensor(
                            own(j), ps[:, j % 2, 0:2 * KEYS].rearrange("p (u k) -> p u k", u=2),
                            score_bias[:, b * KEYS:(b + 1) * KEYS].unsqueeze(1).to_broadcast([P, 2, KEYS]), ALU.add)
                        dve.drain()
                        nc.vector.tensor_reduce(mx[:, j % 2, :], own(j), AX_X, ALU.max)
                        dve.drain()
                        nc.vector.tensor_tensor(own(j), own(j), mx[:, j % 2, :].unsqueeze(2).to_broadcast([P, 2, KEYS]),
                                                ALU.subtract).then_inc(centred, 1)
                    if 2 <= j <= PAIRS + 1:
                        k = j - 2
                        dve.wait_ge(out_ready, k + 1)
                        x2 = pair_of(core["x"], k)
                        nc.vector.scalar_tensor_tensor(x2, ps[:, 5 + k % 2, :], gate, x2, ALU.mult,
                                                       ALU.add).then_inc(out_added, 1)
                        dve.drain()
                        norm_measure(dve, k, tiles_of(core["x"]))
                        norm_normalise(dve, k, tiles_of(core["x"]), tiles_of(core["xn"]))
        clear_semaphores()


def stage_adapter(core, a):
    nc, ps = core["nc"], core["ps"]
    gate = core["gate_ffn"][:, 1:2]
    R = 64
    with ExitStack() as ctx:
        def sb(part, shape, dtype=F32):
            return ctx.enter_context(nc.sbuf_tensor(f"l1f_{part}", shape, dtype))

        sem, clear_semaphores = named_semaphores(nc, "l1f")
        w_in, made = sem("w_in"), sem("made")
        inv_made, inv_turned, sums_made, squares_made = sem("inv_made"), sem("inv_turned"), sem("sums_made"), sem("squares_made")
        means_wide, losses_ready, chosen, hot_turned = sem("means_wide"), sem("losses_ready"), sem("chosen"), sem("hot_turned")
        hot_stored, gathered = sem("hot_stored"), sem("gathered")
        step_ready, step_stored = sem("step_ready"), sem("step_stored")
        const_made, bias_added = sem("const_made"), sem("bias_added")
        hid_ready, hid_stored, out_ready, out_added = sem("hid_ready"), sem("hid_stored"), sem("out_ready"), sem("out_added")
        norm_measure, norm_root, norm_normalise, norm_turn, norm_store, norm_stored = layer_norm(core, ctx, sem, "l1f_norm", on_vector=True)
        base, base_t = sb("base", [P, DC, D]), sb("base_t", [P, DC, D])
        base_row = sb("base_row", [P, D])
        mu, sigma = sb("mu", [E, D]), sb("sigma", [E, D])
        inv = sb("inv", [E, 3, D])
        inv_t = sb("inv_t", [P, 3, DC, E])
        down_b, up_b, conv_b = sb("down_b", [E, R]), sb("up_b", [E, D]), sb("conv_b", [E, D])
        sums = sb("sums", [P, 2, DC, B])
        junk = sb("junk", [P, TOK])
        wide = sb("wide", [P, 3, DC, B, P])
        iota_e, iota_p = sb("iota_e", [P, E]), sb("iota_p", [P, 1])
        loss, cand, hot = sb("loss", [P, B, E]), sb("cand", [P, B, E]), sb("hot", [P, B, E])
        low, index = sb("low", [P, B]), sb("index", [P, B])
        where_f = sb("where_f", [P, 3, B])
        where = sb("where", [P, 3, B], I32)
        hot_t = sb("hot_t", [E, B, P])
        down = sb("down", [P, B, DC, P])
        conv, up = sb("conv", [P, B, DC, D]), sb("up", [R, B, D])
        conv_t, up_t = sb("conv_t", [P, B, DC, D]), sb("up_t", [P, B, DC, P])
        up_wide = sb("up_wide", [P, DC, B, P])
        down_col = sb("down_col", [P, B])
        fold = sb("fold", [P, B, D])
        const = sb("const", [P, B, D])
        ht = sb("ht", [P, 2, PAIR])
        loads = [(base[:, :, :], a["L1_ffn_base_W"].rearrange("(c p) d -> p c d", p=P)),
                 (base_row[:, :], rows(a["L1_ffn_base_b"])), (mu[:, :], a["L1_ffn_disc_mu"]),
                 (sigma[:, :], a["L1_ffn_disc_sigma"]), (down_b[:, :], a["L1_ffn_down_b"]),
                 (up_b[:, :], a["L1_ffn_up_b"]), (conv_b[:, :], a["L1_ffn_conv_b"])]
        down_rows = a["L1_ffn_down_W"].rearrange("e d r -> (e d) r")
        conv_rows = a["L1_ffn_conv_W"].rearrange("e o d -> (e o) d")
        up_rows = a["L1_ffn_up_W"].rearrange("e r d -> (e r) d")
        GATHERS = B * (2 * DC + 1)

        def turned(dst_part, src, ident_rows, cols):
            return lambda bank: nc.tensor.transpose(ps[0:cols, bank, dst_part:dst_part + ident_rows], src,
                                                    core["ident"][0:ident_rows, 0:ident_rows])

        def product(rows_n, c0, cols, parts):
            def go(bank):
                for n, (lhs, rhs) in enumerate(parts):
                    last = nc.tensor.matmul(ps[0:rows_n, bank, c0:c0 + cols], lhs, rhs, start=(n == 0),
                                            stop=(n == len(parts) - 1))
                return last
            return go

        steps = [([turned(dc * D + oc * P, base[:, oc, dc * P:(dc + 1) * P], P, P) for dc in range(DC) for oc in range(DC)],
                  P, 2 * D, base_t[:, :, :].rearrange("p c d -> p (c d)"))]
        for b in range(B):
            steps.append(([turned(dc * D + oc * P, conv[:, b, oc, dc * P:(dc + 1) * P], P, P)
                           for dc in range(DC) for oc in range(DC)], P, 2 * D,
                          conv_t[:, b].rearrange("p c d -> p (c d)")))
            for dc in range(DC):
                steps.append(([turned(0, up[:, b, dc * P:(dc + 1) * P], R, P)], P, R, up_t[:, b, dc, 0:R]))
        for dc in range(DC):
            steps.append(([product(P, 0, B * P, [(up_b[:, dc * P:(dc + 1) * P], hot_t[:, :, :].rearrange("e b n -> e (b n)"))])],
                          P, B * P, up_wide[:, dc].rearrange("p b n -> p (b n)")))
        steps.append(([product(R, 0, B * P, [(down_b[:, :], hot_t[:, :, :].rearrange("e b n -> e (b n)"))])], R, B * P, None))
        for b in range(B):
            steps.append(([product(P, 0, D, [(up_t[:, b, dc, :], conv_t[:, b, dc, :]) for dc in range(DC)])],
                          P, D, fold[:, b, :]))
            steps.append(([product(P, 0, D, [(up_wide[:, dc, b, :], conv_t[:, b, dc, :]) for dc in range(DC)]
                                   + [(hot_t[:, b, :], conv_b[:, :])])], P, D, const[:, b, :]))

        with nc.Block() as block:
            @block.sync
            def _(sp):
                for dst, src in loads:
                    sp.dma_start(dst, src).then_inc(w_in, 16)

            @block.gpsimd
            def _(pool):
                nc.gpsimd.memset(down[:, :, :, :], 0.0).then_inc(made, 1)
                nc.gpsimd.memset(up_t[:, :, :, :], 0.0).then_inc(made, 1)
                nc.gpsimd.memset(wide[:, 2], 1.0).then_inc(made, 1)
                nc.gpsimd.memset(down_col[:, :], 0.0).then_inc(made, 1)
                nc.gpsimd.iota(iota_e[:, :], [[1, E]], base=0, channel_multiplier=0,
                               allow_small_or_imprecise_dtypes=True).then_inc(made, 1)
                nc.gpsimd.iota(iota_p[:, :], [[0, 1]], base=0, channel_multiplier=1,
                               allow_small_or_imprecise_dtypes=True).then_inc(made, 1)
                pool.wait_ge(made, 6)
                pool.wait_ge(chosen, 2)

                def gather(dst, src, index, bound):
                    pool.indirect_dma_start(dst, None, src, bass.IndirectOffsetOnAxis(ap=index, axis=0),
                                            bounds_check=bound - 1, oob_is_err=False).then_inc(gathered, 16)

                for b in range(B):
                    for c in range(DC):
                        gather(conv[:, b, c, :], conv_rows, where[:, c, b:b + 1], E * D)
                        gather(down[:, b, c, 0:R], down_rows, where[:, c, b:b + 1], E * D)
                    gather(up[:, b, :], up_rows, where[0:R, 2, b:b + 1], E * R)
                pool.wait_ge(const_made, 1)
                for j in range(PAIRS):
                    for u in range(2):
                        i = 2 * j + u
                        last = nc.gpsimd.tensor_tensor(core["x"][:, i, :], core["x"][:, i, :], const[:, j // (PAIRS // B), :], ALU.add)
                    last.then_inc(bias_added, 1)

            @block.tensor
            def _(pe):
                pe.wait_ge(inv_made, 1)
                for k in range(3):
                    for dc in range(DC):
                        last = nc.tensor.transpose(ps[:, 2, (k * DC + dc) * E:(k * DC + dc + 1) * E],
                                                   inv[:, k, dc * P:(dc + 1) * P], core["ident"][0:E, 0:E])
                last.then_inc(inv_turned, 1)
                pe.wait_ge(means_wide, 2)
                for b in range(B):
                    for n in range(3 * DC):
                        k, dc = n // DC, n % DC
                        last = nc.tensor.matmul(ps[:, 3, b * E:(b + 1) * E], wide[:, k, dc, b, :], inv_t[:, k, dc, :],
                                                start=(n == 0), stop=(n == 3 * DC - 1))
                last.then_inc(losses_ready, 1)
                pe.wait_ge(chosen, 1)
                for b in range(B):
                    last = nc.tensor.transpose(ps[0:E, 2, b * P:(b + 1) * P], hot[:, b, :], core["ident"][:, :])
                last.then_inc(hot_turned, 1)
                pe.wait_ge(hot_stored, 1)
                for n, (emit, _, _, _) in enumerate(steps):
                    if n == 1:
                        pe.wait_ge(gathered, 16 * GATHERS)
                    if n >= 2:
                        pe.wait_ge(step_stored, n - 1)
                    if n >= 7 + DC + 1:
                        pe.wait_ge(step_stored, n if n == 7 + DC + 1 else n - 1)
                    for go in emit:
                        last = go(n % 2)
                    last.then_inc(step_ready, 1)
                pe.wait_ge(step_stored, len(steps))
                for j in range(PAIRS + 3):
                    if j < PAIRS:
                        b = j // (PAIRS // B)
                        if j >= 2:
                            pe.wait_ge(hid_stored, j - 1)
                        for dc in range(DC):
                            last = nc.tensor.matmul(ps[:, 2 + j % 2, 0:PAIR], down[:, b, dc, :],
                                                    core["xt"][:, dc, PAIR * j:PAIR * (j + 1)],
                                                    start=(dc == 0), stop=(dc == DC - 1))
                        last.then_inc(hid_ready, 1)
                    if 1 <= j <= PAIRS:
                        k = j - 1
                        pe.wait_ge(hid_stored, k + 1)
                        if k >= 2:
                            pe.wait_ge(out_added, k - 1)
                        for u in range(2):
                            i = 2 * k + u
                            out = ps[:, 4 + k % 2, u * D:(u + 1) * D]
                            for dc in range(DC):
                                nc.tensor.matmul(out, core["xt"][:, dc, i * P:(i + 1) * P], base_t[:, dc, :],
                                                 start=(dc == 0), stop=False)
                            last = nc.tensor.matmul(out, ht[:, k % 2, u * P:(u + 1) * P], fold[:, k // (PAIRS // B), :],
                                                    start=False, stop=True)
                        last.then_inc(out_ready, 1)
                    if j >= 3:
                        norm_turn(pe, j - 3, tiles_of(core["xn"]))

            @block.scalar
            def _(act):
                for dc in range(DC):
                    for b in range(B):
                        last = nc.scalar.activation(junk[:, :], core["xt"][:, dc, b * TOK:(b + 1) * TOK], ACT.Square,
                                                    accum_out=sums[:, 1, dc, b:b + 1])
                        act.drain()
                nc.scalar.activation(junk[:, 0:1], core["xt"][:, 0, 0:1], ACT.Copy).then_inc(squares_made, 1)
                act.wait_ge(inv_turned, 1)
                copy_bank(nc, inv_t[:, :, :, :].rearrange("p k c e -> p (k c e)"), ps[:, 2, 0:3 * DC * E]).then_inc(means_wide, 1)
                act.wait_ge(hot_turned, 1)
                copy_bank(nc, hot_t[:, :, :].rearrange("e b n -> e (b n)"), ps[0:E, 2, 0:B * P]).then_inc(hot_stored, 1)
                act.wait_ge(made, 6)
                for n, (_, rows_n, cols, dst) in enumerate(steps):
                    act.wait_ge(step_ready, n + 1)
                    if dst is None:
                        last = nc.scalar.activation(
                            down_col[0:R, :], ps[0:R, n % 2, 0:B * P].rearrange("p (b n) -> p b n", b=B)[:, :, 0], ACT.Copy)
                    else:
                        last = copy_bank(nc, dst, ps[0:rows_n, n % 2, 0:cols])
                    last.then_inc(step_stored, 1)
                for j in range(PAIRS + 3):
                    if j < PAIRS:
                        act.wait_ge(hid_ready, j + 1)
                        if j >= 2:
                            act.wait_ge(out_ready, j - 1)
                        nc.scalar.activation(ht[:, j % 2, :], ps[:, 2 + j % 2, 0:PAIR], ACT.Relu,
                                             bias=down_col[:, j // (PAIRS // B):j // (PAIRS // B) + 1]).then_inc(hid_stored, 1)
                    if j >= 3:
                        norm_store(act, j - 3, [(core["xt"], None, None)])

            @block.vector
            def _(dve):
                tt, ts = nc.vector.tensor_tensor, nc.vector.tensor_scalar
                dve.wait_ge(w_in, 16 * len(loads))
                tt(sigma[:, :], sigma[:, :], sigma[:, :], ALU.mult)
                dve.drain()
                nc.vector.reciprocal(inv[:, 0, :], sigma[:, :])
                dve.drain()
                tt(inv[:, 1, :], mu[:, :], inv[:, 0, :], ALU.mult)
                dve.drain()
                tt(inv[:, 2, :], mu[:, :], inv[:, 1, :], ALU.mult)
                dve.drain()
                ts(inv[:, 1, :], inv[:, 1, :], -2.0, None, ALU.mult).then_inc(inv_made, 1)
                nc.vector.tensor_reduce(sums[:, 0].rearrange("p c b -> p (c b)"),
                                        core["xt"][:, :, :].rearrange("p c (b n) -> p (c b) n", b=B), AX_X, ALU.add)
                dve.drain()
                dve.wait_ge(squares_made, 1)
                dve.wait_ge(made, 6)
                for k in range(2):
                    last = ts(wide[:, k], sums[:, 1 - k].unsqueeze(3).to_broadcast([P, DC, B, P]), 1.0 / TOK, None, ALU.mult)
                last.then_inc(means_wide, 1)
                dve.wait_ge(losses_ready, 1)
                nc.vector.tensor_copy(loss[:, :, :].rearrange("p b e -> p (b e)"), ps[:, 3, 0:B * E])
                dve.drain()
                nc.vector.tensor_reduce(low[:, :], loss[:, :, :], AX_X, ALU.min)
                dve.drain()
                tt(cand[:, :, :], loss[:, :, :], low[:, :].unsqueeze(2).to_broadcast([P, B, E]), ALU.is_equal)
                dve.drain()
                nc.vector.scalar_tensor_tensor(cand[:, :, :], cand[:, :, :], -float(E),
                                               iota_e[:, :].unsqueeze(1).to_broadcast([P, B, E]), ALU.mult, ALU.add)
                dve.drain()
                nc.vector.tensor_reduce(low[:, :], cand[:, :, :], AX_X, ALU.min)
                dve.drain()
                tt(hot[:, :, :], cand[:, :, :], low[:, :].unsqueeze(2).to_broadcast([P, B, E]),
                   ALU.is_equal).then_inc(chosen, 1)
                ts(index[:, :], low[:, :], float(E), None, ALU.add)
                dve.drain()
                for k, (size, first_row) in enumerate(((D, 0), (D, P), (R, 0))):
                    ts(where_f[:, k, :], index[:, :], float(size), float(first_row), ALU.mult, ALU.add)
                dve.drain()
                ts(where_f[:, :, :].rearrange("p k b -> p (k b)"), where_f[:, :, :].rearrange("p k b -> p (k b)"),
                   iota_p[:, 0:1], None, ALU.add)
                dve.drain()
                nc.vector.tensor_copy(where[:, :, :], where_f[:, :, :]).then_inc(chosen, 1)
                dve.wait_ge(step_stored, len(steps))
                tt(const[:, :, :], const[:, :, :], base_row[:, :].unsqueeze(1).to_broadcast([P, B, D]), ALU.add)
                dve.drain()
                ts(const[:, :, :], const[:, :, :], gate, None, ALU.mult).then_inc(const_made, 1)
                for j in range(PAIRS + 3):
                    if 2 <= j <= PAIRS + 1:
                        k = j - 2
                        dve.wait_ge(out_ready, k + 1)
                        dve.wait_ge(bias_added, k + 1)
                        x2 = pair_of(core["x"], k)
                        nc.vector.scalar_tensor_tensor(x2, ps[:, 4 + k % 2, :], gate, x2, ALU.mult,
                                                       ALU.add).then_inc(out_added, 1)
                        dve.drain()
                        norm_measure(dve, k, tiles_of(core["x"]))
                        norm_normalise(dve, k, tiles_of(core["x"]), tiles_of(core["xn"]))
        clear_semaphores()


def layout_l2(core, a):
    def layout(sb, wq_t, wo):
        wkv = sb("wkv", [P, 4, KD])
        wkv_t = sb("wkv_t", [P, 2, D])
        won = sb("won", [P, DC, D])
        loads = [(wq_t[:, :, :], a["L2_xattn_Wq"].rearrange("(c p) d -> p c d", p=P)),
                 (wkv[:, :, :], a["L2_xattn_Wkv"].rearrange("(c p) k -> p c k", p=P)),
                 (won[:, :, :], a["L2_xattn_Wo"].rearrange("(c p) n -> p c n", p=P))]
        turns = [([wkv[:, c, :] for c in range(4)], wkv_t[:, :, :].rearrange("p a n -> p (a n)")),
                 ([won[:, oc, c * P:(c + 1) * P] for c in range(DC) for oc in range(DC)],
                  wo[:, :, :].rearrange("p c n -> p (c n)"))]
        return loads, turns, wkv_t[:, 0, :], wkv_t[:, 1, :]
    return layout


def stage_low_rank(core, a):
    nc, ps = core["nc"], core["ps"]
    gate = core["gate_ffn"][:, 2:3]
    R = 64
    with ExitStack() as ctx:
        def sb(part, shape):
            return ctx.enter_context(nc.sbuf_tensor(f"l2f_{part}", shape, F32))

        sem, clear_semaphores = named_semaphores(nc, "l2f")
        w_in, zeroed, bias_made, bias_added = sem("w_in"), sem("zeroed"), sem("bias_made"), sem("bias_added")
        p_ready, p_stored, hid_ready, hid_stored = sem("p_ready"), sem("p_stored"), sem("hid_ready"), sem("hid_stored")
        q_ready, q_stored, out_ready, out_added = sem("q_ready"), sem("q_stored"), sem("out_ready"), sem("out_added")
        norm_measure, norm_root, norm_normalise, norm_turn, norm_store, norm_stored = layer_norm(core, ctx, sem, "l2f_norm", on_vector=True)
        u1, v1 = sb("u1", [P, DC, P]), sb("v1", [P, FF])
        u2, v2 = sb("u2", [P, FC, P]), sb("v2", [P, D])
        b1, b2 = sb("b1", [P, FC]), sb("b2", [P, D])
        pr = sb("pr", [P, 2, PAIR])
        ht = sb("ht", [P, 2, FC, PAIR])
        qr = sb("qr", [P, 2, PAIR])
        loads = [(u1[:, :, 0:R], a["L2_ffn_U1"].rearrange("(c p) r -> p c r", p=P)), (v1[0:R, :], a["L2_ffn_V1"]),
                 (u2[:, :, 0:R], a["L2_ffn_U2"].rearrange("(c p) r -> p c r", p=P)), (v2[0:R, :], a["L2_ffn_V2"]),
                 (b1[:, :], columns(a["L2_ffn_b1"])), (b2[:, :], rows(a["L2_ffn_b2"]))]

        with nc.Block() as block:
            @block.sync
            def _(sp):
                sp.wait_ge(zeroed, 4)
                for dst, src in loads:
                    sp.dma_start(dst, src).then_inc(w_in, 16)

            @block.gpsimd
            def _(pool):
                for n, padding in enumerate((u1[:, :, R:P], v1[R:P, :], u2[:, :, R:P], v2[R:P, :])):
                    if n >= 1:
                        pool.wait_ge(zeroed, n)
                    nc.gpsimd.memset(padding, 0.0).then_inc(zeroed, 1)
                pool.wait_ge(bias_made, 1)
                for j in range(PAIRS):
                    for u in range(2):
                        i = 2 * j + u
                        last = nc.gpsimd.tensor_tensor(core["x"][:, i, :], core["x"][:, i, :], b2[:, :], ALU.add)
                    last.then_inc(bias_added, 1)

            @block.tensor
            def _(pe):
                pe.wait_ge(w_in, 16 * len(loads))

                def first_rank(j):
                    if j >= 2:
                        pe.wait_ge(p_stored, j - 1)
                    for dc in range(DC):
                        last = nc.tensor.matmul(ps[:, 6 + j % 2, 0:PAIR], u1[:, dc, :], core["xt"][:, dc, PAIR * j:PAIR * (j + 1)],
                                                start=(dc == 0), stop=(dc == DC - 1))
                    last.then_inc(p_ready, 1)

                def second_rank(k):
                    pe.wait_ge(hid_stored, FC * (k + 1))
                    if k >= 1:
                        pe.wait_ge(q_stored, k)
                    for f in range(FC):
                        last = nc.tensor.matmul(ps[:, 4, 0:PAIR], u2[:, f, :], ht[:, k % 2, f, :], start=(f == 0),
                                                stop=(f == FC - 1))
                    last.then_inc(q_ready, 1)

                def output(k):
                    pe.wait_ge(q_stored, k + 1)
                    if k >= 1:
                        pe.wait_ge(out_added, k)
                    for u in range(2):
                        last = nc.tensor.matmul(ps[:, 5, u * D:(u + 1) * D], qr[:, k % 2, u * P:(u + 1) * P], v2[:, :],
                                                start=True, stop=True)
                    last.then_inc(out_ready, 1)

                first_rank(0)
                for j in range(PAIRS + 2):
                    if j + 1 < PAIRS:
                        first_rank(j + 1)
                    if j < PAIRS:
                        pe.wait_ge(p_stored, j + 1)
                        for f in range(FC):
                            n = FC * j + f
                            if n >= 4:
                                pe.wait_ge(hid_stored, n - 3)
                            nc.tensor.matmul(ps[:, n % 4, 0:PAIR], v1[:, f * P:(f + 1) * P], pr[:, j % 2, :],
                                             start=True, stop=True).then_inc(hid_ready, 1)
                    if 1 <= j <= PAIRS:
                        second_rank(j - 1)
                    if 2 <= j <= PAIRS + 1:
                        output(j - 2)

            @block.scalar
            def _(act):
                act.wait_ge(w_in, 16 * len(loads))

                def store_p(j):
                    act.wait_ge(p_ready, j + 1)
                    if j >= 2:
                        act.wait_ge(hid_ready, FC * (j - 1))
                    copy_bank(nc, pr[:, j % 2, :], ps[:, 6 + j % 2, 0:PAIR]).then_inc(p_stored, 1)

                store_p(0)
                for j in range(PAIRS + 1):
                    if j + 1 < PAIRS:
                        store_p(j + 1)
                    if j < PAIRS:
                        for f in range(FC):
                            n = FC * j + f
                            act.wait_ge(hid_ready, n + 1)
                            if j >= 2 and f == 0:
                                act.wait_ge(q_ready, j - 1)
                            nc.scalar.activation(ht[:, j % 2, f, :], ps[:, n % 4, 0:PAIR], ACT.Gelu_apprx_tanh,
                                                 bias=b1[:, f:f + 1]).then_inc(hid_stored, 1)
                    if 1 <= j <= PAIRS:
                        k = j - 1
                        act.wait_ge(q_ready, k + 1)
                        if k >= 2:
                            act.wait_ge(out_ready, k - 1)
                        copy_bank(nc, qr[:, k % 2, :], ps[:, 4, 0:PAIR]).then_inc(q_stored, 1)

            @block.vector
            def _(dve):
                dve.wait_ge(w_in, 16 * len(loads))
                nc.vector.tensor_scalar(b2[:, :], b2[:, :], gate, None, ALU.mult).then_inc(bias_made, 1)
                for j in range(PAIRS):
                    dve.wait_ge(out_ready, j + 1)
                    dve.wait_ge(bias_added, j + 1)
                    x2 = pair_of(core["x"], j)
                    nc.vector.scalar_tensor_tensor(x2, ps[:, 5, :], gate, x2, ALU.mult, ALU.add).then_inc(out_added, 1)
                    dve.drain()
                    norm_measure(dve, j, tiles_of(core["x"]))
                    norm_normalise(dve, j, tiles_of(core["x"]), tiles_of(core["xn"]))
        clear_semaphores()


L3_HEADS, L3_WIDTH = 16, 32
GROUP = P // L3_WIDTH
GROUPS = L3_HEADS // GROUP
ENTRIES = B * GROUPS
KC = TOK // P


def self_attention_scratch(nc):
    def dram(name, shape, dtype):
        return nc.dram_tensor(name, shape, dtype, kind="Internal").ap()

    parts = [[dram(f"l3_{kind}_part{m}", [ENTRIES + 1, P, TOK], BF16) for m in range(3)] for kind in ("q", "k")]
    values = dram("l3_values", [ENTRIES + 1, P, KC, P], F32)
    heads_out = dram("l3_heads_out", [ENTRIES, P, TOK], F32)
    return parts, values, heads_out


def stage_self_project(core, a, x1, scratch):
    nc, ps = core["nc"], core["ps"]
    q_k_parts, v_scratch, out_scratch = scratch
    HD = L3_HEADS * L3_WIDTH
    BANKS = HD // PAIR
    with ExitStack() as ctx:
        def sb(part, shape, dtype=F32):
            return ctx.enter_context(nc.sbuf_tensor(f"l3p_{part}", shape, dtype))

        sem, clear_semaphores = named_semaphores(nc, "l3p")
        w_in = sem("w_in")
        qk_ready, high_made, rest_made = sem("qk_ready"), sem("high_made"), sem("rest_made")
        mid_made, low_made = sem("mid_made"), sem("low_made")
        v_ready, v_stored = sem("v_ready"), sem("v_stored")
        sent = [sem("sent0"), sem("sent1")]
        norm1_measure, norm1_root, norm1_normalise, norm1_turn, norm1_store, norm1_stored = layer_norm(core, ctx, sem, "l3p_norm1", on_vector=True)
        norm2_measure, norm2_root, norm2_normalise, norm2_turn, norm2_store, norm2_stored = layer_norm(core, ctx, sem, "l3p_norm2", on_vector=True)
        wq, wk, wv = sb("wq", [P, DC, HD]), sb("wk", [P, DC, HD]), sb("wv", [P, DC, HD])
        ln1 = sb("ln1", [P, 2, D])
        gb = sb("gb", [P, 4, DC])
        yt = sb("yt", [P, DC, T])
        parts = sb("parts", [P, 2, 3, 2 * BANKS, 512], BF16)
        rest = sb("rest", [P, 2 * BANKS, 512])
        vs = sb("vs", [P, 2, 2, HD])
        loads = [(ln1[:, 0, :], rows(a["L3_xattn_ln1_g"])), (ln1[:, 1, :], rows(a["L3_xattn_ln1_b"]))]
        loads += [(gb[:, k, :], columns(a["L3_xattn_a1_" + n])) for k, n in enumerate(("lnx_g", "lnx_b", "lny_g", "lny_b"))]
        loads += [(w[:, c, :].rearrange("p (h d) -> p h d", h=L3_HEADS),
                   a["L3_xattn_a1_" + n].rearrange("h (c p) d -> c p h d", p=P)[c])
                  for w, n in ((wq, "wq"), (wk, "wk"), (wv, "wv")) for c in range(DC)]

        with nc.Block() as block:
            @block.sync
            def _(sp):
                for dst, src in loads:
                    sp.dma_start(dst, src).then_inc(w_in, 16)
                total = [0, 0]
                for k in range(PAIRS):
                    b, p, at = k // (PAIRS // B), k % 2, (k % (PAIRS // B)) * PAIR
                    places = [(b * GROUPS, GROUPS)]
                    if b == 0:
                        places.append((ENTRIES, 1))
                    sp.wait_ge(low_made, 2 * BANKS * (k + 1))
                    for first_entry, groups in places:
                        for kind in range(2):
                            for m in range(3):
                                sp.dma_start(
                                    q_k_parts[kind][m][first_entry:first_entry + groups, :, at:at + PAIR].rearrange("g p n -> p g n"),
                                    parts[:, p, m, kind * BANKS:(kind + 1) * BANKS, :].rearrange(
                                        "p m (g n) -> p (m g) n", n=PAIR)[:, 0:groups, :]).then_inc(sent[p], 16)
                                total[p] += 16
                    sp.wait_ge(v_stored, 2 * (k + 1))
                    for first_entry, groups in places:
                        for u in range(2):
                            sp.dma_start(
                                v_scratch[first_entry:first_entry + groups, :, at // P + u, :].rearrange("g p n -> p g n"),
                                vs[:, p, u, 0:groups * P].rearrange("p (g n) -> p g n", n=P)).then_inc(sent[p], 16)
                            total[p] += 16
                for p in range(2):
                    sp.wait_ge(sent[p], total[p])

            def sent_before(k):
                return sum(16 * 8 * (2 if q < PAIRS // B else 1) for q in range(k % 2, k, 2))

            @block.tensor
            def _(pe):
                pe.wait_ge(w_in, 16 * len(loads))
                for j in range(PAIRS + 1):
                    if j < PAIRS:
                        norm2_turn(pe, j, tiles_of(core["xn"]))
                    if j >= 1:
                        k = j - 1
                        pe.wait_ge(norm2_stored, k + 1)
                        for m in range(2 * BANKS):
                            w, src = (wq, core["xt"]) if m < BANKS else (wk, yt)
                            if k >= 1:
                                pe.wait_ge(rest_made, 2 * BANKS * (k - 1) + m + 1)
                            for h in range(2):
                                g = 2 * (m % BANKS) + h
                                for dc in range(DC):
                                    last = nc.tensor.matmul(ps[:, m, h * PAIR:(h + 1) * PAIR],
                                                            w[:, dc, g * P:(g + 1) * P],
                                                            src[:, dc, PAIR * k:PAIR * (k + 1)],
                                                            start=(dc == 0), stop=(dc == DC - 1))
                            last.then_inc(qk_ready, 1)
                        for u in range(2):
                            if k >= 1:
                                pe.wait_ge(v_stored, 2 * (k - 1) + u + 1)
                            for dc in range(DC):
                                last = nc.tensor.matmul(ps[:, 4 + u, :], yt[:, dc, (2 * k + u) * P:(2 * k + u + 1) * P],
                                                        wv[:, dc, :], start=(dc == 0), stop=(dc == DC - 1))
                            last.then_inc(v_ready, 1)

            @block.scalar
            def _(act):
                act.wait_ge(w_in, 16 * len(loads))

                def high(k, m):
                    n = 2 * BANKS * k + m
                    act.wait_ge(qk_ready, n + 1)
                    if m == 0 and k >= 2:
                        act.wait_ge(sent[k % 2], sent_before(k))
                    nc.scalar.activation(parts[:, k % 2, 0, m, :], ps[:, m, :], ACT.Copy,
                                         scale=L3_WIDTH ** -0.5 if m < BANKS else 1.0).then_inc(high_made, 1)

                def mid(k, m):
                    act.wait_ge(rest_made, 2 * BANKS * k + m + 1)
                    copy_bank(nc, parts[:, k % 2, 1, m, :], rest[:, m, :]).then_inc(mid_made, 1)

                for j in range(PAIRS + 1):
                    if j < PAIRS:
                        norm2_store(act, j, [(core["xt"], gb[:, 0, :], gb[:, 1, :]), (yt, gb[:, 2, :], gb[:, 3, :])])
                    if j >= 1:
                        k = j - 1
                        high(k, 0)
                        for m in range(1, 2 * BANKS):
                            high(k, m)
                            mid(k, m - 1)
                        mid(k, 2 * BANKS - 1)
                        for u in range(2):
                            act.wait_ge(v_ready, 2 * k + u + 1)
                            copy_bank(nc, vs[:, k % 2, u, :], ps[:, 4 + u, :]).then_inc(v_stored, 1)

            @block.vector
            def _(dve):
                def remainder(k, m):
                    n = 2 * BANKS * k + m
                    dve.wait_ge(high_made, n + 1)
                    nc.vector.scalar_tensor_tensor(rest[:, m, :], ps[:, m, :], L3_WIDTH ** -0.5 if m < BANKS else 1.0,
                                                   parts[:, k % 2, 0, m, :], ALU.mult, ALU.subtract).then_inc(rest_made, 1)

                def low(k, m):
                    dve.wait_ge(mid_made, 2 * BANKS * k + m + 1)
                    nc.vector.tensor_tensor(parts[:, k % 2, 2, m, :], rest[:, m, :], parts[:, k % 2, 1, m, :],
                                            ALU.subtract).then_inc(low_made, 1)

                dve.wait_ge(w_in, 16 * len(loads))
                def both_norms(j):
                    norm1_measure(dve, j, tiles_of(core["xn"]))
                    norm1_normalise(dve, j, tiles_of(core["xn"]), tiles_of(x1))
                    affine_rows(nc, dve, x1[:, 2 * j:2 * j + 2, :], ln1)
                    norm2_measure(dve, j, tiles_of(x1))
                    norm2_normalise(dve, j, tiles_of(x1), tiles_of(core["xn"]))

                both_norms(0)
                both_norms(1)
                for k in range(PAIRS):
                    if k + 2 < PAIRS:
                        both_norms(k + 2)
                    remainder(k, 0)
                    for m in range(1, 2 * BANKS):
                        remainder(k, m)
                        low(k, m - 1)
                    low(k, 2 * BANKS - 1)
        clear_semaphores()


def affine_rows(nc, dve, pair, gb):
    for k, op in enumerate((ALU.mult, ALU.add)):
        dve.drain()
        nc.vector.tensor_tensor(pair, pair, gb[:, k, :].unsqueeze(1).to_broadcast([P, 2, D]), op)
    dve.drain()


def stage_self_attention(core, scratch):
    nc, ps = core["nc"], core["ps"]
    q_k_parts, v_scratch, out_scratch = scratch
    R, W = GROUP, L3_WIDTH
    RING = 8
    TURN = 5
    STORE = TURN
    OUT = TURN + R + 1
    UNITS = KC * R
    SLOTS = (((0, 0, 1, 1), (0, 1, 0, 1)),
             ((0, 2, 1, 2), (2, 0, 2, 1)))
    LOADS = 2 * 2 * 4 + 1

    ORDER = [q // 2 if q % 2 == 0 else KC - 1 - q // 2 for q in range(KC)]

    def tile_of(v):
        return ORDER[v % UNITS // R]

    groups = []
    for u in range(UNITS):
        n = KC - tile_of(u)
        sizes = [n] if n <= 4 else [(n + 1) // 2, n // 2]
        for q, size in enumerate(sizes):
            groups.append((u, sum(sizes[:q]), size))
    BANKFULS = len(groups)
    assert BANKFULS % 2 == 0

    def groups_through(u):
        return sum(1 for g in groups if g[0] <= u)

    with ExitStack() as ctx:
        def sb(part, shape, dtype=F32):
            return ctx.enter_context(nc.sbuf_tensor(f"l3s_{part}", shape, dtype))

        outer, clear_outer = named_semaphores(nc, "l3s_outer")
        loaded = [outer("loaded0"), outer("loaded1")]
        stack = [[[sb(f"stack{p}{kind}{s}", [P, R, TOK], BF16) for s in range(2)] for kind in range(2)] for p in range(2)]
        values = sb("values", [P, 2, KC, P])
        pt = sb("pt", [P, 2, R, KC, P])
        heads_out = sb("heads_out", [P, 2, TOK])
        mx, sm = sb("mx", [P, RING]), sb("sm", [P, RING])
        ex = ([core["xn"][:, 4 * n:4 * n + 4, :].rearrange("p a d -> p (a d)") for n in range(4)]
              + [core["xt"][:, n // 2, TOK * (n % 2):TOK * (n % 2 + 1)] for n in range(4)])

        def load(sp, entry, p):
            for kind in range(2):
                for s in range(2):
                    for m in range(4):
                        src = q_k_parts[kind][SLOTS[s][kind][m]][bass.ds(entry, 1)]
                        sp.dma_start(stack[p][kind][s][m * W:(m + 1) * W, :, :],
                                     src.rearrange("a (r d) n -> d (a r) n", d=W)).then_inc(loaded[p], 16)
            sp.dma_start(values[:, p], v_scratch[bass.ds(entry, 1)].rearrange("a p c n -> p (a c) n")).then_inc(loaded[p], 16)

        load(nc.sync, 0, 0)
        with nc.Fori(0, ENTRIES // 2) as jj:
            sem, clear_semaphores = named_semaphores(nc, "l3s")
            scores_ready, measured, exped, inverted = sem("scores_ready"), sem("measured"), sem("exped"), sem("inverted")
            masked, turned, stored = sem("masked"), sem("turned"), [sem("stored0"), sem("stored1")]
            out_ready, out_stored = sem("out_ready"), sem("out_stored")
            out_sent = sem("out_sent")

            with nc.Block() as block:
                @block.sync
                def _(sp):
                    load(sp, 2 * jj + 1, 1)
                    sp.wait_ge(out_ready, KC)
                    load(sp, 2 * jj + 2, 0)
                    for p in range(2):
                        sp.wait_ge(out_stored, KC * (p + 1))
                        sp.dma_start(out_scratch[bass.ds(2 * jj + p, 1)].rearrange("a p n -> p (a n)"),
                                     heads_out[:, p, :]).then_inc(out_sent, 16)
                    sp.wait_ge(out_sent, 32)

                @block.gpsimd
                def _(pool):
                    for v in range(2 * UNITS):
                        si = tile_of(v)
                        pool.wait_ge(inverted, v + 1)
                        nc.gpsimd.tensor_tensor(ex[v % RING][:, si * P:], ex[v % RING][:, si * P:],
                                                sm[:, v % RING:v % RING + 1].to_broadcast([P, TOK - si * P]), ALU.mult)
                        pool.drain()
                        nc.gpsimd.affine_select(out=ex[v % RING][:, si * P:(si + 1) * P], in_=ex[v % RING][:, si * P:(si + 1) * P],
                                                compare_op=ALU.is_gt, fill=0.0, base=0, pattern=[[1, P]],
                                                channel_multiplier=-1).then_inc(masked, 1)

                @block.tensor
                def _(pe):
                    def ends_at(si):
                        return max(range(si, KC), key=lambda c: ((c - si) % R, c))

                    def scores(v):
                        p, si, r = v // UNITS, tile_of(v), v % R
                        if v >= 2:
                            pe.wait_ge(exped, v - 1)
                        for h in range(2):
                            for s in range(2):
                                last = nc.tensor.matmul(ps[:, 2 * (v % 2) + h, :],
                                                        stack[p][0][s][:, r, si * P:(si + 1) * P],
                                                        stack[p][1][s][:, r, h * 512:(h + 1) * 512],
                                                        start=(s == 0), stop=(s == 1))
                        last.then_inc(scores_ready, 1)

                    def turn(v):
                        p, si = v // UNITS, tile_of(v)
                        pe.wait_ge(masked, v + 1)
                        for g, (u, c0, size) in enumerate(groups):
                            if u != v % UNITS:
                                continue
                            n = BANKFULS * p + g
                            if n >= 2:
                                pe.wait_ge(stored[n % 2], n // 2)
                            for c in range(size):
                                last = nc.tensor.transpose(ps[:, 4 + n % 2, c * P:(c + 1) * P],
                                                           ex[v % RING][:, (si + c0 + c) * P:(si + c0 + c + 1) * P],
                                                           core["ident"][:, :])
                            last.then_inc(turned, 1)

                    def output(w, q):
                        p, si = w // KC, ORDER[w % KC]
                        chunks = [c for c in range(si, KC) if (c - si) % R == q]
                        if q == 0:
                            n = BANKFULS * p + groups_through(w % KC * R + R - 1)
                            pe.wait_ge(stored[0], (n + 1) // 2)
                            pe.wait_ge(stored[1], n // 2)
                            if w >= 2:
                                pe.wait_ge(out_stored, w - 1)
                        for c in chunks:
                            for r in range(R):
                                last = nc.tensor.matmul(ps[r * W:(r + 1) * W, 6 + w % 2, 0:P],
                                                        values[:, p, c, r * W:(r + 1) * W],
                                                        pt[:, w % 2, r, c - si, :], start=(c == si),
                                                        stop=(c == ends_at(si)))
                        if chunks and chunks[-1] == ends_at(si):
                            last.then_inc(out_ready, 1)

                    for v in range(2 * UNITS + OUT):
                        if v == 0:
                            pe.wait_ge(loaded[0], 16 * LOADS * jj + 16 * LOADS)
                        if v == UNITS:
                            pe.wait_ge(loaded[1], 16 * LOADS * jj + 16 * LOADS)
                        if v < 2 * UNITS:
                            scores(v)
                        if TURN <= v < 2 * UNITS + TURN:
                            turn(v - TURN)
                        if v >= OUT:
                            output((v - OUT) // R, (v - OUT) % R)

                def store_turned(eng, op, v, side):
                    if v >= 2 * UNITS:
                        return
                    p, w = v // UNITS, v // R
                    for g, (u, c0, size) in enumerate(groups):
                        n = BANKFULS * p + g
                        if u != v % UNITS or n % 2 != side:
                            continue
                        eng.wait_ge(turned, n + 1)
                        if w >= 2:
                            eng.wait_ge(out_ready, w - 1)
                        dst = pt[:, w % 2, v % R, c0:c0 + size, :].rearrange("p c n -> p (c n)")
                        src = ps[:, 4 + side, 0:size * P]
                        if side == 0:
                            last = op.activation(dst, src, ACT.Copy)
                        else:
                            last = op.tensor_copy(dst, src)
                        last.then_inc(stored[side], 1)

                @block.scalar
                def _(act):
                    for v in range(2 * UNITS + OUT):
                        if v >= STORE:
                            store_turned(act, nc.scalar, v - STORE, 0)
                        if v < 2 * UNITS:
                            act.wait_ge(measured, v + 1)
                            if v >= RING:
                                act.wait_ge(turned, BANKFULS * ((v - RING) // UNITS) + groups_through((v - RING) % UNITS))
                            nc.scalar.activation(ex[v % RING][:, :], ps[:, 2 * (v % 2):2 * (v % 2) + 2, :].rearrange("p a n -> p (a n)"),
                                                 ACT.Exp, bias=mx[:, v % RING:v % RING + 1],
                                                 accum_out=sm[:, v % RING:v % RING + 1]).then_inc(exped, 1)
                        if v >= OUT and (v - OUT) % R == R - 1:
                            w = (v - OUT) // R
                            act.wait_ge(out_ready, w + 1)
                            si = ORDER[w % KC]
                            copy_bank(nc, heads_out[:, w // KC, si * P:(si + 1) * P],
                                      ps[:, 6 + w % 2, 0:P]).then_inc(out_stored, 1)

                @block.vector
                def _(dve):
                    for v in range(2 * UNITS + OUT):
                        if v < 2 * UNITS:
                            dve.wait_ge(scores_ready, v + 1)
                            nc.vector.tensor_reduce(mx[:, v % RING:v % RING + 1],
                                                    ps[:, 2 * (v % 2):2 * (v % 2) + 2, :].rearrange("p a n -> p (a n)"),
                                                    AX_X, ALU.max, negate=True).then_inc(measured, 1)
                        if v >= STORE:
                            store_turned(dve, nc.vector, v - STORE, 1)
                        if 1 <= v <= 2 * UNITS:
                            dve.wait_ge(exped, v)
                            nc.vector.reciprocal(sm[:, (v - 1) % RING:(v - 1) % RING + 1],
                                                 sm[:, (v - 1) % RING:(v - 1) % RING + 1]).then_inc(inverted, 1)
            clear_semaphores()
        nc.sync.wait_ge(loaded[0], 16 * LOADS * (ENTRIES // 2 + 1))
        nc.all_engine_barrier()
        clear_outer()


def stage_self_out(core, a, x1, xo, scratch):
    nc, ps = core["nc"], core["ps"]
    q_k_parts, v_scratch, out_scratch = scratch
    G = GROUPS
    with ExitStack() as ctx:
        def sb(part, shape):
            return ctx.enter_context(nc.sbuf_tensor(f"l3o_{part}", shape, F32))

        sem, clear_semaphores = named_semaphores(nc, "l3o")
        w_in, bias_added, out_ready, out_added = sem("w_in"), sem("bias_added"), sem("out_ready"), sem("out_added")
        heads_in = [sem(f"heads_in{j}") for j in range(PAIRS)]
        norm_measure, norm_root, norm_normalise, norm_turn, norm_store, norm_stored = layer_norm(core, ctx, sem, "l3o_norm", on_vector=True)
        w = sb("w", [P, G, D])
        bias_row = sb("bias_row", [P, D])
        gb = sb("gb", [P, 2, DC])
        heads = sb("heads", [P, 4, G, PAIR])
        loads = [(w[:, :, :], a["L3_xattn_a1_li1_w"].rearrange("(g p) n -> p g n", p=P)),
                 (bias_row[:, :], rows(a["L3_xattn_a1_li1_b"])),
                 (gb[:, 0, :], columns(a["L3_xattn_a1_ln3_g"])), (gb[:, 1, :], columns(a["L3_xattn_a1_ln3_b"]))]

        def xo_tile(i):
            return xo[:, i, :]

        with nc.Block() as block:
            @block.sync
            def _(sp):
                for dst, src in loads:
                    sp.dma_start(dst, src).then_inc(w_in, 16)
                for j in range(PAIRS):
                    b, at = j // (PAIRS // B), (j % (PAIRS // B)) * PAIR
                    if j >= 4:
                        sp.wait_ge(out_ready, j - 3)
                    sp.dma_start(heads[:, j % 4], out_scratch[b * G:(b + 1) * G, :, at:at + PAIR].rearrange("g p n -> p g n")
                                 ).then_inc(heads_in[j], 16)

            @block.gpsimd
            def _(pool):
                pool.wait_ge(w_in, 16 * len(loads))
                for j in range(PAIRS):
                    for u in range(2):
                        last = nc.gpsimd.tensor_tensor(xo_tile(2 * j + u), x1[:, 2 * j + u, :], bias_row[:, :], ALU.add)
                    last.then_inc(bias_added, 1)

            @block.tensor
            def _(pe):
                pe.wait_ge(w_in, 16 * len(loads))
                for j in range(PAIRS + 2):
                    if j < PAIRS:
                        pe.wait_ge(heads_in[j], 16)
                        if j >= 2:
                            pe.wait_ge(out_added, j - 1)
                        for u in range(2):
                            for g in range(G):
                                last = nc.tensor.matmul(ps[:, j % 2, u * D:(u + 1) * D], heads[:, j % 4, g, u * P:(u + 1) * P],
                                                        w[:, g, :], start=(g == 0), stop=(g == G - 1))
                        last.then_inc(out_ready, 1)
                    if j >= 2:
                        norm_turn(pe, j - 2, tiles_of(core["xn"]))

            @block.scalar
            def _(act):
                act.wait_ge(w_in, 16 * len(loads))
                for j in range(PAIRS):
                    norm_store(act, j, [(core["xt"], gb[:, 0, :], gb[:, 1, :])])

            @block.vector
            def _(dve):
                for j in range(PAIRS):
                    dve.wait_ge(out_ready, j + 1)
                    dve.wait_ge(bias_added, j + 1)
                    x2 = pair_of(xo, j)
                    nc.vector.tensor_tensor(x2, ps[:, j % 2, :], x2, ALU.add).then_inc(out_added, 1)
                    dve.drain()
                    norm_measure(dve, j, xo_tile)
                    norm_normalise(dve, j, xo_tile, tiles_of(core["xn"]))
        clear_semaphores()


def stage_mlp(core, a, pfx, x1, xo, second):
    nc, ps = core["nc"], core["ps"]
    name = "l3m2" if second else "l3m1"
    gate = core["gate_attn"][:, 3:4]
    with ExitStack() as ctx:
        def sb(part, shape):
            return ctx.enter_context(nc.sbuf_tensor(f"{name}_{part}", shape, F32))

        sem, clear_semaphores = named_semaphores(nc, name)
        w_in, summed, hid_ready, hid_stored = sem("w_in"), sem("summed"), sem("hid_ready"), sem("hid_stored")
        out_ready, out_added = sem("out_ready"), sem("out_added")
        norm1_measure, norm1_root, norm1_normalise, norm1_turn, norm1_store, norm1_stored = layer_norm(core, ctx, sem, name + "_norm1", on_vector=True)
        norm2_measure, norm2_root, norm2_normalise, norm2_turn, norm2_store, norm2_stored = layer_norm(core, ctx, sem, name + "_norm2", on_vector=True)
        w2, b2 = sb("w2", [P, DC, FF]), sb("b2", [P, FC])
        w3, b3 = sb("w3", [P, FC, D]), sb("b3", [P, D])
        gb = sb("gb", [P, 2, DC])
        ht = sb("ht", [P, 2, FC, PAIR])
        loads = [(w2[:, :, :], a[pfx + "li2_w"].rearrange("(c p) n -> p c n", p=P)), (b2[:, :], columns(a[pfx + "li2_b"])),
                 (w3[:, :, :], a[pfx + "li3_w"].rearrange("(c p) n -> p c n", p=P)), (b3[:, :], rows(a[pfx + "li3_b"]))]
        if second:
            loads += [(gb[:, k, :], columns(a["L3_ffn_" + n])) for k, n in enumerate(("ln_gamma", "ln_beta"))]
        else:
            ln2 = sb("ln2", [P, 2, D])
            loads += [(gb[:, k, :], columns(a["L3_xattn_a2_lnx_" + n])) for k, n in enumerate("gb")]
            loads += [(ln2[:, k, :], rows(a["L3_xattn_ln2_" + n])) for k, n in enumerate("gb")]

        def x1_tile(i):
            return x1[:, i, :]

        whole, middle = (tiles_of(core["x"]), tiles_of(core["xn"])) if second else (x1_tile, x1_tile)

        with nc.Block() as block:
            @block.sync
            def _(sp):
                for dst, src in loads:
                    sp.dma_start(dst, src).then_inc(w_in, 16)

            @block.gpsimd
            def _(pool):
                pool.wait_ge(w_in, 16 * len(loads))
                for j in range(PAIRS):
                    for u in range(2):
                        i = 2 * j + u
                        nc.gpsimd.tensor_tensor(xo[:, i, :], xo[:, i, :], x1[:, i, :], ALU.add)
                    pool.drain()
                    for u in range(2):
                        i = 2 * j + u
                        last = nc.gpsimd.tensor_tensor(xo[:, i, :], xo[:, i, :], b3[:, :], ALU.add)
                    last.then_inc(summed, 1)

            @block.tensor
            def _(pe):
                pe.wait_ge(w_in, 16 * len(loads))
                for j in range(PAIRS + 3):
                    if j < PAIRS:
                        for f in range(FC):
                            n = FC * j + f
                            if n >= 4:
                                pe.wait_ge(hid_stored, n - 3)
                            for dc in range(DC):
                                last = nc.tensor.matmul(ps[:, n % 4, 0:PAIR], w2[:, dc, f * P:(f + 1) * P],
                                                        core["xt"][:, dc, PAIR * j:PAIR * (j + 1)],
                                                        start=(dc == 0), stop=(dc == DC - 1))
                            last.then_inc(hid_ready, 1)
                    if j >= 3:
                        norm2_turn(pe, j - 3, tiles_of(core["xn"]))
                    if 1 <= j <= PAIRS:
                        k = j - 1
                        pe.wait_ge(hid_stored, FC * (k + 1))
                        if k >= 2:
                            pe.wait_ge(out_added, k - 1)
                        for u in range(2):
                            for f in range(FC):
                                last = nc.tensor.matmul(ps[:, 4 + k % 2, u * D:(u + 1) * D], ht[:, k % 2, f, u * P:(u + 1) * P],
                                                        w3[:, f, :], start=(f == 0), stop=(f == FC - 1))
                        last.then_inc(out_ready, 1)

            @block.scalar
            def _(act):
                act.wait_ge(w_in, 16 * len(loads))
                for j in range(PAIRS + 3):
                    if j < PAIRS:
                        for f in range(FC):
                            n = FC * j + f
                            act.wait_ge(hid_ready, n + 1)
                            if f == 0 and j >= 2:
                                act.wait_ge(out_ready, j - 1)
                            nc.scalar.activation(ht[:, j % 2, f, :], ps[:, n % 4, 0:PAIR], ACT.Gelu,
                                                 bias=b2[:, f:f + 1]).then_inc(hid_stored, 1)
                    if j >= 3:
                        norm2_store(act, j - 3, [(core["xt"], gb[:, 0, :], gb[:, 1, :])])

            @block.vector
            def _(dve):
                dve.wait_ge(w_in, 16 * len(loads))
                for j in range(PAIRS):
                    dve.wait_ge(out_ready, j + 1)
                    dve.wait_ge(summed, j + 1)
                    xo2 = pair_of(xo, j)
                    if second:
                        nc.vector.tensor_tensor(xo2, ps[:, 4 + j % 2, :], xo2, ALU.add).then_inc(out_added, 1)
                        dve.drain()
                        x2 = pair_of(core["x"], j)
                        nc.vector.scalar_tensor_tensor(x2, xo2, gate, x2, ALU.mult, ALU.add)
                    else:
                        nc.vector.tensor_tensor(pair_of(x1, j), ps[:, 4 + j % 2, :], xo2, ALU.add).then_inc(out_added, 1)
                    dve.drain()
                    norm1_measure(dve, j, whole)
                    norm1_normalise(dve, j, whole, middle)
                    if second:
                        dve.drain()
                    else:
                        affine_rows(nc, dve, x1[:, 2 * j:2 * j + 2, :], ln2)
                    norm2_measure(dve, j, middle)
                    norm2_normalise(dve, j, middle, tiles_of(core["xn"]))
        clear_semaphores()


def layout_l3(core, a):
    def layout(sb, wq_t, wo):
        H, W = 16, 32
        HD = H * W
        wq = sb("wq", [P, DC, HD])
        wk, wv = sb("wk", [P, HD]), sb("wv", [P, HD])
        by_head = [(wk[:, :], a["L3_xattn_a2_wk"]), (wv[:, :], a["L3_xattn_a2_wv"])]
        by_head += [(wq[:, c, :], a["L3_xattn_a2_wq"][:, c * P:(c + 1) * P, :]) for c in range(DC)]
        loads = [(dst.rearrange("p (h d) -> p h d", h=H), src.rearrange("h p d -> p h d")) for dst, src in by_head]
        loads += [(wo[:, :, :], a["L3_xattn_a2_li1_w"].rearrange("(c p) n -> p c n", p=P))]
        turns = [([wq[:, dc, c * P:(c + 1) * P] for c in (2 * q, 2 * q + 1) for dc in range(DC)],
                  wq_t[:, 2 * q:2 * q + 2, :].rearrange("p c d -> p (c d)")) for q in range(2)]
        return loads, turns, wk, wv
    return layout


def layer_3(core, a):
    nc = core["nc"]
    scratch = self_attention_scratch(nc)
    with ExitStack() as ctx:
        x1 = ctx.enter_context(nc.sbuf_tensor("l3_x1", [P, TILES, D], F32))
        stage_self_project(core, a, x1, scratch)
        stage_self_attention(core, scratch)
        xo = ctx.enter_context(nc.sbuf_tensor("l3_xo", [P, TILES, D], F32))
        stage_self_out(core, a, x1, xo, scratch)
        stage_mlp(core, a, "L3_xattn_a1_", x1, xo, False)
        stage_attention(core, a, "l3a", 32, 32 ** -0.5, layout_l3(core, a), lambda i: x1[:, i, :], lambda i: xo[:, i, :],
                        None, "L3_xattn_a2_li1_b", ("L3_xattn_a2_ln3_g", "L3_xattn_a2_ln3_b"), core["ctx_norm_t"])
        stage_mlp(core, a, "L3_xattn_a2_", x1, xo, True)
    stage_experts(core, a, "l3f", top=2, rows_tiles=TOP2_TILES, capacity=None, router="L3_ffn_router_w",
                  w1="L3_ffn_gate_up_w", w2="L3_ffn_down_w", swiglu=True, gate=core["gate_ffn"][:, 3:4],
                  affine=("L3_ffn_ln_gamma", "L3_ffn_ln_beta"),
                  shared=("L3_ffn_shared_gate_up_w", "L3_ffn_shared_down_w"), norm_behind=False)


def build_program(nc, a, out):
    a = dict(a, out=out)
    with ExitStack() as ctx:
        ctx.enter_context(nc.allow_non_contiguous_dma(reason="vectors of up to 1024 values, one per partition"))
        core = make_core(nc, ctx)
        stage_start(core, a)
        stage_attention(core, a, "l0a", 64, 64 ** -0.5, layout_l0(core, a), tiles_of(core["x"]), tiles_of(core["x"]),
                        core["gate_attn"][:, 0:1], "L0_xattn_bo", None, core["ctx_t"])
        stage_experts(core, a, "l0f", top=1, rows_tiles=E, capacity=T // E, router="L0_ffn_Wr", w1="L0_ffn_W1",
                      w2="L0_ffn_W2", swiglu=False, gate=core["gate_ffn"][:, 0:1])
        stage_one_head(core, a)
        stage_adapter(core, a)
        stage_attention(core, a, "l2a", 16, 16 ** -0.5, layout_l2(core, a), tiles_of(core["x"]), tiles_of(core["x"]),
                        core["gate_attn"][:, 2:3], None, None, core["ctx_t"])
        stage_low_rank(core, a)
        layer_3(core, a)


_INS = ['x', 'ctx_512', 'g_xattn', 'g_ffn', 'L0_xattn_Wq', 'L0_xattn_Wk', 'L0_xattn_Wv', 'L0_xattn_Wo', 'L0_xattn_bo',
        'L0_ffn_Wr', 'L0_ffn_W1', 'L0_ffn_W2', 'L1_xattn_Wq', 'L1_xattn_bq', 'L1_xattn_Wk', 'L1_xattn_bk',
        'L1_xattn_Wv', 'L1_xattn_bv', 'L1_ffn_base_W', 'L1_ffn_base_b', 'L1_ffn_disc_mu', 'L1_ffn_disc_sigma',
        'L1_ffn_down_W', 'L1_ffn_down_b', 'L1_ffn_up_W', 'L1_ffn_up_b', 'L1_ffn_conv_W', 'L1_ffn_conv_b',
        'L2_xattn_Wq', 'L2_xattn_Wkv', 'L2_xattn_Wo', 'L2_ffn_U1', 'L2_ffn_V1', 'L2_ffn_b1', 'L2_ffn_U2', 'L2_ffn_V2',
        'L2_ffn_b2', 'L3_xattn_ln1_g', 'L3_xattn_ln1_b', 'L3_xattn_ln2_g', 'L3_xattn_ln2_b', 'L3_xattn_a1_wq',
        'L3_xattn_a1_wk', 'L3_xattn_a1_wv', 'L3_xattn_a1_li1_w', 'L3_xattn_a1_li1_b', 'L3_xattn_a1_lnx_g',
        'L3_xattn_a1_lnx_b', 'L3_xattn_a1_lny_g', 'L3_xattn_a1_lny_b', 'L3_xattn_a1_ln3_g', 'L3_xattn_a1_ln3_b',
        'L3_xattn_a1_li2_w', 'L3_xattn_a1_li2_b', 'L3_xattn_a1_li3_w', 'L3_xattn_a1_li3_b', 'L3_xattn_a2_wq',
        'L3_xattn_a2_wk', 'L3_xattn_a2_wv', 'L3_xattn_a2_li1_w', 'L3_xattn_a2_li1_b', 'L3_xattn_a2_lnx_g',
        'L3_xattn_a2_lnx_b', 'L3_xattn_a2_lny_g', 'L3_xattn_a2_lny_b', 'L3_xattn_a2_ln3_g', 'L3_xattn_a2_ln3_b',
        'L3_xattn_a2_li2_w', 'L3_xattn_a2_li2_b', 'L3_xattn_a2_li3_w', 'L3_xattn_a2_li3_b', 'L3_ffn_ln_gamma',
        'L3_ffn_ln_beta', 'L3_ffn_router_w', 'L3_ffn_gate_up_w', 'L3_ffn_down_w', 'L3_ffn_shared_gate_up_w',
        'L3_ffn_shared_down_w']


def kernel(**inputs):
    import numpy as _np
    import concourse.bacc as _bacc
    from concourse import mybir as _mybir
    from concourse.bass_utils import run_bass_kernel_spmd as _run

    nc = _bacc.Bacc("TRN2", target_bir_lowering=False, num_devices=1)
    arrays, args = {}, {}
    for name in _INS:
        array = _np.ascontiguousarray(inputs[name])
        arrays[f"in_{name}_dram"] = array
        args[name] = nc.dram_tensor(f"in_{name}_dram", array.shape, _mybir.dt.from_np(array.dtype),
                                    kind="ExternalInput").ap()
    out = nc.dram_tensor("out_0_dram", (B, TOK, D), _mybir.dt.float32, kind="ExternalOutput").ap()
    build_program(nc, args, out)
    r = _run(nc, [arrays], core_ids=[0])
    return r.results[0]["out_0_dram"]
```

```python
from contextlib import ExitStack

import concourse.bass as bass
from concourse import mybir

F32 = mybir.dt.float32
I32 = mybir.dt.int32
BF16 = mybir.dt.bfloat16
ALU = mybir.AluOpType
ACT = mybir.ActivationFunctionType
AX_X = mybir.AxisListType.X

P = 128
D = 256
DC = D // P
B = 2
T = 2048
TILES = T // P
PAIRS = TILES // 2
TOK = T // B
KEYS = 64
KD = 128
FF = 1024
FC = FF // P
E = 8
PAIR = 2 * P
TOP2_TILES = 2 * T // PAIR + E - 1
EPS = 1e-5
AREA_WORDS = (3400, 4900)
NEWTON_SEED = float(0x5F3759DF)


def named_semaphores(nc, stage):
    taken = []

    def sem(name):
        taken.append(nc.alloc_semaphore(f"{stage}_{name}"))
        return taken[-1]

    def clear_semaphores():
        nc.clear_and_free_semaphores(taken)
        nc.all_engine_barrier()

    return sem, clear_semaphores


def make_core(nc, ctx):
    def sb(name, shape, dtype=F32):
        return ctx.enter_context(nc.sbuf_tensor(name, shape, dtype))

    return {
        "nc": nc,
        "x": sb("x_tokens", [P, TILES, D]),
        "xt": sb("x_features", [P, DC, T]),
        "xn": sb("xn_tokens", [P, TILES, D]),
        "ident": sb("ident", [P, P]),
        "gate_attn": sb("gate_attn", [P, 4]),
        "gate_ffn": sb("gate_ffn", [P, 4]),
        "ctx_t": sb("ctx_t", [P, B * KEYS]),
        "ctx_norm_t": sb("ctx_norm_t", [P, B * KEYS]),
        "areas": [sb(f"weights{n}", [P, words]) for n, words in enumerate(AREA_WORDS)],
        "ps": ctx.enter_context(nc.psum_tensor("banks", [P, 8, 512], F32)),
    }


def plan_weights(core, area, name, make):
    used = 0

    def carve(shape):
        nonlocal used
        size = 1
        for n in shape[1:]:
            size *= n
        part = core["areas"][area][0:shape[0], used:used + size]
        used += size
        assert used <= AREA_WORDS[area], (name, used)
        if len(shape) == 2:
            return part
        if len(shape) == 3:
            return part.rearrange("p (a b) -> p a b", b=shape[2])
        return part.rearrange("p (a b c) -> p a b c", b=shape[2], c=shape[3])

    loads, needed = make(carve)
    return loads, core["nc"].alloc_semaphore(f"{name}_weights_in"), 16 * len(loads), needed


def fetch(sp, plan):
    loads, weights_in, _, _ = plan
    for dst, src in loads:
        sp.dma_start(dst, src).then_inc(weights_in, 16)


def tiles_of(tensor):
    return lambda i: tensor[:, i, :]


def pair_of(tensor, j):
    return tensor[:, 2 * j:2 * j + 2, :].rearrange("p u d -> p (u d)")


def rows(ap, n=P):
    return ap.rearrange("(a n) -> a n", a=1).partition_broadcast(n)


def columns(ap):
    return ap.rearrange("(c p) -> p c", p=P)


def newton_root(eng, drain, var, v, t, y):
    eng.tensor_scalar(v, var, EPS, None, ALU.add)
    drain()
    eng.tensor_scalar(y.bitcast(I32), v.bitcast(I32), -0.5, NEWTON_SEED, ALU.mult, ALU.add)
    drain()
    for step in range(3):
        eng.tensor_tensor(t, y, y, ALU.mult)
        drain()
        eng.tensor_tensor(t, t, v, ALU.mult)
        drain()
        eng.tensor_scalar(t, t, -0.5, 1.5, ALU.mult, ALU.add)
        drain()
        last = eng.tensor_tensor(y, t, y, ALU.mult)
        if step < 2:
            drain()
    return last


def vector_root(nc, dve, var, h, t, y):
    nc.vector.tensor_scalar(t, var, EPS, None, ALU.add)
    nc.vector.tensor_scalar(h, var, EPS, -0.5, ALU.add, ALU.mult)
    dve.drain()
    nc.vector.tensor_scalar(y.bitcast(I32), t.bitcast(I32), -0.5, NEWTON_SEED, ALU.mult, ALU.add)
    dve.drain()
    for step in range(3):
        nc.vector.tensor_tensor(t, y, y, ALU.mult)
        dve.drain()
        nc.vector.tensor_tensor(t, t, h, ALU.mult)
        dve.drain()
        nc.vector.scalar_tensor_tensor(y, t, 1.5, y, ALU.add, ALU.mult)
        dve.drain()


def layer_norm(core, ctx, sem, name, on_vector=False):
    nc, ps = core["nc"], core["ps"]

    def sb(part, shape):
        return ctx.enter_context(nc.sbuf_tensor(f"{name}_{part}", shape, F32))

    stats = sb("stats", [P, 2, 2, 6])
    mv = sb("mv", [P, 2, 2, 2])
    rs = sb("rs", [P, 2, 2])
    v = sb("v", [P, 2])
    t = sb("t", [P, 2])
    measured, rooted, normalised = sem(name + "_measured"), sem(name + "_rooted"), sem(name + "_normalised")
    turned, stored = sem(name + "_turned"), sem(name + "_stored")

    def measure(dve, j, src):
        p = j % 2
        for u in range(2):
            nc.vector.bn_stats(stats[:, p, u, :], src(2 * j + u))
        dve.drain()
        nc.vector.bn_aggr(mv[:, p, 0, :], stats[:, p, 0, :])
        last = nc.vector.bn_aggr(mv[:, p, 1, :], stats[:, p, 1, :])
        if on_vector:
            dve.drain()
            vector_root(nc, dve, mv[:, p, :, 1], v[:, :], t[:, :], rs[:, p, :])
        else:
            last.then_inc(measured, 1)

    def root(pool, j):
        assert not on_vector
        pool.wait_ge(measured, j + 1)
        if j >= 2:
            pool.wait_ge(normalised, j - 1)
        newton_root(nc.gpsimd, pool.drain, mv[:, j % 2, :, 1], v[:, :], t[:, :], rs[:, j % 2, :]).then_inc(rooted, 1)

    def normalise(dve, j, src, dst):
        if not on_vector:
            dve.wait_ge(rooted, j + 1)
        p = j % 2
        for u in range(2):
            last = nc.vector.tensor_scalar(dst(2 * j + u), src(2 * j + u), mv[:, p, u, 0:1],
                                           rs[:, p, u:u + 1], ALU.subtract, ALU.mult)
        last.then_inc(normalised, 1)

    def turn(pe, j, src, bank=7):
        pe.wait_ge(normalised, j + 1)
        if j >= 1:
            pe.wait_ge(stored, j)
        for c in range(DC):
            for u in range(2):
                last = nc.tensor.transpose(ps[:, bank, c * PAIR + u * P:c * PAIR + (u + 1) * P],
                                           src(2 * j + u)[:, c * P:(c + 1) * P], core["ident"][:, :])
        last.then_inc(turned, 1)

    def store(act, j, dsts, bank=7):
        act.wait_ge(turned, j + 1)
        for dst, gamma, beta in dsts:
            if gamma is None:
                last = nc.scalar.activation(dst[:, :, PAIR * j:PAIR * (j + 1)],
                                            ps[:, bank, :].rearrange("p (c n) -> p c n", c=DC), ACT.Copy)
            else:
                for c in range(DC):
                    last = nc.scalar.activation(
                        dst[:, c, PAIR * j:PAIR * (j + 1)], ps[:, bank, c * PAIR:(c + 1) * PAIR],
                        ACT.Identity, bias=beta[:, c:c + 1], scale=gamma[:, c:c + 1])
        last.then_inc(stored, 1)

    return measure, root, normalise, turn, store, stored


def opening(core, a, ctx, sem):
    nc, ps = core["nc"], core["ps"]

    def sb(name, shape):
        return ctx.enter_context(nc.sbuf_tensor(f"open_{name}", shape, F32))

    x_in, small_in = [sem(f"x_in{j}") for j in range(PAIRS)], sem("small_in")
    ident_zero, ident_made = sem("ident_zero"), sem("ident_made")
    ctx_normalised, ctx_turned, ctx_stored = sem("ctx_normalised"), sem("ctx_turned"), sem("ctx_stored")
    gates_made = sem("gates_made")
    x_normalised, x_turned, x_stored = sem("x_normalised"), sem("x_turned"), sem("x_stored")
    c_in, c_norm = sb("c_in", [P, KD]), sb("c_norm", [P, KD])
    c_stats, c_mv, c_small = sb("c_stats", [P, 6]), sb("c_mv", [P, 2]), sb("c_small", [P, 3])
    c_gb, g_in = sb("c_gb", [P, 2]), sb("g_in", [P, 8])
    stats, mv = sb("stats", [P, TILES, 6]), sb("mv", [P, TILES, 2])
    h, t, rs = sb("h", [P, TILES]), sb("t", [P, TILES]), sb("rs", [P, TILES])

    def sync(sp):
        for j in range(PAIRS):
            sp.dma_start(core["x"][:, 2 * j:2 * j + 2, :],
                         a["x"].rearrange("b (t p) d -> p (b t) d", p=P)[:, 2 * j:2 * j + 2, :]).then_inc(x_in[j], 16)

    def scalar(act):
        act.dma_start(c_in[:, :], a["ctx_512"].rearrange("b k d -> (b k) d")).then_inc(small_in, 16)
        act.dma_start(g_in[:, 0:4], rows(a["g_xattn"])).then_inc(small_in, 16)
        act.dma_start(g_in[:, 4:8], rows(a["g_ffn"])).then_inc(small_in, 16)
        act.dma_start(c_gb[:, 0:1], columns(a["L3_xattn_a2_lny_g"])).then_inc(small_in, 16)
        act.dma_start(c_gb[:, 1:2], columns(a["L3_xattn_a2_lny_b"])).then_inc(small_in, 16)
        act.wait_ge(small_in, 80)
        nc.scalar.activation(core["gate_attn"][:, :], g_in[:, 0:4], ACT.Tanh)
        nc.scalar.activation(core["gate_ffn"][:, :], g_in[:, 4:8], ACT.Tanh).then_inc(gates_made, 1)
        act.wait_ge(ctx_turned, 2)
        nc.scalar.activation(core["ctx_t"][:, :], ps[:, 0, 0:P], ACT.Copy)
        nc.scalar.activation(core["ctx_norm_t"][:, :], ps[:, 1, 0:P], ACT.Identity,
                             bias=c_gb[:, 1:2], scale=c_gb[:, 0:1]).then_inc(ctx_stored, 1)
        for j in range(PAIRS):
            act.wait_ge(x_turned, j + 1)
            nc.scalar.activation(core["xt"][:, :, PAIR * j:PAIR * (j + 1)],
                                 ps[:, 6 + j % 2, :].rearrange("p (c n) -> p c n", c=DC), ACT.Copy).then_inc(x_stored, 1)

    def gpsimd(pool):
        nc.gpsimd.memset(core["ident"][:, :], 0.0).then_inc(ident_zero, 1)
        pool.wait_ge(ident_zero, 1)
        nc.gpsimd.affine_select(out=core["ident"][:, :], in_=core["ident"][:, :], compare_op=ALU.not_equal,
                                fill=1.0, base=0, pattern=[[-1, P]], channel_multiplier=1).then_inc(ident_made, 1)

    def vector(dve):
        dve.wait_ge(small_in, 80)
        nc.vector.bn_stats(c_stats[:, :], c_in[:, :])
        dve.drain()
        nc.vector.bn_aggr(c_mv[:, :], c_stats[:, :])
        dve.drain()
        vector_root(nc, dve, c_mv[:, 1:2], c_small[:, 0:1], c_small[:, 1:2], c_small[:, 2:3])
        nc.vector.tensor_scalar(c_norm[:, :], c_in[:, :], c_mv[:, 0:1], c_small[:, 2:3],
                                ALU.subtract, ALU.mult).then_inc(ctx_normalised, 1)
        for i in range(TILES):
            if i % 2 == 0:
                dve.wait_ge(x_in[i // 2], 16)
            nc.vector.bn_stats(stats[:, i, :], core["x"][:, i, :])
        dve.drain()
        for i in range(TILES):
            nc.vector.bn_aggr(mv[:, i, :], stats[:, i, :])
        dve.drain()
        vector_root(nc, dve, mv[:, :, 1], h[:, :], t[:, :], rs[:, :])
        for i in range(TILES):
            nc.vector.tensor_scalar(core["xn"][:, i, :], core["x"][:, i, :], mv[:, i, 0:1], rs[:, i:i + 1],
                                    ALU.subtract, ALU.mult).then_inc(x_normalised, 1)
        dve.wait_ge(gates_made, 1)

    def tensor(pe):
        pe.wait_ge(ident_made, 1)
        pe.wait_ge(small_in, 80)
        nc.tensor.transpose(ps[:, 0, 0:P], c_in[:, :], core["ident"][:, :]).then_inc(ctx_turned, 1)
        pe.wait_ge(ctx_normalised, 1)
        nc.tensor.transpose(ps[:, 1, 0:P], c_norm[:, :], core["ident"][:, :]).then_inc(ctx_turned, 1)
        for j in range(PAIRS):
            pe.wait_ge(x_normalised, 2 * j + 2)
            if j >= 2:
                pe.wait_ge(x_stored, j - 1)
            for c in range(DC):
                for u in range(2):
                    last = nc.tensor.transpose(ps[:, 6 + j % 2, c * PAIR + u * P:c * PAIR + (u + 1) * P],
                                               core["xn"][:, 2 * j + u, c * P:(c + 1) * P], core["ident"][:, :])
            last.then_inc(x_turned, 1)
        pe.wait_ge(x_stored, PAIRS)
        pe.wait_ge(ctx_stored, 1)

    return {"sync": sync, "scalar": scalar, "gpsimd": gpsimd, "vector": vector, "tensor": tensor}


def stage_attention(core, a, name, width, scale, plan, following, source, out_tile, gate, bias,
                    norm_out, context, opens=False):
    nc, ps = core["nc"], core["ps"]
    HEADS = 16
    HK = HEADS * KEYS
    chunks = HEADS * width // P
    per = P // width
    narrow = width * 4 <= KEYS
    HEADS_OUT = 3
    OUT = 4 if narrow else 3
    TURN = OUT + 3
    kinds = 1 if narrow else 2
    with ExitStack() as ctx:
        def sb(part, shape):
            return ctx.enter_context(nc.sbuf_tensor(f"{name}_{part}", shape, F32))

        _, weights_in, weights_total, (finish, bias_row, gb) = plan
        wq_t, wo, turns, wk, wv = finish(sb)
        sem, clear_semaphores = named_semaphores(nc, name)
        w_turned, w_stored = sem("w_turned"), sem("w_stored")
        mask_set, mask_made = sem("mask_set"), sem("mask_made")
        kv_ready, kv_stored, blocks_made = sem("kv_ready"), sem("kv_stored"), sem("blocks_made")
        fold_ready, fold_stored = sem("fold_ready"), sem("fold_stored")
        bias_made, bias_added = sem("bias_made"), sem("bias_added")
        scores_ready, centred, exped = sem("scores_ready"), sem("centred"), sem("exped")
        probs_ready, probs_turned, probs_stored = sem("probs_ready"), sem("probs_turned"), sem("probs_stored")
        out_ready, out_added = sem("out_ready"), sem("out_added")
        if narrow:
            ctx_twice_made, values_ready, values_made = sem("ctx_twice_made"), sem("values_ready"), sem("values_made")
            heads_ready, heads_stored = sem("heads_ready"), sem("heads_stored")
        norm_measure, norm_root, norm_normalise, norm_turn, norm_store, norm_stored = layer_norm(core, ctx, sem, name + "_norm")

        mask = sb("mask", [P, per])
        kv = sb("kv", [P, chunks, 2, B, KEYS])
        blk = sb("blk", [P, 2, kinds, B, per, KEYS])
        fold_q = sb("fold_q", [P, B, DC, HK])
        if narrow:
            ctx_twice = sb("ctx_twice", [P, B, 2, KEYS])
            half = sb("half", [P, 2])
            v_blk = sb("v_blk", [P, B, HEADS, width])
            heads = sb("heads", [P, 2, chunks, P])
        else:
            fold_v = sb("fold_v", [P, B, HK // P, D])
        ex = sb("ex", [P, 3, HEADS, KEYS])
        mx = sb("mx", [P, 2, HEADS])
        sm = sb("sm", [P, 2, HEADS])
        pt = sb("pt", [P, 2, HK])
        gamma, beta = (gb[:, 0, :], gb[:, 1, :]) if norm_out else (None, None)

        folds = []
        for c in range(chunks):
            for b in range(B):
                for dc in range(DC):
                    folds.append((c, wq_t[:, c, dc * P:(dc + 1) * P],
                                  blk[:, c % 2, 0, b].rearrange("p h k -> p (h k)"), per * KEYS,
                                  fold_q[:, b, dc, c * per * KEYS:(c + 1) * per * KEYS]))
                for m in range(0 if narrow else per // 2):
                    folds.append((c, blk[:, c % 2, 1, b, 2 * m:2 * m + 2].rearrange("p h k -> p (h k)"),
                                  wo[:, c, :], D, fold_v[:, b, c * per // 2 + m, :]))
        per_chunk = len(folds) // chunks

        before = opening(core, a, ctx, sem) if opens else {}

        with nc.Block() as block:
            @block.sync
            def _(sp):
                if opens:
                    before["sync"](sp)
                    fetch(sp, plan)
                fetch(sp, following)

            @block.gpsimd
            def _(pool):
                if opens:
                    before["gpsimd"](pool)
                nc.gpsimd.memset(mask[:, :], 1.0).then_inc(mask_set, 1)
                pool.wait_ge(mask_set, 1)
                nc.gpsimd.affine_select(out=mask[:, :], in_=mask[:, :], compare_op=ALU.is_ge, fill=0.0, base=0,
                                        pattern=[[-width, per]], channel_multiplier=1).then_inc(mask_set, 1)
                pool.wait_ge(mask_set, 2)
                nc.gpsimd.affine_select(out=mask[:, :], in_=mask[:, :], compare_op=ALU.is_ge, fill=0.0,
                                        base=width - 1, pattern=[[width, per]],
                                        channel_multiplier=-1).then_inc(mask_made, 1)
                if narrow:
                    pool.wait_ge(mask_made, 1)
                    nc.gpsimd.memset(half[:, :], 1.0).then_inc(mask_made, 1)
                    pool.wait_ge(mask_made, 2)
                    nc.gpsimd.affine_select(out=half[:, 0:1], in_=half[:, 0:1], compare_op=ALU.is_ge, fill=0.0,
                                            base=KEYS - 1, pattern=[[0, 1]], channel_multiplier=-1).then_inc(mask_made, 1)
                    nc.gpsimd.affine_select(out=half[:, 1:2], in_=half[:, 1:2], compare_op=ALU.is_ge, fill=0.0,
                                            base=-KEYS, pattern=[[0, 1]], channel_multiplier=1).then_inc(mask_made, 1)
                if bias:
                    pool.wait_ge(bias_made, 1)
                for j in range(PAIRS):
                    if bias:
                        for u in range(2):
                            i = 2 * j + u
                            last = nc.gpsimd.tensor_tensor(out_tile(i), source(i), bias_row[:, :], ALU.add)
                        last.then_inc(bias_added, 1)
                    if j >= 1:
                        norm_root(pool, j - 1)
                norm_root(pool, PAIRS - 1)

            @block.tensor
            def _(pe):
                if opens:
                    before["tensor"](pe)
                pe.wait_ge(weights_in, weights_total)
                for n, (srcs, _) in enumerate(turns):
                    if n >= 2:
                        pe.wait_ge(w_stored, n - 1)
                    for q, src in enumerate(srcs):
                        last = nc.tensor.transpose(ps[:, n % 2, q * P:(q + 1) * P], src, core["ident"][:, :])
                    last.then_inc(w_turned, 1)
                pe.wait_ge(w_stored, len(turns))

                def keys_values(c):
                    if c >= 2:
                        pe.wait_ge(kv_stored, c - 1)
                    for kind, w in enumerate((wk, wv)[:kinds]):
                        last = nc.tensor.matmul(ps[:, c % 2, kind * P:(kind + 1) * P], w[:, c * P:(c + 1) * P],
                                                context[:, :], start=True, stop=True)
                    last.then_inc(kv_ready, 1)

                keys_values(0)
                for n, (c, lhs, rhs, cols, _) in enumerate(folds):
                    if n % per_chunk == 0:
                        if c + 1 < chunks:
                            keys_values(c + 1)
                        pe.wait_ge(blocks_made, c + 1)
                    if n >= 4:
                        pe.wait_ge(fold_stored, n - 3)
                    nc.tensor.matmul(ps[:, 2 + n % 4, 0:cols], lhs, rhs, start=True,
                                     stop=True).then_inc(fold_ready, 1)
                pe.wait_ge(fold_stored, len(folds))
                if narrow:
                    pe.wait_ge(ctx_twice_made, 1)
                    for b in range(B):
                        nc.tensor.matmul(ps[:, 6 + b, 0:HEADS * width], ctx_twice[:, b].rearrange("p a k -> p (a k)"),
                                         wv[:, :], start=True, stop=True).then_inc(values_ready, 1)
                    pe.wait_ge(values_made, B)

                for i in range(TILES + TURN):
                    if i < TILES:
                        b = i // (TILES // B)
                        if i >= 2:
                            pe.wait_ge(centred, i - 1)
                        for h in range(2):
                            for dc in range(DC):
                                last = nc.tensor.matmul(ps[:, 2 * (i % 2) + h, :], core["xt"][:, dc, i * P:(i + 1) * P],
                                                        fold_q[:, b, dc, h * 512:(h + 1) * 512],
                                                        start=(dc == 0), stop=(dc == DC - 1))
                        last.then_inc(scores_ready, 1)
                    if 2 <= i <= TILES + 1:
                        k = i - 2
                        pe.wait_ge(probs_ready, k + 1)
                        if k >= 1:
                            pe.wait_ge(probs_stored, k)
                        for c in range(HK // P):
                            last = nc.tensor.transpose(ps[:, 4 + c // 4, (c % 4) * P:(c % 4 + 1) * P],
                                                       ex[:, k % 3, 2 * c:2 * c + 2, :].rearrange("p h k -> p (h k)"),
                                                       core["ident"][:, :])
                        last.then_inc(probs_turned, 1)
                    if narrow and HEADS_OUT <= i < TILES + HEADS_OUT:
                        k = i - HEADS_OUT
                        pe.wait_ge(probs_stored, k + 1)
                        if k >= 1:
                            pe.wait_ge(heads_stored, k)
                            if i > TURN:
                                pe.wait_ge(norm_stored, (i - TURN - 1) // 2 + 1)
                        for c in range(HK // P):
                            row = 2 * c * width
                            last = nc.tensor.matmul(
                                ps[row % P:row % P + 2 * width, 7, row // P * P:(row // P + 1) * P],
                                v_blk[:, k // (TILES // B), 2 * c:2 * c + 2, :].rearrange("p h d -> p (h d)"),
                                pt[:, k % 2, c * P:(c + 1) * P], start=True, stop=True)
                        last.then_inc(heads_ready, 1)
                    if narrow and OUT <= i < TILES + OUT:
                        k = i - OUT
                        pe.wait_ge(heads_stored, k + 1)
                        if k >= 1:
                            pe.wait_ge(out_added, k)
                        for c in range(chunks):
                            last = nc.tensor.matmul(ps[:, 6, 0:D], heads[:, k % 2, c, :], wo[:, c, :],
                                                    start=(c == 0), stop=(c == chunks - 1))
                        last.then_inc(out_ready, 1)
                    if not narrow and OUT <= i < TILES + OUT:
                        k = i - OUT
                        pe.wait_ge(probs_stored, k + 1)
                        if k >= 1:
                            pe.wait_ge(out_added, k)
                        for c in range(HK // P):
                            last = nc.tensor.matmul(ps[:, 6, 0:D],
                                                    pt[:, k % 2, c * P:(c + 1) * P],
                                                    fold_v[:, k // (TILES // B), c, :],
                                                    start=(c == 0), stop=(c == HK // P - 1))
                        last.then_inc(out_ready, 1)
                    if i >= TURN and (i - TURN) % 2 == 0:
                        if narrow:
                            pe.wait_ge(heads_stored, min(i - HEADS_OUT + 1, TILES))
                        norm_turn(pe, (i - TURN) // 2, tiles_of(core["xn"]))

            @block.scalar
            def _(act):
                if opens:
                    before["scalar"](act)
                for n, (srcs, dst) in enumerate(turns):
                    act.wait_ge(w_turned, n + 1)
                    nc.scalar.activation(dst, ps[:, n % 2, 0:P * len(srcs)], ACT.Copy).then_inc(w_stored, 1)

                def store_kv(c):
                    act.wait_ge(kv_ready, c + 1)
                    nc.scalar.activation(kv[:, c, 0:kinds].rearrange("p a b k -> p (a b k)"), ps[:, c % 2, 0:kinds * P],
                                         ACT.Copy).then_inc(kv_stored, 1)

                store_kv(0)
                for n, (c, _, _, cols, dst) in enumerate(folds):
                    if n % per_chunk == 0 and c + 1 < chunks:
                        store_kv(c + 1)
                    act.wait_ge(fold_ready, n + 1)
                    nc.scalar.activation(dst, ps[:, 2 + n % 4, 0:cols], ACT.Copy).then_inc(fold_stored, 1)

                for i in range(TILES + TURN):
                    if i < TILES:
                        act.wait_ge(centred, i + 1)
                        nc.scalar.activation(ex[:, i % 3], ex[:, i % 3], ACT.Exp, scale=scale).then_inc(exped, 1)
                    if 2 <= i <= TILES + 1:
                        k = i - 2
                        act.wait_ge(probs_turned, k + 1)
                        if k >= 2:
                            act.wait_ge(heads_ready if narrow else out_ready, k - 1)
                        nc.scalar.activation(pt[:, k % 2, :], ps[:, 4:6, :].rearrange("p a n -> p (a n)"),
                                             ACT.Copy).then_inc(probs_stored, 1)
                    if narrow and HEADS_OUT <= i < TILES + HEADS_OUT:
                        k = i - HEADS_OUT
                        act.wait_ge(heads_ready, k + 1)
                        if k >= 2:
                            act.wait_ge(out_ready, k - 1)
                        copy_bank(nc, heads[:, k % 2].rearrange("p c n -> p (c n)"), ps[:, 7, 0:HEADS * width]).then_inc(heads_stored, 1)
                    if i >= TURN and (i - TURN) % 2 == 0:
                        norm_store(act, (i - TURN) // 2, [(core["xt"], gamma, beta)])

            @block.vector
            def _(dve):
                if opens:
                    before["vector"](dve)
                dve.wait_ge(weights_in, weights_total)
                if not bias:
                    pass
                elif gate is None:
                    nc.vector.tensor_copy(bias_row[:, 0:1], bias_row[:, 0:1]).then_inc(bias_made, 1)
                else:
                    nc.vector.tensor_scalar(bias_row[:, :], bias_row[:, :], gate, None, ALU.mult).then_inc(bias_made, 1)
                if narrow:
                    nc.vector.tensor_copy(ctx_twice[:, :, :, :], context[:, :].rearrange("p (b k) -> p b k", b=B)
                                          .unsqueeze(2).to_broadcast([P, B, 2, KEYS])).then_inc(ctx_twice_made, 1)
                dve.wait_ge(mask_made, 1)
                for c in range(chunks):
                    dve.wait_ge(kv_stored, c + 1)
                    if c >= 2:
                        dve.wait_ge(fold_ready, per_chunk * (c - 1))
                    for kind in range(kinds):
                        for b in range(B):
                            last = nc.vector.tensor_tensor(
                                blk[:, c % 2, kind, b],
                                kv[:, c, kind, b, :].unsqueeze(1).to_broadcast([P, per, KEYS]),
                                mask[:, :].unsqueeze(2).to_broadcast([P, per, KEYS]), ALU.mult)
                    last.then_inc(blocks_made, 1)

                if narrow:
                    dve.wait_ge(mask_made, 4)
                    for b in range(B):
                        dve.wait_ge(values_ready, b + 1)
                        nc.vector.tensor_tensor(
                            v_blk[:, b].rearrange("p (m e) d -> p m e d", e=2),
                            ps[:, 6 + b, 0:HEADS * width].rearrange("p (m e d) -> p m e d", e=2, d=width),
                            half[:, :].unsqueeze(1).unsqueeze(3).to_broadcast([P, HEADS // 2, 2, width]),
                            ALU.mult).then_inc(values_made, 1)

                for i in range(TILES + OUT + 2):
                    if i < TILES:
                        dve.wait_ge(scores_ready, i + 1)
                        scores = ps[:, 2 * (i % 2):2 * (i % 2) + 2, :].rearrange("p a (h k) -> p (a h) k", k=KEYS)
                        nc.vector.tensor_reduce(mx[:, i % 2, :], scores, AX_X, ALU.max)
                        dve.drain()
                        if i >= 3:
                            dve.wait_ge(probs_turned, i - 2)
                        nc.vector.tensor_tensor(ex[:, i % 3], scores,
                                                mx[:, i % 2, :].unsqueeze(2).to_broadcast([P, HEADS, KEYS]),
                                                ALU.subtract).then_inc(centred, 1)
                    if 1 <= i <= TILES:
                        k = i - 1
                        dve.wait_ge(exped, k + 1)
                        nc.vector.tensor_reduce(sm[:, k % 2, :], ex[:, k % 3], AX_X, ALU.add)
                        dve.drain()
                        nc.vector.reciprocal(sm[:, k % 2, :], sm[:, k % 2, :])
                        dve.drain()
                        nc.vector.tensor_tensor(ex[:, k % 3], ex[:, k % 3],
                                                sm[:, k % 2, :].unsqueeze(2).to_broadcast([P, HEADS, KEYS]),
                                                ALU.mult).then_inc(probs_ready, 1)
                    if i >= OUT + 2 and (i - OUT) % 2 == 0:
                        norm_normalise(dve, (i - OUT - 2) // 2, out_tile, tiles_of(core["xn"]))
                    if OUT <= i < TILES + OUT:
                        k = i - OUT
                        dve.wait_ge(out_ready, k + 1)
                        if bias:
                            dve.wait_ge(bias_added, k // 2 + 1)
                        out = ps[:, 6, 0:D]
                        if gate is None:
                            nc.vector.tensor_tensor(out_tile(k), out, out_tile(k), ALU.add).then_inc(out_added, 1)
                        else:
                            nc.vector.scalar_tensor_tensor(out_tile(k), out, gate, out_tile(k), ALU.mult,
                                                           ALU.add).then_inc(out_added, 1)
                        if k % 2 == 1:
                            dve.drain()
                            norm_measure(dve, k // 2, out_tile)
        clear_semaphores()


def attention_weights(a, layout, bias, norm_out):
    def make(carve):
        loads, finish = layout(carve)
        bias_row, gb = carve([P, D]), carve([P, 2, DC])
        if bias:
            loads = loads + [(bias_row[:, :], rows(a[bias]))]
        if norm_out:
            loads = loads + [(gb[:, k, :], columns(a[n])) for k, n in enumerate(norm_out)]
        return loads, (finish, bias_row, gb)
    return make


def layout_l0(a):
    def layout(carve):
        wq, wk, wv, wo = carve([P, DC, 1024]), carve([P, 1024]), carve([P, 1024]), carve([P, 8, D])
        loads = [(wq[:, :, :], a["L0_xattn_Wq"].rearrange("(c p) n -> p c n", p=P)),
                 (wk[:, :], a["L0_xattn_Wk"]), (wv[:, :], a["L0_xattn_Wv"]),
                 (wo[:, :, :], a["L0_xattn_Wo"].rearrange("(c p) n -> p c n", p=P))]

        def finish(sb):
            wq_t = sb("wq_t", [P, 8, D])
            turns = [([wq[:, dc, c * P:(c + 1) * P] for c in (2 * q, 2 * q + 1) for dc in range(DC)],
                      wq_t[:, 2 * q:2 * q + 2, :].rearrange("p c d -> p (c d)")) for q in range(4)]
            return wq_t, wo, turns, wk, wv
        return loads, finish
    return layout


def first(t):
    return isinstance(t, int) and t == 0


def later(t):
    return not (isinstance(t, int) and t < 2)


def copy_bank(nc, dst, bank_ap):
    return nc.scalar.activation(dst, bank_ap, ACT.Copy)


def experts_weights(a, router, affine=None, shared=None):
    def make(carve):
        wr, gb, s1, s2 = carve([P, DC, E]), None, None, None
        loads = [(wr[:, :, :], a[router].rearrange("(c p) e -> p c e", p=P))]
        if affine:
            gb = carve([P, 2, DC])
            loads += [(gb[:, k, :], columns(a[n])) for k, n in enumerate(affine)]
        if shared:
            s1, s2 = carve([P, DC, 512]), carve([P, 2, D])
            loads += [(s1[:, :, :], a[shared[0]].rearrange("(c p) n -> p c n", p=P)),
                      (s2[:, :, :], a[shared[1]].rearrange("(c p) n -> p c n", p=P))]
        return loads, (wr, gb, s1, s2)
    return make


def stage_experts(core, a, name, *, top, rows_tiles, capacity, plan, following, w1, w2, swiglu, gate,
                  norm_behind=True):
    nc, ps = core["nc"], core["ps"]
    ROWS = rows_tiles * PAIR
    WIDE = 2 * FF if swiglu else FF
    HALF = 2 if swiglu else 1
    xs = nc.dram_tensor(f"{name}_rows", [ROWS, D], F32, kind="Internal").ap()
    ys = nc.dram_tensor(f"{name}_results", [ROWS + P, D], F32, kind="Internal").ap()
    with ExitStack() as ctx:
        def sb(part, shape, dtype=F32):
            return ctx.enter_context(nc.sbuf_tensor(f"{name}_{part}", shape, dtype))

        sem, clear_semaphores = named_semaphores(nc, name)
        made, zeroed = sem("made"), sem("zeroed")
        logits_ready, shifted, exped = sem("logits_ready"), sem("shifted"), sem("exped")
        chosen, counted, slots_made = sem("chosen"), sem("counted"), sem("slots_made")
        scattered = sem("scattered")
        if not capacity:
            owners_made = sem("owners_made")
        w1_in, w2_in = [sem("w1_in0"), sem("w1_in1")], [sem("w2_in0"), sem("w2_in1")]
        rows_in, y_sent = [sem("rows_in0"), sem("rows_in1")], [sem("y_sent0"), sem("y_sent1")]
        rows_turned, rows_stored = sem("rows_turned"), sem("rows_stored")
        hid_ready, hid_stored = sem("hid_ready"), sem("hid_stored")
        clipped, silued = sem("clipped"), sem("silued")
        out_ready, y_stored = sem("out_ready"), sem("y_stored")
        gathered, added = [sem(f"gathered{q}") for q in range(4)], sem("added")
        if norm_behind:
            norm_measure, norm_root, norm_normalise, norm_turn, norm_store, norm_stored = layer_norm(core, ctx, sem, name + "_norm", on_vector=True)
        else:
            x_sent = sem("x_sent")

        tri = sb("tri", [P, P])
        ones = sb("ones", [P, P])
        iota_e = sb("iota_e", [P, E])
        iota_t = sb("iota_t", [P, rows_tiles])
        pr = sb("pr", [P, TILES, E])
        eq = sb("eq", [P, TILES, E])
        hot = [sb(f"hot{k}", [P, TILES, E]) for k in range(top)]
        hots = sb("hots", [P, TILES, E])
        best = sb("best", [P, top, TILES])
        col = sb("col", [P, 2, TILES])
        total = sb("total", [P, TILES, E])
        scan = [sb("scan0", [P, TILES, E]), sb("scan1", [P, TILES, E])]
        ends = [sb("ends0", [P, E]), sb("ends1", [P, E])]
        need = sb("need", [P, E])
        need_i = sb("need_i", [P, E], I32)
        owner = sb("owner", [P, rows_tiles, E])
        owner_f = sb("owner_f", [P, rows_tiles])
        owner_i = sb("owner_i", [P, rows_tiles], I32)
        slot_f = sb("slot_f", [P, TILES])
        slot = sb("slot", [P, top, TILES], I32)
        weight = sb("weight", [P, top, TILES])
        zero = sb("zero", [P, 2 * D])
        w1_sb = sb("w1", [P, 2, DC, WIDE])
        w2_sb = sb("w2", [P, 2, FC, D])
        xr = sb("xr", [P, 2, 2, D])
        xrt = sb("xrt", [P, 2, DC, PAIR])
        sg = sb("sg", [P, 4, PAIR])
        ht = sb("ht", [P, 2, FC, PAIR])
        yt = sb("yt", [P, 2, 2, D])
        yg = sb("yg", [P, 4, D])
        _, weights_in, weights_total, (wr, gb, s1, s2) = plan
        affine, shared = gb is not None, s1 is not None
        if shared:
            FS = 256
            SC = FS // P
            s_hid_ready, s_clipped, s_silued = sem("s_hid_ready"), sem("s_clipped"), sem("s_silued")
            s_hid_stored, s_out_ready, s_added = sem("s_hid_stored"), sem("s_out_ready"), sem("s_added")

        w1_rows = a[w1].rearrange("e (c p) n -> e p c n", p=P)
        w2_rows = a[w2].rearrange("e (c p) n -> e p c n", p=P)
        xs_rows = xs.rearrange("(t u p) d -> t p u d", u=2, p=P)
        ys_rows = ys[0:ROWS, :].rearrange("(t u p) d -> t p u d", u=2, p=P)
        zero_loads = rows_tiles

        LOOPS = (rows_tiles - 4) // 2
        FIRST_LEFT = 3 + 2 * LOOPS

        with nc.Block() as block:
            @block.sync
            def _(sp):
                if following:
                    fetch(sp, following)
                sp.wait_ge(made, 6)
                for n in range(zero_loads):
                    sp.dma_start(xs.rearrange("(n p r) d -> n p (r d)", p=P, r=2)[n], zero[:, :]).then_inc(zeroed, 16)
                sp.dma_start(ys[ROWS:ROWS + P, :], zero[:, 0:D]).then_inc(zeroed, 16)

                def expert_of(t):
                    return t if capacity else sp.value_load(owner_i[0:1, bass.ds(t, 1)], min_val=0, max_val=E - 1)

                def load_w1(e, p):
                    sp.dma_start(w1_sb[:, p], w1_rows[bass.ds(e, 1)].rearrange("a p c n -> p (a c) n")).then_inc(w1_in[p], 16)

                def load_w2(e, p):
                    sp.dma_start(w2_sb[:, p], w2_rows[bass.ds(e, 1)].rearrange("a p c n -> p (a c) n")).then_inc(w2_in[p], 16)

                def load_rows(t, p):
                    sp.dma_start(xr[:, p], xs_rows[bass.ds(t, 1)].rearrange("a p u d -> p (a u) d")).then_inc(rows_in[p], 16)

                def load(jj, p):
                    t = 2 * jj + p
                    e = expert_of(t)
                    sp.wait_ge(hid_ready, FC * (t - 1))
                    load_w1(e, p)
                    sp.wait_ge(rows_turned, t - 1)
                    load_rows(t, p)
                    sp.wait_ge(out_ready, t - 1)
                    load_w2(e, p)

                if not capacity:
                    sp.wait_ge(owners_made, 1)
                for t in range(2):
                    e = expert_of(t)
                    load_w1(e, t)
                    load_w2(e, t)
                sp.wait_ge(slots_made, 1)
                sp.wait_ge(scattered, 16 * TILES * top)
                for t in range(2):
                    load_rows(t, t)
                load(1, 0)
                with sp.Fori(1, 1 + LOOPS) as jj:
                    load(jj, 1)
                    load(jj + 1, 0)
                for t in range(FIRST_LEFT, rows_tiles):
                    load(t // 2, t % 2)
                if not norm_behind:
                    for i in range(TILES):
                        sp.wait_ge(added, top * (i + 1))
                        sp.dma_start(a["out"].rearrange("b (t p) d -> p (b t) d", p=P)[:, i, :],
                                     core["x"][:, i, :]).then_inc(x_sent, 16)
                    sp.wait_ge(x_sent, 16 * TILES)

            @block.gpsimd
            def _(pool):
                nc.gpsimd.memset(tri[:, :], 1.0).then_inc(made, 1)
                nc.gpsimd.memset(ones[:, :], 1.0).then_inc(made, 1)
                nc.gpsimd.memset(zero[:, :], 0.0).then_inc(made, 1)
                nc.gpsimd.iota(iota_e[:, :], [[1, E]], base=0, channel_multiplier=0,
                               allow_small_or_imprecise_dtypes=True).then_inc(made, 1)
                nc.gpsimd.iota(iota_t[:, :], [[1, rows_tiles]], base=0, channel_multiplier=0,
                               allow_small_or_imprecise_dtypes=True).then_inc(made, 1)
                pool.wait_ge(made, 5)
                nc.gpsimd.affine_select(out=tri[:, :], in_=tri[:, :], compare_op=ALU.is_gt, fill=0.0, base=0,
                                        pattern=[[1, P]], channel_multiplier=-1).then_inc(made, 1)
                pool.wait_ge(zeroed, 16 * (zero_loads + 1))
                pool.wait_ge(slots_made, 1)
                for k in range(top):
                    for i in range(TILES):
                        pool.indirect_dma_start(xs, bass.IndirectOffsetOnAxis(ap=slot[:, k, i:i + 1], axis=0),
                                                core["xn"][:, i, :], None, bounds_check=ROWS - 1,
                                                oob_is_err=False).then_inc(scattered, 16)

                def send(jj, p):
                    t = 2 * jj + p
                    pool.wait_ge(y_stored, t + 1)
                    pool.dma_start(ys_rows[bass.ds(t, 1)].rearrange("a p u d -> p (a u) d"), yt[:, p]).then_inc(y_sent[p], 16)

                for t in range(3):
                    send(t // 2, t % 2)
                with pool.Fori(1, 1 + LOOPS) as jj:
                    send(jj, 1)
                    send(jj + 1, 0)
                for t in range(FIRST_LEFT, rows_tiles):
                    send(t // 2, t % 2)
                for p in range(2):
                    pool.wait_ge(y_sent[p], 16 * ((rows_tiles + 1 - p) // 2))
                for n in range(TILES * top):
                    i, k = n // top, n % top
                    if n >= 4:
                        pool.wait_ge(added, n - 3)
                    pool.indirect_dma_start(yg[:, n % 4, :], None, ys,
                                            bass.IndirectOffsetOnAxis(ap=slot[:, k, i:i + 1], axis=0),
                                            bounds_check=ROWS + P - 1, oob_is_err=False).then_inc(gathered[n % 4], 16)

            @block.tensor
            def _(pe):
                pe.wait_ge(weights_in, weights_total)
                for i in range(TILES):
                    for dc in range(DC):
                        last = nc.tensor.matmul(ps[:, 0, i * E:(i + 1) * E], core["xt"][:, dc, i * P:(i + 1) * P],
                                                wr[:, dc, :], start=(dc == 0), stop=(dc == DC - 1))
                last.then_inc(logits_ready, 1)
                pe.wait_ge(made, 6)
                pe.wait_ge(chosen, 1)
                nc.tensor.matmul(ps[:, 5, 0:P], tri[:, :], hots[:, :, :].rearrange("p t e -> p (t e)"),
                                 start=True, stop=True)
                nc.tensor.matmul(ps[:, 6, 0:P], ones[:, :], hots[:, :, :].rearrange("p t e -> p (t e)"),
                                 start=True, stop=True).then_inc(counted, 1)

                if shared:
                    for j in range(PAIRS + 1):
                        if j < PAIRS:
                            for f in range(SC):
                                n = SC * j + f
                                if n >= 2:
                                    pe.wait_ge(s_hid_stored, n - 1)
                                for h in range(2):
                                    for dc in range(DC):
                                        last = nc.tensor.matmul(
                                            ps[:, 1 + n % 2, h * PAIR:(h + 1) * PAIR],
                                            s1[:, dc, h * FS + f * P:h * FS + (f + 1) * P],
                                            core["xt"][:, dc, PAIR * j:PAIR * (j + 1)],
                                            start=(dc == 0), stop=(dc == DC - 1))
                                last.then_inc(s_hid_ready, 1)
                        if j >= 1:
                            q = j - 1
                            pe.wait_ge(s_hid_stored, SC * j)
                            if q >= 2:
                                pe.wait_ge(s_added, q - 1)
                            for u in range(2):
                                for f in range(SC):
                                    last = nc.tensor.matmul(ps[:, 3 + q % 2, u * D:(u + 1) * D],
                                                            ht[:, q % 2, f, u * P:(u + 1) * P], s2[:, f, :],
                                                            start=(f == 0), stop=(f == SC - 1))
                            last.then_inc(s_out_ready, 1)
                    pe.wait_ge(s_added, PAIRS)

                def turn(jj, p):
                    t = 2 * jj + p
                    pe.wait_ge(rows_in[p], 16 * jj + 16)
                    if not first(t):
                        pe.wait_ge(rows_stored, t)
                    for c in range(DC):
                        for u in range(2):
                            last = nc.tensor.transpose(ps[:, 7, c * PAIR + u * P:c * PAIR + (u + 1) * P],
                                                       xr[:, p, u, c * P:(c + 1) * P], core["ident"][:, :])
                    last.then_inc(rows_turned, 1)

                def hidden(jj, p):
                    t = 2 * jj + p
                    pe.wait_ge(w1_in[p], 16 * jj + 16)
                    pe.wait_ge(rows_stored, t + 1)
                    for f in range(FC):
                        if not (first(t) and f < 4):
                            pe.wait_ge(hid_stored, FC * t + (f - 3))
                        for h in range(HALF):
                            for dc in range(DC):
                                last = nc.tensor.matmul(ps[:, f % 4, h * PAIR:(h + 1) * PAIR],
                                                        w1_sb[:, p, dc, h * FF + f * P:h * FF + (f + 1) * P],
                                                        xrt[:, p, dc, :], start=(dc == 0), stop=(dc == DC - 1))
                        last.then_inc(hid_ready, 1)

                def output(jj, p):
                    t = 2 * jj + p
                    pe.wait_ge(w2_in[p], 16 * jj + 16)
                    pe.wait_ge(hid_stored, FC * t + FC)
                    if later(t):
                        pe.wait_ge(y_stored, t - 1)
                    for u in range(2):
                        for f in range(FC):
                            last = nc.tensor.matmul(ps[:, 4 + p, u * D:(u + 1) * D],
                                                    ht[:, p, f, u * P:(u + 1) * P], w2_sb[:, p, f, :],
                                                    start=(f == 0), stop=(f == FC - 1))
                    last.then_inc(out_ready, 1)

                pe.wait_ge(slots_made, 1)
                turn(0, 0)
                for t in range(3):
                    hidden(t // 2, t % 2)
                    turn((t + 1) // 2, (t + 1) % 2)
                    if t >= 1:
                        output((t - 1) // 2, (t - 1) % 2)
                with pe.Fori(1, 1 + LOOPS) as jj:
                    hidden(jj, 1)
                    turn(jj + 1, 0)
                    output(jj, 0)
                    hidden(jj + 1, 0)
                    turn(jj + 1, 1)
                    output(jj, 1)
                for t in range(FIRST_LEFT, rows_tiles):
                    hidden(t // 2, t % 2)
                    if t + 1 < rows_tiles:
                        turn((t + 1) // 2, (t + 1) % 2)
                    output((t - 1) // 2, (t - 1) % 2)
                output((rows_tiles - 1) // 2, (rows_tiles - 1) % 2)
                if norm_behind:
                    for j in range(PAIRS):
                        norm_turn(pe, j, tiles_of(core["xn"]))

            @block.scalar
            def _(act):
                act.wait_ge(weights_in, weights_total)
                act.wait_ge(shifted, 1)
                nc.scalar.activation(pr[:, :, :], pr[:, :, :], ACT.Exp).then_inc(exped, 1)
                if shared:
                    for n in range(SC * PAIRS):
                        act.wait_ge(s_clipped, n + 1)
                        nc.scalar.activation(sg[:, n % 4, :], sg[:, n % 4, :], ACT.Silu).then_inc(s_silued, 1)

                def store_rows(jj, p):
                    t = 2 * jj + p
                    act.wait_ge(rows_turned, t + 1)
                    if later(t):
                        act.wait_ge(hid_ready, FC * (t - 1))
                    if affine:
                        for c in range(DC):
                            last = nc.scalar.activation(xrt[:, p, c, :], ps[:, 7, c * PAIR:(c + 1) * PAIR], ACT.Identity,
                                                        bias=gb[:, 1, c:c + 1], scale=gb[:, 0, c:c + 1])
                    else:
                        last = copy_bank(nc, xrt[:, p].rearrange("p c n -> p (c n)"), ps[:, 7, :])
                    last.then_inc(rows_stored, 1)

                def activate(jj, p):
                    t = 2 * jj + p
                    for f in range(FC):
                        if swiglu:
                            act.wait_ge(clipped, FC * t + (f + 1))
                            nc.scalar.activation(sg[:, f % 4, :], sg[:, f % 4, :], ACT.Silu).then_inc(silued, 1)
                        else:
                            act.wait_ge(hid_ready, FC * t + (f + 1))
                            if f == 0 and later(t):
                                act.wait_ge(out_ready, t - 1)
                            nc.scalar.activation(ht[:, p, f, :], ps[:, f % 4, 0:PAIR], ACT.Relu).then_inc(hid_stored, 1)

                def store_y(jj, p):
                    t = 2 * jj + p
                    act.wait_ge(out_ready, t + 1)
                    if later(t):
                        act.wait_ge(y_sent[p], 16 * jj)
                    copy_bank(nc, yt[:, p].rearrange("p u d -> p (u d)"), ps[:, 4 + p, :]).then_inc(y_stored, 1)

                store_rows(0, 0)
                for t in range(3):
                    activate(t // 2, t % 2)
                    store_rows((t + 1) // 2, (t + 1) % 2)
                    if t >= 1:
                        store_y((t - 1) // 2, (t - 1) % 2)
                with act.Fori(1, 1 + LOOPS) as jj:
                    activate(jj, 1)
                    store_rows(jj + 1, 0)
                    store_y(jj, 0)
                    activate(jj + 1, 0)
                    store_rows(jj + 1, 1)
                    store_y(jj, 1)
                for t in range(FIRST_LEFT, rows_tiles):
                    activate(t // 2, t % 2)
                    if t + 1 < rows_tiles:
                        store_rows((t + 1) // 2, (t + 1) % 2)
                    store_y((t - 1) // 2, (t - 1) % 2)
                store_y((rows_tiles - 1) // 2, (rows_tiles - 1) % 2)
                if norm_behind:
                    for j in range(PAIRS):
                        norm_store(act, j, [(core["xt"], None, None)])

            @block.vector
            def _(dve):
                def over_experts(x):
                    return x.unsqueeze(2).to_broadcast([P, TILES, E])

                def over_tiles(x):
                    return x.unsqueeze(1).to_broadcast([P, TILES, E])

                tt, stt, ts = nc.vector.tensor_tensor, nc.vector.scalar_tensor_tensor, nc.vector.tensor_scalar
                reduce = nc.vector.tensor_reduce
                dve.wait_ge(logits_ready, 1)
                logits = ps[:, 0, 0:TILES * E].rearrange("p (t e) -> p t e", e=E)
                reduce(col[:, 0, :], logits, AX_X, ALU.max)
                dve.drain()
                tt(pr[:, :, :], logits, over_experts(col[:, 0, :]), ALU.subtract).then_inc(shifted, 1)
                dve.wait_ge(exped, 1)
                reduce(col[:, 0, :], pr[:, :, :], AX_X, ALU.add)
                dve.drain()
                nc.vector.reciprocal(col[:, 0, :], col[:, 0, :])
                dve.drain()
                tt(pr[:, :, :], pr[:, :, :], over_experts(col[:, 0, :]), ALU.mult)
                dve.wait_ge(made, 6)
                for k in range(top):
                    dve.drain()
                    reduce(best[:, k, :], pr[:, :, :], AX_X, ALU.max)
                    dve.drain()
                    tt(eq[:, :, :], pr[:, :, :], over_experts(best[:, k, :]), ALU.is_equal)
                    dve.drain()
                    stt(eq[:, :, :], eq[:, :, :], -float(E), over_tiles(iota_e[:, :]), ALU.mult, ALU.add)
                    dve.drain()
                    reduce(col[:, 1, :], eq[:, :, :], AX_X, ALU.min)
                    dve.drain()
                    tt(hot[k][:, :, :], eq[:, :, :], over_experts(col[:, 1, :]), ALU.is_equal)
                    dve.drain()
                    if k + 1 < top:
                        stt(pr[:, :, :], hot[k][:, :, :], -2.0, pr[:, :, :], ALU.mult, ALU.add)
                if top == 1:
                    nc.vector.tensor_copy(hots[:, :, :], hot[0][:, :, :]).then_inc(chosen, 1)
                    ts(weight[:, 0, :], best[:, 0, :], gate, None, ALU.mult)
                else:
                    tt(hots[:, :, :], hot[0][:, :, :], hot[1][:, :, :], ALU.add).then_inc(chosen, 1)
                    tt(col[:, 0, :], best[:, 0, :], best[:, 1, :], ALU.add)
                    dve.drain()
                    nc.vector.reciprocal(col[:, 0, :], col[:, 0, :])
                    dve.drain()
                    for k in range(2):
                        stt(weight[:, k, :], best[:, k, :], gate, col[:, 0, :], ALU.mult, ALU.mult)
                dve.wait_ge(counted, 1)
                counts = ps[:, 6, 0:TILES * E].rearrange("p (t e) -> p t e", e=E)
                nc.vector.tensor_copy(total[:, :, :], counts)
                nc.vector.tensor_copy(scan[0][:, :, :], counts)
                dve.drain()
                for n, step in enumerate((1, 2, 4, 8)):
                    x, y = scan[n % 2], scan[1 - n % 2]
                    nc.vector.tensor_copy(y[:, 0:step, :], x[:, 0:step, :])
                    tt(y[:, step:, :], x[:, step:, :], x[:, 0:TILES - step, :], ALU.add)
                    dve.drain()
                if capacity:
                    ts(ends[0][:, :], iota_e[:, :], float(capacity), None, ALU.mult)
                else:
                    ts(need_i[:, :], scan[0][:, TILES - 1, :], float(PAIR - 1), None, ALU.add)
                    dve.drain()
                    ts(need_i[:, :], need_i[:, :], 8, None, ALU.arith_shift_right)
                    dve.drain()
                    nc.vector.tensor_copy(need[:, :], need_i[:, :])
                    nc.vector.tensor_copy(ends[0][:, :], need_i[:, :])
                    dve.drain()
                    for n, step in enumerate((1, 2, 4)):
                        x, y = ends[n % 2], ends[1 - n % 2]
                        nc.vector.tensor_copy(y[:, 0:step], x[:, 0:step])
                        tt(y[:, step:], x[:, step:], x[:, 0:E - step], ALU.add)
                        dve.drain()
                    tt(owner[:, :, :], iota_t[:, :].unsqueeze(2).to_broadcast([P, rows_tiles, E]),
                       ends[1][:, :].unsqueeze(1).to_broadcast([P, rows_tiles, E]), ALU.is_ge)
                    dve.drain()
                    reduce(owner_f[:, :], owner[:, :, :], AX_X, ALU.add)
                    dve.drain()
                    ts(owner_i[:, :], owner_f[:, :], float(E - 1), None, ALU.min).then_inc(owners_made, 1)
                    tt(ends[0][:, :], ends[1][:, :], need[:, :], ALU.subtract)
                    dve.drain()
                    ts(ends[0][:, :], ends[0][:, :], float(PAIR), None, ALU.mult)
                tt(scan[0][:, :, :], scan[0][:, :, :], total[:, :, :], ALU.subtract)
                dve.drain()
                tt(scan[0][:, :, :], scan[0][:, :, :], ps[:, 5, 0:TILES * E].rearrange("p (t e) -> p t e", e=E), ALU.add)
                dve.drain()
                tt(scan[1][:, :, :], scan[0][:, :, :], over_tiles(ends[0][:, :]), ALU.add)
                dve.drain()
                for k in range(top):
                    tt(eq[:, :, :], hot[k][:, :, :], scan[1][:, :, :], ALU.mult)
                    dve.drain()
                    reduce(slot_f[:, :], eq[:, :, :], AX_X, ALU.add)
                    dve.drain()
                    if capacity:
                        tt(eq[:, :, :], hot[k][:, :, :], scan[0][:, :, :], ALU.mult)
                        dve.drain()
                        reduce(col[:, 0, :], eq[:, :, :], AX_X, ALU.add)
                        dve.drain()
                        ts(col[:, 0, :], col[:, 0, :], float(capacity), None, ALU.is_lt)
                        dve.drain()
                        stt(slot_f[:, :], slot_f[:, :], float(-ROWS), col[:, 0, :], ALU.add, ALU.mult)
                        dve.drain()
                        ts(slot_f[:, :], slot_f[:, :], float(ROWS), None, ALU.add)
                        dve.drain()
                    last = nc.vector.tensor_copy(slot[:, k, :], slot_f[:, :])
                    dve.drain()
                nc.vector.tensor_copy(slot_f[:, :], slot_f[:, :]).then_inc(slots_made, 1)

                if shared:
                    def s_clip(n):
                        dve.wait_ge(s_hid_ready, n + 1)
                        ts(sg[:, n % 4, :], ps[:, 1 + n % 2, 0:PAIR], 10.0, -10.0, ALU.min,
                           ALU.max).then_inc(s_clipped, 1)

                    def s_multiply(n):
                        q = n // SC
                        dve.wait_ge(s_silued, n + 1)
                        if q >= 2:
                            dve.wait_ge(s_out_ready, q - 1)
                        tt(ht[:, q % 2, n % SC, :], sg[:, n % 4, :], ps[:, 1 + n % 2, PAIR:2 * PAIR],
                           ALU.mult).then_inc(s_hid_stored, 1)

                    for j in range(PAIRS + 1):
                        if j < PAIRS:
                            s_clip(2 * j)
                            s_clip(2 * j + 1)
                            s_multiply(2 * j)
                            s_multiply(2 * j + 1)
                        if j >= 1:
                            q = j - 1
                            dve.wait_ge(s_out_ready, j)
                            x2 = core["x"][:, 2 * q:2 * q + 2, :].rearrange("p u d -> p (u d)")
                            stt(x2, ps[:, 3 + q % 2, :], gate, x2, ALU.mult, ALU.add).then_inc(s_added, 1)

                if swiglu:
                    def clip(t, f):
                        dve.wait_ge(hid_ready, FC * t + (f + 1))
                        ts(sg[:, f % 4, :], ps[:, f % 4, 0:PAIR], 10.0, -10.0, ALU.min, ALU.max).then_inc(clipped, 1)

                    def multiply(t, p, f):
                        dve.wait_ge(silued, FC * t + (f + 1))
                        if f == 0 and later(t):
                            dve.wait_ge(out_ready, t - 1)
                        tt(ht[:, p, f, :], sg[:, f % 4, :], ps[:, f % 4, PAIR:2 * PAIR], ALU.mult).then_inc(hid_stored, 1)

                    def gates(jj, p):
                        t = 2 * jj + p
                        clip(t, 0)
                        for f in range(1, FC):
                            clip(t, f)
                            multiply(t, p, f - 1)
                        multiply(t, p, FC - 1)

                    for t in range(3):
                        gates(t // 2, t % 2)
                    with dve.Fori(1, 1 + LOOPS) as jj:
                        gates(jj, 1)
                        gates(jj + 1, 0)
                    for t in range(FIRST_LEFT, rows_tiles):
                        gates(t // 2, t % 2)
                for n in range(TILES * top):
                    i, k = n // top, n % top
                    dve.wait_ge(gathered[n % 4], 16 * (n // 4 + 1))
                    stt(core["x"][:, i, :], yg[:, n % 4, :], weight[:, k, i:i + 1], core["x"][:, i, :], ALU.mult,
                        ALU.add).then_inc(added, 1)
                    dve.drain()
                    if norm_behind and n % (2 * top) == 2 * top - 1:
                        j = n // (2 * top)
                        norm_measure(dve, j, tiles_of(core["x"]))
                        norm_normalise(dve, j, tiles_of(core["x"]), tiles_of(core["xn"]))
        clear_semaphores()


def one_head_weights(a):
    def make(carve):
        wq, wq_t = carve([P, DC, D]), carve([P, DC, D])
        wk, wv = carve([P, D]), carve([P, D])
        bq, bk, bv = carve([P, DC]), carve([P, DC]), carve([P, D])
        loads = [(wq[:, :, :], a["L1_xattn_Wq"].rearrange("(c p) n -> p c n", p=P)), (wk[:, :], a["L1_xattn_Wk"]),
                 (wv[:, :], a["L1_xattn_Wv"]), (bq[:, :], columns(a["L1_xattn_bq"])),
                 (bk[:, :], columns(a["L1_xattn_bk"])), (bv[:, :], rows(a["L1_xattn_bv"]))]
        return loads, (wq, wq_t, wk, wv, bq, bk, bv)
    return make


def stage_one_head(core, a, plan, following):
    nc, ps = core["nc"], core["ps"]
    gate = core["gate_attn"][:, 1:2]
    BK = B * KEYS
    with ExitStack() as ctx:
        _, weights_in, weights_total, (wq, wq_t, wk, wv, bq, bk, bv) = plan

        def sb(part, shape):
            return ctx.enter_context(nc.sbuf_tensor(f"l1a_{part}", shape, F32))

        sem, clear_semaphores = named_semaphores(nc, "l1a")
        zeroed, w_ready, w_stored = sem("zeroed"), sem("w_ready"), sem("w_stored")
        kv_ready, kv_stored, fold_ready, fold_stored = sem("kv_ready"), sem("kv_stored"), sem("fold_ready"), sem("fold_stored")
        values_made = sem("values_made")
        scores_ready, centred, exped = sem("scores_ready"), sem("centred"), sem("exped")
        probs_ready, probs_turned, probs_stored = sem("probs_ready"), sem("probs_turned"), sem("probs_stored")
        out_ready, out_added = sem("out_ready"), sem("out_added")
        norm_measure, norm_root, norm_normalise, norm_turn, norm_store, norm_stored = layer_norm(core, ctx, sem, "l1a_norm", on_vector=True)
        bq_wide = sb("bq_wide", [P, DC, P])
        keys_t, values = sb("keys_t", [P, DC, BK]), sb("values", [P, D])
        fold_q, score_bias = sb("fold_q", [P, DC, BK]), sb("score_bias", [P, BK])
        ex = sb("ex", [P, B, 2, 2, BK])
        mx, sm = sb("mx", [P, 2, 2]), sb("sm", [P, 2, 2])
        pt = sb("pt", [P, 2, PAIR])
        def own(j):
            b = j // (PAIRS // B)
            return ex[:, b, j % 2, :, b * KEYS:(b + 1) * KEYS]

        with nc.Block() as block:
            @block.sync
            def _(sp):
                fetch(sp, following)

            @block.gpsimd
            def _(pool):
                nc.gpsimd.memset(ex[:, :, :, :, :], 0.0).then_inc(zeroed, 1)

            @block.tensor
            def _(pe):
                pe.wait_ge(weights_in, weights_total)
                for ec in range(DC):
                    for dc in range(DC):
                        last = nc.tensor.transpose(ps[:, 0, ec * D + dc * P:ec * D + (dc + 1) * P],
                                                   wq[:, dc, ec * P:(ec + 1) * P], core["ident"][:, :])
                last.then_inc(w_ready, 1)
                for ec in range(DC):
                    nc.tensor.matmul(ps[:, 1, ec * BK:(ec + 1) * BK], wk[:, ec * P:(ec + 1) * P], core["ctx_t"][:, :],
                                     start=True, stop=True)
                nc.tensor.matmul(ps[:, 2, 0:D], core["ctx_t"][:, :], wv[:, :], start=True, stop=True).then_inc(kv_ready, 1)
                pe.wait_ge(w_stored, 1)
                pe.wait_ge(kv_stored, 1)
                pe.wait_ge(values_made, 1)
                for dc in range(DC):
                    for ec in range(DC):
                        nc.tensor.matmul(ps[:, 3, dc * BK:(dc + 1) * BK], wq_t[:, ec, dc * P:(dc + 1) * P],
                                         keys_t[:, ec, :], start=(ec == 0), stop=(ec == DC - 1))
                for ec in range(DC):
                    last = nc.tensor.matmul(ps[:, 4, 0:BK], bq_wide[:, ec, :], keys_t[:, ec, :],
                                            start=(ec == 0), stop=(ec == DC - 1))
                last.then_inc(fold_ready, 1)
                pe.wait_ge(fold_stored, 2)
                for j in range(PAIRS + 3):
                    if j < PAIRS:
                        b = j // (PAIRS // B)
                        if j >= 2:
                            pe.wait_ge(centred, j - 1)
                        for u in range(2):
                            i = 2 * j + u
                            for dc in range(DC):
                                last = nc.tensor.matmul(ps[:, j % 2, u * KEYS:(u + 1) * KEYS],
                                                        core["xt"][:, dc, i * P:(i + 1) * P],
                                                        fold_q[:, dc, b * KEYS:(b + 1) * KEYS],
                                                        start=(dc == 0), stop=(dc == DC - 1))
                        last.then_inc(scores_ready, 1)
                    if 1 <= j <= PAIRS:
                        k = j - 1
                        pe.wait_ge(probs_ready, k + 1)
                        if k >= 1:
                            pe.wait_ge(probs_stored, k)
                        for u in range(2):
                            last = nc.tensor.transpose(ps[:, 4, u * P:(u + 1) * P],
                                                       ex[:, k // (PAIRS // B), k % 2, u, :], core["ident"][:, :])
                        last.then_inc(probs_turned, 1)
                    if j >= 3:
                        norm_turn(pe, j - 3, tiles_of(core["xn"]))
                    if 2 <= j <= PAIRS + 1:
                        k = j - 2
                        pe.wait_ge(probs_stored, k + 1)
                        if k >= 2:
                            pe.wait_ge(out_added, k - 1)
                        for u in range(2):
                            last = nc.tensor.matmul(ps[:, 5 + k % 2, u * D:(u + 1) * D], pt[:, k % 2, u * P:(u + 1) * P],
                                                    values[:, :], start=True, stop=True)
                        last.then_inc(out_ready, 1)

            @block.scalar
            def _(act):
                act.wait_ge(w_ready, 1)
                copy_bank(nc, wq_t[:, :, :].rearrange("p c d -> p (c d)"), ps[:, 0, :]).then_inc(w_stored, 1)
                act.wait_ge(kv_ready, 1)
                for ec in range(DC):
                    last = nc.scalar.activation(keys_t[:, ec, :], ps[:, 1, ec * BK:(ec + 1) * BK], ACT.Identity,
                                                bias=bk[:, ec:ec + 1])
                last.then_inc(kv_stored, 1)
                act.wait_ge(fold_ready, 1)
                copy_bank(nc, fold_q[:, :, :].rearrange("p c k -> p (c k)"), ps[:, 3, 0:DC * BK]).then_inc(fold_stored, 1)
                copy_bank(nc, score_bias[:, :], ps[:, 4, 0:BK]).then_inc(fold_stored, 1)
                for j in range(PAIRS + 3):
                    if j < PAIRS:
                        act.wait_ge(centred, j + 1)
                        nc.scalar.activation(own(j), own(j), ACT.Exp).then_inc(exped, 1)
                    if 1 <= j <= PAIRS:
                        k = j - 1
                        act.wait_ge(probs_turned, k + 1)
                        if k >= 2:
                            act.wait_ge(out_ready, k - 1)
                        copy_bank(nc, pt[:, k % 2, :], ps[:, 4, 0:PAIR]).then_inc(probs_stored, 1)
                    if j >= 3:
                        norm_store(act, j - 3, [(core["xt"], None, None)])

            @block.vector
            def _(dve):
                dve.wait_ge(weights_in, weights_total)
                nc.vector.tensor_copy(bq_wide[:, :, :], bq[:, :].unsqueeze(2).to_broadcast([P, DC, P]))
                dve.wait_ge(kv_ready, 1)
                nc.vector.tensor_tensor(values[:, :], ps[:, 2, 0:D], bv[:, :], ALU.add).then_inc(values_made, 1)
                dve.wait_ge(fold_stored, 2)
                dve.wait_ge(zeroed, 1)
                for j in range(PAIRS + 3):
                    if 1 <= j <= PAIRS:
                        k = j - 1
                        dve.wait_ge(exped, k + 1)
                        nc.vector.tensor_reduce(sm[:, k % 2, :], own(k), AX_X, ALU.add)
                        dve.drain()
                        nc.vector.reciprocal(sm[:, k % 2, :], sm[:, k % 2, :])
                        dve.drain()
                        nc.vector.tensor_tensor(own(k), own(k), sm[:, k % 2, :].unsqueeze(2).to_broadcast([P, 2, KEYS]),
                                                ALU.mult).then_inc(probs_ready, 1)
                    if j < PAIRS:
                        b = j // (PAIRS // B)
                        dve.wait_ge(scores_ready, j + 1)
                        if j >= 2:
                            dve.wait_ge(probs_turned, j - 1)
                        nc.vector.tensor_tensor(
                            own(j), ps[:, j % 2, 0:2 * KEYS].rearrange("p (u k) -> p u k", u=2),
                            score_bias[:, b * KEYS:(b + 1) * KEYS].unsqueeze(1).to_broadcast([P, 2, KEYS]), ALU.add)
                        dve.drain()
                        nc.vector.tensor_reduce(mx[:, j % 2, :], own(j), AX_X, ALU.max)
                        dve.drain()
                        nc.vector.tensor_tensor(own(j), own(j), mx[:, j % 2, :].unsqueeze(2).to_broadcast([P, 2, KEYS]),
                                                ALU.subtract).then_inc(centred, 1)
                    if 2 <= j <= PAIRS + 1:
                        k = j - 2
                        dve.wait_ge(out_ready, k + 1)
                        x2 = pair_of(core["x"], k)
                        nc.vector.scalar_tensor_tensor(x2, ps[:, 5 + k % 2, :], gate, x2, ALU.mult,
                                                       ALU.add).then_inc(out_added, 1)
                        dve.drain()
                        norm_measure(dve, k, tiles_of(core["x"]))
                        norm_normalise(dve, k, tiles_of(core["x"]), tiles_of(core["xn"]))
        clear_semaphores()


def adapter_weights(a):
    R = 64

    def make(carve):
        base = carve([P, DC, D])
        base_row = carve([P, D])
        mu, sigma = carve([E, D]), carve([E, D])
        down_b, up_b, conv_b = carve([E, R]), carve([E, D]), carve([E, D])
        loads = [(base[:, :, :], a["L1_ffn_base_W"].rearrange("(c p) d -> p c d", p=P)),
                 (base_row[:, :], rows(a["L1_ffn_base_b"])), (mu[:, :], a["L1_ffn_disc_mu"]),
                 (sigma[:, :], a["L1_ffn_disc_sigma"]), (down_b[:, :], a["L1_ffn_down_b"]),
                 (up_b[:, :], a["L1_ffn_up_b"]), (conv_b[:, :], a["L1_ffn_conv_b"])]
        return loads, (base, base_row, mu, sigma, down_b, up_b, conv_b)
    return make


def stage_adapter(core, a, plan, following):
    nc, ps = core["nc"], core["ps"]
    gate = core["gate_ffn"][:, 1:2]
    R = 64
    with ExitStack() as ctx:
        _, weights_in, weights_total, (base, base_row, mu, sigma, down_b, up_b, conv_b) = plan

        def sb(part, shape, dtype=F32):
            return ctx.enter_context(nc.sbuf_tensor(f"l1f_{part}", shape, dtype))

        sem, clear_semaphores = named_semaphores(nc, "l1f")
        made = sem("made")
        inv_made, inv_turned, sums_made, squares_made = sem("inv_made"), sem("inv_turned"), sem("sums_made"), sem("squares_made")
        means_wide, losses_ready, chosen, hot_turned = sem("means_wide"), sem("losses_ready"), sem("chosen"), sem("hot_turned")
        hot_stored, gathered = sem("hot_stored"), sem("gathered")
        step_ready, step_stored = sem("step_ready"), sem("step_stored")
        const_made, bias_added = sem("const_made"), sem("bias_added")
        hid_ready, hid_stored, out_ready, out_added = sem("hid_ready"), sem("hid_stored"), sem("out_ready"), sem("out_added")
        norm_measure, norm_root, norm_normalise, norm_turn, norm_store, norm_stored = layer_norm(core, ctx, sem, "l1f_norm", on_vector=True)
        base_t = sb("base_t", [P, DC, D])
        inv = sb("inv", [E, 3, D])
        inv_t = sb("inv_t", [P, 3, DC, E])
        sums = sb("sums", [P, 2, DC, B])
        junk = sb("junk", [P, TOK])
        wide = sb("wide", [P, 3, DC, B, P])
        iota_e, iota_p = sb("iota_e", [P, E]), sb("iota_p", [P, 1])
        loss, cand, hot = sb("loss", [P, B, E]), sb("cand", [P, B, E]), sb("hot", [P, B, E])
        low, index = sb("low", [P, B]), sb("index", [P, B])
        where_f = sb("where_f", [P, 3, B])
        where = sb("where", [P, 3, B], I32)
        hot_t = sb("hot_t", [E, B, P])
        down = sb("down", [P, B, DC, P])
        conv, up = sb("conv", [P, B, DC, D]), sb("up", [R, B, D])
        conv_t, up_t = sb("conv_t", [P, B, DC, D]), sb("up_t", [P, B, DC, P])
        up_wide = sb("up_wide", [P, DC, B, P])
        down_col = sb("down_col", [P, B])
        fold = sb("fold", [P, B, D])
        const = sb("const", [P, B, D])
        ht = sb("ht", [P, 2, PAIR])
        down_rows = a["L1_ffn_down_W"].rearrange("e d r -> (e d) r")
        conv_rows = a["L1_ffn_conv_W"].rearrange("e o d -> (e o) d")
        up_rows = a["L1_ffn_up_W"].rearrange("e r d -> (e r) d")
        GATHERS = B * (2 * DC + 1)

        def turned(dst_part, src, ident_rows, cols):
            return lambda bank: nc.tensor.transpose(ps[0:cols, bank, dst_part:dst_part + ident_rows], src,
                                                    core["ident"][0:ident_rows, 0:ident_rows])

        def product(rows_n, c0, cols, parts):
            def go(bank):
                for n, (lhs, rhs) in enumerate(parts):
                    last = nc.tensor.matmul(ps[0:rows_n, bank, c0:c0 + cols], lhs, rhs, start=(n == 0),
                                            stop=(n == len(parts) - 1))
                return last
            return go

        steps = [([turned(dc * D + oc * P, base[:, oc, dc * P:(dc + 1) * P], P, P) for dc in range(DC) for oc in range(DC)],
                  P, 2 * D, base_t[:, :, :].rearrange("p c d -> p (c d)"))]
        for b in range(B):
            steps.append(([turned(dc * D + oc * P, conv[:, b, oc, dc * P:(dc + 1) * P], P, P)
                           for dc in range(DC) for oc in range(DC)], P, 2 * D,
                          conv_t[:, b].rearrange("p c d -> p (c d)")))
            for dc in range(DC):
                steps.append(([turned(0, up[:, b, dc * P:(dc + 1) * P], R, P)], P, R, up_t[:, b, dc, 0:R]))
        for dc in range(DC):
            steps.append(([product(P, 0, B * P, [(up_b[:, dc * P:(dc + 1) * P], hot_t[:, :, :].rearrange("e b n -> e (b n)"))])],
                          P, B * P, up_wide[:, dc].rearrange("p b n -> p (b n)")))
        steps.append(([product(R, 0, B * P, [(down_b[:, :], hot_t[:, :, :].rearrange("e b n -> e (b n)"))])], R, B * P, None))
        for b in range(B):
            steps.append(([product(P, 0, D, [(up_t[:, b, dc, :], conv_t[:, b, dc, :]) for dc in range(DC)])],
                          P, D, fold[:, b, :]))
            steps.append(([product(P, 0, D, [(up_wide[:, dc, b, :], conv_t[:, b, dc, :]) for dc in range(DC)]
                                   + [(hot_t[:, b, :], conv_b[:, :])])], P, D, const[:, b, :]))

        with nc.Block() as block:
            @block.sync
            def _(sp):
                fetch(sp, following)

            @block.gpsimd
            def _(pool):
                nc.gpsimd.memset(down[:, :, :, :], 0.0).then_inc(made, 1)
                nc.gpsimd.memset(up_t[:, :, :, :], 0.0).then_inc(made, 1)
                nc.gpsimd.memset(wide[:, 2], 1.0).then_inc(made, 1)
                nc.gpsimd.memset(down_col[:, :], 0.0).then_inc(made, 1)
                nc.gpsimd.iota(iota_e[:, :], [[1, E]], base=0, channel_multiplier=0,
                               allow_small_or_imprecise_dtypes=True).then_inc(made, 1)
                nc.gpsimd.iota(iota_p[:, :], [[0, 1]], base=0, channel_multiplier=1,
                               allow_small_or_imprecise_dtypes=True).then_inc(made, 1)
                pool.wait_ge(made, 6)
                pool.wait_ge(chosen, 2)

                def gather(dst, src, index, bound):
                    pool.indirect_dma_start(dst, None, src, bass.IndirectOffsetOnAxis(ap=index, axis=0),
                                            bounds_check=bound - 1, oob_is_err=False).then_inc(gathered, 16)

                for b in range(B):
                    for c in range(DC):
                        gather(conv[:, b, c, :], conv_rows, where[:, c, b:b + 1], E * D)
                        gather(down[:, b, c, 0:R], down_rows, where[:, c, b:b + 1], E * D)
                    gather(up[:, b, :], up_rows, where[0:R, 2, b:b + 1], E * R)
                pool.wait_ge(const_made, 1)
                for j in range(PAIRS):
                    for u in range(2):
                        i = 2 * j + u
                        last = nc.gpsimd.tensor_tensor(core["x"][:, i, :], core["x"][:, i, :], const[:, j // (PAIRS // B), :], ALU.add)
                    last.then_inc(bias_added, 1)

            @block.tensor
            def _(pe):
                pe.wait_ge(inv_made, 1)
                for k in range(3):
                    for dc in range(DC):
                        last = nc.tensor.transpose(ps[:, 2, (k * DC + dc) * E:(k * DC + dc + 1) * E],
                                                   inv[:, k, dc * P:(dc + 1) * P], core["ident"][0:E, 0:E])
                last.then_inc(inv_turned, 1)
                pe.wait_ge(means_wide, 2)
                for b in range(B):
                    for n in range(3 * DC):
                        k, dc = n // DC, n % DC
                        last = nc.tensor.matmul(ps[:, 3, b * E:(b + 1) * E], wide[:, k, dc, b, :], inv_t[:, k, dc, :],
                                                start=(n == 0), stop=(n == 3 * DC - 1))
                last.then_inc(losses_ready, 1)
                pe.wait_ge(chosen, 1)
                for b in range(B):
                    last = nc.tensor.transpose(ps[0:E, 2, b * P:(b + 1) * P], hot[:, b, :], core["ident"][:, :])
                last.then_inc(hot_turned, 1)
                pe.wait_ge(hot_stored, 1)
                for n, (emit, _, _, _) in enumerate(steps):
                    if n == 1:
                        pe.wait_ge(gathered, 16 * GATHERS)
                    if n >= 2:
                        pe.wait_ge(step_stored, n - 1)
                    if n >= 7 + DC + 1:
                        pe.wait_ge(step_stored, n if n == 7 + DC + 1 else n - 1)
                    for go in emit:
                        last = go(n % 2)
                    last.then_inc(step_ready, 1)
                pe.wait_ge(step_stored, len(steps))
                for j in range(PAIRS + 3):
                    if j < PAIRS:
                        b = j // (PAIRS // B)
                        if j >= 2:
                            pe.wait_ge(hid_stored, j - 1)
                        for dc in range(DC):
                            last = nc.tensor.matmul(ps[:, 2 + j % 2, 0:PAIR], down[:, b, dc, :],
                                                    core["xt"][:, dc, PAIR * j:PAIR * (j + 1)],
                                                    start=(dc == 0), stop=(dc == DC - 1))
                        last.then_inc(hid_ready, 1)
                    if 1 <= j <= PAIRS:
                        k = j - 1
                        pe.wait_ge(hid_stored, k + 1)
                        if k >= 2:
                            pe.wait_ge(out_added, k - 1)
                        for u in range(2):
                            i = 2 * k + u
                            out = ps[:, 4 + k % 2, u * D:(u + 1) * D]
                            for dc in range(DC):
                                nc.tensor.matmul(out, core["xt"][:, dc, i * P:(i + 1) * P], base_t[:, dc, :],
                                                 start=(dc == 0), stop=False)
                            last = nc.tensor.matmul(out, ht[:, k % 2, u * P:(u + 1) * P], fold[:, k // (PAIRS // B), :],
                                                    start=False, stop=True)
                        last.then_inc(out_ready, 1)
                    if j >= 3:
                        norm_turn(pe, j - 3, tiles_of(core["xn"]))

            @block.scalar
            def _(act):
                for dc in range(DC):
                    for b in range(B):
                        last = nc.scalar.activation(junk[:, :], core["xt"][:, dc, b * TOK:(b + 1) * TOK], ACT.Square,
                                                    accum_out=sums[:, 1, dc, b:b + 1])
                        act.drain()
                nc.scalar.activation(junk[:, 0:1], core["xt"][:, 0, 0:1], ACT.Copy).then_inc(squares_made, 1)
                act.wait_ge(inv_turned, 1)
                copy_bank(nc, inv_t[:, :, :, :].rearrange("p k c e -> p (k c e)"), ps[:, 2, 0:3 * DC * E]).then_inc(means_wide, 1)
                act.wait_ge(hot_turned, 1)
                copy_bank(nc, hot_t[:, :, :].rearrange("e b n -> e (b n)"), ps[0:E, 2, 0:B * P]).then_inc(hot_stored, 1)
                act.wait_ge(made, 6)
                for n, (_, rows_n, cols, dst) in enumerate(steps):
                    act.wait_ge(step_ready, n + 1)
                    if dst is None:
                        last = nc.scalar.activation(
                            down_col[0:R, :], ps[0:R, n % 2, 0:B * P].rearrange("p (b n) -> p b n", b=B)[:, :, 0], ACT.Copy)
                    else:
                        last = copy_bank(nc, dst, ps[0:rows_n, n % 2, 0:cols])
                    last.then_inc(step_stored, 1)
                for j in range(PAIRS + 3):
                    if j < PAIRS:
                        act.wait_ge(hid_ready, j + 1)
                        if j >= 2:
                            act.wait_ge(out_ready, j - 1)
                        nc.scalar.activation(ht[:, j % 2, :], ps[:, 2 + j % 2, 0:PAIR], ACT.Relu,
                                             bias=down_col[:, j // (PAIRS // B):j // (PAIRS // B) + 1]).then_inc(hid_stored, 1)
                    if j >= 3:
                        norm_store(act, j - 3, [(core["xt"], None, None)])

            @block.vector
            def _(dve):
                tt, ts = nc.vector.tensor_tensor, nc.vector.tensor_scalar
                dve.wait_ge(weights_in, weights_total)
                tt(sigma[:, :], sigma[:, :], sigma[:, :], ALU.mult)
                dve.drain()
                nc.vector.reciprocal(inv[:, 0, :], sigma[:, :])
                dve.drain()
                tt(inv[:, 1, :], mu[:, :], inv[:, 0, :], ALU.mult)
                dve.drain()
                tt(inv[:, 2, :], mu[:, :], inv[:, 1, :], ALU.mult)
                dve.drain()
                ts(inv[:, 1, :], inv[:, 1, :], -2.0, None, ALU.mult).then_inc(inv_made, 1)
                nc.vector.tensor_reduce(sums[:, 0].rearrange("p c b -> p (c b)"),
                                        core["xt"][:, :, :].rearrange("p c (b n) -> p (c b) n", b=B), AX_X, ALU.add)
                dve.drain()
                dve.wait_ge(squares_made, 1)
                dve.wait_ge(made, 6)
                for k in range(2):
                    last = ts(wide[:, k], sums[:, 1 - k].unsqueeze(3).to_broadcast([P, DC, B, P]), 1.0 / TOK, None, ALU.mult)
                last.then_inc(means_wide, 1)
                dve.wait_ge(losses_ready, 1)
                nc.vector.tensor_copy(loss[:, :, :].rearrange("p b e -> p (b e)"), ps[:, 3, 0:B * E])
                dve.drain()
                nc.vector.tensor_reduce(low[:, :], loss[:, :, :], AX_X, ALU.min)
                dve.drain()
                tt(cand[:, :, :], loss[:, :, :], low[:, :].unsqueeze(2).to_broadcast([P, B, E]), ALU.is_equal)
                dve.drain()
                nc.vector.scalar_tensor_tensor(cand[:, :, :], cand[:, :, :], -float(E),
                                               iota_e[:, :].unsqueeze(1).to_broadcast([P, B, E]), ALU.mult, ALU.add)
                dve.drain()
                nc.vector.tensor_reduce(low[:, :], cand[:, :, :], AX_X, ALU.min)
                dve.drain()
                tt(hot[:, :, :], cand[:, :, :], low[:, :].unsqueeze(2).to_broadcast([P, B, E]),
                   ALU.is_equal).then_inc(chosen, 1)
                ts(index[:, :], low[:, :], float(E), None, ALU.add)
                dve.drain()
                for k, (size, first_row) in enumerate(((D, 0), (D, P), (R, 0))):
                    ts(where_f[:, k, :], index[:, :], float(size), float(first_row), ALU.mult, ALU.add)
                dve.drain()
                ts(where_f[:, :, :].rearrange("p k b -> p (k b)"), where_f[:, :, :].rearrange("p k b -> p (k b)"),
                   iota_p[:, 0:1], None, ALU.add)
                dve.drain()
                nc.vector.tensor_copy(where[:, :, :], where_f[:, :, :]).then_inc(chosen, 1)
                dve.wait_ge(step_stored, len(steps))
                tt(const[:, :, :], const[:, :, :], base_row[:, :].unsqueeze(1).to_broadcast([P, B, D]), ALU.add)
                dve.drain()
                ts(const[:, :, :], const[:, :, :], gate, None, ALU.mult).then_inc(const_made, 1)
                for j in range(PAIRS + 3):
                    if 2 <= j <= PAIRS + 1:
                        k = j - 2
                        dve.wait_ge(out_ready, k + 1)
                        dve.wait_ge(bias_added, k + 1)
                        x2 = pair_of(core["x"], k)
                        nc.vector.scalar_tensor_tensor(x2, ps[:, 4 + k % 2, :], gate, x2, ALU.mult,
                                                       ALU.add).then_inc(out_added, 1)
                        dve.drain()
                        norm_measure(dve, k, tiles_of(core["x"]))
                        norm_normalise(dve, k, tiles_of(core["x"]), tiles_of(core["xn"]))
        clear_semaphores()


def layout_l2(a):
    def layout(carve):
        wq_t, wkv, won = carve([P, DC, D]), carve([P, 4, KD]), carve([P, DC, D])
        loads = [(wq_t[:, :, :], a["L2_xattn_Wq"].rearrange("(c p) d -> p c d", p=P)),
                 (wkv[:, :, :], a["L2_xattn_Wkv"].rearrange("(c p) k -> p c k", p=P)),
                 (won[:, :, :], a["L2_xattn_Wo"].rearrange("(c p) n -> p c n", p=P))]

        def finish(sb):
            wkv_t, wo = sb("wkv_t", [P, 2, D]), sb("wo", [P, DC, D])
            turns = [([wkv[:, c, :] for c in range(4)], wkv_t[:, :, :].rearrange("p a n -> p (a n)")),
                     ([won[:, oc, c * P:(c + 1) * P] for c in range(DC) for oc in range(DC)],
                      wo[:, :, :].rearrange("p c n -> p (c n)"))]
            return wq_t, wo, turns, wkv_t[:, 0, :], wkv_t[:, 1, :]
        return loads, finish
    return layout


def low_rank_weights(a):
    R = 64

    def make(carve):
        u1, v1 = carve([P, DC, P]), carve([P, FF])
        u2, v2 = carve([P, FC, P]), carve([P, D])
        b1, b2 = carve([P, FC]), carve([P, D])
        loads = [(u1[:, :, 0:R], a["L2_ffn_U1"].rearrange("(c p) r -> p c r", p=P)), (v1[0:R, :], a["L2_ffn_V1"]),
                 (u2[:, :, 0:R], a["L2_ffn_U2"].rearrange("(c p) r -> p c r", p=P)), (v2[0:R, :], a["L2_ffn_V2"]),
                 (b1[:, :], columns(a["L2_ffn_b1"])), (b2[:, :], rows(a["L2_ffn_b2"]))]
        return loads, (u1, v1, u2, v2, b1, b2)
    return make


def stage_low_rank(core, a, plan, following):
    nc, ps = core["nc"], core["ps"]
    gate = core["gate_ffn"][:, 2:3]
    R = 64
    with ExitStack() as ctx:
        _, weights_in, weights_total, (u1, v1, u2, v2, b1, b2) = plan

        def sb(part, shape):
            return ctx.enter_context(nc.sbuf_tensor(f"l2f_{part}", shape, F32))

        sem, clear_semaphores = named_semaphores(nc, "l2f")
        zeroed, bias_made, bias_added = sem("zeroed"), sem("bias_made"), sem("bias_added")
        p_ready, p_stored, hid_ready, hid_stored = sem("p_ready"), sem("p_stored"), sem("hid_ready"), sem("hid_stored")
        q_ready, q_stored, out_ready, out_added = sem("q_ready"), sem("q_stored"), sem("out_ready"), sem("out_added")
        norm_measure, norm_root, norm_normalise, norm_turn, norm_store, norm_stored = layer_norm(core, ctx, sem, "l2f_norm", on_vector=True)
        pr = sb("pr", [P, 2, PAIR])
        ht = sb("ht", [P, 2, FC, PAIR])
        qr = sb("qr", [P, 2, PAIR])
        with nc.Block() as block:
            @block.sync
            def _(sp):
                fetch(sp, following)

            @block.gpsimd
            def _(pool):
                for n, padding in enumerate((u1[:, :, R:P], v1[R:P, :], u2[:, :, R:P], v2[R:P, :])):
                    if n >= 1:
                        pool.wait_ge(zeroed, n)
                    nc.gpsimd.memset(padding, 0.0).then_inc(zeroed, 1)
                pool.wait_ge(zeroed, 4)
                pool.wait_ge(bias_made, 1)
                for j in range(PAIRS):
                    for u in range(2):
                        i = 2 * j + u
                        last = nc.gpsimd.tensor_tensor(core["x"][:, i, :], core["x"][:, i, :], b2[:, :], ALU.add)
                    last.then_inc(bias_added, 1)

            @block.tensor
            def _(pe):
                pe.wait_ge(weights_in, weights_total)
                pe.wait_ge(zeroed, 4)

                def first_rank(j):
                    if j >= 2:
                        pe.wait_ge(p_stored, j - 1)
                    for dc in range(DC):
                        last = nc.tensor.matmul(ps[:, 6 + j % 2, 0:PAIR], u1[:, dc, :], core["xt"][:, dc, PAIR * j:PAIR * (j + 1)],
                                                start=(dc == 0), stop=(dc == DC - 1))
                    last.then_inc(p_ready, 1)

                def second_rank(k):
                    pe.wait_ge(hid_stored, FC * (k + 1))
                    if k >= 1:
                        pe.wait_ge(q_stored, k)
                    for f in range(FC):
                        last = nc.tensor.matmul(ps[:, 4, 0:PAIR], u2[:, f, :], ht[:, k % 2, f, :], start=(f == 0),
                                                stop=(f == FC - 1))
                    last.then_inc(q_ready, 1)

                def output(k):
                    pe.wait_ge(q_stored, k + 1)
                    if k >= 1:
                        pe.wait_ge(out_added, k)
                    for u in range(2):
                        last = nc.tensor.matmul(ps[:, 5, u * D:(u + 1) * D], qr[:, k % 2, u * P:(u + 1) * P], v2[:, :],
                                                start=True, stop=True)
                    last.then_inc(out_ready, 1)

                first_rank(0)
                for j in range(PAIRS + 2):
                    if j + 1 < PAIRS:
                        first_rank(j + 1)
                    if j < PAIRS:
                        pe.wait_ge(p_stored, j + 1)
                        for f in range(FC):
                            n = FC * j + f
                            if n >= 4:
                                pe.wait_ge(hid_stored, n - 3)
                            nc.tensor.matmul(ps[:, n % 4, 0:PAIR], v1[:, f * P:(f + 1) * P], pr[:, j % 2, :],
                                             start=True, stop=True).then_inc(hid_ready, 1)
                    if 1 <= j <= PAIRS:
                        second_rank(j - 1)
                    if 2 <= j <= PAIRS + 1:
                        output(j - 2)

            @block.scalar
            def _(act):
                act.wait_ge(weights_in, weights_total)

                def store_p(j):
                    act.wait_ge(p_ready, j + 1)
                    if j >= 2:
                        act.wait_ge(hid_ready, FC * (j - 1))
                    copy_bank(nc, pr[:, j % 2, :], ps[:, 6 + j % 2, 0:PAIR]).then_inc(p_stored, 1)

                store_p(0)
                for j in range(PAIRS + 1):
                    if j + 1 < PAIRS:
                        store_p(j + 1)
                    if j < PAIRS:
                        for f in range(FC):
                            n = FC * j + f
                            act.wait_ge(hid_ready, n + 1)
                            if j >= 2 and f == 0:
                                act.wait_ge(q_ready, j - 1)
                            nc.scalar.activation(ht[:, j % 2, f, :], ps[:, n % 4, 0:PAIR], ACT.Gelu_apprx_tanh,
                                                 bias=b1[:, f:f + 1]).then_inc(hid_stored, 1)
                    if 1 <= j <= PAIRS:
                        k = j - 1
                        act.wait_ge(q_ready, k + 1)
                        if k >= 2:
                            act.wait_ge(out_ready, k - 1)
                        copy_bank(nc, qr[:, k % 2, :], ps[:, 4, 0:PAIR]).then_inc(q_stored, 1)

            @block.vector
            def _(dve):
                dve.wait_ge(weights_in, weights_total)
                nc.vector.tensor_scalar(b2[:, :], b2[:, :], gate, None, ALU.mult).then_inc(bias_made, 1)
                for j in range(PAIRS):
                    dve.wait_ge(out_ready, j + 1)
                    dve.wait_ge(bias_added, j + 1)
                    x2 = pair_of(core["x"], j)
                    nc.vector.scalar_tensor_tensor(x2, ps[:, 5, :], gate, x2, ALU.mult, ALU.add).then_inc(out_added, 1)
                    dve.drain()
                    norm_measure(dve, j, tiles_of(core["x"]))
                    norm_normalise(dve, j, tiles_of(core["x"]), tiles_of(core["xn"]))
        clear_semaphores()


L3_HEADS, L3_WIDTH = 16, 32
GROUP = P // L3_WIDTH
GROUPS = L3_HEADS // GROUP
ENTRIES = B * GROUPS
KC = TOK // P


def self_attention_scratch(nc):
    def dram(name, shape, dtype):
        return nc.dram_tensor(name, shape, dtype, kind="Internal").ap()

    parts = [[dram(f"l3_{kind}_part{m}", [ENTRIES + 1, P, TOK], BF16) for m in range(3)] for kind in ("q", "k")]
    values = dram("l3_values", [ENTRIES + 1, P, KC, P], F32)
    heads_out = dram("l3_heads_out", [ENTRIES, P, TOK], F32)
    return parts, values, heads_out


def self_project_weights(a):
    HD = L3_HEADS * L3_WIDTH

    def make(carve):
        wq, wk, wv = carve([P, DC, HD]), carve([P, DC, HD]), carve([P, DC, HD])
        ln1 = carve([P, 2, D])
        gb = carve([P, 4, DC])
        loads = [(ln1[:, 0, :], rows(a["L3_xattn_ln1_g"])), (ln1[:, 1, :], rows(a["L3_xattn_ln1_b"]))]
        loads += [(gb[:, k, :], columns(a["L3_xattn_a1_" + n])) for k, n in enumerate(("lnx_g", "lnx_b", "lny_g", "lny_b"))]
        loads += [(w[:, c, :].rearrange("p (h d) -> p h d", h=L3_HEADS),
                   a["L3_xattn_a1_" + n].rearrange("h (c p) d -> c p h d", p=P)[c])
                  for w, n in ((wq, "wq"), (wk, "wk"), (wv, "wv")) for c in range(DC)]
        return loads, (wq, wk, wv, ln1, gb)
    return make


def stage_self_project(core, a, x1, scratch, plan, following):
    nc, ps = core["nc"], core["ps"]
    q_k_parts, v_scratch, out_scratch = scratch
    HD = L3_HEADS * L3_WIDTH
    BANKS = HD // PAIR
    with ExitStack() as ctx:
        _, weights_in, weights_total, (wq, wk, wv, ln1, gb) = plan

        def sb(part, shape, dtype=F32):
            return ctx.enter_context(nc.sbuf_tensor(f"l3p_{part}", shape, dtype))

        sem, clear_semaphores = named_semaphores(nc, "l3p")
        qk_ready, high_made, rest_made = sem("qk_ready"), sem("high_made"), sem("rest_made")
        mid_made, low_made = sem("mid_made"), sem("low_made")
        v_ready, v_stored = sem("v_ready"), sem("v_stored")
        sent = [sem("sent0"), sem("sent1")]
        norm1_measure, norm1_root, norm1_normalise, norm1_turn, norm1_store, norm1_stored = layer_norm(core, ctx, sem, "l3p_norm1", on_vector=True)
        norm2_measure, norm2_root, norm2_normalise, norm2_turn, norm2_store, norm2_stored = layer_norm(core, ctx, sem, "l3p_norm2", on_vector=True)
        yt = sb("yt", [P, DC, T])
        parts = sb("parts", [P, 2, 3, 2 * BANKS, 512], BF16)
        rest = sb("rest", [P, 2 * BANKS, 512])
        vs = sb("vs", [P, 2, 2, HD])
        with nc.Block() as block:
            @block.sync
            def _(sp):
                total = [0, 0]
                for k in range(PAIRS):
                    b, p, at = k // (PAIRS // B), k % 2, (k % (PAIRS // B)) * PAIR
                    places = [(b * GROUPS, GROUPS)]
                    if b == 0:
                        places.append((ENTRIES, 1))
                    sp.wait_ge(low_made, 2 * BANKS * (k + 1))
                    for first_entry, groups in places:
                        for kind in range(2):
                            for m in range(3):
                                sp.dma_start(
                                    q_k_parts[kind][m][first_entry:first_entry + groups, :, at:at + PAIR].rearrange("g p n -> p g n"),
                                    parts[:, p, m, kind * BANKS:(kind + 1) * BANKS, :].rearrange(
                                        "p m (g n) -> p (m g) n", n=PAIR)[:, 0:groups, :]).then_inc(sent[p], 16)
                                total[p] += 16
                    sp.wait_ge(v_stored, 2 * (k + 1))
                    for first_entry, groups in places:
                        for u in range(2):
                            sp.dma_start(
                                v_scratch[first_entry:first_entry + groups, :, at // P + u, :].rearrange("g p n -> p g n"),
                                vs[:, p, u, 0:groups * P].rearrange("p (g n) -> p g n", n=P)).then_inc(sent[p], 16)
                            total[p] += 16
                for p in range(2):
                    sp.wait_ge(sent[p], total[p])

            def sent_before(k):
                return sum(16 * 8 * (2 if q < PAIRS // B else 1) for q in range(k % 2, k, 2))

            @block.tensor
            def _(pe):
                pe.wait_ge(weights_in, weights_total)
                for j in range(PAIRS + 1):
                    if j < PAIRS:
                        norm2_turn(pe, j, tiles_of(core["xn"]))
                    if j >= 1:
                        k = j - 1
                        pe.wait_ge(norm2_stored, k + 1)
                        for m in range(2 * BANKS):
                            w, src = (wq, core["xt"]) if m < BANKS else (wk, yt)
                            if k >= 1:
                                pe.wait_ge(rest_made, 2 * BANKS * (k - 1) + m + 1)
                            for h in range(2):
                                g = 2 * (m % BANKS) + h
                                for dc in range(DC):
                                    last = nc.tensor.matmul(ps[:, m, h * PAIR:(h + 1) * PAIR],
                                                            w[:, dc, g * P:(g + 1) * P],
                                                            src[:, dc, PAIR * k:PAIR * (k + 1)],
                                                            start=(dc == 0), stop=(dc == DC - 1))
                            last.then_inc(qk_ready, 1)
                        for u in range(2):
                            if k >= 1:
                                pe.wait_ge(v_stored, 2 * (k - 1) + u + 1)
                            for dc in range(DC):
                                last = nc.tensor.matmul(ps[:, 4 + u, :], yt[:, dc, (2 * k + u) * P:(2 * k + u + 1) * P],
                                                        wv[:, dc, :], start=(dc == 0), stop=(dc == DC - 1))
                            last.then_inc(v_ready, 1)

            @block.scalar
            def _(act):
                act.wait_ge(weights_in, weights_total)

                def high(k, m):
                    n = 2 * BANKS * k + m
                    act.wait_ge(qk_ready, n + 1)
                    if m == 0 and k >= 2:
                        act.wait_ge(sent[k % 2], sent_before(k))
                    nc.scalar.activation(parts[:, k % 2, 0, m, :], ps[:, m, :], ACT.Copy,
                                         scale=L3_WIDTH ** -0.5 if m < BANKS else 1.0).then_inc(high_made, 1)

                def mid(k, m):
                    act.wait_ge(rest_made, 2 * BANKS * k + m + 1)
                    copy_bank(nc, parts[:, k % 2, 1, m, :], rest[:, m, :]).then_inc(mid_made, 1)

                for j in range(PAIRS + 1):
                    if j < PAIRS:
                        norm2_store(act, j, [(core["xt"], gb[:, 0, :], gb[:, 1, :]), (yt, gb[:, 2, :], gb[:, 3, :])])
                    if j >= 1:
                        k = j - 1
                        high(k, 0)
                        for m in range(1, 2 * BANKS):
                            high(k, m)
                            mid(k, m - 1)
                        mid(k, 2 * BANKS - 1)
                        for u in range(2):
                            act.wait_ge(v_ready, 2 * k + u + 1)
                            copy_bank(nc, vs[:, k % 2, u, :], ps[:, 4 + u, :]).then_inc(v_stored, 1)

            @block.vector
            def _(dve):
                def remainder(k, m):
                    n = 2 * BANKS * k + m
                    dve.wait_ge(high_made, n + 1)
                    nc.vector.scalar_tensor_tensor(rest[:, m, :], ps[:, m, :], L3_WIDTH ** -0.5 if m < BANKS else 1.0,
                                                   parts[:, k % 2, 0, m, :], ALU.mult, ALU.subtract).then_inc(rest_made, 1)

                def low(k, m):
                    dve.wait_ge(mid_made, 2 * BANKS * k + m + 1)
                    nc.vector.tensor_tensor(parts[:, k % 2, 2, m, :], rest[:, m, :], parts[:, k % 2, 1, m, :],
                                            ALU.subtract).then_inc(low_made, 1)

                dve.wait_ge(weights_in, weights_total)
                def both_norms(j):
                    norm1_measure(dve, j, tiles_of(core["xn"]))
                    norm1_normalise(dve, j, tiles_of(core["xn"]), tiles_of(x1))
                    affine_rows(nc, dve, x1[:, 2 * j:2 * j + 2, :], ln1)
                    norm2_measure(dve, j, tiles_of(x1))
                    norm2_normalise(dve, j, tiles_of(x1), tiles_of(core["xn"]))

                both_norms(0)
                both_norms(1)
                for k in range(PAIRS):
                    if k + 2 < PAIRS:
                        both_norms(k + 2)
                    remainder(k, 0)
                    for m in range(1, 2 * BANKS):
                        remainder(k, m)
                        low(k, m - 1)
                    low(k, 2 * BANKS - 1)
        clear_semaphores()


def affine_rows(nc, dve, pair, gb):
    for k, op in enumerate((ALU.mult, ALU.add)):
        dve.drain()
        nc.vector.tensor_tensor(pair, pair, gb[:, k, :].unsqueeze(1).to_broadcast([P, 2, D]), op)
    dve.drain()


def stage_self_attention(core, scratch, following):
    nc, ps = core["nc"], core["ps"]
    q_k_parts, v_scratch, out_scratch = scratch
    R, W = GROUP, L3_WIDTH
    RING = 8
    TURN = 5
    STORE = TURN
    OUT = TURN + R + 1
    UNITS = KC * R
    SLOTS = (((0, 0, 1, 1), (0, 1, 0, 1)),
             ((0, 2, 1, 2), (2, 0, 2, 1)))
    LOADS = 2 * 2 * 4 + 1

    ORDER = [q // 2 if q % 2 == 0 else KC - 1 - q // 2 for q in range(KC)]

    def tile_of(v):
        return ORDER[v % UNITS // R]

    groups = []
    for u in range(UNITS):
        n = KC - tile_of(u)
        sizes = [n] if n <= 4 else [(n + 1) // 2, n // 2]
        for q, size in enumerate(sizes):
            groups.append((u, sum(sizes[:q]), size))
    BANKFULS = len(groups)
    assert BANKFULS % 2 == 0

    def groups_through(u):
        return sum(1 for g in groups if g[0] <= u)

    with ExitStack() as ctx:
        def sb(part, shape, dtype=F32):
            return ctx.enter_context(nc.sbuf_tensor(f"l3s_{part}", shape, dtype))

        outer, clear_outer = named_semaphores(nc, "l3s_outer")
        loaded = [outer("loaded0"), outer("loaded1")]
        stack = [[[sb(f"stack{p}{kind}{s}", [P, R, TOK], BF16) for s in range(2)] for kind in range(2)] for p in range(2)]
        values = sb("values", [P, 2, KC, P])
        pt = sb("pt", [P, 2, R, KC, P])
        heads_out = core["areas"][1][:, 0:2 * TOK].rearrange("p (a n) -> p a n", a=2)
        mx, sm = sb("mx", [P, RING]), sb("sm", [P, RING])
        ex = ([core["xn"][:, 4 * n:4 * n + 4, :].rearrange("p a d -> p (a d)") for n in range(4)]
              + [core["xt"][:, n // 2, TOK * (n % 2):TOK * (n % 2 + 1)] for n in range(4)])

        def load(sp, entry, p):
            for kind in range(2):
                for s in range(2):
                    for m in range(4):
                        src = q_k_parts[kind][SLOTS[s][kind][m]][bass.ds(entry, 1)]
                        sp.dma_start(stack[p][kind][s][m * W:(m + 1) * W, :, :],
                                     src.rearrange("a (r d) n -> d (a r) n", d=W)).then_inc(loaded[p], 16)
            sp.dma_start(values[:, p], v_scratch[bass.ds(entry, 1)].rearrange("a p c n -> p (a c) n")).then_inc(loaded[p], 16)

        load(nc.sync, 0, 0)
        fetch(nc.sync, following)
        with nc.Fori(0, ENTRIES // 2) as jj:
            sem, clear_semaphores = named_semaphores(nc, "l3s")
            scores_ready, measured, exped, inverted = sem("scores_ready"), sem("measured"), sem("exped"), sem("inverted")
            masked, turned, stored = sem("masked"), sem("turned"), [sem("stored0"), sem("stored1")]
            out_ready, out_stored = sem("out_ready"), sem("out_stored")
            out_sent = sem("out_sent")

            with nc.Block() as block:
                @block.sync
                def _(sp):
                    load(sp, 2 * jj + 1, 1)
                    sp.wait_ge(out_ready, KC)
                    load(sp, 2 * jj + 2, 0)
                    for p in range(2):
                        sp.wait_ge(out_stored, KC * (p + 1))
                        sp.dma_start(out_scratch[bass.ds(2 * jj + p, 1)].rearrange("a p n -> p (a n)"),
                                     heads_out[:, p, :]).then_inc(out_sent, 16)
                    sp.wait_ge(out_sent, 32)

                @block.gpsimd
                def _(pool):
                    for v in range(2 * UNITS):
                        si = tile_of(v)
                        pool.wait_ge(inverted, v + 1)
                        nc.gpsimd.tensor_tensor(ex[v % RING][:, si * P:], ex[v % RING][:, si * P:],
                                                sm[:, v % RING:v % RING + 1].to_broadcast([P, TOK - si * P]), ALU.mult)
                        pool.drain()
                        nc.gpsimd.affine_select(out=ex[v % RING][:, si * P:(si + 1) * P], in_=ex[v % RING][:, si * P:(si + 1) * P],
                                                compare_op=ALU.is_gt, fill=0.0, base=0, pattern=[[1, P]],
                                                channel_multiplier=-1).then_inc(masked, 1)

                @block.tensor
                def _(pe):
                    def ends_at(si):
                        return max(range(si, KC), key=lambda c: ((c - si) % R, c))

                    def scores(v):
                        p, si, r = v // UNITS, tile_of(v), v % R
                        if v >= 2:
                            pe.wait_ge(exped, v - 1)
                        for h in range(2):
                            for s in range(2):
                                last = nc.tensor.matmul(ps[:, 2 * (v % 2) + h, :],
                                                        stack[p][0][s][:, r, si * P:(si + 1) * P],
                                                        stack[p][1][s][:, r, h * 512:(h + 1) * 512],
                                                        start=(s == 0), stop=(s == 1))
                        last.then_inc(scores_ready, 1)

                    def turn(v):
                        p, si = v // UNITS, tile_of(v)
                        pe.wait_ge(masked, v + 1)
                        for g, (u, c0, size) in enumerate(groups):
                            if u != v % UNITS:
                                continue
                            n = BANKFULS * p + g
                            if n >= 2:
                                pe.wait_ge(stored[n % 2], n // 2)
                            for c in range(size):
                                last = nc.tensor.transpose(ps[:, 4 + n % 2, c * P:(c + 1) * P],
                                                           ex[v % RING][:, (si + c0 + c) * P:(si + c0 + c + 1) * P],
                                                           core["ident"][:, :])
                            last.then_inc(turned, 1)

                    def output(w, q):
                        p, si = w // KC, ORDER[w % KC]
                        chunks = [c for c in range(si, KC) if (c - si) % R == q]
                        if q == 0:
                            n = BANKFULS * p + groups_through(w % KC * R + R - 1)
                            pe.wait_ge(stored[0], (n + 1) // 2)
                            pe.wait_ge(stored[1], n // 2)
                            if w >= 2:
                                pe.wait_ge(out_stored, w - 1)
                        for c in chunks:
                            for r in range(R):
                                last = nc.tensor.matmul(ps[r * W:(r + 1) * W, 6 + w % 2, 0:P],
                                                        values[:, p, c, r * W:(r + 1) * W],
                                                        pt[:, w % 2, r, c - si, :], start=(c == si),
                                                        stop=(c == ends_at(si)))
                        if chunks and chunks[-1] == ends_at(si):
                            last.then_inc(out_ready, 1)

                    for v in range(2 * UNITS + OUT):
                        if v == 0:
                            pe.wait_ge(loaded[0], 16 * LOADS * jj + 16 * LOADS)
                        if v == UNITS:
                            pe.wait_ge(loaded[1], 16 * LOADS * jj + 16 * LOADS)
                        if v < 2 * UNITS:
                            scores(v)
                        if TURN <= v < 2 * UNITS + TURN:
                            turn(v - TURN)
                        if v >= OUT:
                            output((v - OUT) // R, (v - OUT) % R)

                def store_turned(eng, op, v, side):
                    if v >= 2 * UNITS:
                        return
                    p, w = v // UNITS, v // R
                    for g, (u, c0, size) in enumerate(groups):
                        n = BANKFULS * p + g
                        if u != v % UNITS or n % 2 != side:
                            continue
                        eng.wait_ge(turned, n + 1)
                        if w >= 2:
                            eng.wait_ge(out_ready, w - 1)
                        dst = pt[:, w % 2, v % R, c0:c0 + size, :].rearrange("p c n -> p (c n)")
                        src = ps[:, 4 + side, 0:size * P]
                        if side == 0:
                            last = op.activation(dst, src, ACT.Copy)
                        else:
                            last = op.tensor_copy(dst, src)
                        last.then_inc(stored[side], 1)

                @block.scalar
                def _(act):
                    for v in range(2 * UNITS + OUT):
                        if v >= STORE:
                            store_turned(act, nc.scalar, v - STORE, 0)
                        if v < 2 * UNITS:
                            act.wait_ge(measured, v + 1)
                            if v >= RING:
                                act.wait_ge(turned, BANKFULS * ((v - RING) // UNITS) + groups_through((v - RING) % UNITS))
                            nc.scalar.activation(ex[v % RING][:, :], ps[:, 2 * (v % 2):2 * (v % 2) + 2, :].rearrange("p a n -> p (a n)"),
                                                 ACT.Exp, bias=mx[:, v % RING:v % RING + 1],
                                                 accum_out=sm[:, v % RING:v % RING + 1]).then_inc(exped, 1)
                        if v >= OUT and (v - OUT) % R == R - 1:
                            w = (v - OUT) // R
                            act.wait_ge(out_ready, w + 1)
                            si = ORDER[w % KC]
                            copy_bank(nc, heads_out[:, w // KC, si * P:(si + 1) * P],
                                      ps[:, 6 + w % 2, 0:P]).then_inc(out_stored, 1)

                @block.vector
                def _(dve):
                    for v in range(2 * UNITS + OUT):
                        if v < 2 * UNITS:
                            dve.wait_ge(scores_ready, v + 1)
                            nc.vector.tensor_reduce(mx[:, v % RING:v % RING + 1],
                                                    ps[:, 2 * (v % 2):2 * (v % 2) + 2, :].rearrange("p a n -> p (a n)"),
                                                    AX_X, ALU.max, negate=True).then_inc(measured, 1)
                        if v >= STORE:
                            store_turned(dve, nc.vector, v - STORE, 1)
                        if 1 <= v <= 2 * UNITS:
                            dve.wait_ge(exped, v)
                            nc.vector.reciprocal(sm[:, (v - 1) % RING:(v - 1) % RING + 1],
                                                 sm[:, (v - 1) % RING:(v - 1) % RING + 1]).then_inc(inverted, 1)
            clear_semaphores()
        nc.sync.wait_ge(loaded[0], 16 * LOADS * (ENTRIES // 2 + 1))
        nc.all_engine_barrier()
        clear_outer()


def self_out_weights(a):
    def make(carve):
        w = carve([P, GROUPS, D])
        bias_row = carve([P, D])
        gb = carve([P, 2, DC])
        loads = [(w[:, :, :], a["L3_xattn_a1_li1_w"].rearrange("(g p) n -> p g n", p=P)),
                 (bias_row[:, :], rows(a["L3_xattn_a1_li1_b"])),
                 (gb[:, 0, :], columns(a["L3_xattn_a1_ln3_g"])), (gb[:, 1, :], columns(a["L3_xattn_a1_ln3_b"]))]
        return loads, (w, bias_row, gb)
    return make


def stage_self_out(core, a, x1, xo, scratch, plan, following):
    nc, ps = core["nc"], core["ps"]
    q_k_parts, v_scratch, out_scratch = scratch
    G = GROUPS
    with ExitStack() as ctx:
        _, weights_in, weights_total, (w, bias_row, gb) = plan

        def sb(part, shape):
            return ctx.enter_context(nc.sbuf_tensor(f"l3o_{part}", shape, F32))

        sem, clear_semaphores = named_semaphores(nc, "l3o")
        bias_added, out_ready, out_added = sem("bias_added"), sem("out_ready"), sem("out_added")
        heads_in = [sem(f"heads_in{j}") for j in range(PAIRS)]
        norm_measure, norm_root, norm_normalise, norm_turn, norm_store, norm_stored = layer_norm(core, ctx, sem, "l3o_norm", on_vector=True)
        heads = sb("heads", [P, 4, G, PAIR])
        def xo_tile(i):
            return xo[:, i, :]

        with nc.Block() as block:
            @block.sync
            def _(sp):
                for j in range(PAIRS):
                    b, at = j // (PAIRS // B), (j % (PAIRS // B)) * PAIR
                    if j >= 4:
                        sp.wait_ge(out_ready, j - 3)
                    sp.dma_start(heads[:, j % 4], out_scratch[b * G:(b + 1) * G, :, at:at + PAIR].rearrange("g p n -> p g n")
                                 ).then_inc(heads_in[j], 16)
                    if j == 3:
                        fetch(sp, following)

            @block.gpsimd
            def _(pool):
                pool.wait_ge(weights_in, weights_total)
                for j in range(PAIRS):
                    for u in range(2):
                        last = nc.gpsimd.tensor_tensor(xo_tile(2 * j + u), x1[:, 2 * j + u, :], bias_row[:, :], ALU.add)
                    last.then_inc(bias_added, 1)

            @block.tensor
            def _(pe):
                pe.wait_ge(weights_in, weights_total)
                for j in range(PAIRS + 2):
                    if j < PAIRS:
                        pe.wait_ge(heads_in[j], 16)
                        if j >= 2:
                            pe.wait_ge(out_added, j - 1)
                        for u in range(2):
                            for g in range(G):
                                last = nc.tensor.matmul(ps[:, j % 2, u * D:(u + 1) * D], heads[:, j % 4, g, u * P:(u + 1) * P],
                                                        w[:, g, :], start=(g == 0), stop=(g == G - 1))
                        last.then_inc(out_ready, 1)
                    if j >= 2:
                        norm_turn(pe, j - 2, tiles_of(core["xn"]))

            @block.scalar
            def _(act):
                act.wait_ge(weights_in, weights_total)
                for j in range(PAIRS):
                    norm_store(act, j, [(core["xt"], gb[:, 0, :], gb[:, 1, :])])

            @block.vector
            def _(dve):
                for j in range(PAIRS):
                    dve.wait_ge(out_ready, j + 1)
                    dve.wait_ge(bias_added, j + 1)
                    x2 = pair_of(xo, j)
                    nc.vector.tensor_tensor(x2, ps[:, j % 2, :], x2, ALU.add).then_inc(out_added, 1)
                    dve.drain()
                    norm_measure(dve, j, xo_tile)
                    norm_normalise(dve, j, xo_tile, tiles_of(core["xn"]))
        clear_semaphores()


def mlp_weights(a, pfx, second):
    def make(carve):
        w2, b2 = carve([P, DC, FF]), carve([P, FC])
        w3, b3 = carve([P, FC, D]), carve([P, D])
        gb, ln2 = carve([P, 2, DC]), None
        loads = [(w2[:, :, :], a[pfx + "li2_w"].rearrange("(c p) n -> p c n", p=P)), (b2[:, :], columns(a[pfx + "li2_b"])),
                 (w3[:, :, :], a[pfx + "li3_w"].rearrange("(c p) n -> p c n", p=P)), (b3[:, :], rows(a[pfx + "li3_b"]))]
        if second:
            loads += [(gb[:, k, :], columns(a["L3_ffn_" + n])) for k, n in enumerate(("ln_gamma", "ln_beta"))]
        else:
            ln2 = carve([P, 2, D])
            loads += [(gb[:, k, :], columns(a["L3_xattn_a2_lnx_" + n])) for k, n in enumerate("gb")]
            loads += [(ln2[:, k, :], rows(a["L3_xattn_ln2_" + n])) for k, n in enumerate("gb")]
        return loads, (w2, b2, w3, b3, gb, ln2)
    return make


def stage_mlp(core, x1, xo, second, plan, following):
    nc, ps = core["nc"], core["ps"]
    name = "l3m2" if second else "l3m1"
    gate = core["gate_attn"][:, 3:4]
    with ExitStack() as ctx:
        _, weights_in, weights_total, (w2, b2, w3, b3, gb, ln2) = plan

        def sb(part, shape):
            return ctx.enter_context(nc.sbuf_tensor(f"{name}_{part}", shape, F32))

        sem, clear_semaphores = named_semaphores(nc, name)
        summed, hid_ready, hid_stored = sem("summed"), sem("hid_ready"), sem("hid_stored")
        out_ready, out_added = sem("out_ready"), sem("out_added")
        norm1_measure, norm1_root, norm1_normalise, norm1_turn, norm1_store, norm1_stored = layer_norm(core, ctx, sem, name + "_norm1", on_vector=True)
        norm2_measure, norm2_root, norm2_normalise, norm2_turn, norm2_store, norm2_stored = layer_norm(core, ctx, sem, name + "_norm2", on_vector=True)
        ht = sb("ht", [P, 2, FC, PAIR])

        def x1_tile(i):
            return x1[:, i, :]

        whole, middle = (tiles_of(core["x"]), tiles_of(core["xn"])) if second else (x1_tile, x1_tile)

        with nc.Block() as block:
            @block.sync
            def _(sp):
                fetch(sp, following)

            @block.gpsimd
            def _(pool):
                pool.wait_ge(weights_in, weights_total)
                for j in range(PAIRS):
                    for u in range(2):
                        i = 2 * j + u
                        nc.gpsimd.tensor_tensor(xo[:, i, :], xo[:, i, :], x1[:, i, :], ALU.add)
                    pool.drain()
                    for u in range(2):
                        i = 2 * j + u
                        last = nc.gpsimd.tensor_tensor(xo[:, i, :], xo[:, i, :], b3[:, :], ALU.add)
                    last.then_inc(summed, 1)

            @block.tensor
            def _(pe):
                pe.wait_ge(weights_in, weights_total)
                for j in range(PAIRS + 3):
                    if j < PAIRS:
                        for f in range(FC):
                            n = FC * j + f
                            if n >= 4:
                                pe.wait_ge(hid_stored, n - 3)
                            for dc in range(DC):
                                last = nc.tensor.matmul(ps[:, n % 4, 0:PAIR], w2[:, dc, f * P:(f + 1) * P],
                                                        core["xt"][:, dc, PAIR * j:PAIR * (j + 1)],
                                                        start=(dc == 0), stop=(dc == DC - 1))
                            last.then_inc(hid_ready, 1)
                    if j >= 3:
                        norm2_turn(pe, j - 3, tiles_of(core["xn"]))
                    if 1 <= j <= PAIRS:
                        k = j - 1
                        pe.wait_ge(hid_stored, FC * (k + 1))
                        if k >= 2:
                            pe.wait_ge(out_added, k - 1)
                        for u in range(2):
                            for f in range(FC):
                                last = nc.tensor.matmul(ps[:, 4 + k % 2, u * D:(u + 1) * D], ht[:, k % 2, f, u * P:(u + 1) * P],
                                                        w3[:, f, :], start=(f == 0), stop=(f == FC - 1))
                        last.then_inc(out_ready, 1)

            @block.scalar
            def _(act):
                act.wait_ge(weights_in, weights_total)
                for j in range(PAIRS + 3):
                    if j < PAIRS:
                        for f in range(FC):
                            n = FC * j + f
                            act.wait_ge(hid_ready, n + 1)
                            if f == 0 and j >= 2:
                                act.wait_ge(out_ready, j - 1)
                            nc.scalar.activation(ht[:, j % 2, f, :], ps[:, n % 4, 0:PAIR], ACT.Gelu,
                                                 bias=b2[:, f:f + 1]).then_inc(hid_stored, 1)
                    if j >= 3:
                        norm2_store(act, j - 3, [(core["xt"], gb[:, 0, :], gb[:, 1, :])])

            @block.vector
            def _(dve):
                dve.wait_ge(weights_in, weights_total)
                for j in range(PAIRS):
                    dve.wait_ge(out_ready, j + 1)
                    dve.wait_ge(summed, j + 1)
                    xo2 = pair_of(xo, j)
                    if second:
                        nc.vector.tensor_tensor(xo2, ps[:, 4 + j % 2, :], xo2, ALU.add).then_inc(out_added, 1)
                        dve.drain()
                        x2 = pair_of(core["x"], j)
                        nc.vector.scalar_tensor_tensor(x2, xo2, gate, x2, ALU.mult, ALU.add)
                    else:
                        nc.vector.tensor_tensor(pair_of(x1, j), ps[:, 4 + j % 2, :], xo2, ALU.add).then_inc(out_added, 1)
                    dve.drain()
                    norm1_measure(dve, j, whole)
                    norm1_normalise(dve, j, whole, middle)
                    if second:
                        dve.drain()
                    else:
                        affine_rows(nc, dve, x1[:, 2 * j:2 * j + 2, :], ln2)
                    norm2_measure(dve, j, middle)
                    norm2_normalise(dve, j, middle, tiles_of(core["xn"]))
        clear_semaphores()


def layout_l3(a):
    def layout(carve):
        HD = L3_HEADS * L3_WIDTH
        wq, wk, wv, wo = carve([P, DC, HD]), carve([P, HD]), carve([P, HD]), carve([P, HD // P, D])
        by_head = [(wk[:, :], a["L3_xattn_a2_wk"]), (wv[:, :], a["L3_xattn_a2_wv"])]
        by_head += [(wq[:, c, :], a["L3_xattn_a2_wq"][:, c * P:(c + 1) * P, :]) for c in range(DC)]
        loads = [(dst.rearrange("p (h d) -> p h d", h=L3_HEADS), src.rearrange("h p d -> p h d")) for dst, src in by_head]
        loads += [(wo[:, :, :], a["L3_xattn_a2_li1_w"].rearrange("(c p) n -> p c n", p=P))]

        def finish(sb):
            wq_t = sb("wq_t", [P, HD // P, D])
            turns = [([wq[:, dc, c * P:(c + 1) * P] for c in (2 * q, 2 * q + 1) for dc in range(DC)],
                      wq_t[:, 2 * q:2 * q + 2, :].rearrange("p c d -> p (c d)")) for q in range(2)]
            return wq_t, wo, turns, wk, wv
        return loads, finish
    return layout


def layer_3(core, a, plans):
    nc = core["nc"]
    scratch = self_attention_scratch(nc)
    with ExitStack() as ctx:
        x1 = ctx.enter_context(nc.sbuf_tensor("l3_x1", [P, TILES, D], F32))
        stage_self_project(core, a, x1, scratch, plans["l3p"], None)
        stage_self_attention(core, scratch, plans["l3o"])
        xo = ctx.enter_context(nc.sbuf_tensor("l3_xo", [P, TILES, D], F32))
        stage_self_out(core, a, x1, xo, scratch, plans["l3o"], plans["l3m1"])
        stage_mlp(core, x1, xo, False, plans["l3m1"], plans["l3a"])
        stage_attention(core, a, "l3a", 32, 32 ** -0.5, plans["l3a"], plans["l3m2"], tiles_of(x1), tiles_of(xo),
                        None, True, True, core["ctx_norm_t"])
        stage_mlp(core, x1, xo, True, plans["l3m2"], plans["l3f"])
    stage_experts(core, a, "l3f", top=2, rows_tiles=TOP2_TILES, capacity=None, plan=plans["l3f"], following=None,
                  w1="L3_ffn_gate_up_w", w2="L3_ffn_down_w", swiglu=True, gate=core["gate_ffn"][:, 3:4],
                  norm_behind=False)


def build_program(nc, a, out):
    a = dict(a, out=out)
    with ExitStack() as ctx:
        ctx.enter_context(nc.allow_non_contiguous_dma(reason="vectors of up to 1024 values, one per partition"))
        core = make_core(nc, ctx)
        makes = {
            "l0f": experts_weights(a, "L0_ffn_Wr"),
            "l1a": one_head_weights(a),
            "l1f": adapter_weights(a),
            "l2a": attention_weights(a, layout_l2(a), None, None),
            "l2f": low_rank_weights(a),
            "l3p": self_project_weights(a),
            "l3o": self_out_weights(a),
            "l3m1": mlp_weights(a, "L3_xattn_a1_", False),
            "l3a": attention_weights(a, layout_l3(a), "L3_xattn_a2_li1_b", ("L3_xattn_a2_ln3_g", "L3_xattn_a2_ln3_b")),
            "l3m2": mlp_weights(a, "L3_xattn_a2_", True),
            "l3f": experts_weights(a, "L3_ffn_router_w", ("L3_ffn_ln_gamma", "L3_ffn_ln_beta"),
                                   ("L3_ffn_shared_gate_up_w", "L3_ffn_shared_down_w")),
        }
        plans = {name: plan_weights(core, n % 2, name, make) for n, (name, make) in enumerate(makes.items())}
        with ExitStack() as first_ctx:
            def carve(shape):
                return first_ctx.enter_context(nc.sbuf_tensor(f"l0a_weights{nc.next_id()}", shape, F32))

            loads, needed = attention_weights(a, layout_l0(a), "L0_xattn_bo", None)(carve)
            plan = (loads, nc.alloc_semaphore("l0a_weights_in"), 16 * len(loads), needed)
            stage_attention(core, a, "l0a", 64, 64 ** -0.5, plan, plans["l0f"], tiles_of(core["x"]), tiles_of(core["x"]),
                            core["gate_attn"][:, 0:1], True, None, core["ctx_t"], opens=True)
        stage_experts(core, a, "l0f", top=1, rows_tiles=E, capacity=T // E, plan=plans["l0f"], following=plans["l1a"],
                      w1="L0_ffn_W1", w2="L0_ffn_W2", swiglu=False, gate=core["gate_ffn"][:, 0:1])
        stage_one_head(core, a, plans["l1a"], plans["l1f"])
        stage_adapter(core, a, plans["l1f"], plans["l2a"])
        stage_attention(core, a, "l2a", 16, 16 ** -0.5, plans["l2a"], plans["l2f"], tiles_of(core["x"]), tiles_of(core["x"]),
                        core["gate_attn"][:, 2:3], None, None, core["ctx_t"])
        stage_low_rank(core, a, plans["l2f"], plans["l3p"])
        layer_3(core, a, plans)


_INS = ['x', 'ctx_512', 'g_xattn', 'g_ffn', 'L0_xattn_Wq', 'L0_xattn_Wk', 'L0_xattn_Wv', 'L0_xattn_Wo', 'L0_xattn_bo',
        'L0_ffn_Wr', 'L0_ffn_W1', 'L0_ffn_W2', 'L1_xattn_Wq', 'L1_xattn_bq', 'L1_xattn_Wk', 'L1_xattn_bk',
        'L1_xattn_Wv', 'L1_xattn_bv', 'L1_ffn_base_W', 'L1_ffn_base_b', 'L1_ffn_disc_mu', 'L1_ffn_disc_sigma',
        'L1_ffn_down_W', 'L1_ffn_down_b', 'L1_ffn_up_W', 'L1_ffn_up_b', 'L1_ffn_conv_W', 'L1_ffn_conv_b',
        'L2_xattn_Wq', 'L2_xattn_Wkv', 'L2_xattn_Wo', 'L2_ffn_U1', 'L2_ffn_V1', 'L2_ffn_b1', 'L2_ffn_U2', 'L2_ffn_V2',
        'L2_ffn_b2', 'L3_xattn_ln1_g', 'L3_xattn_ln1_b', 'L3_xattn_ln2_g', 'L3_xattn_ln2_b', 'L3_xattn_a1_wq',
        'L3_xattn_a1_wk', 'L3_xattn_a1_wv', 'L3_xattn_a1_li1_w', 'L3_xattn_a1_li1_b', 'L3_xattn_a1_lnx_g',
        'L3_xattn_a1_lnx_b', 'L3_xattn_a1_lny_g', 'L3_xattn_a1_lny_b', 'L3_xattn_a1_ln3_g', 'L3_xattn_a1_ln3_b',
        'L3_xattn_a1_li2_w', 'L3_xattn_a1_li2_b', 'L3_xattn_a1_li3_w', 'L3_xattn_a1_li3_b', 'L3_xattn_a2_wq',
        'L3_xattn_a2_wk', 'L3_xattn_a2_wv', 'L3_xattn_a2_li1_w', 'L3_xattn_a2_li1_b', 'L3_xattn_a2_lnx_g',
        'L3_xattn_a2_lnx_b', 'L3_xattn_a2_lny_g', 'L3_xattn_a2_lny_b', 'L3_xattn_a2_ln3_g', 'L3_xattn_a2_ln3_b',
        'L3_xattn_a2_li2_w', 'L3_xattn_a2_li2_b', 'L3_xattn_a2_li3_w', 'L3_xattn_a2_li3_b', 'L3_ffn_ln_gamma',
        'L3_ffn_ln_beta', 'L3_ffn_router_w', 'L3_ffn_gate_up_w', 'L3_ffn_down_w', 'L3_ffn_shared_gate_up_w',
        'L3_ffn_shared_down_w']


def kernel(**inputs):
    import numpy as _np
    import concourse.bacc as _bacc
    from concourse import mybir as _mybir
    from concourse.bass_utils import run_bass_kernel_spmd as _run

    nc = _bacc.Bacc("TRN2", target_bir_lowering=False, num_devices=1)
    arrays, args = {}, {}
    for name in _INS:
        array = _np.ascontiguousarray(inputs[name])
        arrays[f"in_{name}_dram"] = array
        args[name] = nc.dram_tensor(f"in_{name}_dram", array.shape, _mybir.dt.from_np(array.dtype),
                                    kind="ExternalInput").ap()
    out = nc.dram_tensor("out_0_dram", (B, TOK, D), _mybir.dt.float32, kind="ExternalOutput").ap()
    build_program(nc, args, out)
    r = _run(nc, [arrays], core_ids=[0])
    return r.results[0]["out_0_dram"]
```

```python
from contextlib import ExitStack

import concourse.bass as bass
from concourse import mybir

F32 = mybir.dt.float32
I32 = mybir.dt.int32
BF16 = mybir.dt.bfloat16
ALU = mybir.AluOpType
ACT = mybir.ActivationFunctionType
AX_X = mybir.AxisListType.X

P = 128
D = 256
DC = D // P
B = 2
T = 2048
TILES = T // P
PAIRS = TILES // 2
TOK = T // B
KEYS = 64
KD = 128
FF = 1024
FC = FF // P
E = 8
PAIR = 2 * P
TOP2_FULL = 2 * T // PAIR - 1
TOP2_HALF = (2 * T + (P - 1) * E) // P - 2 * TOP2_FULL
EPS = 1e-5
AREA_WORDS = (3400, 4900)
NEWTON_SEED = float(0x5F3759DF)


def named_semaphores(nc, stage):
    taken = []

    def sem(name):
        taken.append(nc.alloc_semaphore(f"{stage}_{name}"))
        return taken[-1]

    def clear_semaphores():
        nc.clear_and_free_semaphores(taken)
        nc.all_engine_barrier()

    return sem, clear_semaphores


def make_core(nc, ctx):
    def sb(name, shape, dtype=F32):
        return ctx.enter_context(nc.sbuf_tensor(name, shape, dtype))

    return {
        "nc": nc,
        "x": sb("x_tokens", [P, TILES, D]),
        "xt": sb("x_features", [P, DC, T]),
        "xn": sb("xn_tokens", [P, TILES, D]),
        "ident": sb("ident", [P, P]),
        "gate_attn": sb("gate_attn", [P, 4]),
        "gate_ffn": sb("gate_ffn", [P, 4]),
        "ctx_t": sb("ctx_t", [P, B * KEYS]),
        "ctx_norm_t": sb("ctx_norm_t", [P, B * KEYS]),
        "areas": [sb(f"weights{n}", [P, words]) for n, words in enumerate(AREA_WORDS)],
        "ps": ctx.enter_context(nc.psum_tensor("banks", [P, 8, 512], F32)),
    }


def plan_weights(core, area, name, make):
    used = 0

    def carve(shape):
        nonlocal used
        size = 1
        for n in shape[1:]:
            size *= n
        part = core["areas"][area][0:shape[0], used:used + size]
        used += size
        assert used <= AREA_WORDS[area], (name, used)
        if len(shape) == 2:
            return part
        if len(shape) == 3:
            return part.rearrange("p (a b) -> p a b", b=shape[2])
        return part.rearrange("p (a b c) -> p a b c", b=shape[2], c=shape[3])

    loads, needed = make(carve)
    return loads, core["nc"].alloc_semaphore(f"{name}_weights_in"), 16 * len(loads), needed


def fetch(sp, plan):
    loads, weights_in, _, _ = plan
    for dst, src in loads:
        sp.dma_start(dst, src).then_inc(weights_in, 16)


def tiles_of(tensor):
    return lambda i: tensor[:, i, :]


def pair_of(tensor, j):
    return tensor[:, 2 * j:2 * j + 2, :].rearrange("p u d -> p (u d)")


def rows(ap, n=P):
    return ap.rearrange("(a n) -> a n", a=1).partition_broadcast(n)


def columns(ap):
    return ap.rearrange("(c p) -> p c", p=P)


def newton_root(eng, drain, var, v, t, y):
    eng.tensor_scalar(v, var, EPS, None, ALU.add)
    drain()
    eng.tensor_scalar(y.bitcast(I32), v.bitcast(I32), -0.5, NEWTON_SEED, ALU.mult, ALU.add)
    drain()
    for step in range(3):
        eng.tensor_tensor(t, y, y, ALU.mult)
        drain()
        eng.tensor_tensor(t, t, v, ALU.mult)
        drain()
        eng.tensor_scalar(t, t, -0.5, 1.5, ALU.mult, ALU.add)
        drain()
        last = eng.tensor_tensor(y, t, y, ALU.mult)
        if step < 2:
            drain()
    return last


def vector_root(nc, dve, var, h, t, y):
    nc.vector.tensor_scalar(t, var, EPS, None, ALU.add)
    nc.vector.tensor_scalar(h, var, EPS, -0.5, ALU.add, ALU.mult)
    dve.drain()
    nc.vector.tensor_scalar(y.bitcast(I32), t.bitcast(I32), -0.5, NEWTON_SEED, ALU.mult, ALU.add)
    dve.drain()
    for step in range(3):
        nc.vector.tensor_tensor(t, y, y, ALU.mult)
        dve.drain()
        nc.vector.tensor_tensor(t, t, h, ALU.mult)
        dve.drain()
        nc.vector.scalar_tensor_tensor(y, t, 1.5, y, ALU.add, ALU.mult)
        dve.drain()


def layer_norm(core, ctx, sem, name, on_vector=False, two_pairs=False):
    nc, ps = core["nc"], core["ps"]

    def sb(part, shape):
        return ctx.enter_context(nc.sbuf_tensor(f"{name}_{part}", shape, F32))

    stats = sb("stats", [P, 2, 2, 6])
    mv = sb("mv", [P, 2, 2, 2])
    rs = sb("rs", [P, 2, 2])
    v = sb("v", [P, 4])
    t = sb("t", [P, 4])
    measured, rooted, normalised = sem(name + "_measured"), sem(name + "_rooted"), sem(name + "_normalised")
    turned, stored = sem(name + "_turned"), sem(name + "_stored")

    def measure(dve, j, src):
        p = j % 2
        for u in range(2):
            nc.vector.bn_stats(stats[:, p, u, :], src(2 * j + u))
        if two_pairs and p == 0:
            return
        dve.drain()
        for q in range(0 if two_pairs else p, p + 1):
            for u in range(2):
                last = nc.vector.bn_aggr(mv[:, q, u, :], stats[:, q, u, :])
        if two_pairs:
            dve.drain()
            vector_root(nc, dve, mv[:, :, :, 1].rearrange("p q u -> p (q u)"), v[:, :], t[:, :],
                        rs[:, :, :].rearrange("p q u -> p (q u)"))
        elif on_vector:
            dve.drain()
            vector_root(nc, dve, mv[:, p, :, 1], v[:, 0:2], t[:, 0:2], rs[:, p, :])
        else:
            last.then_inc(measured, 1)

    def root(pool, j):
        assert not on_vector
        pool.wait_ge(measured, j + 1)
        if j >= 2:
            pool.wait_ge(normalised, j - 1)
        newton_root(nc.gpsimd, pool.drain, mv[:, j % 2, :, 1], v[:, 0:2], t[:, 0:2], rs[:, j % 2, :]).then_inc(rooted, 1)

    def normalise(dve, j, src, dst):
        if not on_vector:
            dve.wait_ge(rooted, j + 1)
        if two_pairs and j % 2 == 0:
            return
        for pair in range(j - 1 if two_pairs else j, j + 1):
            p = pair % 2
            for u in range(2):
                last = nc.vector.tensor_scalar(dst(2 * pair + u), src(2 * pair + u), mv[:, p, u, 0:1],
                                               rs[:, p, u:u + 1], ALU.subtract, ALU.mult)
            last.then_inc(normalised, 1)

    def turn(pe, j, src, bank=7):
        pe.wait_ge(normalised, j + 1)
        if j >= 1:
            pe.wait_ge(stored, j)
        for c in range(DC):
            for u in range(2):
                last = nc.tensor.transpose(ps[:, bank, c * PAIR + u * P:c * PAIR + (u + 1) * P],
                                           src(2 * j + u)[:, c * P:(c + 1) * P], core["ident"][:, :])
        last.then_inc(turned, 1)

    def store(act, j, dsts, bank=7):
        act.wait_ge(turned, j + 1)
        for dst, gamma, beta in dsts:
            if gamma is None:
                last = nc.scalar.activation(dst[:, :, PAIR * j:PAIR * (j + 1)],
                                            ps[:, bank, :].rearrange("p (c n) -> p c n", c=DC), ACT.Copy)
            else:
                for c in range(DC):
                    last = nc.scalar.activation(
                        dst[:, c, PAIR * j:PAIR * (j + 1)], ps[:, bank, c * PAIR:(c + 1) * PAIR],
                        ACT.Identity, bias=beta[:, c:c + 1], scale=gamma[:, c:c + 1])
        last.then_inc(stored, 1)

    return measure, root, normalise, turn, store, stored


def opening(core, a, ctx, sem):
    nc, ps = core["nc"], core["ps"]

    def sb(name, shape):
        return ctx.enter_context(nc.sbuf_tensor(f"open_{name}", shape, F32))

    x_in, small_in = [sem(f"x_in{j}") for j in range(PAIRS)], sem("small_in")
    ident_zero, ident_made = sem("ident_zero"), sem("ident_made")
    ctx_normalised, ctx_turned, ctx_stored = sem("ctx_normalised"), sem("ctx_turned"), sem("ctx_stored")
    gates_made = sem("gates_made")
    x_normalised, x_turned, x_stored = sem("x_normalised"), sem("x_turned"), sem("x_stored")
    c_in, c_norm = sb("c_in", [P, KD]), sb("c_norm", [P, KD])
    c_stats, c_mv, c_small = sb("c_stats", [P, 6]), sb("c_mv", [P, 2]), sb("c_small", [P, 3])
    c_gb, g_in = sb("c_gb", [P, 2]), sb("g_in", [P, 8])
    stats, mv = sb("stats", [P, TILES, 6]), sb("mv", [P, TILES, 2])
    h, t, rs = sb("h", [P, TILES]), sb("t", [P, TILES]), sb("rs", [P, TILES])

    def sync(sp):
        for j in range(PAIRS):
            sp.dma_start(core["x"][:, 2 * j:2 * j + 2, :],
                         a["x"].rearrange("b (t p) d -> p (b t) d", p=P)[:, 2 * j:2 * j + 2, :]).then_inc(x_in[j], 16)

    def scalar(act):
        act.dma_start(c_in[:, :], a["ctx_512"].rearrange("b k d -> (b k) d")).then_inc(small_in, 16)
        act.dma_start(g_in[:, 0:4], rows(a["g_xattn"])).then_inc(small_in, 16)
        act.dma_start(g_in[:, 4:8], rows(a["g_ffn"])).then_inc(small_in, 16)
        act.dma_start(c_gb[:, 0:1], columns(a["L3_xattn_a2_lny_g"])).then_inc(small_in, 16)
        act.dma_start(c_gb[:, 1:2], columns(a["L3_xattn_a2_lny_b"])).then_inc(small_in, 16)
        act.wait_ge(small_in, 80)
        nc.scalar.activation(core["gate_attn"][:, :], g_in[:, 0:4], ACT.Tanh)
        nc.scalar.activation(core["gate_ffn"][:, :], g_in[:, 4:8], ACT.Tanh).then_inc(gates_made, 1)
        act.wait_ge(ctx_turned, 2)
        nc.scalar.activation(core["ctx_t"][:, :], ps[:, 0, 0:P], ACT.Copy)
        nc.scalar.activation(core["ctx_norm_t"][:, :], ps[:, 1, 0:P], ACT.Identity,
                             bias=c_gb[:, 1:2], scale=c_gb[:, 0:1]).then_inc(ctx_stored, 1)
        for j in range(PAIRS):
            act.wait_ge(x_turned, j + 1)
            nc.scalar.activation(core["xt"][:, :, PAIR * j:PAIR * (j + 1)],
                                 ps[:, 6 + j % 2, :].rearrange("p (c n) -> p c n", c=DC), ACT.Copy).then_inc(x_stored, 1)

    def gpsimd(pool):
        nc.gpsimd.memset(core["ident"][:, :], 0.0).then_inc(ident_zero, 1)
        pool.wait_ge(ident_zero, 1)
        nc.gpsimd.affine_select(out=core["ident"][:, :], in_=core["ident"][:, :], compare_op=ALU.not_equal,
                                fill=1.0, base=0, pattern=[[-1, P]], channel_multiplier=1).then_inc(ident_made, 1)

    def vector(dve):
        dve.wait_ge(small_in, 80)
        nc.vector.bn_stats(c_stats[:, :], c_in[:, :])
        dve.drain()
        nc.vector.bn_aggr(c_mv[:, :], c_stats[:, :])
        dve.drain()
        vector_root(nc, dve, c_mv[:, 1:2], c_small[:, 0:1], c_small[:, 1:2], c_small[:, 2:3])
        nc.vector.tensor_scalar(c_norm[:, :], c_in[:, :], c_mv[:, 0:1], c_small[:, 2:3],
                                ALU.subtract, ALU.mult).then_inc(ctx_normalised, 1)
        for i in range(TILES):
            if i % 2 == 0:
                dve.wait_ge(x_in[i // 2], 16)
            nc.vector.bn_stats(stats[:, i, :], core["x"][:, i, :])
        dve.drain()
        for i in range(TILES):
            nc.vector.bn_aggr(mv[:, i, :], stats[:, i, :])
        dve.drain()
        vector_root(nc, dve, mv[:, :, 1], h[:, :], t[:, :], rs[:, :])
        for i in range(TILES):
            nc.vector.tensor_scalar(core["xn"][:, i, :], core["x"][:, i, :], mv[:, i, 0:1], rs[:, i:i + 1],
                                    ALU.subtract, ALU.mult).then_inc(x_normalised, 1)
        dve.wait_ge(gates_made, 1)

    def tensor(pe):
        pe.wait_ge(ident_made, 1)
        pe.wait_ge(small_in, 80)
        nc.tensor.transpose(ps[:, 0, 0:P], c_in[:, :], core["ident"][:, :]).then_inc(ctx_turned, 1)
        pe.wait_ge(ctx_normalised, 1)
        nc.tensor.transpose(ps[:, 1, 0:P], c_norm[:, :], core["ident"][:, :]).then_inc(ctx_turned, 1)
        for j in range(PAIRS):
            pe.wait_ge(x_normalised, 2 * j + 2)
            if j >= 2:
                pe.wait_ge(x_stored, j - 1)
            for c in range(DC):
                for u in range(2):
                    last = nc.tensor.transpose(ps[:, 6 + j % 2, c * PAIR + u * P:c * PAIR + (u + 1) * P],
                                               core["xn"][:, 2 * j + u, c * P:(c + 1) * P], core["ident"][:, :])
            last.then_inc(x_turned, 1)
        pe.wait_ge(x_stored, PAIRS)
        pe.wait_ge(ctx_stored, 1)

    return {"sync": sync, "scalar": scalar, "gpsimd": gpsimd, "vector": vector, "tensor": tensor}


def stage_attention(core, a, name, width, scale, plan, following, source, out_tile, gate, bias,
                    norm_out, context, opens=False):
    nc, ps = core["nc"], core["ps"]
    HEADS = 16
    HK = HEADS * KEYS
    chunks = HEADS * width // P
    per = P // width
    narrow = width * 4 <= KEYS
    HEADS_OUT = 3
    OUT = 4 if narrow else 3
    TURN = OUT + 3
    kinds = 1 if narrow else 2
    with ExitStack() as ctx:
        def sb(part, shape):
            return ctx.enter_context(nc.sbuf_tensor(f"{name}_{part}", shape, F32))

        _, weights_in, weights_total, (finish, bias_row, gb) = plan
        wq_t, wo, turns, wk, wv = finish(sb)
        sem, clear_semaphores = named_semaphores(nc, name)
        w_turned, w_stored = sem("w_turned"), sem("w_stored")
        mask_set, mask_made = sem("mask_set"), sem("mask_made")
        kv_ready, kv_stored, blocks_made = sem("kv_ready"), sem("kv_stored"), sem("blocks_made")
        fold_ready, fold_stored = sem("fold_ready"), sem("fold_stored")
        bias_made, bias_added = sem("bias_made"), sem("bias_added")
        scores_ready, centred, exped = sem("scores_ready"), sem("centred"), sem("exped")
        probs_ready, probs_turned, probs_stored = sem("probs_ready"), sem("probs_turned"), sem("probs_stored")
        out_ready, out_added = sem("out_ready"), sem("out_added")
        if narrow:
            ctx_twice_made, values_ready, values_made = sem("ctx_twice_made"), sem("values_ready"), sem("values_made")
            heads_ready, heads_stored = sem("heads_ready"), sem("heads_stored")
        (norm_measure, norm_root, norm_normalise, norm_turn, norm_store,
         norm_stored) = layer_norm(core, ctx, sem, name + "_norm")

        mask = sb("mask", [P, per])
        kv = sb("kv", [P, chunks, 2, B, KEYS])
        blk = sb("blk", [P, 2, kinds, B, per, KEYS])
        fold_q = sb("fold_q", [P, B, DC, HK])
        if narrow:
            ctx_twice = sb("ctx_twice", [P, B, 2, KEYS])
            half = sb("half", [P, 2])
            v_blk = sb("v_blk", [P, B, HEADS, width])
            heads = sb("heads", [P, 2, chunks, P])
        else:
            fold_v = sb("fold_v", [P, B, HK // P, D])
        ex = sb("ex", [P, 3, HEADS, KEYS])
        mx = sb("mx", [P, 2, HEADS])
        sm = sb("sm", [P, 2, HEADS])
        pt = sb("pt", [P, 2, HK])
        gamma, beta = (gb[:, 0, :], gb[:, 1, :]) if norm_out else (None, None)

        folds = []
        for c in range(chunks):
            for b in range(B):
                for dc in range(DC):
                    folds.append((c, wq_t[:, c, dc * P:(dc + 1) * P],
                                  blk[:, c % 2, 0, b].rearrange("p h k -> p (h k)"), per * KEYS,
                                  fold_q[:, b, dc, c * per * KEYS:(c + 1) * per * KEYS]))
                for m in range(0 if narrow else per // 2):
                    folds.append((c, blk[:, c % 2, 1, b, 2 * m:2 * m + 2].rearrange("p h k -> p (h k)"),
                                  wo[:, c, :], D, fold_v[:, b, c * per // 2 + m, :]))
        per_chunk = len(folds) // chunks

        before = opening(core, a, ctx, sem) if opens else {}

        with nc.Block() as block:
            @block.sync
            def _(sp):
                if opens:
                    before["sync"](sp)
                    fetch(sp, plan)
                fetch(sp, following)

            @block.gpsimd
            def _(pool):
                if opens:
                    before["gpsimd"](pool)
                nc.gpsimd.memset(mask[:, :], 1.0).then_inc(mask_set, 1)
                pool.wait_ge(mask_set, 1)
                nc.gpsimd.affine_select(out=mask[:, :], in_=mask[:, :], compare_op=ALU.is_ge, fill=0.0, base=0,
                                        pattern=[[-width, per]], channel_multiplier=1).then_inc(mask_set, 1)
                pool.wait_ge(mask_set, 2)
                nc.gpsimd.affine_select(out=mask[:, :], in_=mask[:, :], compare_op=ALU.is_ge, fill=0.0,
                                        base=width - 1, pattern=[[width, per]],
                                        channel_multiplier=-1).then_inc(mask_made, 1)
                if narrow:
                    pool.wait_ge(mask_made, 1)
                    nc.gpsimd.memset(half[:, :], 1.0).then_inc(mask_made, 1)
                    pool.wait_ge(mask_made, 2)
                    nc.gpsimd.affine_select(out=half[:, 0:1], in_=half[:, 0:1], compare_op=ALU.is_ge, fill=0.0,
                                            base=KEYS - 1, pattern=[[0, 1]], channel_multiplier=-1).then_inc(mask_made, 1)
                    nc.gpsimd.affine_select(out=half[:, 1:2], in_=half[:, 1:2], compare_op=ALU.is_ge, fill=0.0,
                                            base=-KEYS, pattern=[[0, 1]], channel_multiplier=1).then_inc(mask_made, 1)
                if bias:
                    pool.wait_ge(bias_made, 1)
                for j in range(PAIRS):
                    if bias:
                        for u in range(2):
                            i = 2 * j + u
                            last = nc.gpsimd.tensor_tensor(out_tile(i), source(i), bias_row[:, :], ALU.add)
                        last.then_inc(bias_added, 1)
                    if j >= 1:
                        norm_root(pool, j - 1)
                norm_root(pool, PAIRS - 1)

            @block.tensor
            def _(pe):
                if opens:
                    before["tensor"](pe)
                pe.wait_ge(weights_in, weights_total)
                for n, (srcs, _) in enumerate(turns):
                    if n >= 2:
                        pe.wait_ge(w_stored, n - 1)
                    for q, src in enumerate(srcs):
                        last = nc.tensor.transpose(ps[:, n % 2, q * P:(q + 1) * P], src, core["ident"][:, :])
                    last.then_inc(w_turned, 1)
                pe.wait_ge(w_stored, len(turns))

                def keys_values(c):
                    if c >= 2:
                        pe.wait_ge(kv_stored, c - 1)
                    for kind, w in enumerate((wk, wv)[:kinds]):
                        last = nc.tensor.matmul(ps[:, c % 2, kind * P:(kind + 1) * P], w[:, c * P:(c + 1) * P],
                                                context[:, :], start=True, stop=True)
                    last.then_inc(kv_ready, 1)

                keys_values(0)
                for n, (c, lhs, rhs, cols, _) in enumerate(folds):
                    if n % per_chunk == 0:
                        if c + 1 < chunks:
                            keys_values(c + 1)
                        pe.wait_ge(blocks_made, c + 1)
                    if n >= 4:
                        pe.wait_ge(fold_stored, n - 3)
                    nc.tensor.matmul(ps[:, 2 + n % 4, 0:cols], lhs, rhs, start=True,
                                     stop=True).then_inc(fold_ready, 1)
                pe.wait_ge(fold_stored, len(folds))
                if narrow:
                    pe.wait_ge(ctx_twice_made, 1)
                    for b in range(B):
                        nc.tensor.matmul(ps[:, 6 + b, 0:HEADS * width], ctx_twice[:, b].rearrange("p a k -> p (a k)"),
                                         wv[:, :], start=True, stop=True).then_inc(values_ready, 1)
                    pe.wait_ge(values_made, B)

                for i in range(TILES + TURN):
                    if i < TILES:
                        b = i // (TILES // B)
                        if i >= 2:
                            pe.wait_ge(centred, i - 1)
                        for h in range(2):
                            for dc in range(DC):
                                last = nc.tensor.matmul(ps[:, 2 * (i % 2) + h, :], core["xt"][:, dc, i * P:(i + 1) * P],
                                                        fold_q[:, b, dc, h * 512:(h + 1) * 512],
                                                        start=(dc == 0), stop=(dc == DC - 1))
                        last.then_inc(scores_ready, 1)
                    if 2 <= i <= TILES + 1:
                        k = i - 2
                        pe.wait_ge(probs_ready, k + 1)
                        if k >= 1:
                            pe.wait_ge(probs_stored, k)
                        for c in range(HK // P):
                            last = nc.tensor.transpose(ps[:, 4 + c // 4, (c % 4) * P:(c % 4 + 1) * P],
                                                       ex[:, k % 3, 2 * c:2 * c + 2, :].rearrange("p h k -> p (h k)"),
                                                       core["ident"][:, :])
                        last.then_inc(probs_turned, 1)
                    if narrow and HEADS_OUT <= i < TILES + HEADS_OUT:
                        k = i - HEADS_OUT
                        pe.wait_ge(probs_stored, k + 1)
                        if k >= 1:
                            pe.wait_ge(heads_stored, k)
                            if i > TURN:
                                pe.wait_ge(norm_stored, (i - TURN - 1) // 2 + 1)
                        for c in range(HK // P):
                            row = 2 * c * width
                            last = nc.tensor.matmul(
                                ps[row % P:row % P + 2 * width, 7, row // P * P:(row // P + 1) * P],
                                v_blk[:, k // (TILES // B), 2 * c:2 * c + 2, :].rearrange("p h d -> p (h d)"),
                                pt[:, k % 2, c * P:(c + 1) * P], start=True, stop=True)
                        last.then_inc(heads_ready, 1)
                    if narrow and OUT <= i < TILES + OUT:
                        k = i - OUT
                        pe.wait_ge(heads_stored, k + 1)
                        if k >= 1:
                            pe.wait_ge(out_added, k)
                        for c in range(chunks):
                            last = nc.tensor.matmul(ps[:, 6, 0:D], heads[:, k % 2, c, :], wo[:, c, :],
                                                    start=(c == 0), stop=(c == chunks - 1))
                        last.then_inc(out_ready, 1)
                    if not narrow and OUT <= i < TILES + OUT:
                        k = i - OUT
                        pe.wait_ge(probs_stored, k + 1)
                        if k >= 1:
                            pe.wait_ge(out_added, k)
                        for c in range(HK // P):
                            last = nc.tensor.matmul(ps[:, 6, 0:D],
                                                    pt[:, k % 2, c * P:(c + 1) * P],
                                                    fold_v[:, k // (TILES // B), c, :],
                                                    start=(c == 0), stop=(c == HK // P - 1))
                        last.then_inc(out_ready, 1)
                    if i >= TURN and (i - TURN) % 2 == 0:
                        if narrow:
                            pe.wait_ge(heads_stored, min(i - HEADS_OUT + 1, TILES))
                        norm_turn(pe, (i - TURN) // 2, tiles_of(core["xn"]))

            @block.scalar
            def _(act):
                if opens:
                    before["scalar"](act)
                for n, (srcs, dst) in enumerate(turns):
                    act.wait_ge(w_turned, n + 1)
                    nc.scalar.activation(dst, ps[:, n % 2, 0:P * len(srcs)], ACT.Copy).then_inc(w_stored, 1)

                def store_kv(c):
                    act.wait_ge(kv_ready, c + 1)
                    nc.scalar.activation(kv[:, c, 0:kinds].rearrange("p a b k -> p (a b k)"), ps[:, c % 2, 0:kinds * P],
                                         ACT.Copy).then_inc(kv_stored, 1)

                store_kv(0)
                for n, (c, _, _, cols, dst) in enumerate(folds):
                    if n % per_chunk == 0 and c + 1 < chunks:
                        store_kv(c + 1)
                    act.wait_ge(fold_ready, n + 1)
                    nc.scalar.activation(dst, ps[:, 2 + n % 4, 0:cols], ACT.Copy).then_inc(fold_stored, 1)

                for i in range(TILES + TURN):
                    if i < TILES:
                        act.wait_ge(centred, i + 1)
                        nc.scalar.activation(ex[:, i % 3], ex[:, i % 3], ACT.Exp, scale=scale).then_inc(exped, 1)
                    if 2 <= i <= TILES + 1:
                        k = i - 2
                        act.wait_ge(probs_turned, k + 1)
                        if k >= 2:
                            act.wait_ge(heads_ready if narrow else out_ready, k - 1)
                        nc.scalar.activation(pt[:, k % 2, :], ps[:, 4:6, :].rearrange("p a n -> p (a n)"),
                                             ACT.Copy).then_inc(probs_stored, 1)
                    if narrow and HEADS_OUT <= i < TILES + HEADS_OUT:
                        k = i - HEADS_OUT
                        act.wait_ge(heads_ready, k + 1)
                        if k >= 2:
                            act.wait_ge(out_ready, k - 1)
                        copy_bank(nc, heads[:, k % 2].rearrange("p c n -> p (c n)"), ps[:, 7, 0:HEADS * width]).then_inc(heads_stored, 1)
                    if i >= TURN and (i - TURN) % 2 == 0:
                        norm_store(act, (i - TURN) // 2, [(core["xt"], gamma, beta)])

            @block.vector
            def _(dve):
                if opens:
                    before["vector"](dve)
                dve.wait_ge(weights_in, weights_total)
                if bias and gate is None:
                    nc.vector.tensor_copy(bias_row[:, 0:1], bias_row[:, 0:1]).then_inc(bias_made, 1)
                elif bias:
                    nc.vector.tensor_scalar(bias_row[:, :], bias_row[:, :], gate, None, ALU.mult).then_inc(bias_made, 1)
                if narrow:
                    nc.vector.tensor_copy(ctx_twice[:, :, :, :], context[:, :].rearrange("p (b k) -> p b k", b=B)
                                          .unsqueeze(2).to_broadcast([P, B, 2, KEYS])).then_inc(ctx_twice_made, 1)
                dve.wait_ge(mask_made, 1)
                for c in range(chunks):
                    dve.wait_ge(kv_stored, c + 1)
                    if c >= 2:
                        dve.wait_ge(fold_ready, per_chunk * (c - 1))
                    for kind in range(kinds):
                        for b in range(B):
                            last = nc.vector.tensor_tensor(
                                blk[:, c % 2, kind, b],
                                kv[:, c, kind, b, :].unsqueeze(1).to_broadcast([P, per, KEYS]),
                                mask[:, :].unsqueeze(2).to_broadcast([P, per, KEYS]), ALU.mult)
                    last.then_inc(blocks_made, 1)

                if narrow:
                    dve.wait_ge(mask_made, 4)
                    for b in range(B):
                        dve.wait_ge(values_ready, b + 1)
                        nc.vector.tensor_tensor(
                            v_blk[:, b].rearrange("p (m e) d -> p m e d", e=2),
                            ps[:, 6 + b, 0:HEADS * width].rearrange("p (m e d) -> p m e d", e=2, d=width),
                            half[:, :].unsqueeze(1).unsqueeze(3).to_broadcast([P, HEADS // 2, 2, width]),
                            ALU.mult).then_inc(values_made, 1)

                for i in range(TILES + OUT + 2):
                    if i < TILES:
                        dve.wait_ge(scores_ready, i + 1)
                        scores = ps[:, 2 * (i % 2):2 * (i % 2) + 2, :].rearrange("p a (h k) -> p (a h) k", k=KEYS)
                        nc.vector.tensor_reduce(mx[:, i % 2, :], scores, AX_X, ALU.max)
                        dve.drain()
                        if i >= 3:
                            dve.wait_ge(probs_turned, i - 2)
                        nc.vector.tensor_tensor(ex[:, i % 3], scores,
                                                mx[:, i % 2, :].unsqueeze(2).to_broadcast([P, HEADS, KEYS]),
                                                ALU.subtract).then_inc(centred, 1)
                    if 1 <= i <= TILES:
                        k = i - 1
                        dve.wait_ge(exped, k + 1)
                        nc.vector.tensor_reduce(sm[:, k % 2, :], ex[:, k % 3], AX_X, ALU.add)
                        dve.drain()
                        nc.vector.reciprocal(sm[:, k % 2, :], sm[:, k % 2, :])
                        dve.drain()
                        nc.vector.tensor_tensor(ex[:, k % 3], ex[:, k % 3],
                                                sm[:, k % 2, :].unsqueeze(2).to_broadcast([P, HEADS, KEYS]),
                                                ALU.mult).then_inc(probs_ready, 1)
                    if i >= OUT + 2 and (i - OUT) % 2 == 0:
                        norm_normalise(dve, (i - OUT - 2) // 2, out_tile, tiles_of(core["xn"]))
                    if OUT <= i < TILES + OUT:
                        k = i - OUT
                        dve.wait_ge(out_ready, k + 1)
                        if bias:
                            dve.wait_ge(bias_added, k // 2 + 1)
                        out = ps[:, 6, 0:D]
                        if gate is None:
                            nc.vector.tensor_tensor(out_tile(k), out, out_tile(k), ALU.add).then_inc(out_added, 1)
                        else:
                            nc.vector.scalar_tensor_tensor(out_tile(k), out, gate, out_tile(k), ALU.mult,
                                                           ALU.add).then_inc(out_added, 1)
                        if k % 2 == 1:
                            dve.drain()
                            norm_measure(dve, k // 2, out_tile)
        clear_semaphores()


def attention_weights(a, layout, bias, norm_out):
    def make(carve):
        loads, finish = layout(carve)
        bias_row, gb = carve([P, D]), carve([P, 2, DC])
        if bias:
            loads = loads + [(bias_row[:, :], rows(a[bias]))]
        if norm_out:
            loads = loads + [(gb[:, k, :], columns(a[n])) for k, n in enumerate(norm_out)]
        return loads, (finish, bias_row, gb)
    return make


def layout_l0(a):
    def layout(carve):
        wq, wk, wv, wo = carve([P, DC, 1024]), carve([P, 1024]), carve([P, 1024]), carve([P, 8, D])
        loads = [(wq[:, :, :], a["L0_xattn_Wq"].rearrange("(c p) n -> p c n", p=P)),
                 (wk[:, :], a["L0_xattn_Wk"]), (wv[:, :], a["L0_xattn_Wv"]),
                 (wo[:, :, :], a["L0_xattn_Wo"].rearrange("(c p) n -> p c n", p=P))]

        def finish(sb):
            wq_t = sb("wq_t", [P, 8, D])
            turns = [([wq[:, dc, c * P:(c + 1) * P] for c in (2 * q, 2 * q + 1) for dc in range(DC)],
                      wq_t[:, 2 * q:2 * q + 2, :].rearrange("p c d -> p (c d)")) for q in range(4)]
            return wq_t, wo, turns, wk, wv
        return loads, finish
    return layout


def first(t):
    return isinstance(t, int) and t == 0


def later(t):
    return not (isinstance(t, int) and t < 2)


def copy_bank(nc, dst, bank_ap):
    return nc.scalar.activation(dst, bank_ap, ACT.Copy)


def experts_weights(a, router, affine=None, shared=None):
    def make(carve):
        wr, gb, s1, s2 = carve([P, DC, E]), None, None, None
        loads = [(wr[:, :, :], a[router].rearrange("(c p) e -> p c e", p=P))]
        if affine:
            gb = carve([P, 2, DC])
            loads += [(gb[:, k, :], columns(a[n])) for k, n in enumerate(affine)]
        if shared:
            s1, s2 = carve([P, DC, 512]), carve([P, 2, D])
            loads += [(s1[:, :, :], a[shared[0]].rearrange("(c p) n -> p c n", p=P)),
                      (s2[:, :, :], a[shared[1]].rearrange("(c p) n -> p c n", p=P))]
        return loads, (wr, gb, s1, s2)
    return make


def stage_experts(core, a, name, *, top, full, half, capacity, plan, following, w1, w2, swiglu, gate,
                  norm_behind=True):
    nc, ps = core["nc"], core["ps"]
    tiles = full + half
    ROWS = full * PAIR + half * P
    WIDE = 2 * FF if swiglu else FF
    HALF = 2 if swiglu else 1
    xs = nc.dram_tensor(f"{name}_rows", [ROWS, D], F32, kind="Internal").ap()
    ys = nc.dram_tensor(f"{name}_results", [ROWS + P, D], F32, kind="Internal").ap()
    with ExitStack() as ctx:
        def sb(part, shape, dtype=F32):
            return ctx.enter_context(nc.sbuf_tensor(f"{name}_{part}", shape, dtype))

        sem, clear_semaphores = named_semaphores(nc, name)
        made, zeroed = sem("made"), sem("zeroed")
        raw_ready, raw_stored = sem("raw_ready"), sem("raw_stored")
        logits_ready, shifted, exped = sem("logits_ready"), sem("shifted"), sem("exped")
        chosen, counted, slots_made = sem("chosen"), sem("counted"), sem("slots_made")
        scattered = sem("scattered")
        if not capacity:
            owners_made = sem("owners_made")
        w1_in, w2_in = [sem("w1_in0"), sem("w1_in1")], [sem("w2_in0"), sem("w2_in1")]
        rows_in, y_sent = [sem("rows_in0"), sem("rows_in1")], [sem("y_sent0"), sem("y_sent1")]
        rows_turned, rows_stored = sem("rows_turned"), sem("rows_stored")
        hid_ready, hid_stored = sem("hid_ready"), sem("hid_stored")
        clipped, silued = sem("clipped"), sem("silued")
        out_ready, y_stored = sem("out_ready"), sem("y_stored")
        gathered, added = [sem(f"gathered{q}") for q in range(4)], sem("added")
        if norm_behind:
            (norm_measure, norm_root, norm_normalise, norm_turn, norm_store,
             norm_stored) = layer_norm(core, ctx, sem, name + "_norm", on_vector=True, two_pairs=True)
        else:
            x_sent = sem("x_sent")

        tri = sb("tri", [P, P])
        ones = sb("ones", [P, P])
        iota_e = sb("iota_e", [P, E])
        iota_t = sb("iota_t", [P, max(full, half)])
        raw = sb("raw", [E, T])
        pr = sb("pr", [P, TILES, E])
        eq = sb("eq", [P, TILES, E])
        hot = [sb(f"hot{k}", [P, TILES, E]) for k in range(top)]
        hots = sb("hots", [P, TILES, E])
        best = sb("best", [P, top, TILES])
        col = sb("col", [P, 2, TILES])
        total = sb("total", [P, TILES, E])
        scan = [sb("scan0", [P, TILES, E]), sb("scan1", [P, TILES, E])]
        begin = sb("begin", [P, E])
        if not capacity:
            sums = [sb(f"sums{n}", [P, E]) for n in range(3)]
            rows_f, left, left_over, room = sb("rows_f", [P, E]), sb("left", [P, E]), sb("left_over", [P, E]), sb("room", [P, E])
            wanted, fulls, halves = sb("wanted", [P, E]), sb("fulls", [P, E]), sb("halves", [P, E])
            beyond, jump = sb("beyond", [P, E]), sb("jump", [P, E])
            whole_i = sb("whole_i", [P, E], I32)
        owner = sb("owner", [P, max(full, half), E])
        owner_f = sb("owner_f", [P, tiles])
        owner_i = sb("owner_i", [P, tiles], I32)
        slot_f = sb("slot_f", [P, TILES])
        slot = sb("slot", [P, top, TILES], I32)
        weight = sb("weight", [P, top, TILES])
        zero_rows = 3 if ROWS % (3 * P) == 0 else 2
        zero = sb("zero", [P, zero_rows * D])
        w1_sb = sb("w1", [P, 2, DC, WIDE])
        w2_sb = sb("w2", [P, 2, FC, D])
        xr = sb("xr", [P, 2, 2, D])
        xrt = sb("xrt", [P, 2, DC, PAIR])
        sg = sb("sg", [P, 4, PAIR])
        ht = sb("ht", [P, 2, FC, PAIR])
        yt = sb("yt", [P, 2, 2, D])
        yg = sb("yg", [P, 4, D])
        _, weights_in, weights_total, (wr, gb, s1, s2) = plan
        affine, shared = gb is not None, s1 is not None
        if shared:
            FS = 256
            SC = FS // P
            s_hid_ready, s_clipped, s_silued = sem("s_hid_ready"), sem("s_clipped"), sem("s_silued")
            s_hid_stored, s_out_ready, s_added = sem("s_hid_stored"), sem("s_out_ready"), sem("s_added")

        w1_rows = a[w1].rearrange("e (c p) n -> e p c n", p=P)
        w2_rows = a[w2].rearrange("e (c p) n -> e p c n", p=P)

        def tile_rows(scratch_rows, t, size):
            if size == PAIR:
                where, t = scratch_rows[0:full * PAIR, :], t
            else:
                where, t = scratch_rows[full * PAIR:ROWS, :], t - full
            return where.rearrange("(t u p) d -> t p u d", u=size // P, p=P)[bass.ds(t, 1)].rearrange("a p u d -> p (a u) d")

        zero_loads = ROWS // (P * zero_rows)

        def size_of(t):
            return 0 if not 0 <= t < tiles else PAIR if t < full else P

        def over_tiles_in_turn(eng, step):
            t = 0
            while t < tiles:
                loops = 0
                if t >= 3 and t % 2 == 1:
                    while all(size_of(q) == size_of(t - 1) for q in range(t - 1, t + 2 * loops + 3)):
                        loops += 1
                if loops:
                    size = size_of(t)
                    with eng.Fori(t // 2, t // 2 + loops) as jj:
                        step(jj, 1, size, size, size)
                        step(jj + 1, 0, size, size, size)
                    t += 2 * loops
                else:
                    step(t // 2, t % 2, size_of(t - 1), size_of(t), size_of(t + 1))
                    t += 1

        with nc.Block() as block:
            @block.sync
            def _(sp):
                if following:
                    fetch(sp, following)
                sp.wait_ge(made, 6)
                for n in range(zero_loads):
                    sp.dma_start(xs.rearrange("(n p r) d -> n p (r d)", p=P, r=zero_rows)[n], zero[:, :]).then_inc(zeroed, 16)
                sp.dma_start(ys[ROWS:ROWS + P, :], zero[:, 0:D]).then_inc(zeroed, 16)

                def expert_of(t):
                    return t if capacity else sp.value_load(owner_i[0:1, bass.ds(t, 1)], min_val=0, max_val=E - 1)

                def load_w1(e, p):
                    sp.dma_start(w1_sb[:, p], w1_rows[bass.ds(e, 1)].rearrange("a p c n -> p (a c) n")).then_inc(w1_in[p], 16)

                def load_w2(e, p):
                    sp.dma_start(w2_sb[:, p], w2_rows[bass.ds(e, 1)].rearrange("a p c n -> p (a c) n")).then_inc(w2_in[p], 16)

                def load_rows(t, p, size):
                    sp.dma_start(xr[:, p, 0:size // P], tile_rows(xs, t, size)).then_inc(rows_in[p], 16)

                def load(jj, p, before, size, after):
                    t = 2 * jj + p
                    if not later(t):
                        return
                    sp.wait_ge(hid_ready, FC * (t - 1))
                    load_w1(expert_of(t), p)
                    sp.wait_ge(rows_turned, t - 1)
                    load_rows(t, p, size)
                    if later(t - 1):
                        sp.wait_ge(out_ready, t - 2)
                        load_w2(expert_of(t - 1), 1 - p)

                if not capacity:
                    sp.wait_ge(owners_made, 1)
                for t in range(2):
                    e = expert_of(t)
                    load_w1(e, t)
                    load_w2(e, t)
                sp.wait_ge(slots_made, 1)
                sp.wait_ge(scattered, 16 * TILES * top)
                for t in range(2):
                    load_rows(t, t, PAIR)
                over_tiles_in_turn(sp, load)
                sp.wait_ge(out_ready, tiles - 2)
                load_w2(expert_of(tiles - 1), (tiles - 1) % 2)
                if not norm_behind:
                    for i in range(TILES):
                        sp.wait_ge(added, top * (i + 1))
                        sp.dma_start(a["out"].rearrange("b (t p) d -> p (b t) d", p=P)[:, i, :],
                                     core["x"][:, i, :]).then_inc(x_sent, 16)
                    sp.wait_ge(x_sent, 16 * TILES)

            @block.gpsimd
            def _(pool):
                nc.gpsimd.memset(tri[:, :], 1.0).then_inc(made, 1)
                nc.gpsimd.memset(ones[:, :], 1.0).then_inc(made, 1)
                nc.gpsimd.memset(zero[:, :], 0.0).then_inc(made, 1)
                nc.gpsimd.iota(iota_e[:, :], [[1, E]], base=0, channel_multiplier=0,
                               allow_small_or_imprecise_dtypes=True).then_inc(made, 1)
                nc.gpsimd.iota(iota_t[:, :], [[1, max(full, half)]], base=0, channel_multiplier=0,
                               allow_small_or_imprecise_dtypes=True).then_inc(made, 1)
                pool.wait_ge(made, 5)
                nc.gpsimd.affine_select(out=tri[:, :], in_=tri[:, :], compare_op=ALU.is_gt, fill=0.0, base=0,
                                        pattern=[[1, P]], channel_multiplier=-1).then_inc(made, 1)
                pool.wait_ge(zeroed, 16 * (zero_loads + 1))
                pool.wait_ge(slots_made, 1)
                for k in range(top):
                    for i in range(TILES):
                        pool.indirect_dma_start(xs, bass.IndirectOffsetOnAxis(ap=slot[:, k, i:i + 1], axis=0),
                                                core["xn"][:, i, :], None, bounds_check=ROWS - 1,
                                                oob_is_err=False).then_inc(scattered, 16)

                def send(jj, p, before, size, after):
                    t = 2 * jj + p
                    pool.wait_ge(y_stored, t + 1)
                    pool.dma_start(tile_rows(ys, t, size), yt[:, p, 0:size // P]).then_inc(y_sent[p], 16)

                over_tiles_in_turn(pool, send)
                for p in range(2):
                    pool.wait_ge(y_sent[p], 16 * ((tiles + 1 - p) // 2))
                for n in range(TILES * top):
                    i, k = n // top, n % top
                    if n >= 4:
                        pool.wait_ge(added, n - 3)
                    pool.indirect_dma_start(yg[:, n % 4, :], None, ys,
                                            bass.IndirectOffsetOnAxis(ap=slot[:, k, i:i + 1], axis=0),
                                            bounds_check=ROWS + P - 1, oob_is_err=False).then_inc(gathered[n % 4], 16)

            @block.tensor
            def _(pe):
                pe.wait_ge(weights_in, weights_total)
                for g in range(T // 512):
                    for dc in range(DC):
                        last = nc.tensor.matmul(ps[0:E, g, :], wr[:, dc, :], core["xt"][:, dc, g * 512:(g + 1) * 512],
                                                start=(dc == 0), stop=(dc == DC - 1))
                    last.then_inc(raw_ready, 1)
                for i in range(TILES):
                    pe.wait_ge(raw_stored, i * P // 512 + 1)
                    last = nc.tensor.transpose(ps[:, 4, i * E:(i + 1) * E], raw[:, i * P:(i + 1) * P],
                                               core["ident"][0:E, 0:E])
                last.then_inc(logits_ready, 1)
                pe.wait_ge(made, 6)
                pe.wait_ge(chosen, 1)
                nc.tensor.matmul(ps[:, 5, 0:P], tri[:, :], hots[:, :, :].rearrange("p t e -> p (t e)"),
                                 start=True, stop=True)
                nc.tensor.matmul(ps[:, 6, 0:P], ones[:, :], hots[:, :, :].rearrange("p t e -> p (t e)"),
                                 start=True, stop=True).then_inc(counted, 1)

                if shared:
                    for j in range(PAIRS + 1):
                        if j < PAIRS:
                            for f in range(SC):
                                n = SC * j + f
                                if n >= 2:
                                    pe.wait_ge(s_hid_stored, n - 1)
                                for h in range(2):
                                    for dc in range(DC):
                                        last = nc.tensor.matmul(
                                            ps[:, 1 + n % 2, h * PAIR:(h + 1) * PAIR],
                                            s1[:, dc, h * FS + f * P:h * FS + (f + 1) * P],
                                            core["xt"][:, dc, PAIR * j:PAIR * (j + 1)],
                                            start=(dc == 0), stop=(dc == DC - 1))
                                last.then_inc(s_hid_ready, 1)
                        if j >= 1:
                            q = j - 1
                            pe.wait_ge(s_hid_stored, SC * j)
                            if q >= 2:
                                pe.wait_ge(s_added, q - 1)
                            for u in range(2):
                                for f in range(SC):
                                    last = nc.tensor.matmul(ps[:, 3 + q % 2, u * D:(u + 1) * D],
                                                            ht[:, q % 2, f, u * P:(u + 1) * P], s2[:, f, :],
                                                            start=(f == 0), stop=(f == SC - 1))
                            last.then_inc(s_out_ready, 1)
                    pe.wait_ge(s_added, PAIRS)

                def turn(jj, p, size):
                    t = 2 * jj + p
                    pe.wait_ge(rows_in[p], 16 * jj + 16)
                    if not first(t):
                        pe.wait_ge(rows_stored, t)
                    for c in range(DC):
                        for u in range(size // P):
                            last = nc.tensor.transpose(ps[:, 7, c * PAIR + u * P:c * PAIR + (u + 1) * P],
                                                       xr[:, p, u, c * P:(c + 1) * P], core["ident"][:, :])
                    last.then_inc(rows_turned, 1)

                def hidden(jj, p, size):
                    t = 2 * jj + p
                    pe.wait_ge(w1_in[p], 16 * jj + 16)
                    pe.wait_ge(rows_stored, t + 1)
                    for f in range(FC):
                        if not (first(t) and f < 4):
                            pe.wait_ge(hid_stored, FC * t + (f - 3))
                        for h in range(HALF):
                            for dc in range(DC):
                                last = nc.tensor.matmul(ps[:, f % 4, h * PAIR:h * PAIR + size],
                                                        w1_sb[:, p, dc, h * FF + f * P:h * FF + (f + 1) * P],
                                                        xrt[:, p, dc, 0:size], start=(dc == 0), stop=(dc == DC - 1))
                        last.then_inc(hid_ready, 1)

                def output(jj, p, size):
                    t = 2 * jj + p
                    pe.wait_ge(w2_in[p], 16 * jj + 16)
                    pe.wait_ge(hid_stored, FC * t + FC)
                    if later(t):
                        pe.wait_ge(y_stored, t - 1)
                    for u in range(size // P):
                        for f in range(FC):
                            last = nc.tensor.matmul(ps[:, 4 + p, u * D:(u + 1) * D],
                                                    ht[:, p, f, u * P:(u + 1) * P], w2_sb[:, p, f, :],
                                                    start=(f == 0), stop=(f == FC - 1))
                    last.then_inc(out_ready, 1)

                pe.wait_ge(slots_made, 1)
                turn(0, 0, PAIR)

                def product_steps(jj, p, before, size, after):
                    hidden(jj, p, size)
                    if after:
                        turn(jj + p, 1 - p, after)
                    if before:
                        output(jj + p - 1, 1 - p, before)

                over_tiles_in_turn(pe, product_steps)
                output((tiles - 1) // 2, (tiles - 1) % 2, size_of(tiles - 1))
                if norm_behind:
                    for j in range(PAIRS):
                        norm_turn(pe, j, tiles_of(core["xn"]))

            @block.scalar
            def _(act):
                act.wait_ge(weights_in, weights_total)
                for g in range(T // 512):
                    act.wait_ge(raw_ready, g + 1)
                    copy_bank(nc, raw[:, g * 512:(g + 1) * 512], ps[0:E, g, :]).then_inc(raw_stored, 1)
                act.wait_ge(shifted, 1)
                nc.scalar.activation(pr[:, :, :], pr[:, :, :], ACT.Exp).then_inc(exped, 1)
                if shared:
                    for n in range(SC * PAIRS):
                        act.wait_ge(s_clipped, n + 1)
                        nc.scalar.activation(sg[:, n % 4, :], sg[:, n % 4, :], ACT.Silu).then_inc(s_silued, 1)

                def store_rows(jj, p, size):
                    t = 2 * jj + p
                    act.wait_ge(rows_turned, t + 1)
                    if later(t):
                        act.wait_ge(hid_ready, FC * (t - 1))
                    if affine:
                        for c in range(DC):
                            last = nc.scalar.activation(xrt[:, p, c, 0:size], ps[:, 7, c * PAIR:c * PAIR + size], ACT.Identity,
                                                        bias=gb[:, 1, c:c + 1], scale=gb[:, 0, c:c + 1])
                    else:
                        last = copy_bank(nc, xrt[:, p].rearrange("p c n -> p (c n)"), ps[:, 7, :])
                    last.then_inc(rows_stored, 1)

                def activate(jj, p, size):
                    t = 2 * jj + p
                    for f in range(FC):
                        if swiglu:
                            act.wait_ge(clipped, FC * t + (f + 1))
                            nc.scalar.activation(sg[:, f % 4, 0:size], sg[:, f % 4, 0:size], ACT.Silu).then_inc(silued, 1)
                        else:
                            act.wait_ge(hid_ready, FC * t + (f + 1))
                            if f == 0 and later(t):
                                act.wait_ge(out_ready, t - 1)
                            nc.scalar.activation(ht[:, p, f, :], ps[:, f % 4, 0:PAIR], ACT.Relu).then_inc(hid_stored, 1)

                def store_y(jj, p, size):
                    t = 2 * jj + p
                    act.wait_ge(out_ready, t + 1)
                    if later(t):
                        act.wait_ge(y_sent[p], 16 * jj)
                    copy_bank(nc, yt[:, p, 0:size // P].rearrange("p u d -> p (u d)"),
                              ps[:, 4 + p, 0:size // P * D]).then_inc(y_stored, 1)

                store_rows(0, 0, PAIR)

                def activation_steps(jj, p, before, size, after):
                    activate(jj, p, size)
                    if after:
                        store_rows(jj + p, 1 - p, after)
                    if before:
                        store_y(jj + p - 1, 1 - p, before)

                over_tiles_in_turn(act, activation_steps)
                store_y((tiles - 1) // 2, (tiles - 1) % 2, size_of(tiles - 1))
                if norm_behind:
                    for j in range(PAIRS):
                        norm_store(act, j, [(core["xt"], None, None)])

            @block.vector
            def _(dve):
                def over_experts(x):
                    return x.unsqueeze(2).to_broadcast([P, TILES, E])

                def over_tiles(x):
                    return x.unsqueeze(1).to_broadcast([P, TILES, E])

                tt, stt, ts = nc.vector.tensor_tensor, nc.vector.scalar_tensor_tensor, nc.vector.tensor_scalar
                reduce = nc.vector.tensor_reduce
                dve.wait_ge(logits_ready, 1)
                logits = ps[:, 4, 0:TILES * E].rearrange("p (t e) -> p t e", e=E)
                reduce(col[:, 0, :], logits, AX_X, ALU.max)
                dve.drain()
                tt(pr[:, :, :], logits, over_experts(col[:, 0, :]), ALU.subtract).then_inc(shifted, 1)
                dve.wait_ge(exped, 1)
                reduce(col[:, 0, :], pr[:, :, :], AX_X, ALU.add)
                dve.drain()
                nc.vector.reciprocal(col[:, 0, :], col[:, 0, :])
                dve.drain()
                tt(pr[:, :, :], pr[:, :, :], over_experts(col[:, 0, :]), ALU.mult)
                dve.wait_ge(made, 6)
                for k in range(top):
                    dve.drain()
                    reduce(best[:, k, :], pr[:, :, :], AX_X, ALU.max)
                    dve.drain()
                    tt(eq[:, :, :], pr[:, :, :], over_experts(best[:, k, :]), ALU.is_equal)
                    dve.drain()
                    stt(eq[:, :, :], eq[:, :, :], -float(E), over_tiles(iota_e[:, :]), ALU.mult, ALU.add)
                    dve.drain()
                    reduce(col[:, 1, :], eq[:, :, :], AX_X, ALU.min)
                    dve.drain()
                    tt(hot[k][:, :, :], eq[:, :, :], over_experts(col[:, 1, :]), ALU.is_equal)
                    dve.drain()
                    if k + 1 < top:
                        stt(pr[:, :, :], hot[k][:, :, :], -2.0, pr[:, :, :], ALU.mult, ALU.add)
                if top == 1:
                    nc.vector.tensor_copy(hots[:, :, :], hot[0][:, :, :]).then_inc(chosen, 1)
                    ts(weight[:, 0, :], best[:, 0, :], gate, None, ALU.mult)
                else:
                    tt(hots[:, :, :], hot[0][:, :, :], hot[1][:, :, :], ALU.add).then_inc(chosen, 1)
                    tt(col[:, 0, :], best[:, 0, :], best[:, 1, :], ALU.add)
                    dve.drain()
                    nc.vector.reciprocal(col[:, 0, :], col[:, 0, :])
                    dve.drain()
                    for k in range(2):
                        stt(weight[:, k, :], best[:, k, :], gate, col[:, 0, :], ALU.mult, ALU.mult)
                dve.wait_ge(counted, 1)
                counts = ps[:, 6, 0:TILES * E].rearrange("p (t e) -> p t e", e=E)
                nc.vector.tensor_copy(total[:, :, :], counts)
                nc.vector.tensor_copy(scan[0][:, :, :], counts)
                dve.drain()
                for n, step in enumerate((1, 2, 4, 8)):
                    x, y = scan[n % 2], scan[1 - n % 2]
                    nc.vector.tensor_copy(y[:, 0:step, :], x[:, 0:step, :])
                    tt(y[:, step:, :], x[:, step:, :], x[:, 0:TILES - step, :], ALU.add)
                    dve.drain()
                if capacity:
                    ts(begin[:, :], iota_e[:, :], float(capacity), None, ALU.mult)
                else:
                    def running_sums(x):
                        nc.vector.tensor_copy(sums[0][:, :], x[:, :])
                        dve.drain()
                        for n, step in enumerate((1, 2, 4)):
                            src, dst = (sums[0], sums[1], sums[0])[n], (sums[1], sums[0], sums[2])[n]
                            nc.vector.tensor_copy(dst[:, 0:step], src[:, 0:step])
                            tt(dst[:, step:], src[:, step:], src[:, 0:E - step], ALU.add)
                            dve.drain()

                    def shifted_down(dst, src, add, bits):
                        ts(whole_i[:, :], src[:, :], float(add), None, ALU.add)
                        dve.drain()
                        ts(whole_i[:, :], whole_i[:, :], bits, None, ALU.arith_shift_right)
                        dve.drain()
                        nc.vector.tensor_copy(dst[:, :], whole_i[:, :])
                        dve.drain()

                    def granted(dst, room_before, want):
                        stt(dst[:, :], room_before[:, :], 0.0, want[:, :], ALU.max, ALU.min)
                        dve.drain()

                    nc.vector.tensor_copy(rows_f[:, :], scan[0][:, TILES - 1, :])
                    dve.drain()
                    shifted_down(wanted, rows_f, 0, 8)
                    running_sums(wanted)
                    ts(left_over[:, :], sums[2][:, E - 1:E].to_broadcast([P, E]), -1.0, float(full), ALU.mult, ALU.add)
                    tt(room[:, :], wanted[:, :], sums[2][:, :], ALU.subtract)
                    dve.drain()
                    ts(room[:, :], room[:, :], float(full), None, ALU.add)
                    stt(left[:, :], wanted[:, :], float(-PAIR), rows_f[:, :], ALU.mult, ALU.add)
                    dve.drain()
                    granted(fulls, room, wanted)
                    ts(wanted[:, :], left[:, :], float(P + 1), None, ALU.is_ge)
                    dve.drain()
                    running_sums(wanted)
                    tt(room[:, :], wanted[:, :], sums[2][:, :], ALU.subtract)
                    dve.drain()
                    tt(room[:, :], room[:, :], left_over[:, :], ALU.add)
                    dve.drain()
                    granted(left, room, wanted)
                    tt(fulls[:, :], fulls[:, :], left[:, :], ALU.add)
                    dve.drain()
                    ts(beyond[:, :], fulls[:, :], float(PAIR), None, ALU.mult)
                    dve.drain()
                    tt(left[:, :], rows_f[:, :], beyond[:, :], ALU.subtract)
                    dve.drain()
                    ts(left[:, :], left[:, :], 0.0, None, ALU.max)
                    dve.drain()
                    shifted_down(halves, left, P - 1, 7)

                    for first_tile, n, mine in ((0, full, fulls), (full, half, halves)):
                        running_sums(mine)
                        tt(owner[:, 0:n, :], iota_t[:, 0:n].unsqueeze(2).to_broadcast([P, n, E]),
                           sums[2][:, :].unsqueeze(1).to_broadcast([P, n, E]), ALU.is_ge)
                        dve.drain()
                        reduce(owner_f[:, first_tile:first_tile + n], owner[:, 0:n, :], AX_X, ALU.add)
                        dst = begin if mine is fulls else jump
                        tt(dst[:, :], sums[2][:, :], mine[:, :], ALU.subtract)
                        dve.drain()
                        ts(dst[:, :], dst[:, :], float(PAIR if mine is fulls else P), None, ALU.mult)
                        dve.drain()
                    ts(owner_i[:, :], owner_f[:, :], float(E - 1), None, ALU.min).then_inc(owners_made, 1)
                    stt(jump[:, :], jump[:, :], float(full * PAIR), beyond[:, :], ALU.add, ALU.subtract)
                    dve.drain()
                    tt(jump[:, :], jump[:, :], begin[:, :], ALU.subtract)
                tt(scan[0][:, :, :], scan[0][:, :, :], total[:, :, :], ALU.subtract)
                dve.drain()
                tt(scan[0][:, :, :], scan[0][:, :, :], ps[:, 5, 0:TILES * E].rearrange("p (t e) -> p t e", e=E), ALU.add)
                dve.drain()
                tt(scan[1][:, :, :], scan[0][:, :, :], over_tiles(begin[:, :]), ALU.add)
                if not capacity:
                    tt(eq[:, :, :], scan[0][:, :, :], over_tiles(beyond[:, :]), ALU.is_ge)
                    dve.drain()
                    tt(eq[:, :, :], eq[:, :, :], over_tiles(jump[:, :]), ALU.mult)
                    dve.drain()
                    tt(scan[1][:, :, :], scan[1][:, :, :], eq[:, :, :], ALU.add)
                dve.drain()
                for k in range(top):
                    tt(eq[:, :, :], hot[k][:, :, :], scan[1][:, :, :], ALU.mult)
                    dve.drain()
                    reduce(slot_f[:, :], eq[:, :, :], AX_X, ALU.add)
                    dve.drain()
                    if capacity:
                        tt(eq[:, :, :], hot[k][:, :, :], scan[0][:, :, :], ALU.mult)
                        dve.drain()
                        reduce(col[:, 0, :], eq[:, :, :], AX_X, ALU.add)
                        dve.drain()
                        ts(col[:, 0, :], col[:, 0, :], float(capacity), None, ALU.is_lt)
                        dve.drain()
                        stt(slot_f[:, :], slot_f[:, :], float(-ROWS), col[:, 0, :], ALU.add, ALU.mult)
                        dve.drain()
                        ts(slot_f[:, :], slot_f[:, :], float(ROWS), None, ALU.add)
                        dve.drain()
                    last = nc.vector.tensor_copy(slot[:, k, :], slot_f[:, :])
                    dve.drain()
                nc.vector.tensor_copy(slot_f[:, :], slot_f[:, :]).then_inc(slots_made, 1)

                if shared:
                    def s_clip(n):
                        dve.wait_ge(s_hid_ready, n + 1)
                        ts(sg[:, n % 4, :], ps[:, 1 + n % 2, 0:PAIR], 10.0, -10.0, ALU.min,
                           ALU.max).then_inc(s_clipped, 1)

                    def s_multiply(n):
                        q = n // SC
                        dve.wait_ge(s_silued, n + 1)
                        if q >= 2:
                            dve.wait_ge(s_out_ready, q - 1)
                        tt(ht[:, q % 2, n % SC, :], sg[:, n % 4, :], ps[:, 1 + n % 2, PAIR:2 * PAIR],
                           ALU.mult).then_inc(s_hid_stored, 1)

                    for j in range(PAIRS + 1):
                        if j < PAIRS:
                            s_clip(2 * j)
                            s_clip(2 * j + 1)
                            s_multiply(2 * j)
                            s_multiply(2 * j + 1)
                        if j >= 1:
                            q = j - 1
                            dve.wait_ge(s_out_ready, j)
                            x2 = core["x"][:, 2 * q:2 * q + 2, :].rearrange("p u d -> p (u d)")
                            stt(x2, ps[:, 3 + q % 2, :], gate, x2, ALU.mult, ALU.add).then_inc(s_added, 1)

                if swiglu:
                    def clip(t, f, size):
                        dve.wait_ge(hid_ready, FC * t + (f + 1))
                        ts(sg[:, f % 4, 0:size], ps[:, f % 4, 0:size], 10.0, -10.0, ALU.min, ALU.max).then_inc(clipped, 1)

                    def multiply(t, p, f, size):
                        dve.wait_ge(silued, FC * t + (f + 1))
                        if f == 0 and later(t):
                            dve.wait_ge(out_ready, t - 1)
                        tt(ht[:, p, f, 0:size], sg[:, f % 4, 0:size], ps[:, f % 4, PAIR:PAIR + size], ALU.mult).then_inc(hid_stored, 1)

                    def gates(jj, p, before, size, after):
                        t = 2 * jj + p
                        clip(t, 0, size)
                        for f in range(1, FC):
                            clip(t, f, size)
                            multiply(t, p, f - 1, size)
                        multiply(t, p, FC - 1, size)

                    over_tiles_in_turn(dve, gates)
                for n in range(TILES * top):
                    i, k = n // top, n % top
                    dve.wait_ge(gathered[n % 4], 16 * (n // 4 + 1))
                    stt(core["x"][:, i, :], yg[:, n % 4, :], weight[:, k, i:i + 1], core["x"][:, i, :], ALU.mult,
                        ALU.add).then_inc(added, 1)
                    dve.drain()
                    if norm_behind and n % (2 * top) == 2 * top - 1:
                        j = n // (2 * top)
                        norm_measure(dve, j, tiles_of(core["x"]))
                        norm_normalise(dve, j, tiles_of(core["x"]), tiles_of(core["xn"]))
        clear_semaphores()


def one_head_weights(a):
    def make(carve):
        wq, wq_t = carve([P, DC, D]), carve([P, DC, D])
        wk, wv = carve([P, D]), carve([P, D])
        bq, bk, bv = carve([P, DC]), carve([P, DC]), carve([P, D])
        loads = [(wq[:, :, :], a["L1_xattn_Wq"].rearrange("(c p) n -> p c n", p=P)), (wk[:, :], a["L1_xattn_Wk"]),
                 (wv[:, :], a["L1_xattn_Wv"]), (bq[:, :], columns(a["L1_xattn_bq"])),
                 (bk[:, :], columns(a["L1_xattn_bk"])), (bv[:, :], rows(a["L1_xattn_bv"]))]
        return loads, (wq, wq_t, wk, wv, bq, bk, bv)
    return make


def stage_one_head(core, a, plan, following):
    nc, ps = core["nc"], core["ps"]
    gate = core["gate_attn"][:, 1:2]
    BK = B * KEYS
    with ExitStack() as ctx:
        _, weights_in, weights_total, (wq, wq_t, wk, wv, bq, bk, bv) = plan

        def sb(part, shape):
            return ctx.enter_context(nc.sbuf_tensor(f"l1a_{part}", shape, F32))

        sem, clear_semaphores = named_semaphores(nc, "l1a")
        zeroed, w_ready, w_stored = sem("zeroed"), sem("w_ready"), sem("w_stored")
        kv_ready, kv_stored, fold_ready, fold_stored = sem("kv_ready"), sem("kv_stored"), sem("fold_ready"), sem("fold_stored")
        values_made = sem("values_made")
        scores_ready, centred, exped = sem("scores_ready"), sem("centred"), sem("exped")
        probs_ready, probs_turned, probs_stored = sem("probs_ready"), sem("probs_turned"), sem("probs_stored")
        out_ready, out_added = sem("out_ready"), sem("out_added")
        (norm_measure, norm_root, norm_normalise, norm_turn, norm_store,
         norm_stored) = layer_norm(core, ctx, sem, "l1a_norm", on_vector=True, two_pairs=True)
        bq_wide = sb("bq_wide", [P, DC, P])
        keys_t, values = sb("keys_t", [P, DC, BK]), sb("values", [P, D])
        fold_q, score_bias = sb("fold_q", [P, DC, BK]), sb("score_bias", [P, BK])
        ex = sb("ex", [P, B, 2, 2, BK])
        mx, sm = sb("mx", [P, 2, 2]), sb("sm", [P, 2, 2])
        pt = sb("pt", [P, 2, PAIR])
        def own(j):
            b = j // (PAIRS // B)
            return ex[:, b, j % 2, :, b * KEYS:(b + 1) * KEYS]

        with nc.Block() as block:
            @block.sync
            def _(sp):
                fetch(sp, following)

            @block.gpsimd
            def _(pool):
                nc.gpsimd.memset(ex[:, :, :, :, :], 0.0).then_inc(zeroed, 1)

            @block.tensor
            def _(pe):
                pe.wait_ge(weights_in, weights_total)
                for ec in range(DC):
                    for dc in range(DC):
                        last = nc.tensor.transpose(ps[:, 0, ec * D + dc * P:ec * D + (dc + 1) * P],
                                                   wq[:, dc, ec * P:(ec + 1) * P], core["ident"][:, :])
                last.then_inc(w_ready, 1)
                for ec in range(DC):
                    nc.tensor.matmul(ps[:, 1, ec * BK:(ec + 1) * BK], wk[:, ec * P:(ec + 1) * P], core["ctx_t"][:, :],
                                     start=True, stop=True)
                nc.tensor.matmul(ps[:, 2, 0:D], core["ctx_t"][:, :], wv[:, :], start=True, stop=True).then_inc(kv_ready, 1)
                pe.wait_ge(w_stored, 1)
                pe.wait_ge(kv_stored, 1)
                pe.wait_ge(values_made, 1)
                for dc in range(DC):
                    for ec in range(DC):
                        nc.tensor.matmul(ps[:, 3, dc * BK:(dc + 1) * BK], wq_t[:, ec, dc * P:(dc + 1) * P],
                                         keys_t[:, ec, :], start=(ec == 0), stop=(ec == DC - 1))
                for ec in range(DC):
                    last = nc.tensor.matmul(ps[:, 4, 0:BK], bq_wide[:, ec, :], keys_t[:, ec, :],
                                            start=(ec == 0), stop=(ec == DC - 1))
                last.then_inc(fold_ready, 1)
                pe.wait_ge(fold_stored, 2)
                for j in range(PAIRS + 4):
                    if j < PAIRS:
                        b = j // (PAIRS // B)
                        if j >= 2:
                            pe.wait_ge(centred, j - 1)
                        for u in range(2):
                            i = 2 * j + u
                            for dc in range(DC):
                                last = nc.tensor.matmul(ps[:, j % 2, u * KEYS:(u + 1) * KEYS],
                                                        core["xt"][:, dc, i * P:(i + 1) * P],
                                                        fold_q[:, dc, b * KEYS:(b + 1) * KEYS],
                                                        start=(dc == 0), stop=(dc == DC - 1))
                        last.then_inc(scores_ready, 1)
                    if 1 <= j <= PAIRS:
                        k = j - 1
                        pe.wait_ge(probs_ready, k + 1)
                        if k >= 1:
                            pe.wait_ge(probs_stored, k)
                        for u in range(2):
                            last = nc.tensor.transpose(ps[:, 4, u * P:(u + 1) * P],
                                                       ex[:, k // (PAIRS // B), k % 2, u, :], core["ident"][:, :])
                        last.then_inc(probs_turned, 1)
                    if j >= 4:
                        norm_turn(pe, j - 4, tiles_of(core["xn"]))
                    if 2 <= j <= PAIRS + 1:
                        k = j - 2
                        pe.wait_ge(probs_stored, k + 1)
                        if k >= 2:
                            pe.wait_ge(out_added, k - 1)
                        for u in range(2):
                            last = nc.tensor.matmul(ps[:, 5 + k % 2, u * D:(u + 1) * D], pt[:, k % 2, u * P:(u + 1) * P],
                                                    values[:, :], start=True, stop=True)
                        last.then_inc(out_ready, 1)

            @block.scalar
            def _(act):
                act.wait_ge(w_ready, 1)
                copy_bank(nc, wq_t[:, :, :].rearrange("p c d -> p (c d)"), ps[:, 0, :]).then_inc(w_stored, 1)
                act.wait_ge(kv_ready, 1)
                for ec in range(DC):
                    last = nc.scalar.activation(keys_t[:, ec, :], ps[:, 1, ec * BK:(ec + 1) * BK], ACT.Identity,
                                                bias=bk[:, ec:ec + 1])
                last.then_inc(kv_stored, 1)
                act.wait_ge(fold_ready, 1)
                copy_bank(nc, fold_q[:, :, :].rearrange("p c k -> p (c k)"), ps[:, 3, 0:DC * BK]).then_inc(fold_stored, 1)
                copy_bank(nc, score_bias[:, :], ps[:, 4, 0:BK]).then_inc(fold_stored, 1)
                for j in range(PAIRS + 4):
                    if j < PAIRS:
                        act.wait_ge(centred, j + 1)
                        nc.scalar.activation(own(j), own(j), ACT.Exp).then_inc(exped, 1)
                    if 1 <= j <= PAIRS:
                        k = j - 1
                        act.wait_ge(probs_turned, k + 1)
                        if k >= 2:
                            act.wait_ge(out_ready, k - 1)
                        copy_bank(nc, pt[:, k % 2, :], ps[:, 4, 0:PAIR]).then_inc(probs_stored, 1)
                    if j >= 4:
                        norm_store(act, j - 4, [(core["xt"], None, None)])

            @block.vector
            def _(dve):
                dve.wait_ge(weights_in, weights_total)
                nc.vector.tensor_copy(bq_wide[:, :, :], bq[:, :].unsqueeze(2).to_broadcast([P, DC, P]))
                dve.wait_ge(kv_ready, 1)
                nc.vector.tensor_tensor(values[:, :], ps[:, 2, 0:D], bv[:, :], ALU.add).then_inc(values_made, 1)
                dve.wait_ge(fold_stored, 2)
                dve.wait_ge(zeroed, 1)
                for j in range(PAIRS + 4):
                    if 1 <= j <= PAIRS:
                        k = j - 1
                        dve.wait_ge(exped, k + 1)
                        nc.vector.tensor_reduce(sm[:, k % 2, :], own(k), AX_X, ALU.add)
                        dve.drain()
                        nc.vector.reciprocal(sm[:, k % 2, :], sm[:, k % 2, :])
                        dve.drain()
                        nc.vector.tensor_tensor(own(k), own(k), sm[:, k % 2, :].unsqueeze(2).to_broadcast([P, 2, KEYS]),
                                                ALU.mult).then_inc(probs_ready, 1)
                    if j < PAIRS:
                        b = j // (PAIRS // B)
                        dve.wait_ge(scores_ready, j + 1)
                        if j >= 2:
                            dve.wait_ge(probs_turned, j - 1)
                        nc.vector.tensor_tensor(
                            own(j), ps[:, j % 2, 0:2 * KEYS].rearrange("p (u k) -> p u k", u=2),
                            score_bias[:, b * KEYS:(b + 1) * KEYS].unsqueeze(1).to_broadcast([P, 2, KEYS]), ALU.add)
                        dve.drain()
                        nc.vector.tensor_reduce(mx[:, j % 2, :], own(j), AX_X, ALU.max)
                        dve.drain()
                        nc.vector.tensor_tensor(own(j), own(j), mx[:, j % 2, :].unsqueeze(2).to_broadcast([P, 2, KEYS]),
                                                ALU.subtract).then_inc(centred, 1)
                    if 2 <= j <= PAIRS + 1:
                        k = j - 2
                        dve.wait_ge(out_ready, k + 1)
                        x2 = pair_of(core["x"], k)
                        nc.vector.scalar_tensor_tensor(x2, ps[:, 5 + k % 2, :], gate, x2, ALU.mult,
                                                       ALU.add).then_inc(out_added, 1)
                        dve.drain()
                        norm_measure(dve, k, tiles_of(core["x"]))
                        norm_normalise(dve, k, tiles_of(core["x"]), tiles_of(core["xn"]))
        clear_semaphores()


def adapter_weights(a):
    R = 64

    def make(carve):
        base = carve([P, DC, D])
        base_row = carve([P, D])
        mu, sigma = carve([E, D]), carve([E, D])
        down_b, up_b, conv_b = carve([E, R]), carve([E, D]), carve([E, D])
        loads = [(base[:, :, :], a["L1_ffn_base_W"].rearrange("(c p) d -> p c d", p=P)),
                 (base_row[:, :], rows(a["L1_ffn_base_b"])), (mu[:, :], a["L1_ffn_disc_mu"]),
                 (sigma[:, :], a["L1_ffn_disc_sigma"]), (down_b[:, :], a["L1_ffn_down_b"]),
                 (up_b[:, :], a["L1_ffn_up_b"]), (conv_b[:, :], a["L1_ffn_conv_b"])]
        return loads, (base, base_row, mu, sigma, down_b, up_b, conv_b)
    return make


def stage_adapter(core, a, plan, following):
    nc, ps = core["nc"], core["ps"]
    gate = core["gate_ffn"][:, 1:2]
    R = 64
    with ExitStack() as ctx:
        _, weights_in, weights_total, (base, base_row, mu, sigma, down_b, up_b, conv_b) = plan

        def sb(part, shape, dtype=F32):
            return ctx.enter_context(nc.sbuf_tensor(f"l1f_{part}", shape, dtype))

        sem, clear_semaphores = named_semaphores(nc, "l1f")
        made = sem("made")
        inv_made, inv_turned, sums_made, squares_made = sem("inv_made"), sem("inv_turned"), sem("sums_made"), sem("squares_made")
        means_wide, losses_ready, chosen, hot_turned = sem("means_wide"), sem("losses_ready"), sem("chosen"), sem("hot_turned")
        hot_stored, gathered = sem("hot_stored"), sem("gathered")
        step_ready, step_stored = sem("step_ready"), sem("step_stored")
        const_made, bias_added = sem("const_made"), sem("bias_added")
        hid_ready, hid_stored, out_ready, out_added = sem("hid_ready"), sem("hid_stored"), sem("out_ready"), sem("out_added")
        (norm_measure, norm_root, norm_normalise, norm_turn, norm_store,
         norm_stored) = layer_norm(core, ctx, sem, "l1f_norm", on_vector=True, two_pairs=True)
        base_t = sb("base_t", [P, DC, D])
        inv = sb("inv", [E, 3, D])
        inv_t = sb("inv_t", [P, 3, DC, E])
        sums = sb("sums", [P, 2, DC, B])
        junk = sb("junk", [P, TOK])
        wide = sb("wide", [P, 3, DC, B, P])
        iota_e, iota_p = sb("iota_e", [P, E]), sb("iota_p", [P, 1])
        loss, cand, hot = sb("loss", [P, B, E]), sb("cand", [P, B, E]), sb("hot", [P, B, E])
        low, index = sb("low", [P, B]), sb("index", [P, B])
        where_f = sb("where_f", [P, 3, B])
        where = sb("where", [P, 3, B], I32)
        hot_t = sb("hot_t", [E, B, P])
        down = sb("down", [P, B, DC, P])
        conv, up = sb("conv", [P, B, DC, D]), sb("up", [R, B, D])
        conv_t, up_t = sb("conv_t", [P, B, DC, D]), sb("up_t", [P, B, DC, P])
        up_wide = sb("up_wide", [P, DC, B, P])
        down_col = sb("down_col", [P, B])
        fold = sb("fold", [P, B, D])
        const = sb("const", [P, B, D])
        ht = sb("ht", [P, 2, PAIR])
        down_rows = a["L1_ffn_down_W"].rearrange("e d r -> (e d) r")
        conv_rows = a["L1_ffn_conv_W"].rearrange("e o d -> (e o) d")
        up_rows = a["L1_ffn_up_W"].rearrange("e r d -> (e r) d")
        GATHERS = B * (2 * DC + 1)

        def turned(dst_part, src, ident_rows, cols):
            return lambda bank: nc.tensor.transpose(ps[0:cols, bank, dst_part:dst_part + ident_rows], src,
                                                    core["ident"][0:ident_rows, 0:ident_rows])

        def product(rows_n, c0, cols, parts):
            def go(bank):
                for n, (lhs, rhs) in enumerate(parts):
                    last = nc.tensor.matmul(ps[0:rows_n, bank, c0:c0 + cols], lhs, rhs, start=(n == 0),
                                            stop=(n == len(parts) - 1))
                return last
            return go

        steps = [([turned(dc * D + oc * P, base[:, oc, dc * P:(dc + 1) * P], P, P) for dc in range(DC) for oc in range(DC)],
                  P, 2 * D, base_t[:, :, :].rearrange("p c d -> p (c d)"))]
        for b in range(B):
            steps.append(([turned(dc * D + oc * P, conv[:, b, oc, dc * P:(dc + 1) * P], P, P)
                           for dc in range(DC) for oc in range(DC)], P, 2 * D,
                          conv_t[:, b].rearrange("p c d -> p (c d)")))
            for dc in range(DC):
                steps.append(([turned(0, up[:, b, dc * P:(dc + 1) * P], R, P)], P, R, up_t[:, b, dc, 0:R]))
        for dc in range(DC):
            steps.append(([product(P, 0, B * P, [(up_b[:, dc * P:(dc + 1) * P], hot_t[:, :, :].rearrange("e b n -> e (b n)"))])],
                          P, B * P, up_wide[:, dc].rearrange("p b n -> p (b n)")))
        steps.append(([product(R, 0, B * P, [(down_b[:, :], hot_t[:, :, :].rearrange("e b n -> e (b n)"))])], R, B * P, None))
        for b in range(B):
            steps.append(([product(P, 0, D, [(up_t[:, b, dc, :], conv_t[:, b, dc, :]) for dc in range(DC)])],
                          P, D, fold[:, b, :]))
            steps.append(([product(P, 0, D, [(up_wide[:, dc, b, :], conv_t[:, b, dc, :]) for dc in range(DC)]
                                   + [(hot_t[:, b, :], conv_b[:, :])])], P, D, const[:, b, :]))

        with nc.Block() as block:
            @block.sync
            def _(sp):
                fetch(sp, following)

            @block.gpsimd
            def _(pool):
                nc.gpsimd.memset(down[:, :, :, :], 0.0).then_inc(made, 1)
                nc.gpsimd.memset(up_t[:, :, :, :], 0.0).then_inc(made, 1)
                nc.gpsimd.memset(wide[:, 2], 1.0).then_inc(made, 1)
                nc.gpsimd.memset(down_col[:, :], 0.0).then_inc(made, 1)
                nc.gpsimd.iota(iota_e[:, :], [[1, E]], base=0, channel_multiplier=0,
                               allow_small_or_imprecise_dtypes=True).then_inc(made, 1)
                nc.gpsimd.iota(iota_p[:, :], [[0, 1]], base=0, channel_multiplier=1,
                               allow_small_or_imprecise_dtypes=True).then_inc(made, 1)
                pool.wait_ge(made, 6)
                pool.wait_ge(chosen, 2)

                def gather(dst, src, index, bound):
                    pool.indirect_dma_start(dst, None, src, bass.IndirectOffsetOnAxis(ap=index, axis=0),
                                            bounds_check=bound - 1, oob_is_err=False).then_inc(gathered, 16)

                for b in range(B):
                    for c in range(DC):
                        gather(conv[:, b, c, :], conv_rows, where[:, c, b:b + 1], E * D)
                        gather(down[:, b, c, 0:R], down_rows, where[:, c, b:b + 1], E * D)
                    gather(up[:, b, :], up_rows, where[0:R, 2, b:b + 1], E * R)
                pool.wait_ge(const_made, 1)
                for j in range(PAIRS):
                    for u in range(2):
                        i = 2 * j + u
                        last = nc.gpsimd.tensor_tensor(core["x"][:, i, :], core["x"][:, i, :], const[:, j // (PAIRS // B), :], ALU.add)
                    last.then_inc(bias_added, 1)

            @block.tensor
            def _(pe):
                pe.wait_ge(inv_made, 1)
                for k in range(3):
                    for dc in range(DC):
                        last = nc.tensor.transpose(ps[:, 2, (k * DC + dc) * E:(k * DC + dc + 1) * E],
                                                   inv[:, k, dc * P:(dc + 1) * P], core["ident"][0:E, 0:E])
                last.then_inc(inv_turned, 1)
                pe.wait_ge(means_wide, 2)
                for b in range(B):
                    for n in range(3 * DC):
                        k, dc = n // DC, n % DC
                        last = nc.tensor.matmul(ps[:, 3, b * E:(b + 1) * E], wide[:, k, dc, b, :], inv_t[:, k, dc, :],
                                                start=(n == 0), stop=(n == 3 * DC - 1))
                last.then_inc(losses_ready, 1)
                pe.wait_ge(chosen, 1)
                for b in range(B):
                    last = nc.tensor.transpose(ps[0:E, 2, b * P:(b + 1) * P], hot[:, b, :], core["ident"][:, :])
                last.then_inc(hot_turned, 1)
                pe.wait_ge(hot_stored, 1)
                for n, (emit, _, _, _) in enumerate(steps):
                    if n == 1:
                        pe.wait_ge(gathered, 16 * GATHERS)
                    if n >= 2:
                        pe.wait_ge(step_stored, n - 1)
                    if n >= 7 + DC + 1:
                        pe.wait_ge(step_stored, n if n == 7 + DC + 1 else n - 1)
                    for go in emit:
                        last = go(n % 2)
                    last.then_inc(step_ready, 1)
                pe.wait_ge(step_stored, len(steps))
                for j in range(PAIRS + 3):
                    if j < PAIRS:
                        b = j // (PAIRS // B)
                        if j >= 2:
                            pe.wait_ge(hid_stored, j - 1)
                        for dc in range(DC):
                            last = nc.tensor.matmul(ps[:, 2 + j % 2, 0:PAIR], down[:, b, dc, :],
                                                    core["xt"][:, dc, PAIR * j:PAIR * (j + 1)],
                                                    start=(dc == 0), stop=(dc == DC - 1))
                        last.then_inc(hid_ready, 1)
                    if 1 <= j <= PAIRS:
                        k = j - 1
                        pe.wait_ge(hid_stored, k + 1)
                        if k >= 2:
                            pe.wait_ge(out_added, k - 1)
                        for u in range(2):
                            i = 2 * k + u
                            out = ps[:, 4 + k % 2, u * D:(u + 1) * D]
                            for dc in range(DC):
                                nc.tensor.matmul(out, core["xt"][:, dc, i * P:(i + 1) * P], base_t[:, dc, :],
                                                 start=(dc == 0), stop=False)
                            last = nc.tensor.matmul(out, ht[:, k % 2, u * P:(u + 1) * P], fold[:, k // (PAIRS // B), :],
                                                    start=False, stop=True)
                        last.then_inc(out_ready, 1)
                    if j >= 3:
                        norm_turn(pe, j - 3, tiles_of(core["xn"]))

            @block.scalar
            def _(act):
                for dc in range(DC):
                    for b in range(B):
                        last = nc.scalar.activation(junk[:, :], core["xt"][:, dc, b * TOK:(b + 1) * TOK], ACT.Square,
                                                    accum_out=sums[:, 1, dc, b:b + 1])
                        act.drain()
                nc.scalar.activation(junk[:, 0:1], core["xt"][:, 0, 0:1], ACT.Copy).then_inc(squares_made, 1)
                act.wait_ge(inv_turned, 1)
                copy_bank(nc, inv_t[:, :, :, :].rearrange("p k c e -> p (k c e)"), ps[:, 2, 0:3 * DC * E]).then_inc(means_wide, 1)
                act.wait_ge(hot_turned, 1)
                copy_bank(nc, hot_t[:, :, :].rearrange("e b n -> e (b n)"), ps[0:E, 2, 0:B * P]).then_inc(hot_stored, 1)
                act.wait_ge(made, 6)
                for n, (_, rows_n, cols, dst) in enumerate(steps):
                    act.wait_ge(step_ready, n + 1)
                    if dst is None:
                        last = nc.scalar.activation(
                            down_col[0:R, :], ps[0:R, n % 2, 0:B * P].rearrange("p (b n) -> p b n", b=B)[:, :, 0], ACT.Copy)
                    else:
                        last = copy_bank(nc, dst, ps[0:rows_n, n % 2, 0:cols])
                    last.then_inc(step_stored, 1)
                for j in range(PAIRS + 3):
                    if j < PAIRS:
                        act.wait_ge(hid_ready, j + 1)
                        if j >= 2:
                            act.wait_ge(out_ready, j - 1)
                        nc.scalar.activation(ht[:, j % 2, :], ps[:, 2 + j % 2, 0:PAIR], ACT.Relu,
                                             bias=down_col[:, j // (PAIRS // B):j // (PAIRS // B) + 1]).then_inc(hid_stored, 1)
                    if j >= 3:
                        norm_store(act, j - 3, [(core["xt"], None, None)])

            @block.vector
            def _(dve):
                tt, ts = nc.vector.tensor_tensor, nc.vector.tensor_scalar
                dve.wait_ge(weights_in, weights_total)
                tt(sigma[:, :], sigma[:, :], sigma[:, :], ALU.mult)
                dve.drain()
                nc.vector.reciprocal(inv[:, 0, :], sigma[:, :])
                dve.drain()
                tt(inv[:, 1, :], mu[:, :], inv[:, 0, :], ALU.mult)
                dve.drain()
                tt(inv[:, 2, :], mu[:, :], inv[:, 1, :], ALU.mult)
                dve.drain()
                ts(inv[:, 1, :], inv[:, 1, :], -2.0, None, ALU.mult).then_inc(inv_made, 1)
                nc.vector.tensor_reduce(sums[:, 0].rearrange("p c b -> p (c b)"),
                                        core["xt"][:, :, :].rearrange("p c (b n) -> p (c b) n", b=B), AX_X, ALU.add)
                dve.drain()
                dve.wait_ge(squares_made, 1)
                dve.wait_ge(made, 6)
                for k in range(2):
                    last = ts(wide[:, k], sums[:, 1 - k].unsqueeze(3).to_broadcast([P, DC, B, P]), 1.0 / TOK, None, ALU.mult)
                last.then_inc(means_wide, 1)
                dve.wait_ge(losses_ready, 1)
                nc.vector.tensor_copy(loss[:, :, :].rearrange("p b e -> p (b e)"), ps[:, 3, 0:B * E])
                dve.drain()
                nc.vector.tensor_reduce(low[:, :], loss[:, :, :], AX_X, ALU.min)
                dve.drain()
                tt(cand[:, :, :], loss[:, :, :], low[:, :].unsqueeze(2).to_broadcast([P, B, E]), ALU.is_equal)
                dve.drain()
                nc.vector.scalar_tensor_tensor(cand[:, :, :], cand[:, :, :], -float(E),
                                               iota_e[:, :].unsqueeze(1).to_broadcast([P, B, E]), ALU.mult, ALU.add)
                dve.drain()
                nc.vector.tensor_reduce(low[:, :], cand[:, :, :], AX_X, ALU.min)
                dve.drain()
                tt(hot[:, :, :], cand[:, :, :], low[:, :].unsqueeze(2).to_broadcast([P, B, E]),
                   ALU.is_equal).then_inc(chosen, 1)
                ts(index[:, :], low[:, :], float(E), None, ALU.add)
                dve.drain()
                for k, (size, first_row) in enumerate(((D, 0), (D, P), (R, 0))):
                    ts(where_f[:, k, :], index[:, :], float(size), float(first_row), ALU.mult, ALU.add)
                dve.drain()
                ts(where_f[:, :, :].rearrange("p k b -> p (k b)"), where_f[:, :, :].rearrange("p k b -> p (k b)"),
                   iota_p[:, 0:1], None, ALU.add)
                dve.drain()
                nc.vector.tensor_copy(where[:, :, :], where_f[:, :, :]).then_inc(chosen, 1)
                dve.wait_ge(step_stored, len(steps))
                tt(const[:, :, :], const[:, :, :], base_row[:, :].unsqueeze(1).to_broadcast([P, B, D]), ALU.add)
                dve.drain()
                ts(const[:, :, :], const[:, :, :], gate, None, ALU.mult).then_inc(const_made, 1)
                for j in range(PAIRS + 3):
                    if 2 <= j <= PAIRS + 1:
                        k = j - 2
                        dve.wait_ge(out_ready, k + 1)
                        dve.wait_ge(bias_added, k + 1)
                        x2 = pair_of(core["x"], k)
                        nc.vector.scalar_tensor_tensor(x2, ps[:, 4 + k % 2, :], gate, x2, ALU.mult,
                                                       ALU.add).then_inc(out_added, 1)
                        dve.drain()
                        norm_measure(dve, k, tiles_of(core["x"]))
                        norm_normalise(dve, k, tiles_of(core["x"]), tiles_of(core["xn"]))
        clear_semaphores()


def layout_l2(a):
    def layout(carve):
        wq_t, wkv, won = carve([P, DC, D]), carve([P, 4, KD]), carve([P, DC, D])
        loads = [(wq_t[:, :, :], a["L2_xattn_Wq"].rearrange("(c p) d -> p c d", p=P)),
                 (wkv[:, :, :], a["L2_xattn_Wkv"].rearrange("(c p) k -> p c k", p=P)),
                 (won[:, :, :], a["L2_xattn_Wo"].rearrange("(c p) n -> p c n", p=P))]

        def finish(sb):
            wkv_t, wo = sb("wkv_t", [P, 2, D]), sb("wo", [P, DC, D])
            turns = [([wkv[:, c, :] for c in range(4)], wkv_t[:, :, :].rearrange("p a n -> p (a n)")),
                     ([won[:, oc, c * P:(c + 1) * P] for c in range(DC) for oc in range(DC)],
                      wo[:, :, :].rearrange("p c n -> p (c n)"))]
            return wq_t, wo, turns, wkv_t[:, 0, :], wkv_t[:, 1, :]
        return loads, finish
    return layout


def low_rank_weights(a):
    R = 64

    def make(carve):
        u1, v1 = carve([P, DC, P]), carve([P, FF])
        u2, v2 = carve([P, FC, P]), carve([P, D])
        b1, b2 = carve([P, FC]), carve([P, D])
        loads = [(u1[:, :, 0:R], a["L2_ffn_U1"].rearrange("(c p) r -> p c r", p=P)), (v1[0:R, :], a["L2_ffn_V1"]),
                 (u2[:, :, 0:R], a["L2_ffn_U2"].rearrange("(c p) r -> p c r", p=P)), (v2[0:R, :], a["L2_ffn_V2"]),
                 (b1[:, :], columns(a["L2_ffn_b1"])), (b2[:, :], rows(a["L2_ffn_b2"]))]
        return loads, (u1, v1, u2, v2, b1, b2)
    return make


def stage_low_rank(core, a, plan, following):
    nc, ps = core["nc"], core["ps"]
    gate = core["gate_ffn"][:, 2:3]
    R = 64
    with ExitStack() as ctx:
        _, weights_in, weights_total, (u1, v1, u2, v2, b1, b2) = plan

        def sb(part, shape):
            return ctx.enter_context(nc.sbuf_tensor(f"l2f_{part}", shape, F32))

        sem, clear_semaphores = named_semaphores(nc, "l2f")
        zeroed, bias_made, bias_added = sem("zeroed"), sem("bias_made"), sem("bias_added")
        p_ready, p_stored, hid_ready, hid_stored = sem("p_ready"), sem("p_stored"), sem("hid_ready"), sem("hid_stored")
        q_ready, q_stored, out_ready, out_added = sem("q_ready"), sem("q_stored"), sem("out_ready"), sem("out_added")
        (norm_measure, norm_root, norm_normalise, norm_turn, norm_store,
         norm_stored) = layer_norm(core, ctx, sem, "l2f_norm", on_vector=True)
        pr = sb("pr", [P, 2, PAIR])
        ht = sb("ht", [P, 2, FC, PAIR])
        qr = sb("qr", [P, 2, PAIR])
        with nc.Block() as block:
            @block.sync
            def _(sp):
                fetch(sp, following)

            @block.gpsimd
            def _(pool):
                for n, padding in enumerate((u1[:, :, R:P], v1[R:P, :], u2[:, :, R:P], v2[R:P, :])):
                    if n >= 1:
                        pool.wait_ge(zeroed, n)
                    nc.gpsimd.memset(padding, 0.0).then_inc(zeroed, 1)
                pool.wait_ge(zeroed, 4)
                pool.wait_ge(bias_made, 1)
                for j in range(PAIRS):
                    for u in range(2):
                        i = 2 * j + u
                        last = nc.gpsimd.tensor_tensor(core["x"][:, i, :], core["x"][:, i, :], b2[:, :], ALU.add)
                    last.then_inc(bias_added, 1)

            @block.tensor
            def _(pe):
                pe.wait_ge(weights_in, weights_total)
                pe.wait_ge(zeroed, 4)

                def first_rank(j):
                    if j >= 2:
                        pe.wait_ge(p_stored, j - 1)
                    for dc in range(DC):
                        last = nc.tensor.matmul(ps[:, 6 + j % 2, 0:PAIR], u1[:, dc, :], core["xt"][:, dc, PAIR * j:PAIR * (j + 1)],
                                                start=(dc == 0), stop=(dc == DC - 1))
                    last.then_inc(p_ready, 1)

                def second_rank(k):
                    pe.wait_ge(hid_stored, FC * (k + 1))
                    if k >= 1:
                        pe.wait_ge(q_stored, k)
                    for f in range(FC):
                        last = nc.tensor.matmul(ps[:, 4, 0:PAIR], u2[:, f, :], ht[:, k % 2, f, :], start=(f == 0),
                                                stop=(f == FC - 1))
                    last.then_inc(q_ready, 1)

                def output(k):
                    pe.wait_ge(q_stored, k + 1)
                    if k >= 1:
                        pe.wait_ge(out_added, k)
                    for u in range(2):
                        last = nc.tensor.matmul(ps[:, 5, u * D:(u + 1) * D], qr[:, k % 2, u * P:(u + 1) * P], v2[:, :],
                                                start=True, stop=True)
                    last.then_inc(out_ready, 1)

                first_rank(0)
                for j in range(PAIRS + 2):
                    if j + 1 < PAIRS:
                        first_rank(j + 1)
                    if j < PAIRS:
                        pe.wait_ge(p_stored, j + 1)
                        for f in range(FC):
                            n = FC * j + f
                            if n >= 4:
                                pe.wait_ge(hid_stored, n - 3)
                            nc.tensor.matmul(ps[:, n % 4, 0:PAIR], v1[:, f * P:(f + 1) * P], pr[:, j % 2, :],
                                             start=True, stop=True).then_inc(hid_ready, 1)
                    if 1 <= j <= PAIRS:
                        second_rank(j - 1)
                    if 2 <= j <= PAIRS + 1:
                        output(j - 2)

            @block.scalar
            def _(act):
                act.wait_ge(weights_in, weights_total)

                def store_p(j):
                    act.wait_ge(p_ready, j + 1)
                    if j >= 2:
                        act.wait_ge(hid_ready, FC * (j - 1))
                    copy_bank(nc, pr[:, j % 2, :], ps[:, 6 + j % 2, 0:PAIR]).then_inc(p_stored, 1)

                store_p(0)
                for j in range(PAIRS + 1):
                    if j + 1 < PAIRS:
                        store_p(j + 1)
                    if j < PAIRS:
                        for f in range(FC):
                            n = FC * j + f
                            act.wait_ge(hid_ready, n + 1)
                            if j >= 2 and f == 0:
                                act.wait_ge(q_ready, j - 1)
                            nc.scalar.activation(ht[:, j % 2, f, :], ps[:, n % 4, 0:PAIR], ACT.Gelu_apprx_tanh,
                                                 bias=b1[:, f:f + 1]).then_inc(hid_stored, 1)
                    if 1 <= j <= PAIRS:
                        k = j - 1
                        act.wait_ge(q_ready, k + 1)
                        if k >= 2:
                            act.wait_ge(out_ready, k - 1)
                        copy_bank(nc, qr[:, k % 2, :], ps[:, 4, 0:PAIR]).then_inc(q_stored, 1)

            @block.vector
            def _(dve):
                dve.wait_ge(weights_in, weights_total)
                nc.vector.tensor_scalar(b2[:, :], b2[:, :], gate, None, ALU.mult).then_inc(bias_made, 1)
                for j in range(PAIRS):
                    dve.wait_ge(out_ready, j + 1)
                    dve.wait_ge(bias_added, j + 1)
                    x2 = pair_of(core["x"], j)
                    nc.vector.scalar_tensor_tensor(x2, ps[:, 5, :], gate, x2, ALU.mult, ALU.add).then_inc(out_added, 1)
                    dve.drain()
                    norm_measure(dve, j, tiles_of(core["x"]))
                    norm_normalise(dve, j, tiles_of(core["x"]), tiles_of(core["xn"]))
        clear_semaphores()


L3_HEADS, L3_WIDTH = 16, 32
GROUP = P // L3_WIDTH
GROUPS = L3_HEADS // GROUP
ENTRIES = B * GROUPS
KC = TOK // P


def self_attention_scratch(nc):
    def dram(name, shape, dtype):
        return nc.dram_tensor(name, shape, dtype, kind="Internal").ap()

    parts = [[dram(f"l3_{kind}_part{m}", [ENTRIES + 1, P, TOK], BF16) for m in range(3)] for kind in ("q", "k")]
    values = dram("l3_values", [ENTRIES + 1, P, KC, P], F32)
    heads_out = dram("l3_heads_out", [ENTRIES, P, TOK], F32)
    return parts, values, heads_out


def self_project_weights(a):
    HD = L3_HEADS * L3_WIDTH

    def make(carve):
        wq, wk, wv = carve([P, DC, HD]), carve([P, DC, HD]), carve([P, DC, HD])
        ln1 = carve([P, 2, D])
        gb = carve([P, 4, DC])
        loads = [(ln1[:, 0, :], rows(a["L3_xattn_ln1_g"])), (ln1[:, 1, :], rows(a["L3_xattn_ln1_b"]))]
        loads += [(gb[:, k, :], columns(a["L3_xattn_a1_" + n])) for k, n in enumerate(("lnx_g", "lnx_b", "lny_g", "lny_b"))]
        loads += [(w[:, c, :].rearrange("p (h d) -> p h d", h=L3_HEADS),
                   a["L3_xattn_a1_" + n].rearrange("h (c p) d -> c p h d", p=P)[c])
                  for w, n in ((wq, "wq"), (wk, "wk"), (wv, "wv")) for c in range(DC)]
        return loads, (wq, wk, wv, ln1, gb)
    return make


SLOTS = (((0, 0, 1, 1), (0, 1, 0, 1)),
         ((0, 2, 1, 2), (2, 0, 2, 1)))
LOADS = 2 * 2 * 4 + 1


def place_entries(nc, ctx):
    stack = [[[ctx.enter_context(nc.sbuf_tensor(f"l3_stack{p}{kind}{s}", [P, GROUP, TOK], BF16)) for s in range(2)]
              for kind in range(2)] for p in range(2)]
    values = ctx.enter_context(nc.sbuf_tensor("l3_values_in", [P, 2, KC, P], F32))
    return [nc.alloc_semaphore("l3_loaded0"), nc.alloc_semaphore("l3_loaded1")], stack, values


def load_entry(sp, scratch, entry, n, p):
    q_k_parts, v_scratch, _ = scratch
    loaded, stack, values = entry
    for kind in range(2):
        for s in range(2):
            for m in range(4):
                src = q_k_parts[kind][SLOTS[s][kind][m]][bass.ds(n, 1)]
                sp.dma_start(stack[p][kind][s][m * L3_WIDTH:(m + 1) * L3_WIDTH, :, :],
                             src.rearrange("a (r d) n -> d (a r) n", d=L3_WIDTH)).then_inc(loaded[p], 16)
    sp.dma_start(values[:, p], v_scratch[bass.ds(n, 1)].rearrange("a p c n -> p (a c) n")).then_inc(loaded[p], 16)


def stage_self_project(core, a, x1, scratch, entry, plan):
    nc, ps = core["nc"], core["ps"]
    q_k_parts, v_scratch, out_scratch = scratch
    HD = L3_HEADS * L3_WIDTH
    BANKS = HD // PAIR
    with ExitStack() as ctx:
        _, weights_in, weights_total, (wq, wk, wv, ln1, gb) = plan

        def sb(part, shape, dtype=F32):
            return ctx.enter_context(nc.sbuf_tensor(f"l3p_{part}", shape, dtype))

        sem, clear_semaphores = named_semaphores(nc, "l3p")
        qk_ready, high_made, rest_made = sem("qk_ready"), sem("high_made"), sem("rest_made")
        mid_made, low_made = sem("mid_made"), sem("low_made")
        v_ready, v_stored = sem("v_ready"), sem("v_stored")
        sent = [sem("sent0"), sem("sent1")]
        (norm1_measure, norm1_root, norm1_normalise, norm1_turn, norm1_store,
         norm1_stored) = layer_norm(core, ctx, sem, "l3p_norm1", on_vector=True)
        (norm2_measure, norm2_root, norm2_normalise, norm2_turn, norm2_store,
         norm2_stored) = layer_norm(core, ctx, sem, "l3p_norm2", on_vector=True)
        yt = sb("yt", [P, DC, T])
        places = [entry[1][1][kind][n][:, 2 * h:2 * h + 2, :].rearrange("p r n -> p (r n)").rearrange("p (m n) -> p m n", n=512)
                  for kind in range(2) for n in range(2) for h in range(2)]
        parts = [places[0:3], places[3:6]]
        rest = sb("rest", [P, 2 * BANKS, 512])
        vs = sb("vs", [P, 2, 2, HD])
        with nc.Block() as block:
            @block.sync
            def _(sp):
                total = [0, 0]
                for k in range(PAIRS):
                    b, p, at = k // (PAIRS // B), k % 2, (k % (PAIRS // B)) * PAIR
                    places = [(b * GROUPS, GROUPS)]
                    if b == 0:
                        places.append((ENTRIES, 1))
                    sp.wait_ge(low_made, 2 * BANKS * (k + 1))
                    for first_entry, groups in places:
                        for kind in range(2):
                            for m in range(3):
                                sp.dma_start(
                                    q_k_parts[kind][m][first_entry:first_entry + groups, :, at:at + PAIR].rearrange("g p n -> p g n"),
                                    parts[p][m][:, kind * BANKS:(kind + 1) * BANKS, :].rearrange(
                                        "p m (g n) -> p (m g) n", n=PAIR)[:, 0:groups, :]).then_inc(sent[p], 16)
                                total[p] += 16
                    sp.wait_ge(v_stored, 2 * (k + 1))
                    for first_entry, groups in places:
                        for u in range(2):
                            sp.dma_start(
                                v_scratch[first_entry:first_entry + groups, :, at // P + u, :].rearrange("g p n -> p g n"),
                                vs[:, p, u, 0:groups * P].rearrange("p (g n) -> p g n", n=P)).then_inc(sent[p], 16)
                            total[p] += 16
                    if k == PAIRS // B - 1:
                        for q in range(2):
                            sp.wait_ge(sent[q], total[q])
                        load_entry(sp, scratch, entry, 0, 0)
                for p in range(2):
                    sp.wait_ge(sent[p], total[p])

            def sent_before(k):
                return sum(16 * 8 * (2 if q < PAIRS // B else 1) for q in range(k % 2, k, 2))

            @block.gpsimd
            def _(pool):
                for k in range(PAIRS):
                    for m in range(2 * BANKS):
                        pool.wait_ge(mid_made, 2 * BANKS * k + m + 1)
                        nc.gpsimd.tensor_tensor(parts[k % 2][2][:, m, :], rest[:, m, :], parts[k % 2][1][:, m, :],
                                                ALU.subtract).then_inc(low_made, 1)

            @block.tensor
            def _(pe):
                pe.wait_ge(weights_in, weights_total)
                for j in range(PAIRS + 1):
                    if j < PAIRS:
                        norm2_turn(pe, j, tiles_of(core["xn"]))
                    if j >= 1:
                        k = j - 1
                        pe.wait_ge(norm2_stored, k + 1)
                        for m in range(2 * BANKS):
                            w, src = (wq, core["xt"]) if m < BANKS else (wk, yt)
                            if k >= 1:
                                pe.wait_ge(rest_made, 2 * BANKS * (k - 1) + m + 1)
                            for h in range(2):
                                g = 2 * (m % BANKS) + h
                                for dc in range(DC):
                                    last = nc.tensor.matmul(ps[:, m, h * PAIR:(h + 1) * PAIR],
                                                            w[:, dc, g * P:(g + 1) * P],
                                                            src[:, dc, PAIR * k:PAIR * (k + 1)],
                                                            start=(dc == 0), stop=(dc == DC - 1))
                            last.then_inc(qk_ready, 1)
                        for u in range(2):
                            if k >= 1:
                                pe.wait_ge(v_stored, 2 * (k - 1) + u + 1)
                            for dc in range(DC):
                                last = nc.tensor.matmul(ps[:, 4 + u, :], yt[:, dc, (2 * k + u) * P:(2 * k + u + 1) * P],
                                                        wv[:, dc, :], start=(dc == 0), stop=(dc == DC - 1))
                            last.then_inc(v_ready, 1)

            @block.scalar
            def _(act):
                act.wait_ge(weights_in, weights_total)

                def high(k, m):
                    n = 2 * BANKS * k + m
                    act.wait_ge(qk_ready, n + 1)
                    if m == 0 and k >= 2:
                        act.wait_ge(sent[k % 2], sent_before(k))
                    nc.scalar.activation(parts[k % 2][0][:, m, :], ps[:, m, :], ACT.Copy,
                                         scale=L3_WIDTH ** -0.5 if m < BANKS else 1.0).then_inc(high_made, 1)

                def mid(k, m):
                    act.wait_ge(rest_made, 2 * BANKS * k + m + 1)
                    copy_bank(nc, parts[k % 2][1][:, m, :], rest[:, m, :]).then_inc(mid_made, 1)

                for j in range(PAIRS + 1):
                    if j < PAIRS:
                        norm2_store(act, j, [(core["xt"], gb[:, 0, :], gb[:, 1, :]), (yt, gb[:, 2, :], gb[:, 3, :])])
                    if j >= 1:
                        k = j - 1
                        high(k, 0)
                        for m in range(1, 2 * BANKS):
                            high(k, m)
                            mid(k, m - 1)
                        mid(k, 2 * BANKS - 1)
                        for u in range(2):
                            act.wait_ge(v_ready, 2 * k + u + 1)
                            copy_bank(nc, vs[:, k % 2, u, :], ps[:, 4 + u, :]).then_inc(v_stored, 1)

            @block.vector
            def _(dve):
                def remainder(k, m):
                    n = 2 * BANKS * k + m
                    dve.wait_ge(high_made, n + 1)
                    if k >= 1:
                        dve.wait_ge(low_made, n - 2 * BANKS + 1)
                    nc.vector.scalar_tensor_tensor(rest[:, m, :], ps[:, m, :], L3_WIDTH ** -0.5 if m < BANKS else 1.0,
                                                   parts[k % 2][0][:, m, :], ALU.mult, ALU.subtract).then_inc(rest_made, 1)

                dve.wait_ge(weights_in, weights_total)
                def both_norms(j):
                    norm1_measure(dve, j, tiles_of(core["xn"]))
                    norm1_normalise(dve, j, tiles_of(core["xn"]), tiles_of(x1))
                    affine_rows(nc, dve, x1[:, 2 * j:2 * j + 2, :], ln1)
                    norm2_measure(dve, j, tiles_of(x1))
                    norm2_normalise(dve, j, tiles_of(x1), tiles_of(core["xn"]))

                both_norms(0)
                both_norms(1)
                for k in range(PAIRS):
                    if k + 2 < PAIRS:
                        both_norms(k + 2)
                    for m in range(2 * BANKS):
                        remainder(k, m)
        clear_semaphores()


def affine_rows(nc, dve, pair, gb):
    for k, op in enumerate((ALU.mult, ALU.add)):
        dve.drain()
        nc.vector.tensor_tensor(pair, pair, gb[:, k, :].unsqueeze(1).to_broadcast([P, 2, D]), op)
    dve.drain()


def stage_self_attention(core, scratch, entry, following):
    nc, ps = core["nc"], core["ps"]
    q_k_parts, v_scratch, out_scratch = scratch
    R, W = GROUP, L3_WIDTH
    BODY = 4
    RING = 8
    TURN = 5
    STORE = TURN
    OUT = TURN + R + 1
    UNITS = KC * R
    ORDER = [q // 2 if q % 2 == 0 else KC - 1 - q // 2 for q in range(KC)]

    def tile_of(v):
        return ORDER[v % UNITS // R]

    groups = []
    for u in range(UNITS):
        n = KC - tile_of(u)
        sizes = [n] if n <= 4 else [(n + 1) // 2, n // 2]
        for q, size in enumerate(sizes):
            groups.append((u, sum(sizes[:q]), size))
    BANKFULS = len(groups)
    assert BANKFULS % 2 == 0

    def groups_through(u):
        return sum(1 for g in groups if g[0] <= u)

    with ExitStack() as ctx:
        def sb(part, shape, dtype=F32):
            return ctx.enter_context(nc.sbuf_tensor(f"l3s_{part}", shape, dtype))

        loaded, stack, values = entry
        pt = sb("pt", [P, 2, R, KC, P])
        heads_out = core["areas"][1][:, 0:2 * TOK].rearrange("p (a n) -> p a n", a=2)
        mx, sm = sb("mx", [P, RING]), sb("sm", [P, RING])
        ex = ([core["xn"][:, 4 * n:4 * n + 4, :].rearrange("p a d -> p (a d)") for n in range(4)]
              + [core["xt"][:, n // 2, TOK * (n % 2):TOK * (n % 2 + 1)] for n in range(4)])

        fetch(nc.sync, following)
        with nc.Fori(0, ENTRIES // BODY) as jj:
            sem, clear_semaphores = named_semaphores(nc, "l3s")
            scores_ready, measured, exped, inverted = sem("scores_ready"), sem("measured"), sem("exped"), sem("inverted")
            masked, turned, stored = sem("masked"), sem("turned"), [sem("stored0"), sem("stored1")]
            out_ready, out_stored = sem("out_ready"), sem("out_stored")
            out_sent = [sem(f"out_sent{e}") for e in range(BODY)]

            with nc.Block() as block:
                @block.sync
                def _(sp):
                    load_entry(sp, scratch, entry, BODY * jj + 1, 1)
                    for e in range(BODY):
                        sp.wait_ge(out_ready, KC * (e + 1))
                        if e < BODY - 1:
                            load_entry(sp, scratch, entry, BODY * jj + e + 2, e % 2)
                        sp.wait_ge(out_stored, KC * (e + 1))
                        sp.dma_start(out_scratch[bass.ds(BODY * jj + e, 1)].rearrange("a p n -> p (a n)"),
                                     heads_out[:, e % 2, :]).then_inc(out_sent[e], 16)
                    for e in range(BODY):
                        sp.wait_ge(out_sent[e], 16)

                @block.gpsimd
                def _(pool):
                    for v in range(BODY * UNITS):
                        si = tile_of(v)
                        pool.wait_ge(inverted, v + 1)
                        nc.gpsimd.tensor_tensor(ex[v % RING][:, si * P:], ex[v % RING][:, si * P:],
                                                sm[:, v % RING:v % RING + 1].to_broadcast([P, TOK - si * P]), ALU.mult)
                        pool.drain()
                        nc.gpsimd.affine_select(out=ex[v % RING][:, si * P:(si + 1) * P], in_=ex[v % RING][:, si * P:(si + 1) * P],
                                                compare_op=ALU.is_gt, fill=0.0, base=0, pattern=[[1, P]],
                                                channel_multiplier=-1).then_inc(masked, 1)

                @block.tensor
                def _(pe):
                    def ends_at(si):
                        return max(range(si, KC), key=lambda c: ((c - si) % R, c))

                    def scores(v):
                        p, si, r = v // UNITS % 2, tile_of(v), v % R
                        if v >= 2:
                            pe.wait_ge(exped, v - 1)
                        for h in range(2):
                            for s in range(2):
                                last = nc.tensor.matmul(ps[:, 2 * (v % 2) + h, :],
                                                        stack[p][0][s][:, r, si * P:(si + 1) * P],
                                                        stack[p][1][s][:, r, h * 512:(h + 1) * 512],
                                                        start=(s == 0), stop=(s == 1))
                        last.then_inc(scores_ready, 1)

                    def turn(v):
                        e, si = v // UNITS, tile_of(v)
                        pe.wait_ge(masked, v + 1)
                        for g, (u, c0, size) in enumerate(groups):
                            if u != v % UNITS:
                                continue
                            n = BANKFULS * e + g
                            if n >= 2:
                                pe.wait_ge(stored[n % 2], n // 2)
                            for c in range(size):
                                last = nc.tensor.transpose(ps[:, 4 + n % 2, c * P:(c + 1) * P],
                                                           ex[v % RING][:, (si + c0 + c) * P:(si + c0 + c + 1) * P],
                                                           core["ident"][:, :])
                            last.then_inc(turned, 1)

                    def output(w, q):
                        e, si = w // KC, ORDER[w % KC]
                        chunks = [c for c in range(si, KC) if (c - si) % R == q]
                        if q == 0:
                            n = BANKFULS * e + groups_through(w % KC * R + R - 1)
                            pe.wait_ge(stored[0], (n + 1) // 2)
                            pe.wait_ge(stored[1], n // 2)
                            if w >= 2:
                                pe.wait_ge(out_stored, w - 1)
                        for c in chunks:
                            for r in range(R):
                                last = nc.tensor.matmul(ps[r * W:(r + 1) * W, 6 + w % 2, 0:P],
                                                        values[:, e % 2, c, r * W:(r + 1) * W],
                                                        pt[:, w % 2, r, c - si, :], start=(c == si),
                                                        stop=(c == ends_at(si)))
                        if chunks and chunks[-1] == ends_at(si):
                            last.then_inc(out_ready, 1)

                    for v in range(BODY * UNITS + OUT):
                        if v < BODY * UNITS and v % UNITS == 0:
                            e = v // UNITS
                            pe.wait_ge(loaded[e % 2], 16 * LOADS * (BODY // 2) * jj + 16 * LOADS * (e // 2 + 1))
                        if v < BODY * UNITS:
                            scores(v)
                        if TURN <= v < BODY * UNITS + TURN:
                            turn(v - TURN)
                        if v >= OUT:
                            output((v - OUT) // R, (v - OUT) % R)

                def store_turned(eng, op, v, side):
                    if v >= BODY * UNITS:
                        return
                    e, w = v // UNITS, v // R
                    for g, (u, c0, size) in enumerate(groups):
                        n = BANKFULS * e + g
                        if u != v % UNITS or n % 2 != side:
                            continue
                        eng.wait_ge(turned, n + 1)
                        if w >= 2:
                            eng.wait_ge(out_ready, w - 1)
                        dst = pt[:, w % 2, v % R, c0:c0 + size, :].rearrange("p c n -> p (c n)")
                        src = ps[:, 4 + side, 0:size * P]
                        if side == 0:
                            last = op.activation(dst, src, ACT.Copy)
                        else:
                            last = op.tensor_copy(dst, src)
                        last.then_inc(stored[side], 1)

                @block.scalar
                def _(act):
                    for v in range(BODY * UNITS + OUT):
                        if v >= STORE:
                            store_turned(act, nc.scalar, v - STORE, 0)
                        if v < BODY * UNITS:
                            act.wait_ge(measured, v + 1)
                            if v >= RING:
                                act.wait_ge(turned, BANKFULS * ((v - RING) // UNITS) + groups_through((v - RING) % UNITS))
                            nc.scalar.activation(ex[v % RING][:, :], ps[:, 2 * (v % 2):2 * (v % 2) + 2, :].rearrange("p a n -> p (a n)"),
                                                 ACT.Exp, bias=mx[:, v % RING:v % RING + 1],
                                                 accum_out=sm[:, v % RING:v % RING + 1]).then_inc(exped, 1)
                        if v >= OUT and (v - OUT) % R == R - 1:
                            w = (v - OUT) // R
                            act.wait_ge(out_ready, w + 1)
                            si = ORDER[w % KC]
                            if w % KC == 0 and w // KC >= 2:
                                act.wait_ge(out_sent[w // KC - 2], 16)
                            copy_bank(nc, heads_out[:, w // KC % 2, si * P:(si + 1) * P],
                                      ps[:, 6 + w % 2, 0:P]).then_inc(out_stored, 1)

                @block.vector
                def _(dve):
                    for v in range(BODY * UNITS + OUT):
                        if v < BODY * UNITS:
                            dve.wait_ge(scores_ready, v + 1)
                            nc.vector.tensor_reduce(mx[:, v % RING:v % RING + 1],
                                                    ps[:, 2 * (v % 2):2 * (v % 2) + 2, :].rearrange("p a n -> p (a n)"),
                                                    AX_X, ALU.max, negate=True).then_inc(measured, 1)
                        if v >= STORE:
                            store_turned(dve, nc.vector, v - STORE, 1)
                        if 1 <= v <= BODY * UNITS:
                            dve.wait_ge(exped, v)
                            nc.vector.reciprocal(sm[:, (v - 1) % RING:(v - 1) % RING + 1],
                                                 sm[:, (v - 1) % RING:(v - 1) % RING + 1]).then_inc(inverted, 1)
            clear_semaphores()
        nc.sync.wait_ge(loaded[0], 16 * LOADS * (ENTRIES // 2 + 1))
        nc.all_engine_barrier()


def self_out_weights(a):
    def make(carve):
        w = carve([P, GROUPS, D])
        bias_row = carve([P, D])
        gb = carve([P, 2, DC])
        loads = [(w[:, :, :], a["L3_xattn_a1_li1_w"].rearrange("(g p) n -> p g n", p=P)),
                 (bias_row[:, :], rows(a["L3_xattn_a1_li1_b"])),
                 (gb[:, 0, :], columns(a["L3_xattn_a1_ln3_g"])), (gb[:, 1, :], columns(a["L3_xattn_a1_ln3_b"]))]
        return loads, (w, bias_row, gb)
    return make


def mlp_weights(a, pfx, second):
    def make(carve):
        w2, b2 = carve([P, DC, FF]), carve([P, FC])
        w3, b3 = carve([P, FC, D]), carve([P, D])
        gb, ln2 = carve([P, 2, DC]), None
        loads = [(w2[:, :, :], a[pfx + "li2_w"].rearrange("(c p) n -> p c n", p=P)), (b2[:, :], columns(a[pfx + "li2_b"])),
                 (w3[:, :, :], a[pfx + "li3_w"].rearrange("(c p) n -> p c n", p=P)), (b3[:, :], rows(a[pfx + "li3_b"]))]
        if second:
            loads += [(gb[:, k, :], columns(a["L3_ffn_" + n])) for k, n in enumerate(("ln_gamma", "ln_beta"))]
        else:
            ln2 = carve([P, 2, D])
            loads += [(gb[:, k, :], columns(a["L3_xattn_a2_lnx_" + n])) for k, n in enumerate("gb")]
            loads += [(ln2[:, k, :], rows(a["L3_xattn_ln2_" + n])) for k, n in enumerate("gb")]
        return loads, (w2, b2, w3, b3, gb, ln2)
    return make


def stage_mlp(core, x1, xo, second, plan, following, front=None, heads_scratch=None):
    nc, ps = core["nc"], core["ps"]
    name = "l3m2" if second else "l3m1"
    gate = core["gate_attn"][:, 3:4]
    ring = 1 if front else 2
    with ExitStack() as ctx:
        _, weights_in, weights_total, (w2, b2, w3, b3, gb, ln2) = plan

        def sb(part, shape):
            return ctx.enter_context(nc.sbuf_tensor(f"{name}_{part}", shape, F32))

        sem, clear_semaphores = named_semaphores(nc, name)
        summed, hid_ready, hid_stored = sem("summed"), sem("hid_ready"), sem("hid_stored")
        out_ready, out_added = sem("out_ready"), sem("out_added")
        if front:
            _, front_in, front_total, (w1, b1, front_gb) = front
            bias_added, front_ready, front_added = sem("bias_added"), sem("front_ready"), sem("front_added")
            heads_in = [sem(f"heads_in{j}") for j in range(PAIRS)]
            (norm0_measure, norm0_root, norm0_normalise, norm0_turn, norm0_store,
             norm0_stored) = layer_norm(core, ctx, sem, name + "_norm0", on_vector=True)
            heads = sb("heads", [P, 4, GROUPS, PAIR])
        (norm1_measure, norm1_root, norm1_normalise, norm1_turn, norm1_store,
         norm1_stored) = layer_norm(core, ctx, sem, name + "_norm1", on_vector=True)
        (norm2_measure, norm2_root, norm2_normalise, norm2_turn, norm2_store,
         norm2_stored) = layer_norm(core, ctx, sem, name + "_norm2", on_vector=True)
        ht = sb("ht", [P, 2, FC, PAIR])

        def x1_tile(i):
            return x1[:, i, :]

        whole, middle = (tiles_of(core["x"]), tiles_of(core["xn"])) if second else (x1_tile, x1_tile)

        with nc.Block() as block:
            @block.sync
            def _(sp):
                if front:
                    for j in range(PAIRS):
                        b, at = j // (PAIRS // B), (j % (PAIRS // B)) * PAIR
                        if j >= 4:
                            sp.wait_ge(front_ready, j - 3)
                        sp.dma_start(heads[:, j % 4], heads_scratch[b * GROUPS:(b + 1) * GROUPS, :, at:at + PAIR]
                                     .rearrange("g p n -> p g n")).then_inc(heads_in[j], 16)
                        if j == 1:
                            fetch(sp, plan)
                    sp.wait_ge(norm0_stored, PAIRS)
                fetch(sp, following)

            @block.gpsimd
            def _(pool):
                if front:
                    pool.wait_ge(front_in, front_total)
                    for j in range(PAIRS):
                        for u in range(2):
                            last = nc.gpsimd.tensor_tensor(xo[:, 2 * j + u, :], x1[:, 2 * j + u, :], b1[:, :], ALU.add)
                        last.then_inc(bias_added, 1)
                pool.wait_ge(weights_in, weights_total)
                for j in range(PAIRS):
                    if front:
                        pool.wait_ge(norm0_stored, j + 1)
                    for u in range(2):
                        i = 2 * j + u
                        nc.gpsimd.tensor_tensor(xo[:, i, :], xo[:, i, :], x1[:, i, :], ALU.add)
                    pool.drain()
                    for u in range(2):
                        i = 2 * j + u
                        last = nc.gpsimd.tensor_tensor(xo[:, i, :], xo[:, i, :], b3[:, :], ALU.add)
                    last.then_inc(summed, 1)

            @block.tensor
            def _(pe):
                def front_product(j):
                    pe.wait_ge(heads_in[j], 16)
                    if j >= 1:
                        pe.wait_ge(front_added, j)
                    for u in range(2):
                        for g in range(GROUPS):
                            last = nc.tensor.matmul(ps[:, 5, u * D:(u + 1) * D], heads[:, j % 4, g, u * P:(u + 1) * P],
                                                    w1[:, g, :], start=(g == 0), stop=(g == GROUPS - 1))
                    last.then_inc(front_ready, 1)

                if front:
                    pe.wait_ge(front_in, front_total)
                    front_product(0)
                    front_product(1)
                    norm0_turn(pe, 0, tiles_of(core["xn"]), bank=6)
                pe.wait_ge(weights_in, weights_total)
                for j in range(PAIRS + 3):
                    if j < PAIRS:
                        if front:
                            pe.wait_ge(norm0_stored, j + 1)
                        for f in range(FC):
                            n = FC * j + f
                            if n >= 4:
                                pe.wait_ge(hid_stored, n - 3)
                            for dc in range(DC):
                                last = nc.tensor.matmul(ps[:, n % 4, 0:PAIR], w2[:, dc, f * P:(f + 1) * P],
                                                        core["xt"][:, dc, PAIR * j:PAIR * (j + 1)],
                                                        start=(dc == 0), stop=(dc == DC - 1))
                            last.then_inc(hid_ready, 1)
                    if j >= 3:
                        norm2_turn(pe, j - 3, tiles_of(core["xn"]))
                    if 1 <= j <= PAIRS:
                        k = j - 1
                        pe.wait_ge(hid_stored, FC * (k + 1))
                        if k >= ring:
                            pe.wait_ge(out_added, k - ring + 1)
                        for u in range(2):
                            for f in range(FC):
                                last = nc.tensor.matmul(ps[:, 4 + k % ring, u * D:(u + 1) * D], ht[:, k % 2, f, u * P:(u + 1) * P],
                                                        w3[:, f, :], start=(f == 0), stop=(f == FC - 1))
                        last.then_inc(out_ready, 1)
                    if front and j + 1 < PAIRS:
                        norm0_turn(pe, j + 1, tiles_of(core["xn"]), bank=6)
                    if front and j + 2 < PAIRS:
                        front_product(j + 2)

            @block.scalar
            def _(act):
                if front:
                    act.wait_ge(front_in, front_total)
                    norm0_store(act, 0, [(core["xt"], front_gb[:, 0, :], front_gb[:, 1, :])], bank=6)
                act.wait_ge(weights_in, weights_total)
                for j in range(PAIRS + 3):
                    if j < PAIRS:
                        for f in range(FC):
                            n = FC * j + f
                            act.wait_ge(hid_ready, n + 1)
                            if f == 0 and j >= 2:
                                act.wait_ge(out_ready, j - 1)
                            nc.scalar.activation(ht[:, j % 2, f, :], ps[:, n % 4, 0:PAIR], ACT.Gelu,
                                                 bias=b2[:, f:f + 1]).then_inc(hid_stored, 1)
                    if j >= 3:
                        norm2_store(act, j - 3, [(core["xt"], gb[:, 0, :], gb[:, 1, :])])
                    if front and j + 1 < PAIRS:
                        norm0_store(act, j + 1, [(core["xt"], front_gb[:, 0, :], front_gb[:, 1, :])], bank=6)

            @block.vector
            def _(dve):
                def front_sum(j):
                    dve.wait_ge(front_ready, j + 1)
                    dve.wait_ge(bias_added, j + 1)
                    xo2 = pair_of(xo, j)
                    nc.vector.tensor_tensor(xo2, ps[:, 5, :], xo2, ALU.add).then_inc(front_added, 1)
                    dve.drain()
                    norm0_measure(dve, j, tiles_of(xo))
                    norm0_normalise(dve, j, tiles_of(xo), tiles_of(core["xn"]))

                if front:
                    front_sum(0)
                    front_sum(1)
                dve.wait_ge(weights_in, weights_total)
                for j in range(PAIRS):
                    if front and j + 2 < PAIRS:
                        front_sum(j + 2)
                    dve.wait_ge(out_ready, j + 1)
                    dve.wait_ge(summed, j + 1)
                    xo2 = pair_of(xo, j)
                    if second:
                        nc.vector.tensor_tensor(xo2, ps[:, 4 + j % ring, :], xo2, ALU.add).then_inc(out_added, 1)
                        dve.drain()
                        x2 = pair_of(core["x"], j)
                        nc.vector.scalar_tensor_tensor(x2, xo2, gate, x2, ALU.mult, ALU.add)
                    else:
                        nc.vector.tensor_tensor(pair_of(x1, j), ps[:, 4 + j % ring, :], xo2, ALU.add).then_inc(out_added, 1)
                    dve.drain()
                    norm1_measure(dve, j, whole)
                    norm1_normalise(dve, j, whole, middle)
                    if second:
                        dve.drain()
                    else:
                        affine_rows(nc, dve, x1[:, 2 * j:2 * j + 2, :], ln2)
                    norm2_measure(dve, j, middle)
                    norm2_normalise(dve, j, middle, tiles_of(core["xn"]))
        clear_semaphores()


def layout_l3(a):
    def layout(carve):
        HD = L3_HEADS * L3_WIDTH
        wq, wk, wv, wo = carve([P, DC, HD]), carve([P, HD]), carve([P, HD]), carve([P, HD // P, D])
        by_head = [(wk[:, :], a["L3_xattn_a2_wk"]), (wv[:, :], a["L3_xattn_a2_wv"])]
        by_head += [(wq[:, c, :], a["L3_xattn_a2_wq"][:, c * P:(c + 1) * P, :]) for c in range(DC)]
        loads = [(dst.rearrange("p (h d) -> p h d", h=L3_HEADS), src.rearrange("h p d -> p h d")) for dst, src in by_head]
        loads += [(wo[:, :, :], a["L3_xattn_a2_li1_w"].rearrange("(c p) n -> p c n", p=P))]

        def finish(sb):
            wq_t = sb("wq_t", [P, HD // P, D])
            turns = [([wq[:, dc, c * P:(c + 1) * P] for c in (2 * q, 2 * q + 1) for dc in range(DC)],
                      wq_t[:, 2 * q:2 * q + 2, :].rearrange("p c d -> p (c d)")) for q in range(2)]
            return wq_t, wo, turns, wk, wv
        return loads, finish
    return layout


def layer_3(core, a, plans):
    nc = core["nc"]
    scratch = self_attention_scratch(nc)
    with ExitStack() as ctx:
        x1 = ctx.enter_context(nc.sbuf_tensor("l3_x1", [P, TILES, D], F32))
        with ExitStack() as entries_ctx:
            entry = place_entries(nc, entries_ctx)
            stage_self_project(core, a, x1, scratch, entry, plans["l3p"])
            stage_self_attention(core, scratch, entry, plans["l3o"])
        xo = ctx.enter_context(nc.sbuf_tensor("l3_xo", [P, TILES, D], F32))
        stage_mlp(core, x1, xo, False, plans["l3m1"], plans["l3a"], plans["l3o"], scratch[2])
        stage_attention(core, a, "l3a", 32, 32 ** -0.5, plans["l3a"], plans["l3m2"], tiles_of(x1), tiles_of(xo),
                        None, True, True, core["ctx_norm_t"])
        stage_mlp(core, x1, xo, True, plans["l3m2"], plans["l3f"])
    stage_experts(core, a, "l3f", top=2, full=TOP2_FULL, half=TOP2_HALF, capacity=None, plan=plans["l3f"], following=None,
                  w1="L3_ffn_gate_up_w", w2="L3_ffn_down_w", swiglu=True, gate=core["gate_ffn"][:, 3:4],
                  norm_behind=False)


def build_program(nc, a, out):
    a = dict(a, out=out)
    with ExitStack() as ctx:
        ctx.enter_context(nc.allow_non_contiguous_dma(reason="vectors of up to 1024 values, one per partition"))
        core = make_core(nc, ctx)
        makes = {
            "l0f": experts_weights(a, "L0_ffn_Wr"),
            "l1a": one_head_weights(a),
            "l1f": adapter_weights(a),
            "l2a": attention_weights(a, layout_l2(a), None, None),
            "l2f": low_rank_weights(a),
            "l3p": self_project_weights(a),
            "l3o": self_out_weights(a),
            "l3m1": mlp_weights(a, "L3_xattn_a1_", False),
            "l3a": attention_weights(a, layout_l3(a), "L3_xattn_a2_li1_b", ("L3_xattn_a2_ln3_g", "L3_xattn_a2_ln3_b")),
            "l3m2": mlp_weights(a, "L3_xattn_a2_", True),
            "l3f": experts_weights(a, "L3_ffn_router_w", ("L3_ffn_ln_gamma", "L3_ffn_ln_beta"),
                                   ("L3_ffn_shared_gate_up_w", "L3_ffn_shared_down_w")),
        }
        plans = {name: plan_weights(core, n % 2, name, make) for n, (name, make) in enumerate(makes.items())}
        with ExitStack() as first_ctx:
            def carve(shape):
                return first_ctx.enter_context(nc.sbuf_tensor(f"l0a_weights{nc.next_id()}", shape, F32))

            loads, needed = attention_weights(a, layout_l0(a), "L0_xattn_bo", None)(carve)
            plan = (loads, nc.alloc_semaphore("l0a_weights_in"), 16 * len(loads), needed)
            stage_attention(core, a, "l0a", 64, 64 ** -0.5, plan, plans["l0f"], tiles_of(core["x"]), tiles_of(core["x"]),
                            core["gate_attn"][:, 0:1], True, None, core["ctx_t"], opens=True)
        stage_experts(core, a, "l0f", top=1, full=E, half=0, capacity=T // E, plan=plans["l0f"], following=plans["l1a"],
                      w1="L0_ffn_W1", w2="L0_ffn_W2", swiglu=False, gate=core["gate_ffn"][:, 0:1])
        stage_one_head(core, a, plans["l1a"], plans["l1f"])
        stage_adapter(core, a, plans["l1f"], plans["l2a"])
        stage_attention(core, a, "l2a", 16, 16 ** -0.5, plans["l2a"], plans["l2f"], tiles_of(core["x"]), tiles_of(core["x"]),
                        core["gate_attn"][:, 2:3], None, None, core["ctx_t"])
        stage_low_rank(core, a, plans["l2f"], plans["l3p"])
        layer_3(core, a, plans)


_INS = ['x', 'ctx_512', 'g_xattn', 'g_ffn', 'L0_xattn_Wq', 'L0_xattn_Wk', 'L0_xattn_Wv', 'L0_xattn_Wo', 'L0_xattn_bo',
        'L0_ffn_Wr', 'L0_ffn_W1', 'L0_ffn_W2', 'L1_xattn_Wq', 'L1_xattn_bq', 'L1_xattn_Wk', 'L1_xattn_bk',
        'L1_xattn_Wv', 'L1_xattn_bv', 'L1_ffn_base_W', 'L1_ffn_base_b', 'L1_ffn_disc_mu', 'L1_ffn_disc_sigma',
        'L1_ffn_down_W', 'L1_ffn_down_b', 'L1_ffn_up_W', 'L1_ffn_up_b', 'L1_ffn_conv_W', 'L1_ffn_conv_b',
        'L2_xattn_Wq', 'L2_xattn_Wkv', 'L2_xattn_Wo', 'L2_ffn_U1', 'L2_ffn_V1', 'L2_ffn_b1', 'L2_ffn_U2', 'L2_ffn_V2',
        'L2_ffn_b2', 'L3_xattn_ln1_g', 'L3_xattn_ln1_b', 'L3_xattn_ln2_g', 'L3_xattn_ln2_b', 'L3_xattn_a1_wq',
        'L3_xattn_a1_wk', 'L3_xattn_a1_wv', 'L3_xattn_a1_li1_w', 'L3_xattn_a1_li1_b', 'L3_xattn_a1_lnx_g',
        'L3_xattn_a1_lnx_b', 'L3_xattn_a1_lny_g', 'L3_xattn_a1_lny_b', 'L3_xattn_a1_ln3_g', 'L3_xattn_a1_ln3_b',
        'L3_xattn_a1_li2_w', 'L3_xattn_a1_li2_b', 'L3_xattn_a1_li3_w', 'L3_xattn_a1_li3_b', 'L3_xattn_a2_wq',
        'L3_xattn_a2_wk', 'L3_xattn_a2_wv', 'L3_xattn_a2_li1_w', 'L3_xattn_a2_li1_b', 'L3_xattn_a2_lnx_g',
        'L3_xattn_a2_lnx_b', 'L3_xattn_a2_lny_g', 'L3_xattn_a2_lny_b', 'L3_xattn_a2_ln3_g', 'L3_xattn_a2_ln3_b',
        'L3_xattn_a2_li2_w', 'L3_xattn_a2_li2_b', 'L3_xattn_a2_li3_w', 'L3_xattn_a2_li3_b', 'L3_ffn_ln_gamma',
        'L3_ffn_ln_beta', 'L3_ffn_router_w', 'L3_ffn_gate_up_w', 'L3_ffn_down_w', 'L3_ffn_shared_gate_up_w',
        'L3_ffn_shared_down_w']


def kernel(**inputs):
    import numpy as _np
    import concourse.bacc as _bacc
    from concourse import mybir as _mybir
    from concourse.bass_utils import run_bass_kernel_spmd as _run

    nc = _bacc.Bacc("TRN2", target_bir_lowering=False, num_devices=1)
    arrays, args = {}, {}
    for name in _INS:
        array = _np.ascontiguousarray(inputs[name])
        arrays[f"in_{name}_dram"] = array
        args[name] = nc.dram_tensor(f"in_{name}_dram", array.shape, _mybir.dt.from_np(array.dtype),
                                    kind="ExternalInput").ap()
    out = nc.dram_tensor("out_0_dram", (B, TOK, D), _mybir.dt.float32, kind="ExternalOutput").ap()
    build_program(nc, args, out)
    r = _run(nc, [arrays], core_ids=[0])
    return r.results[0]["out_0_dram"]
```
